# Optimizing a Trainium2 kernel written in Bass

```python
import numpy as np
import jax
import jax.numpy as jnp

def _softmax(x, axis=-1):
    return jax.nn.softmax(x, axis=axis)

def _gelu(x):
    return jax.nn.gelu(x, approximate=True)

def _silu(x):
    return jax.nn.silu(x)

def _sigmoid(x):
    return jax.nn.sigmoid(x)

def _layernorm(x, axis=-1, eps=1e-05):
    m = jnp.mean(x, axis=axis, keepdims=True)
    v = jnp.var(x, axis=axis, keepdims=True)
    return (x - m) / jnp.sqrt(v + eps)

def _scatter_add(tgt, idx, src, axis=0):
    return tgt.at[idx].add(src)

def _segment_sum(src, seg, n):
    return jax.ops.segment_sum(src, seg, n)
kernel_name = 'mk_seq_postln_d4_jaxref_r8_bd7174'

def setup_inputs(seed: int=0):
    np.random.seed(seed)
    _w = jnp.asarray

    def _L0_attn_setup():
        import jax, jax.numpy as jnp
        import numpy as np
        import math
        DIM = 128
        NUM_HEADS = 16
        HEAD_DIM = DIM // NUM_HEADS
        MAX_BIAS = 8.0
        SCALE = HEAD_DIM ** (-0.5)

        def _alibi_slopes(n):

            def pow2(n):
                start = 2.0 ** (-2.0 ** (-(math.log2(n) - 3)))
                return [start * start ** i for i in range(n)]
            if math.log2(n).is_integer():
                return pow2(n)
            c = 2 ** math.floor(math.log2(n))
            return pow2(c) + _alibi_slopes(2 * c)[0::2][:n - c]

        def _rotate_half(t):
            t1, t2 = jnp.split(t, 2, axis=-1)
            return jnp.concatenate([-t2, t1], axis=-1)
        key = jax.random.key(seed)
        k1, k2, k3, k4 = jax.random.split(key, 4)
        B, N, C = (2, 256, DIM)
        x = jax.random.normal(k1, (B, N, C), dtype=jnp.float32)
        qkv_w = jax.random.normal(k2, (3 * C, C), dtype=jnp.float32) * C ** (-0.5)
        proj_w = jax.random.normal(k3, (C, C), dtype=jnp.float32) * C ** (-0.5)
        proj_b = jax.random.normal(k4, (C,), dtype=jnp.float32) * 0.01
        slopes = jnp.asarray(np.array(_alibi_slopes(NUM_HEADS), dtype=np.float32))
        return {'x': x, 'qkv_w': qkv_w, 'proj_w': proj_w, 'proj_b': proj_b, 'slopes': slopes}
    _L0_attn_in = _L0_attn_setup()

    def _L0_ffn_setup():
        import jax, jax.numpy as jnp
        import numpy as np
        D_IN, D_HID = (128, 512)

        def _ternary(key, shape):
            return jax.random.randint(key, shape, -1, 2).astype(jnp.float32)

        def _tlin(x, w, s):
            return jnp.einsum('bsi,oi->bso', x, w) * s
        key = jax.random.key(seed)
        ks = jax.random.split(key, 12)
        inv = lambda fan: 1.0 / np.sqrt(fan).astype(np.float32)
        return {'x': jax.random.normal(ks[0], (4, 256, D_IN), dtype=jnp.float32), 'w1_w': _ternary(ks[1], (D_HID, D_IN)), 'w1_s': jax.random.uniform(ks[2], (D_HID,), dtype=jnp.float32) * inv(D_IN), 'w2_w': _ternary(ks[3], (D_HID, D_IN)), 'w2_s': jax.random.uniform(ks[4], (D_HID,), dtype=jnp.float32) * inv(D_IN), 'h1_w': _ternary(ks[5], (D_HID, D_HID)), 'h1_s': jax.random.uniform(ks[6], (D_HID,), dtype=jnp.float32) * inv(D_HID), 'h2_w': _ternary(ks[7], (D_HID, D_HID)), 'h2_s': jax.random.uniform(ks[8], (D_HID,), dtype=jnp.float32) * inv(D_HID), 'w3_w': _ternary(ks[9], (D_IN, D_HID)), 'w3_s': jax.random.uniform(ks[10], (D_IN,), dtype=jnp.float32) * inv(D_HID)}
    _L0_ffn_in = _L0_ffn_setup()

    def _L1_attn_setup():
        import jax, jax.numpy as jnp
        import numpy as np
        DIM = 128
        DT_RANK = 64
        D_STATE = 16
        BATCH = 2
        SEQ = 256
        EPS = 1e-05

        def _selective_scan(u, delta, A, B, C, D):
            deltaA = jnp.exp(jnp.einsum('bld,dn->bldn', delta, A))
            deltaBu = jnp.einsum('bld,bln->bldn', delta * u, B)

            def step(h, inp):
                dA, dBu, Ct = inp
                h = dA * h + dBu
                y = jnp.einsum('bdn,bn->bd', h, Ct)
                return (h, y)
            h0 = jnp.zeros((u.shape[0], u.shape[2], A.shape[1]), u.dtype)
            xs = (jnp.moveaxis(deltaA, 1, 0), jnp.moveaxis(deltaBu, 1, 0), jnp.moveaxis(C, 1, 0))
            _, ys = jax.lax.scan(step, h0, xs)
            y = jnp.moveaxis(ys, 0, 1)
            return y + u * D

        def _ssm(u, deltaBC_W, dt_W, dt_b, A_log, D):
            A = -jnp.exp(A_log)
            dbc = u @ deltaBC_W.T
            delta = dbc[..., :DT_RANK]
            B = dbc[..., DT_RANK:DT_RANK + D_STATE]
            C = dbc[..., DT_RANK + D_STATE:]
            delta = jax.nn.softplus(delta @ dt_W.T + dt_b)
            return _selective_scan(u, delta, A, B, C, D)
        key = jax.random.key(seed)
        ks = jax.random.split(key, 8)
        s = 0.02
        x = jax.random.normal(ks[0], (BATCH, SEQ, DIM), jnp.float32)
        ln_w = jnp.ones((DIM,), jnp.float32)
        ln_b = jnp.zeros((DIM,), jnp.float32)
        proj_W = jax.random.normal(ks[1], (DIM, DIM), jnp.float32) * s
        proj_b = jnp.zeros((DIM,), jnp.float32)
        fconv_W = jax.random.normal(ks[2], (DIM, DIM), jnp.float32) * s
        fconv_b = jnp.zeros((DIM,), jnp.float32)
        bconv_W = jax.random.normal(ks[3], (DIM, DIM), jnp.float32) * s
        bconv_b = jnp.zeros((DIM,), jnp.float32)
        deltaBC_W = jax.random.normal(ks[4], (DT_RANK + 2 * D_STATE, DIM), jnp.float32) * s
        dt_W = jax.random.normal(ks[5], (DIM, DT_RANK), jnp.float32) * s
        dt_b = jnp.zeros((DIM,), jnp.float32)
        A_log = jnp.log(jnp.tile(jnp.arange(1, D_STATE + 1, dtype=jnp.float32)[None, :], (DIM, 1)))
        D = jnp.ones((DIM,), jnp.float32)
        return dict(x=x, ln_w=ln_w, ln_b=ln_b, proj_W=proj_W, proj_b=proj_b, fconv_W=fconv_W, fconv_b=fconv_b, bconv_W=bconv_W, bconv_b=bconv_b, deltaBC_W=deltaBC_W, dt_W=dt_W, dt_b=dt_b, A_log=A_log, D=D)
    _L1_attn_in = _L1_attn_setup()

    def _L1_ffn_setup():
        import math
        import jax, jax.numpy as jnp
        import numpy as np
        D_MODEL = 128
        D_HIDDEN = 256
        N_EXPERTS = 8
        TOP_K = 2
        CAPACITY_FACTOR = 1.25

        def _moe_forward(x, w_router, w_gate, w_down):
            B, T, D = x.shape
            N = B * T
            xf = x.reshape(N, D)
            logits = xf.astype(jnp.float32) @ w_router.T
            gates = jax.nn.softmax(logits, axis=-1)
            topk_gates, topk_idx = jax.lax.top_k(gates, TOP_K)
            expert_mask = jax.nn.one_hot(topk_idx, N_EXPERTS, dtype=jnp.int32).sum(axis=1)
            capacity = math.ceil(N / N_EXPERTS * CAPACITY_FACTOR)
            position_in_expert = jnp.cumsum(expert_mask, axis=0) - 1
            expert_mask = expert_mask * (position_in_expert < capacity)
            keep = jnp.take_along_axis(expert_mask, topk_idx, axis=1) > 0
            topk_gates = topk_gates * keep
            topk_gates = topk_gates / (topk_gates.sum(axis=-1, keepdims=True) + 1e-06)
            hidden = jax.nn.silu(xf @ w_gate.T)
            combine = (topk_gates[:, :, None] * jax.nn.one_hot(topk_idx, N_EXPERTS, dtype=topk_gates.dtype)).sum(axis=1)
            y = jnp.zeros((N, D), dtype=x.dtype)
            for e in range(N_EXPERTS):
                y = y + combine[:, e:e + 1] * (hidden @ w_down[e].T)
            return y.reshape(B, T, D)
        key = jax.random.key(seed)
        k0, k1, k2, k3 = jax.random.split(key, 4)
        B, T = (2, 256)
        x = jax.random.normal(k0, (B, T, D_MODEL), dtype=jnp.float32)
        w_router = jax.random.normal(k1, (N_EXPERTS, D_MODEL), dtype=jnp.float32) * 0.02
        w_gate = jax.random.normal(k2, (D_HIDDEN, D_MODEL), dtype=jnp.float32) * 0.02
        w_down = jax.random.normal(k3, (N_EXPERTS, D_MODEL, D_HIDDEN), dtype=jnp.float32) * 0.02
        return {'x': x, 'w_router': w_router, 'w_gate': w_gate, 'w_down': w_down}
    _L1_ffn_in = _L1_ffn_setup()

    def _L2_attn_setup():
        import jax, jax.numpy as jnp
        import numpy as np
        HEADS = 8
        K_SIZE = 64
        key = jax.random.key(seed)
        k1, k2, k3, k4 = jax.random.split(key, 4)
        B, C, D = (4, 256, 128)
        return {'x': jax.random.normal(k1, (B, C, D), dtype=jnp.float32), 'Mq': jax.random.normal(k2, (D, HEADS * K_SIZE), dtype=jnp.float32) * 0.02, 'Mk': jax.random.normal(k3, (D, HEADS * K_SIZE), dtype=jnp.float32) * 0.02, 'Mv': jax.random.normal(k4, (D, 128), dtype=jnp.float32) * 0.02}
    _L2_attn_in = _L2_attn_setup()

    def _L2_ffn_setup():
        import jax, jax.numpy as jnp
        import numpy as np
        E, G, TOPK = (32, 16, 2)
        HID, INTER, A_INTER = (128, 256, 128)
        CAP_FACTOR = 1.25
        SCALE = 0.05

        def _stats(x):
            mean = x.mean(-1, keepdims=True)
            std = jnp.std(x, axis=-1, keepdims=True, ddof=1)
            mn = x.min(-1, keepdims=True)
            mx = x.max(-1, keepdims=True)
            l2 = jnp.linalg.norm(x, axis=-1, keepdims=True)
            sp = (jnp.abs(x) < 1e-06).astype(x.dtype).mean(-1, keepdims=True)
            return jnp.concatenate([mean, std, mn, mx, l2, sp], -1)
        key = jax.random.key(seed)
        ks = jax.random.split(key, 8)
        B, N = (4, 128)
        s = lambda k, shape, sc: jax.random.normal(k, shape, jnp.float32) * sc
        return {'x': jax.random.normal(ks[0], (B, N, HID), jnp.float32), 'r1_w': s(ks[1], (HID // 2, HID + 6), 0.02), 'r1_b': jnp.zeros((HID // 2,), jnp.float32), 'r2_w': s(ks[2], (E, HID // 2), 0.02), 'w_up': s(ks[3], (E, 2 * INTER, HID), 0.02), 'w_down': s(ks[4], (E, HID, INTER), 0.02), 'a_up': s(ks[5], (G, 2 * A_INTER, HID), 0.02), 'a_down': s(ks[6], (G, HID, A_INTER), 0.02)}
    _L2_ffn_in = _L2_ffn_setup()

    def _L3_attn_setup():
        import jax, jax.numpy as jnp
        import numpy as np
        B, S, E, H = (2, 256, 128, 16)
        HD = E // H

        def _rope_tables(seq_len, head_dim, dtype=jnp.float32):
            i = jnp.arange(head_dim // 2, dtype=dtype)
            angles = jnp.power(jnp.asarray(10000.0, dtype), 2.0 * i / head_dim)
            theta = jnp.arange(seq_len, dtype=dtype)[:, None] * angles[None, :]
            cos = jnp.cos(theta)[None, :, None, :]
            sin = jnp.sin(theta)[None, :, None, :]
            return (cos, sin)

        def _apply_rope(t, cos, sin):
            tr, ti = (t[..., 0::2], t[..., 1::2])
            out_r = tr * cos - ti * sin
            out_i = tr * sin + ti * cos
            return jnp.stack([out_r, out_i], axis=-1).reshape(t.shape)
        key = jax.random.key(seed)
        ks = jax.random.split(key, 5)
        x = jax.random.normal(ks[0], (B, S, E), dtype=jnp.float32)
        w_q = jax.random.normal(ks[1], (H * HD, E), dtype=jnp.float32) * 0.02
        w_k = jax.random.normal(ks[2], (H * HD, E), dtype=jnp.float32) * 0.02
        w_v = jax.random.normal(ks[3], (H * HD, E), dtype=jnp.float32) * 0.02
        w_o = jax.random.normal(ks[4], (E, H * HD), dtype=jnp.float32) * 0.02
        return {'x': x, 'w_q': w_q, 'w_k': w_k, 'w_v': w_v, 'w_o': w_o}
    _L3_attn_in = _L3_attn_setup()

    def _L3_ffn_setup():
        import jax, jax.numpy as jnp
        import numpy as np
        B, SEQ, D, E, F = (4, 128, 128, 8, 512)
        CAPACITY = 2
        key = jax.random.key(seed)
        ks = jax.random.split(key, 8)
        x = jax.random.normal(ks[0], (B, SEQ, D), jnp.float32)
        gate_weight = jax.random.normal(ks[1], (E, D), jnp.float32) * 0.006
        W1 = jax.random.normal(ks[2], (E, D, F), jnp.float32) * (1.0 / np.sqrt(D))
        b1 = jnp.zeros((E, F), jnp.float32)
        W2 = jax.random.normal(ks[3], (E, F, D), jnp.float32) * (1.0 / np.sqrt(F))
        b2 = jnp.zeros((E, D), jnp.float32)
        Ws1 = jax.random.normal(ks[4], (D, F), jnp.float32) * (1.0 / np.sqrt(D))
        bs1 = jnp.zeros((F,), jnp.float32)
        Ws2 = jax.random.normal(ks[5], (F, D), jnp.float32) * (1.0 / np.sqrt(F))
        bs2 = jnp.zeros((D,), jnp.float32)
        return {'x': x, 'gate_weight': gate_weight, 'W1': W1, 'b1': b1, 'W2': W2, 'b2': b2, 'Ws1': Ws1, 'bs1': bs1, 'Ws2': Ws2, 'bs2': bs2}
    _L3_ffn_in = _L3_ffn_setup()
    _d = {'L0_attn_x': _L0_attn_in['x'], 'L0_attn_qkv_w': _L0_attn_in['qkv_w'], 'L0_attn_proj_w': _L0_attn_in['proj_w'], 'L0_attn_proj_b': _L0_attn_in['proj_b'], 'L0_attn_slopes': _L0_attn_in['slopes'], 'L0_ffn_w1_w': _L0_ffn_in['w1_w'], 'L0_ffn_w1_s': _L0_ffn_in['w1_s'], 'L0_ffn_w2_w': _L0_ffn_in['w2_w'], 'L0_ffn_w2_s': _L0_ffn_in['w2_s'], 'L0_ffn_h1_w': _L0_ffn_in['h1_w'], 'L0_ffn_h1_s': _L0_ffn_in['h1_s'], 'L0_ffn_h2_w': _L0_ffn_in['h2_w'], 'L0_ffn_h2_s': _L0_ffn_in['h2_s'], 'L0_ffn_w3_w': _L0_ffn_in['w3_w'], 'L0_ffn_w3_s': _L0_ffn_in['w3_s'], 'L1_attn_ln_w': _L1_attn_in['ln_w'], 'L1_attn_ln_b': _L1_attn_in['ln_b'], 'L1_attn_proj_W': _L1_attn_in['proj_W'], 'L1_attn_proj_b': _L1_attn_in['proj_b'], 'L1_attn_fconv_W': _L1_attn_in['fconv_W'], 'L1_attn_fconv_b': _L1_attn_in['fconv_b'], 'L1_attn_bconv_W': _L1_attn_in['bconv_W'], 'L1_attn_bconv_b': _L1_attn_in['bconv_b'], 'L1_attn_deltaBC_W': _L1_attn_in['deltaBC_W'], 'L1_attn_dt_W': _L1_attn_in['dt_W'], 'L1_attn_dt_b': _L1_attn_in['dt_b'], 'L1_attn_A_log': _L1_attn_in['A_log'], 'L1_attn_D': _L1_attn_in['D'], 'L1_ffn_w_router': _L1_ffn_in['w_router'], 'L1_ffn_w_gate': _L1_ffn_in['w_gate'], 'L1_ffn_w_down': _L1_ffn_in['w_down'], 'L2_attn_Mq': _L2_attn_in['Mq'], 'L2_attn_Mk': _L2_attn_in['Mk'], 'L2_attn_Mv': _L2_attn_in['Mv'], 'L2_ffn_r1_w': _L2_ffn_in['r1_w'], 'L2_ffn_r1_b': _L2_ffn_in['r1_b'], 'L2_ffn_r2_w': _L2_ffn_in['r2_w'], 'L2_ffn_w_up': _L2_ffn_in['w_up'], 'L2_ffn_w_down': _L2_ffn_in['w_down'], 'L2_ffn_a_up': _L2_ffn_in['a_up'], 'L2_ffn_a_down': _L2_ffn_in['a_down'], 'L3_attn_w_q': _L3_attn_in['w_q'], 'L3_attn_w_k': _L3_attn_in['w_k'], 'L3_attn_w_v': _L3_attn_in['w_v'], 'L3_attn_w_o': _L3_attn_in['w_o'], 'L3_ffn_gate_weight': _L3_ffn_in['gate_weight'], 'L3_ffn_W1': _L3_ffn_in['W1'], 'L3_ffn_b1': _L3_ffn_in['b1'], 'L3_ffn_W2': _L3_ffn_in['W2'], 'L3_ffn_b2': _L3_ffn_in['b2'], 'L3_ffn_Ws1': _L3_ffn_in['Ws1'], 'L3_ffn_bs1': _L3_ffn_in['bs1'], 'L3_ffn_Ws2': _L3_ffn_in['Ws2'], 'L3_ffn_bs2': _L3_ffn_in['bs2']}
    _x0 = _d['L0_attn_x']
    _d['L0_attn_x'] = jax.random.normal(jax.random.fold_in(jax.random.key(seed), 1), (4, 512, 128), dtype=_x0.dtype)
    del _x0
    return _d

def reference(L0_attn_x, L0_attn_qkv_w, L0_attn_proj_w, L0_attn_proj_b, L0_attn_slopes, L0_ffn_w1_w, L0_ffn_w1_s, L0_ffn_w2_w, L0_ffn_w2_s, L0_ffn_h1_w, L0_ffn_h1_s, L0_ffn_h2_w, L0_ffn_h2_s, L0_ffn_w3_w, L0_ffn_w3_s, L1_attn_ln_w, L1_attn_ln_b, L1_attn_proj_W, L1_attn_proj_b, L1_attn_fconv_W, L1_attn_fconv_b, L1_attn_bconv_W, L1_attn_bconv_b, L1_attn_deltaBC_W, L1_attn_dt_W, L1_attn_dt_b, L1_attn_A_log, L1_attn_D, L1_ffn_w_router, L1_ffn_w_gate, L1_ffn_w_down, L2_attn_Mq, L2_attn_Mk, L2_attn_Mv, L2_ffn_r1_w, L2_ffn_r1_b, L2_ffn_r2_w, L2_ffn_w_up, L2_ffn_w_down, L2_ffn_a_up, L2_ffn_a_down, L3_attn_w_q, L3_attn_w_k, L3_attn_w_v, L3_attn_w_o, L3_ffn_gate_weight, L3_ffn_W1, L3_ffn_b1, L3_ffn_W2, L3_ffn_b2, L3_ffn_Ws1, L3_ffn_bs1, L3_ffn_Ws2, L3_ffn_bs2):

    def _L0_attn_ref(x, qkv_w, proj_w, proj_b, slopes):
        import jax, jax.numpy as jnp
        import numpy as np
        import math
        DIM = 128
        NUM_HEADS = 16
        HEAD_DIM = DIM // NUM_HEADS
        MAX_BIAS = 8.0
        SCALE = HEAD_DIM ** (-0.5)

        def _alibi_slopes(n):

            def pow2(n):
                start = 2.0 ** (-2.0 ** (-(math.log2(n) - 3)))
                return [start * start ** i for i in range(n)]
            if math.log2(n).is_integer():
                return pow2(n)
            c = 2 ** math.floor(math.log2(n))
            return pow2(c) + _alibi_slopes(2 * c)[0::2][:n - c]

        def _rotate_half(t):
            t1, t2 = jnp.split(t, 2, axis=-1)
            return jnp.concatenate([-t2, t1], axis=-1)
        B, N, C = x.shape
        H, D = (NUM_HEADS, HEAD_DIM)
        qkv = (x @ qkv_w.T).reshape(B, N, 3, H, D).transpose(2, 0, 3, 1, 4)
        q, k, v = (qkv[0], qkv[1], qkv[2])
        inv_freq = 1.0 / 10000.0 ** (jnp.arange(0, D, 2, dtype=jnp.float32) / D)
        freqs = jnp.arange(N, dtype=jnp.float32)[:, None] * inv_freq[None, :]
        sin = jnp.tile(jnp.sin(freqs), (1, 2))
        cos = jnp.tile(jnp.cos(freqs), (1, 2))
        q = q * cos + _rotate_half(q) * sin
        k = k * cos + _rotate_half(k) * sin
        attn = jnp.einsum('bhqd,bhkd->bhqk', q, k) * SCALE
        pos = jnp.arange(N, dtype=jnp.float32)
        diff = pos[None, :] - pos[:, None]
        diff = jnp.where(diff > 0, 0.0, diff)
        alibi = diff[None, :, :] * slopes[:, None, None] * MAX_BIAS
        attn = attn + alibi[None]
        w = jax.nn.softmax(attn, axis=-1)
        out = jnp.einsum('bhqk,bhkd->bhqd', w, v)
        out = out.transpose(0, 2, 1, 3).reshape(B, N, C)
        return out @ proj_w.T + proj_b

    def _L0_ffn_ref(x, w1_w, w1_s, w2_w, w2_s, h1_w, h1_s, h2_w, h2_s, w3_w, w3_s):
        import jax, jax.numpy as jnp
        import numpy as np
        D_IN, D_HID = (128, 512)

        def _ternary(key, shape):
            return jax.random.randint(key, shape, -1, 2).astype(jnp.float32)

        def _tlin(x, w, s):
            return jnp.einsum('bsi,oi->bso', x, w) * s
        h = jax.nn.silu(_tlin(x, w1_w, w1_s)) * _tlin(x, w2_w, w2_s)
        h = jax.nn.gelu(_tlin(h, h1_w, h1_s), approximate=False)
        h = jax.nn.gelu(_tlin(h, h2_w, h2_s), approximate=False)
        return _tlin(h, w3_w, w3_s)

    def _L1_attn_ref(x, ln_w, ln_b, proj_W, proj_b, fconv_W, fconv_b, bconv_W, bconv_b, deltaBC_W, dt_W, dt_b, A_log, D):
        import jax, jax.numpy as jnp
        import numpy as np
        DIM = 128
        DT_RANK = 64
        D_STATE = 16
        BATCH = 2
        SEQ = 256
        EPS = 1e-05

        def _selective_scan(u, delta, A, B, C, D):
            deltaA = jnp.exp(jnp.einsum('bld,dn->bldn', delta, A))
            deltaBu = jnp.einsum('bld,bln->bldn', delta * u, B)

            def step(h, inp):
                dA, dBu, Ct = inp
                h = dA * h + dBu
                y = jnp.einsum('bdn,bn->bd', h, Ct)
                return (h, y)
            h0 = jnp.zeros((u.shape[0], u.shape[2], A.shape[1]), u.dtype)
            xs = (jnp.moveaxis(deltaA, 1, 0), jnp.moveaxis(deltaBu, 1, 0), jnp.moveaxis(C, 1, 0))
            _, ys = jax.lax.scan(step, h0, xs)
            y = jnp.moveaxis(ys, 0, 1)
            return y + u * D

        def _ssm(u, deltaBC_W, dt_W, dt_b, A_log, D):
            A = -jnp.exp(A_log)
            dbc = u @ deltaBC_W.T
            delta = dbc[..., :DT_RANK]
            B = dbc[..., DT_RANK:DT_RANK + D_STATE]
            C = dbc[..., DT_RANK + D_STATE:]
            delta = jax.nn.softplus(delta @ dt_W.T + dt_b)
            return _selective_scan(u, delta, A, B, C, D)
        skip = x
        mu = jnp.mean(x, axis=-1, keepdims=True)
        var = jnp.var(x, axis=-1, keepdims=True)
        xn = (x - mu) * jax.lax.rsqrt(var + EPS) * ln_w + ln_b
        xp = xn @ proj_W.T + proj_b

        def branch(W, b):
            u = jax.nn.softplus(xp @ W.T + b)
            return _ssm(u, deltaBC_W, dt_W, dt_b, A_log, D)
        x1 = branch(fconv_W, fconv_b)
        x2 = branch(bconv_W, bconv_b)
        z = xp * jax.nn.sigmoid(xp)
        return x1 * z + x2 * z + skip

    def _L1_ffn_ref(x, w_router, w_gate, w_down):
        import math
        import jax, jax.numpy as jnp
        import numpy as np
        D_MODEL = 128
        D_HIDDEN = 256
        N_EXPERTS = 8
        TOP_K = 2
        CAPACITY_FACTOR = 1.25

        def _moe_forward(x, w_router, w_gate, w_down):
            B, T, D = x.shape
            N = B * T
            xf = x.reshape(N, D)
            logits = xf.astype(jnp.float32) @ w_router.T
            gates = jax.nn.softmax(logits, axis=-1)
            topk_gates, topk_idx = jax.lax.top_k(gates, TOP_K)
            expert_mask = jax.nn.one_hot(topk_idx, N_EXPERTS, dtype=jnp.int32).sum(axis=1)
            capacity = math.ceil(N / N_EXPERTS * CAPACITY_FACTOR)
            position_in_expert = jnp.cumsum(expert_mask, axis=0) - 1
            expert_mask = expert_mask * (position_in_expert < capacity)
            keep = jnp.take_along_axis(expert_mask, topk_idx, axis=1) > 0
            topk_gates = topk_gates * keep
            topk_gates = topk_gates / (topk_gates.sum(axis=-1, keepdims=True) + 1e-06)
            hidden = jax.nn.silu(xf @ w_gate.T)
            combine = (topk_gates[:, :, None] * jax.nn.one_hot(topk_idx, N_EXPERTS, dtype=topk_gates.dtype)).sum(axis=1)
            y = jnp.zeros((N, D), dtype=x.dtype)
            for e in range(N_EXPERTS):
                y = y + combine[:, e:e + 1] * (hidden @ w_down[e].T)
            return y.reshape(B, T, D)
        return _moe_forward(x, w_router, w_gate, w_down)

    def _L2_attn_ref(x, Mq, Mk, Mv):
        import jax, jax.numpy as jnp
        import numpy as np
        HEADS = 8
        K_SIZE = 64
        B, C, _ = x.shape
        H, K = (HEADS, K_SIZE)
        V = Mv.shape[1] // H
        q = (x @ Mq).reshape(B, H, C, K)
        k = (x @ Mk).reshape(B, H, C, K)
        v = (x @ Mv).reshape(B, H, C, V)
        scores = jnp.einsum('bhqk,bhck->bhqc', q, k).reshape(B * H, C, C)
        att = jax.nn.softmax(scores / jnp.sqrt(jnp.float32(K)), axis=1)
        att4 = att.reshape(B, C, H, C)
        out = jnp.einsum('bqhc,bhcd->bqhd', att4, v)
        return out.reshape(B, C, H * V)

    def _L2_ffn_ref(x, r1_w, r1_b, r2_w, w_up, w_down, a_up, a_down):
        import jax, jax.numpy as jnp
        import numpy as np
        E, G, TOPK = (32, 16, 2)
        HID, INTER, A_INTER = (128, 256, 128)
        CAP_FACTOR = 1.25
        SCALE = 0.05

        def _stats(x):
            mean = x.mean(-1, keepdims=True)
            std = jnp.std(x, axis=-1, keepdims=True, ddof=1)
            mn = x.min(-1, keepdims=True)
            mx = x.max(-1, keepdims=True)
            l2 = jnp.linalg.norm(x, axis=-1, keepdims=True)
            sp = (jnp.abs(x) < 1e-06).astype(x.dtype).mean(-1, keepdims=True)
            return jnp.concatenate([mean, std, mn, mx, l2, sp], -1)
        B, N, C = x.shape
        xf = x.reshape(-1, C)
        T = xf.shape[0]
        cap = int(CAP_FACTOR * T / E)
        ri = jnp.concatenate([xf, _stats(xf)], -1)
        h = jax.nn.gelu(ri @ r1_w.T + r1_b, approximate=False)
        probs = jax.nn.softmax(h @ r2_w.T, -1)
        topp, topi = jax.lax.top_k(probs, TOPK)
        wnorm = topp / topp.sum(-1, keepdims=True)
        eids = jnp.arange(E)
        hit = topi[..., None] == eids
        routed = hit.any(1)
        Wc = jnp.where(hit, wnorm[..., None], 0.0).sum(1)
        score = jnp.where(routed, probs, -jnp.inf)
        idx = jnp.argsort(-score, axis=0)[:cap].T
        valid = jnp.take_along_axis(routed.T, idx, 1)
        w = jnp.take_along_axis(Wc.T, idx, 1) * valid
        xe = xf[idx]
        up = jnp.einsum('eci,eji->ecj', xe, w_up)
        gate, upv = jnp.split(up, 2, axis=-1)
        hact = jax.nn.silu(gate) * upv
        ye = jnp.einsum('ecj,eoj->eco', hact, w_down)
        out = jnp.zeros((T, C), xf.dtype).at[idx.reshape(-1)].add((w[..., None] * ye).reshape(-1, C))
        Wmask = jnp.zeros((T, E), xf.dtype).at[idx, eids[:, None]].add(w)
        gw = SCALE * Wmask.reshape(T, G, E // G).sum(-1)
        aup = jnp.einsum('tc,gjc->tgj', xf, a_up)
        ag, av = jnp.split(aup, 2, axis=-1)
        ah = jax.nn.silu(ag) * av
        ay = jnp.einsum('tgj,goj->tgo', ah, a_down)
        out = out + jnp.einsum('tg,tgo->to', gw, ay)
        return out.reshape(B, N, C)

    def _L3_attn_ref(x, w_q, w_k, w_v, w_o):
        import jax, jax.numpy as jnp
        import numpy as np
        B, S, E, H = (2, 256, 128, 16)
        HD = E // H

        def _rope_tables(seq_len, head_dim, dtype=jnp.float32):
            i = jnp.arange(head_dim // 2, dtype=dtype)
            angles = jnp.power(jnp.asarray(10000.0, dtype), 2.0 * i / head_dim)
            theta = jnp.arange(seq_len, dtype=dtype)[:, None] * angles[None, :]
            cos = jnp.cos(theta)[None, :, None, :]
            sin = jnp.sin(theta)[None, :, None, :]
            return (cos, sin)

        def _apply_rope(t, cos, sin):
            tr, ti = (t[..., 0::2], t[..., 1::2])
            out_r = tr * cos - ti * sin
            out_i = tr * sin + ti * cos
            return jnp.stack([out_r, out_i], axis=-1).reshape(t.shape)
        b, s, _ = x.shape
        q = (x @ w_q.T).reshape(b, s, H, HD)
        k = (x @ w_k.T).reshape(b, s, H, HD)
        v = (x @ w_v.T).reshape(b, s, H, HD)
        cos, sin = _rope_tables(s, HD, x.dtype)
        q = _apply_rope(q, cos, sin)
        k = _apply_rope(k, cos, sin)
        att = jnp.einsum('bqhd,bkhd->bhqk', q, k) / jnp.sqrt(jnp.asarray(HD, x.dtype))
        att = jax.nn.softmax(att, axis=-1)
        y = jnp.einsum('bhqk,bkhd->bqhd', att, v).reshape(b, s, H * HD)
        return y @ w_o.T

    def _L3_ffn_ref(x, gate_weight, W1, b1, W2, b2, Ws1, bs1, Ws2, bs2):
        import jax, jax.numpy as jnp
        import numpy as np
        B, SEQ, D, E, F = (4, 128, 128, 8, 512)
        CAPACITY = 2
        Bb, s, Dd = x.shape
        Ee = gate_weight.shape[0]
        xf = x.reshape(-1, Dd)
        S = xf.shape[0]
        logits = xf @ gate_weight.T
        scores = jax.nn.softmax(logits, axis=-1).T
        k = S * CAPACITY
        vals, idx = jax.lax.top_k(scores.reshape(-1), k)
        eidx = idx // S
        tidx = idx % S
        gate = jnp.zeros((Ee, S), x.dtype).at[eidx, tidx].add(vals)
        h = jax.nn.gelu(jnp.einsum('sd,edf->esf', xf, W1) + b1[:, None, :], approximate=True)
        y = jnp.einsum('esf,efd->esd', h, W2) + b2[:, None, :]
        out = jnp.einsum('es,esd->sd', gate, y)
        shared = jax.nn.gelu(xf @ Ws1 + bs1, approximate=True) @ Ws2 + bs2
        out = out + shared
        return out.reshape(Bb, s, Dd)
    x = L0_attn_x
    x = _layernorm(x + _L0_attn_ref(x, L0_attn_qkv_w, L0_attn_proj_w, L0_attn_proj_b, L0_attn_slopes), axis=-1)
    x = _layernorm(x + _L0_ffn_ref(x, L0_ffn_w1_w, L0_ffn_w1_s, L0_ffn_w2_w, L0_ffn_w2_s, L0_ffn_h1_w, L0_ffn_h1_s, L0_ffn_h2_w, L0_ffn_h2_s, L0_ffn_w3_w, L0_ffn_w3_s), axis=-1)
    x = _layernorm(x + _L1_attn_ref(x, L1_attn_ln_w, L1_attn_ln_b, L1_attn_proj_W, L1_attn_proj_b, L1_attn_fconv_W, L1_attn_fconv_b, L1_attn_bconv_W, L1_attn_bconv_b, L1_attn_deltaBC_W, L1_attn_dt_W, L1_attn_dt_b, L1_attn_A_log, L1_attn_D), axis=-1)
    x = _layernorm(x + _L1_ffn_ref(x, L1_ffn_w_router, L1_ffn_w_gate, L1_ffn_w_down), axis=-1)
    x = _layernorm(x + _L2_attn_ref(x, L2_attn_Mq, L2_attn_Mk, L2_attn_Mv), axis=-1)
    x = _layernorm(x + _L2_ffn_ref(x, L2_ffn_r1_w, L2_ffn_r1_b, L2_ffn_r2_w, L2_ffn_w_up, L2_ffn_w_down, L2_ffn_a_up, L2_ffn_a_down), axis=-1)
    x = _layernorm(x + _L3_attn_ref(x, L3_attn_w_q, L3_attn_w_k, L3_attn_w_v, L3_attn_w_o), axis=-1)
    x = _layernorm(x + _L3_ffn_ref(x, L3_ffn_gate_weight, L3_ffn_W1, L3_ffn_b1, L3_ffn_W2, L3_ffn_b2, L3_ffn_Ws1, L3_ffn_bs1, L3_ffn_Ws2, L3_ffn_bs2), axis=-1)
    return x

_drawn_inputs = setup_inputs


def setup_inputs(seed=0):
    import zlib

    import numpy as np

    out = dict(_drawn_inputs(seed))
    spreads = {'L1_attn_ln_w': (1.0, 0.6),
     'L1_attn_ln_b': (0.0, 0.551),
     'L1_attn_proj_b': (0.0, 0.1),
     'L1_attn_fconv_b': (0.0, 0.8),
     'L1_attn_bconv_b': (0.0, 0.8),
     'L1_attn_dt_b': (0.0, 0.8),
     'L1_attn_D': (1.0, 0.6),
     'L2_ffn_r1_b': (0.0, 0.8),
     'L3_ffn_b1': (0.0, 0.721),
     'L3_ffn_b2': (0.0, 0.498),
     'L3_ffn_bs1': (0.0, 0.1),
     'L3_ffn_bs2': (0.0, 0.1)}
    factors = {'L0_attn_proj_b': 4.359,
     'L0_ffn_w1_w': 8.0,
     'L0_ffn_w1_s': 8.0,
     'L0_ffn_w2_w': 8.0,
     'L0_ffn_w2_s': 8.0,
     'L0_ffn_h1_w': 8.0,
     'L0_ffn_h1_s': 8.0,
     'L0_ffn_h2_w': 8.0,
     'L0_ffn_h2_s': 8.0,
     'L0_ffn_w3_w': 8.0,
     'L0_ffn_w3_s': 8.0,
     'L1_attn_fconv_W': 8.0,
     'L1_attn_bconv_W': 8.0,
     'L1_attn_deltaBC_W': 4.855,
     'L1_attn_dt_W': 8.0,
     'L1_attn_A_log': 8.0,
     'L2_attn_Mq': 8.0,
     'L2_attn_Mk': 8.0,
     'L2_attn_Mv': 3.977,
     'L2_ffn_r1_w': 8.0,
     'L2_ffn_r2_w': 8.0,
     'L2_ffn_w_up': 8.0,
     'L2_ffn_w_down': 8.0,
     'L2_ffn_a_up': 8.0,
     'L2_ffn_a_down': 8.0,
     'L3_attn_w_q': 8.0,
     'L3_attn_w_k': 8.0,
     'L3_attn_w_v': 8.0,
     'L3_attn_w_o': 8.0}
    for name, (base, spread) in spreads.items():
        noise = np.random.default_rng([zlib.crc32(name.encode()), seed]).standard_normal(out[name].shape)
        drawn = base * np.exp(spread * noise) if base else spread * noise
        out[name] = jnp.asarray(drawn.astype(out[name].dtype))
    for name, factor in factors.items():
        out[name] = (out[name] * factor).astype(out[name].dtype)
    return out
```

```python
import concourse.bass as bass
from concourse import mybir
from contextlib import ExitStack

import numpy as np

F32 = mybir.dt.float32
BF16 = mybir.dt.bfloat16
I32 = mybir.dt.int32
U32 = mybir.dt.uint32
ALU = mybir.AluOpType
ACT = mybir.ActivationFunctionType
AX = mybir.AxisListType

B = 4
N = 512
T = B * N
C = 128
P = 128
TT = T // P
LN_EPS = 1e-5


def cols(i, size=N):
    return bass.ds(i * size, size)


class Core:

    def __init__(self, nc, ctx):
        self.nc, self.ctx = nc, ctx
        self.stage_ctx, self.stage_sems = None, []
        self.norms = 0
        self.norm_sems = [self.sem(f"norm_{n}") for n in ("mean", "centred", "square", "var", "logvar", "rstd")]

    def sb(self, ctx, name, shape, dt=F32):
        return ctx.enter_context(self.nc.sbuf_tensor(name, shape, dt))

    def ps(self, ctx, name, shape, dt=F32):
        return ctx.enter_context(self.nc.psum_tensor(name, shape, dt))

    def sem(self, name):
        ctx = self.ctx if self.stage_ctx is None else self.stage_ctx
        handle = ctx.enter_context(self.nc.semaphore(name))
        self.stage_sems.append(handle)
        return handle

    def run_stage(self, stage, *args):
        self.stage_sems = []
        with ExitStack() as self.stage_ctx:
            stage(self, *args)
            with self.nc.Block() as block:
                @block.gpsimd
                def _(pool):
                    for handle in self.stage_sems:
                        pool.sem_clear(handle)
        self.stage_ctx = None


def layernorm_stage(core, xT, tag, out=None):
    out = xT if out is None else out
    nc = core.nc
    mean_ready, centred_ready, square_ready, var_ready, logvar_ready, rstd_ready = core.norm_sems
    done = core.norms * B
    core.norms += 1
    with ExitStack() as mem:
        centred = core.sb(mem, f"{tag}_xc", [P, T])
        square = core.sb(mem, f"{tag}_sq", [P, T])
        logvar = core.sb(mem, f"{tag}_lv", [P, T])
        rstd = core.sb(mem, f"{tag}_rs", [P, T])
        mean = core.ps(mem, f"{tag}_ps_mean", [P, T])
        var = core.ps(mem, f"{tag}_ps_var", [P, T])
        block = mem.enter_context(nc.Block())

        @block.tensor
        def _(pe):
            for i in range(B):
                nc.tensor.matmul(mean[:, cols(i)], core.avg[:, :], xT[:, cols(i)],
                                 start=True, stop=True).then_inc(mean_ready, 1)
            for i in range(B):
                pe.wait_ge(square_ready, done + i + 1)
                nc.tensor.matmul(var[:, cols(i)], core.avg[:, :], square[:, cols(i)],
                                 start=True, stop=True).then_inc(var_ready, 1)

        @block.gpsimd
        def _(pool):
            for i in range(B):
                pool.wait_ge(centred_ready, done + i + 1)
                nc.gpsimd.tensor_tensor(square[:, cols(i)], centred[:, cols(i)], centred[:, cols(i)],
                                        ALU.mult).then_inc(square_ready, 1)

        @block.scalar
        def _(act):
            for i in range(B):
                act.wait_ge(var_ready, done + i + 1)
                nc.scalar.activation(logvar[:, cols(i)], var[:, cols(i)], ACT.Ln,
                                     bias=core.eps[:, 0:1]).then_inc(logvar_ready, 1)
                act.wait_ge(logvar_ready, done + i + 1)
                nc.scalar.activation(rstd[:, cols(i)], logvar[:, cols(i)], ACT.Exp,
                                     scale=-0.5).then_inc(rstd_ready, 1)

        @block.vector
        def _(dve):
            for i in range(B):
                dve.wait_ge(mean_ready, done + i + 1)
                nc.vector.tensor_tensor(centred[:, cols(i)], xT[:, cols(i)], mean[:, cols(i)],
                                        ALU.subtract).then_inc(centred_ready, 1)
            for i in range(B):
                dve.wait_ge(rstd_ready, done + i + 1)
                nc.vector.tensor_tensor(out[:, cols(i)], centred[:, cols(i)], rstd[:, cols(i)], ALU.mult)


HEADS = 16
HD = C // HEADS
QT = N // P
KT = N // P
UNITS = HEADS * QT
Q_PARTS = (0, 0, 1, 1, 0, 2)
K_PARTS = (0, 1, 0, 1, 2, 0)
STACK = HD * len(Q_PARTS)
WINDOW = N + (QT - 1) * P


def attention_stage(core, A, xT, tag, alibi):
    nc = core.nc
    parts_dram = nc.dram_tensor(f"{tag}_parts", (2, 3, C, T), BF16).ap()
    with ExitStack() as mem:
        v_all = core.sb(mem, f"{tag}_v", [P, TT, C])
        wproj = core.sb(mem, f"{tag}_wproj", [C, C])
        bproj = core.sb(mem, f"{tag}_bproj", [C, 1])
        if alibi:
            bias = core.sb(mem, f"{tag}_bias", [P, HEADS, WINDOW])
        project_and_split(core, A, xT, tag, parts_dram, v_all, wproj, bproj, bias if alibi else None)
        attend(core, A, xT, tag, parts_dram, v_all, wproj, bproj, bias if alibi else None)


def project_and_split(core, A, xT, tag, parts_dram, v_all, wproj, bproj, bias):
    nc = core.nc
    w_loaded = core.sem(f"{tag}_w_loaded")
    x_copied = core.sem(f"{tag}_x_copied")
    qk_ready = core.sem(f"{tag}_qk_ready")
    v_ready = core.sem(f"{tag}_v_ready")
    v_kept = core.sem(f"{tag}_v_kept")
    products = core.sem(f"{tag}_rope_products")
    rotated = core.sem(f"{tag}_rotated")
    high = core.sem(f"{tag}_high")
    rest = core.sem(f"{tag}_rest")
    middle = core.sem(f"{tag}_middle")
    low = core.sem(f"{tag}_low")
    stored = core.sem(f"{tag}_parts_stored")
    window_ready = core.sem(f"{tag}_window")
    with ExitStack() as mem:
        wqkv = core.sb(mem, f"{tag}_wqkv", [C, 5, C])
        rope = core.sb(mem, f"{tag}_rope", [C, 4, N])
        xb = core.sb(mem, f"{tag}_xb", [C, N])
        prod = core.sb(mem, f"{tag}_prod", [C, 2, 2, N])
        qk = core.sb(mem, f"{tag}_qk", [C, 2, N])
        left = core.sb(mem, f"{tag}_left", [C, 2, N])
        parts = core.sb(mem, f"{tag}_p", [C, 2, 3, N], BF16)
        if bias is not None:
            window = core.sb(mem, f"{tag}_window", [P, WINDOW])
            slopes = core.sb(mem, f"{tag}_slopes", [P, HEADS])
        qk_ps = core.ps(mem, f"{tag}_qk_ps", [C, 4, N])
        v_ps = core.ps(mem, f"{tag}_v_ps", [P, KT, C])
        block = mem.enter_context(nc.Block())

        @block.sync
        def _(sp):
            sp.dma_start(wqkv[:, :, :], A[f"{tag}_wqkv"]).then_inc(w_loaded, 16)
            sp.dma_start(rope[:, :, :], A[f"{tag}_rope"]).then_inc(w_loaded, 16)
            sp.dma_start(wproj[:, :], A[f"{tag}_wproj"]).then_inc(w_loaded, 16)
            sp.dma_start(bproj[:, :], A[f"{tag}_bproj"]).then_inc(w_loaded, 16)
            if bias is not None:
                sp.dma_start(window[:, :], A[f"{tag}_window"]).then_inc(w_loaded, 16)
                sp.dma_start(slopes[:, :], A[f"{tag}_slopes"]).then_inc(w_loaded, 16)
            with sp.Fori(0, B) as i:
                sp.wait_ge(low, i + 1)
                sp.dma_start(parts_dram[:, :, :, cols(i)].rearrange("a s c t -> c (a s) t"),
                             parts[:, :, :, :].rearrange("c a s t -> c (a s) t")).then_inc(stored, 16)
            sp.wait_ge(stored, 16 * B)

        @block.tensor
        def _(pe):
            pe.wait_ge(w_loaded, 16 * (6 if bias is not None else 4))
            with pe.Fori(0, B) as i:
                pe.wait_ge(x_copied, i + 1)
                pe.wait_ge(products, 4 * i)
                for n in range(4):
                    nc.tensor.matmul(qk_ps[:, n, :], wqkv[:, n, :], xb[:, :],
                                     start=True, stop=True).then_inc(qk_ready, 1)
                pe.wait_ge(v_kept, i)
                for t in range(KT):
                    last = nc.tensor.matmul(v_ps[:, t, :], xb[:, t * P:(t + 1) * P], wqkv[:, 4, :],
                                            start=True, stop=True)
                last.then_inc(v_ready, 1)

        @block.scalar
        def _(act):
            with act.Fori(0, B) as i:
                act.wait_ge(v_ready, i)
                nc.scalar.activation(xb[:, :], xT[:, cols(i)], ACT.Copy).then_inc(x_copied, 1)
                act.wait_ge(rotated, i + 1)
                act.wait_ge(stored, 16 * i)
                nc.scalar.activation(parts[:, :, 0, :], qk[:, :, :], ACT.Copy).then_inc(high, 1)
                act.wait_ge(v_ready, i + 1)
                nc.scalar.activation(v_all[:, bass.ds(i * KT, KT), :], v_ps[:, :, :],
                                     ACT.Copy).then_inc(v_kept, 1)
                act.wait_ge(rest, i + 1)
                nc.scalar.activation(parts[:, :, 1, :], left[:, :, :], ACT.Copy).then_inc(middle, 1)

        @block.vector
        def _(dve):
            dve.wait_ge(w_loaded, 16 * (6 if bias is not None else 4))
            with dve.Fori(0, B) as i:
                dve.wait_ge(rotated, i)
                for n in range(4):
                    dve.wait_ge(qk_ready, 4 * i + n + 1)
                    nc.vector.tensor_tensor(prod[:, n // 2, n % 2, :], qk_ps[:, n, :], rope[:, n, :],
                                            ALU.mult).then_inc(products, 1)
                dve.wait_ge(products, 4 * i + 4)
                dve.wait_ge(rest, i)
                nc.vector.tensor_tensor(qk[:, :, :], prod[:, :, 0, :], prod[:, :, 1, :],
                                        ALU.add).then_inc(rotated, 1)

        @block.gpsimd
        def _(pool):
            if bias is not None:
                pool.wait_ge(w_loaded, 16 * 6)
                for h in range(HEADS):
                    nc.gpsimd.tensor_scalar(bias[:, h, :], window[:, :], slopes[:, h:h + 1], None, ALU.mult)
            with pool.Fori(0, B) as i:
                pool.wait_ge(high, i + 1)
                nc.gpsimd.tensor_tensor(left[:, :, :], qk[:, :, :], parts[:, :, 0, :],
                                        ALU.subtract).then_inc(rest, 1)
                pool.wait_ge(middle, i + 1)
                nc.gpsimd.tensor_tensor(parts[:, :, 2, :], left[:, :, :], parts[:, :, 1, :],
                                        ALU.subtract).then_inc(low, 1)


def attend(core, A, xT, tag, parts_dram, v_all, wproj, bproj, bias):
    nc = core.nc
    HALF = HEADS // 2
    RING = 4
    TURN, VALUES = 3, 5
    stacks = [core.sem(f"{tag}_stack{n}_loaded") for n in range(2)]
    v_static = core.sem(f"{tag}_v_static")
    scores_ready = core.sem(f"{tag}_scores")
    least_ready = core.sem(f"{tag}_least")
    probs_ready = core.sem(f"{tag}_probs")
    turned = core.sem(f"{tag}_probs_turned")
    kept_dve = core.sem(f"{tag}_turned_kept_dve")
    kept_act = core.sem(f"{tag}_turned_kept_act")
    values_ready = core.sem(f"{tag}_values")
    inverse_ready = core.sem(f"{tag}_inverse")
    heads_ready = core.sem(f"{tag}_heads")
    heads_turned = core.sem(f"{tag}_heads_turned")
    heads_kept = core.sem(f"{tag}_heads_kept")
    projected = core.sem(f"{tag}_projected")
    added = core.sem(f"{tag}_added")
    LOADS = 2 * len(Q_PARTS)

    with ExitStack() as mem:
        qs = core.sb(mem, f"{tag}_qs", [STACK, HEADS, N], BF16)
        ks = core.sb(mem, f"{tag}_ks", [STACK, HEADS, N], BF16)
        vb = core.sb(mem, f"{tag}_vb", [P, KT, C])
        biased = core.sb(mem, f"{tag}_biased", [P, RING, N]) if bias is not None else None
        probs = core.sb(mem, f"{tag}_probs_sb", [P, RING, N])
        probsT = core.sb(mem, f"{tag}_probsT", [P, 2, KT, P])
        least = core.sb(mem, f"{tag}_least_sb", [P, QT, HEADS])
        sums = core.sb(mem, f"{tag}_sums", [P, QT, HEADS])
        inverse = core.sb(mem, f"{tag}_inv", [P, QT, HEADS])
        heads = core.sb(mem, f"{tag}_o", [P, QT, C])
        headsT = core.sb(mem, f"{tag}_oT", [C, N])
        spacer = core.sb(mem, f"{tag}_spacer", [1, 8])
        s_ps = [core.ps(mem, f"{tag}_s_ps{n}", [P, N]) for n in range(RING)]
        t_ps = [core.ps(mem, f"{tag}_t_ps{n}", [P, KT, P]) for n in range(2)]
        o_ps = core.ps(mem, f"{tag}_o_ps", [P, QT, C])
        y_ps = core.ps(mem, f"{tag}_y_ps", [P, N])
        block = mem.enter_context(nc.Block())

        def on_act(u):
            return u % 2 == 1

        @block.sync
        def _(sp):
            def load(half, batch):
                for s in range(len(Q_PARTS)):
                    for a, (dst, part) in enumerate(((qs, Q_PARTS[s]), (ks, K_PARTS[s]))):
                        src = parts_dram[a, part, half * HALF * HD:(half + 1) * HALF * HD, cols(batch)]
                        sp.dma_start(dst[s * HD:(s + 1) * HD, half * HALF:(half + 1) * HALF, :],
                                     src.rearrange("(h d) t -> d h t", d=HD)).then_inc(stacks[half], 16)
            load(0, 0)
            load(1, 0)
            with sp.Fori(1, B) as i:
                sp.wait_ge(scores_ready, i * UNITS - UNITS // 2)
                load(0, i)
                sp.wait_ge(scores_ready, i * UNITS)
                load(1, i)

        @block.gpsimd
        def _(pool):
            with pool.Fori(0, B) as i:
                pool.wait_ge(values_ready, i * UNITS)
                nc.gpsimd.tensor_copy(vb[:, :, :], v_all[:, bass.ds(i * KT, KT), :]).then_inc(v_static, 1)

        @block.tensor
        def _(pe):
            with pe.Fori(0, B) as i:
                def scores(u):
                    h, t = divmod(u, QT)
                    if t == 0 and h % HALF == 0:
                        pe.wait_ge(stacks[h // HALF], (i + 1) * 16 * LOADS)
                    reader = least_ready if bias is not None else probs_ready
                    pe.wait_ge(reader, i * UNITS + max(u - RING + 1, 0))
                    nc.tensor.matmul(s_ps[u % RING][:, :], qs[:, h, t * P:(t + 1) * P], ks[:, h, :],
                                     start=True, stop=True).then_inc(scores_ready, 1)

                def turn(u):
                    pe.wait_ge(probs_ready, i * UNITS + u + 1)
                    pe.wait_ge(kept_act if on_act(u) else kept_dve, i * (UNITS // 2) + u // 2)
                    for k in range(KT):
                        last = nc.tensor.transpose(t_ps[u % 2][:, k, :], probs[:, u % RING, k * P:(k + 1) * P],
                                                   core.ident[:, :])
                    last.then_inc(turned, 1)

                def values(u):
                    h, t = divmod(u, QT)
                    if u == 0:
                        pe.wait_ge(v_static, i + 1)
                        pe.wait_ge(heads_ready, i)
                    pe.wait_ge(kept_act if on_act(u) else kept_dve, i * (UNITS // 2) + u // 2 + 1)
                    for k in range(KT):
                        last = nc.tensor.matmul(o_ps[:, t, h * HD:(h + 1) * HD], probsT[:, u % 2, k, :],
                                                vb[:, k, h * HD:(h + 1) * HD], start=(k == 0), stop=(k == KT - 1))
                    last.then_inc(values_ready, 1)

                for u in range(UNITS + VALUES):
                    if u < UNITS:
                        scores(u)
                    if TURN <= u < UNITS + TURN:
                        turn(u - TURN)
                    if u >= VALUES:
                        values(u - VALUES)
                pe.wait_ge(heads_ready, i + 1)
                pe.wait_ge(added, i)
                for t in range(QT):
                    last = nc.tensor.transpose(y_ps[:, t * P:(t + 1) * P], heads[:, t, :], core.ident[:, :])
                last.then_inc(heads_turned, 1)
                pe.wait_ge(heads_kept, i + 1)
                nc.tensor.matmul(y_ps[:, :], wproj[:, :], headsT[:, :], start=True, stop=True).then_inc(projected, 1)

        @block.scalar
        def _(act):
            with act.Fori(0, B) as i:
                for u in range(UNITS + TURN):
                    if u < UNITS:
                        h, t = divmod(u, QT)
                        act.wait_ge(least_ready, i * UNITS + u + 1)
                        act.wait_ge(turned, i * UNITS + max(u - RING + 1, 0))
                        if u == 0:
                            act.wait_ge(heads_ready, i)
                        src = biased[:, u % RING, :] if bias is not None else s_ps[u % RING][:, :]
                        nc.scalar.activation(probs[:, u % RING, :], src, ACT.Exp, bias=least[:, t, h:h + 1],
                                             scale=-1.0, accum_out=sums[:, t, h:h + 1]).then_inc(probs_ready, 1)
                    v = u - TURN
                    if v >= 0 and on_act(v):
                        act.wait_ge(turned, i * UNITS + v + 1)
                        act.wait_ge(values_ready, i * UNITS + max(v - 1, 0))
                        nc.scalar.activation(probsT[:, v % 2, :, :], t_ps[v % 2][:, :, :],
                                             ACT.Copy).then_inc(kept_act, 1)

        @block.vector
        def _(dve):
            with dve.Fori(0, B) as i:
                for u in range(UNITS + TURN):
                    if u < UNITS:
                        h, t = divmod(u, QT)
                        dve.wait_ge(scores_ready, i * UNITS + u + 1)
                        if bias is not None:
                            dve.wait_ge(probs_ready, i * UNITS + max(u - RING + 1, 0))
                            at = (QT - 1 - t) * P
                            nc.vector.memset(spacer[:, u % 8:u % 8 + 1], 0.0)
                            nc.vector.tensor_tensor_reduce(
                                out=biased[:, u % RING, :], in0=s_ps[u % RING][:, :], in1=bias[:, h, at:at + N],
                                scale=1.0, scalar=3.0e38, op0=ALU.add, op1=ALU.min,
                                accum_out=least[:, t, h:h + 1]).then_inc(least_ready, 1)
                        else:
                            if u == 0:
                                dve.wait_ge(probs_ready, i * UNITS)
                            nc.vector.tensor_reduce(least[:, t, h:h + 1], s_ps[u % RING][:, :], axis=AX.X,
                                                    op=ALU.min).then_inc(least_ready, 1)
                    v = u - TURN
                    if v >= 0 and not on_act(v):
                        dve.wait_ge(turned, i * UNITS + v + 1)
                        dve.wait_ge(values_ready, i * UNITS + max(v - 1, 0))
                        nc.vector.tensor_copy(probsT[:, v % 2, :, :], t_ps[v % 2][:, :, :]).then_inc(kept_dve, 1)
                dve.wait_ge(probs_ready, (i + 1) * UNITS)
                nc.vector.reciprocal(inverse[:, :, :], sums[:, :, :]).then_inc(inverse_ready, 1)
                dve.wait_ge(inverse_ready, i + 1)
                dve.wait_ge(values_ready, (i + 1) * UNITS)
                nc.vector.tensor_tensor(heads[:, :, :].rearrange("p t (h d) -> p (t h) d", d=HD),
                                        o_ps[:, :, :].rearrange("p t (h d) -> p (t h) d", d=HD),
                                        inverse[:, :, :].rearrange("p t h -> p (t h)").unsqueeze(2)
                                        .to_broadcast([P, QT * HEADS, HD]),
                                        ALU.mult).then_inc(heads_ready, 1)
                dve.wait_ge(heads_turned, i + 1)
                nc.vector.tensor_copy(headsT[:, :], y_ps[:, :]).then_inc(heads_kept, 1)
                dve.wait_ge(projected, i + 1)
                nc.vector.scalar_tensor_tensor(out=xT[:, cols(i)], in0=y_ps[:, :], scalar=bproj[:, 0:1],
                                               in1=xT[:, cols(i)], op0=ALU.add, op1=ALU.add).then_inc(added, 1)


HID = 512
HT = HID // P


def gated_mlp_stage(core, A, xT):
    nc = core.nc
    w_loaded = core.sem("f0_w_loaded")
    hidden_loaded = core.sem("f0_hidden_loaded")
    up_ready = core.sem("f0_up")
    silu_ready = core.sem("f0_silu")
    gated_ready = core.sem("f0_gated")
    hid1_ready = core.sem("f0_hid1")
    gelu1_ready = core.sem("f0_gelu1")
    hid2_ready = core.sem("f0_hid2")
    gelu2_ready = core.sem("f0_gelu2")
    out_ready = core.sem("f0_out")
    added = core.sem("f0_added")
    with ExitStack() as mem:
        w12 = core.sb(mem, "f0_w12", [C, 2, HID])
        wh = core.sb(mem, "f0_wh", [P, 2, HT, HID])
        w3 = core.sb(mem, "f0_w3", [P, HT, C])
        scales = core.sb(mem, "f0_scales", [P, 4 * HT + 1])
        silu = core.sb(mem, "f0_silu_sb", [P, 2, N])
        gated = core.sb(mem, "f0_gated_sb", [P, HT, N])
        hid1 = core.sb(mem, "f0_hid1_sb", [P, HT, N])
        hid2 = core.sb(mem, "f0_hid2_sb", [P, HT, N])
        up_ps = [core.ps(mem, f"f0_up_ps{n}", [P, N]) for n in range(4)]
        hid_ps = [core.ps(mem, f"f0_hid_ps{n}", [P, N]) for n in range(HT)]
        block = mem.enter_context(nc.Block())

        def scale(n, m=0):
            return scales[:, n * HT + m:n * HT + m + 1]

        @block.sync
        def _(sp):
            sp.dma_start(w12[:, :, :], A["f0_w12"]).then_inc(w_loaded, 16)
            sp.dma_start(scales[:, :], A["f0_scales"]).then_inc(w_loaded, 16)
            sp.dma_start(wh[:, :, :, :], A["f0_wh"]).then_inc(hidden_loaded, 16)
            sp.dma_start(w3[:, :, :], A["f0_w3"]).then_inc(hidden_loaded, 16)

        @block.tensor
        def _(pe):
            def up(i):
                for m in range(HT):
                    pe.wait_ge(gated_ready, HT * i + max(m - 1, 0))
                    for n in range(2):
                        last = nc.tensor.matmul(up_ps[2 * (m % 2) + n][:, :], w12[:, n, m * P:(m + 1) * P],
                                                xT[:, cols(i)], start=True, stop=True)
                    last.then_inc(up_ready, 1)

            def hidden(layer, src, ready):
                for m in range(HT):
                    for k in range(HT):
                        last = nc.tensor.matmul(hid_ps[m][:, :], wh[:, layer, k, m * P:(m + 1) * P], src[:, k, :],
                                                start=(k == 0), stop=(k == HT - 1))
                    last.then_inc(ready, 1)

            def first(i):
                pe.wait_ge(gated_ready, HT * (i + 1))
                pe.wait_ge(added, i)
                hidden(0, gated, hid1_ready)

            def second_and_out(i):
                pe.wait_ge(gelu1_ready, HT * (i + 1))
                hidden(1, hid1, hid2_ready)
                pe.wait_ge(gelu2_ready, HT * (i + 1))
                for k in range(HT):
                    last = nc.tensor.matmul(hid_ps[0][:, :], w3[:, k, :], hid2[:, k, :],
                                            start=(k == 0), stop=(k == HT - 1))
                last.then_inc(out_ready, 1)

            pe.wait_ge(w_loaded, 32)
            up(0)
            pe.wait_ge(hidden_loaded, 32)
            with pe.Fori(0, B - 1) as i:
                first(i)
                up(i + 1)
                second_and_out(i)
            first(B - 1)
            second_and_out(B - 1)

        @block.scalar
        def _(act):
            def silus(i):
                for m in range(HT):
                    act.wait_ge(up_ready, HT * i + m + 1)
                    act.wait_ge(gated_ready, HT * i + max(m - 1, 0))
                    nc.scalar.activation(silu[:, m % 2, :], up_ps[2 * (m % 2)][:, :], ACT.Silu,
                                         scale=scale(0, m)).then_inc(silu_ready, 1)

            def gelu1(i):
                act.wait_ge(hid2_ready, HT * i)
                for m in range(HT):
                    act.wait_ge(hid1_ready, HT * i + m + 1)
                    nc.scalar.activation(hid1[:, m, :], hid_ps[m][:, :], ACT.Gelu,
                                         scale=scale(2, m)).then_inc(gelu1_ready, 1)

            def gelu2(i):
                act.wait_ge(out_ready, i)
                for m in range(HT):
                    act.wait_ge(hid2_ready, HT * i + m + 1)
                    nc.scalar.activation(hid2[:, m, :], hid_ps[m][:, :], ACT.Gelu,
                                         scale=scale(3, m)).then_inc(gelu2_ready, 1)

            act.wait_ge(w_loaded, 32)
            silus(0)
            with act.Fori(0, B - 1) as i:
                gelu1(i)
                silus(i + 1)
                gelu2(i)
            gelu1(B - 1)
            gelu2(B - 1)

        @block.vector
        def _(dve):
            def gate(i):
                for m in range(HT):
                    dve.wait_ge(silu_ready, HT * i + m + 1)
                    if m == 0:
                        dve.wait_ge(hid1_ready, HT * i)
                    nc.vector.scalar_tensor_tensor(out=gated[:, m, :], in0=up_ps[2 * (m % 2) + 1][:, :],
                                                   scalar=scale(1, m), in1=silu[:, m % 2, :], op0=ALU.mult,
                                                   op1=ALU.mult).then_inc(gated_ready, 1)

            def add(i):
                dve.wait_ge(out_ready, i + 1)
                nc.vector.scalar_tensor_tensor(out=xT[:, cols(i)], in0=hid_ps[0][:, :], scalar=scale(4),
                                               in1=xT[:, cols(i)], op0=ALU.mult, op1=ALU.add).then_inc(added, 1)

            gate(0)
            with dve.Fori(0, B - 1) as i:
                gate(i + 1)
                add(i)
            add(B - 1)


BRANCHES = 2
STATES = 16
DT_RANK = 64
BC = 2 * STATES
STEPS = BRANCHES * STATES


def ssm_stage(core, A, xT):
    nc = core.nc
    with ExitStack() as mem:
        xn = core.sb(mem, "s_xn", [C, T])
        delta = core.sb(mem, "s_delta", [C, BRANCHES, T])
        du = core.sb(mem, "s_du", [C, BRANCHES, T])
        ud = core.sb(mem, "s_ud", [C, T])
        z = core.sb(mem, "s_z", [C, T])
        bc_parts = core.sb(mem, "s_bc_parts", [3 * BC, BRANCHES, T], BF16)
        decay = core.sb(mem, "s_decay", [C, STATES])
        select = core.sb(mem, "s_select", [3 * BC, BC, P], BF16)
        layernorm_stage(core, xT, "s_ln", out=xn)
        ssm_prepare(core, A, xn, delta, du, ud, z, bc_parts, decay, select)
        ssm_scan(core, xT, delta, du, ud, z, bc_parts, decay, select)


def ssm_prepare(core, A, xn, delta, du, ud, z, bc_parts, decay, select):
    nc = core.nc
    loaded = core.sem("s_loaded")
    affine_ready = core.sem("s_affine")
    xp_ps_ready = core.sem("s_xp_ps")
    xp_ready = core.sem("s_xp")
    z_ready = core.sem("s_z_ready")
    v_ps_ready = core.sem("s_v_ps")
    v_kept = core.sem("s_v_kept")
    abs_ready = core.sem("s_abs")
    exp_ready = core.sem("s_exp")
    log_ready = core.sem("s_log")
    u_ready = core.sem("s_u")
    rank_ps_ready = core.sem("s_rank_ps")
    rank_ready = core.sem("s_rank")
    bc_ps_ready = core.sem("s_bc_ps")
    high_ready = core.sem("s_high")
    left_ready = core.sem("s_left")
    middle_ready = core.sem("s_middle")
    exp_a_ready = core.sem("s_exp_a")
    sum_ready = core.sem("s_usum")
    delta_ready = core.sem("s_delta_ready")
    with ExitStack() as mem:
        wide = core.sb(mem, "s_wide", [C, 3, C])
        wdr = core.sb(mem, "s_wdr", [C, DT_RANK])
        wbc = core.sb(mem, "s_wbc", [C, 3 * BC])
        wdt = core.sb(mem, "s_wdt", [BRANCHES * DT_RANK, C])
        cst = core.sb(mem, "s_cst", [C, 7])
        alog = core.sb(mem, "s_alog", [C, STATES])
        xp = core.sb(mem, "s_xp_sb", [C, T])
        v = core.sb(mem, "s_v", [C, BRANCHES, T])
        e = core.sb(mem, "s_e", [C, BRANCHES, T])
        u = core.sb(mem, "s_u_sb", [C, BRANCHES, T])
        rank = core.sb(mem, "s_rank_sb", [BRANCHES * DT_RANK, T])
        left = core.sb(mem, "s_left_sb", [3 * BC, T])
        middle = core.sb(mem, "s_middle_sb", [3 * BC, T], BF16)
        ps = [core.ps(mem, f"s_ps{n}", [P, T]) for n in range(2)]
        block = mem.enter_context(nc.Block())
        LOADS = 7

        @block.sync
        def _(sp):
            for dst, name in ((wide[:, :, :], "wide"), (wdr[:, :], "wdr"), (wbc[:, :], "wbc"), (wdt[:, :], "wdt"),
                              (cst[:, :], "cst"), (alog[:, :], "alog"), (select[:, :, :], "select")):
                sp.dma_start(dst, A[f"s_{name}"]).then_inc(loaded, 16)

        @block.tensor
        def _(pe):
            def product(out, lhsT, rhs, ready):
                for i in range(B):
                    last = nc.tensor.matmul(out[:, cols(i)], lhsT, rhs[:, cols(i)], start=True, stop=True)
                last.then_inc(ready, 1)

            pe.wait_ge(loaded, 16 * LOADS)
            pe.wait_ge(affine_ready, 1)
            product(ps[0], wide[:, 0, :], xn, xp_ps_ready)
            pe.wait_ge(xp_ready, 1)
            product(ps[1], wide[:, 1, :], xp, v_ps_ready)
            pe.wait_ge(z_ready, 1)
            product(ps[0], wide[:, 2, :], xp, v_ps_ready)
            pe.wait_ge(u_ready, 1)
            for r in range(BRANCHES):
                product(ps[1][r * DT_RANK:(r + 1) * DT_RANK, :], wdr[:, :], u[:, r, :], rank_ps_ready)
            product(ps[0][0:3 * BC, :], wbc[:, :], u[:, 0, :], bc_ps_ready)
            pe.wait_ge(rank_ready, 1)
            product(ps[1][0:3 * BC, :], wbc[:, :], u[:, 1, :], bc_ps_ready)
            for r in range(BRANCHES):
                pe.wait_ge(left_ready, r + 1)
                rows = slice(r * DT_RANK, (r + 1) * DT_RANK)
                product(ps[r], wdt[rows, :], rank[rows, :], v_ps_ready)

        @block.scalar
        def _(act):
            act.wait_ge(loaded, 16 * LOADS)
            nc.scalar.activation(decay[:, :], alog[:, :], ACT.Exp).then_inc(exp_a_ready, 1)
            act.wait_ge(xp_ps_ready, 1)
            nc.scalar.activation(xp[:, :], ps[0][:, :], ACT.Identity, bias=cst[:, 2:3]).then_inc(xp_ready, 1)
            nc.scalar.activation(z[:, :], ps[0][:, :], ACT.Silu, bias=cst[:, 2:3]).then_inc(z_ready, 1)

            def softplus_terms(n):
                for r in range(BRANCHES):
                    src = ps[1 - r] if n == 0 else ps[r]
                    bias = cst[:, 3 + r:4 + r] if n == 0 else cst[:, 5:6]
                    act.wait_ge(v_ps_ready, 2 * n + r + 1)
                    if n == 1:
                        act.wait_ge(u_ready, 1)
                    nc.scalar.activation(v[:, r, :], src[:, :], ACT.Identity, bias=bias).then_inc(v_kept, 1)
                    nc.scalar.activation(e[:, r, :], src[:, :], ACT.Abs, bias=bias).then_inc(abs_ready, 1)
                act.wait_ge(abs_ready, 2 * n + 2)
                nc.scalar.activation(e[:, :, :], e[:, :, :], ACT.Exp, scale=-1.0).then_inc(exp_ready, 1)
                act.wait_ge(exp_ready, n + 1)
                nc.scalar.activation(e[:, :, :], e[:, :, :], ACT.Ln, bias=core.one[:, 0:1]).then_inc(log_ready, 1)

            softplus_terms(0)
            act.wait_ge(rank_ps_ready, 2)
            nc.scalar.activation(rank[:, :], ps[1][:, :], ACT.Copy).then_inc(rank_ready, 1)
            softplus_terms(1)

        @block.vector
        def _(dve):
            dve.wait_ge(loaded, 16 * LOADS)
            nc.vector.tensor_scalar(xn[:, :], xn[:, :], cst[:, 0:1], cst[:, 1:2], ALU.mult,
                                    ALU.add).then_inc(affine_ready, 1)
            dve.wait_ge(exp_a_ready, 1)
            nc.vector.tensor_scalar(decay[:, :], decay[:, :], -1.0, None, ALU.mult)
            dve.wait_ge(log_ready, 1)
            nc.vector.scalar_tensor_tensor(out=u[:, :, :], in0=v[:, :, :], scalar=0.0, in1=e[:, :, :],
                                           op0=ALU.max, op1=ALU.add).then_inc(u_ready, 1)
            for r in range(BRANCHES):
                dve.wait_ge(bc_ps_ready, r + 1)
                nc.vector.tensor_copy(bc_parts[:, r, :], ps[r][0:3 * BC, :]).then_inc(high_ready, 1)
                dve.wait_ge(high_ready, r + 1)
                if r == 1:
                    dve.wait_ge(middle_ready, 3)
                nc.vector.tensor_tensor(left[:, :], ps[r][0:3 * BC, :], bc_parts[:, r, :],
                                        ALU.subtract).then_inc(left_ready, 1)
            dve.wait_ge(log_ready, 2)
            nc.vector.scalar_tensor_tensor(out=delta[:, :, :], in0=v[:, :, :], scalar=0.0, in1=e[:, :, :],
                                           op0=ALU.max, op1=ALU.add).then_inc(delta_ready, 1)
            dve.wait_ge(delta_ready, 1)
            nc.vector.tensor_tensor(du[:, :, :], delta[:, :, :], u[:, :, :], ALU.mult)

        @block.gpsimd
        def _(pool):
            pool.wait_ge(u_ready, 1)
            nc.gpsimd.tensor_tensor(ud[:, :], u[:, 0, :], u[:, 1, :], ALU.add).then_inc(sum_ready, 1)
            pool.wait_ge(sum_ready, 1)
            nc.gpsimd.tensor_scalar(ud[:, :], ud[:, :], cst[:, 6:7], None, ALU.mult)
            for r in range(BRANCHES):
                pool.wait_ge(left_ready, r + 1)
                nc.gpsimd.tensor_copy(middle[:, :], left[:, :]).then_inc(middle_ready, 1)
                pool.wait_ge(middle_ready, 3 * r + 1)
                nc.gpsimd.tensor_copy(bc_parts[BC:2 * BC, r, :], middle[BC:2 * BC, :]).then_inc(middle_ready, 1)
                nc.gpsimd.tensor_tensor(bc_parts[2 * BC:3 * BC, r, :], left[2 * BC:3 * BC, :],
                                        middle[2 * BC:3 * BC, :], ALU.subtract).then_inc(middle_ready, 1)
                pool.wait_ge(middle_ready, 3 * r + 3)


def ssm_scan(core, xT, delta, du, ud, z, bc_parts, decay, select):
    nc = core.nc
    RING, C_RING, B_RING = 4, 4, 3
    decay_ready = core.sem("s_decay_ready")
    b_ready = core.sem("s_b_ps")
    c_ready = core.sem("s_c_ps")
    b_kept = core.sem("s_b_kept")
    du_kept = core.sem("s_du_kept")
    input_ready = core.sem("s_input")
    scanned = core.sem("s_scanned")
    read_out = core.sem("s_read_out")
    summed = core.sem("s_summed")
    y_ready = core.sem("s_y")
    gate_ready = core.sem("s_gate")
    finished = core.sem("s_finished")
    with ExitStack() as mem:
        dA = core.sb(mem, "s_dA", [C, RING, N])
        du_b = core.sb(mem, "s_du_b", [C, BRANCHES, N])
        bs = core.sb(mem, "s_bs", [C, RING, N])
        dbu = core.sb(mem, "s_dbu", [C, RING, N])
        h = core.sb(mem, "s_h", [C, RING, N])
        hc = core.sb(mem, "s_hc", [C, RING, N])
        y = core.sb(mem, "s_ysb", [C, N])
        b_ps = [core.ps(mem, f"s_b_ps{n}", [C, N]) for n in range(B_RING)]
        c_ps = [core.ps(mem, f"s_c_ps{n}", [C, N]) for n in range(C_RING)]
        y_ps = core.ps(mem, "s_y_ps", [C, N])
        block = mem.enter_context(nc.Block())

        @block.tensor
        def _(pe):
            with pe.Fori(0, B) as i:
                for s in range(STEPS + RING):
                    if s < STEPS:
                        r, n = divmod(s, STATES)
                        pe.wait_ge(b_kept, i * STEPS + max(s - B_RING + 1, 0))
                        nc.tensor.matmul(b_ps[s % B_RING][:, :], select[:, n, :], bc_parts[:, r, cols(i)],
                                         start=True, stop=True).then_inc(b_ready, 1)
                        pe.wait_ge(read_out, i * STEPS + max(s - C_RING + 1, 0))
                        nc.tensor.matmul(c_ps[s % C_RING][:, :], select[:, STATES + n, :], bc_parts[:, r, cols(i)],
                                         start=True, stop=True).then_inc(c_ready, 1)
                    d = s - RING
                    if d >= 0:
                        if d == 0:
                            pe.wait_ge(gate_ready, i)
                        pe.wait_ge(read_out, i * STEPS + d + 1)
                        nc.tensor.matmul(y_ps[:, :], core.ident[:, :], hc[:, d % RING, :], start=(d == 0),
                                         stop=(d == STEPS - 1)).then_inc(summed, 1)

        @block.scalar
        def _(act):
            with act.Fori(0, B) as i:
                for s in range(STEPS):
                    r, n = divmod(s, STATES)
                    act.wait_ge(scanned, i * STEPS + max(s - RING + 1, 0))
                    act.wait_ge(b_ready, i * STEPS + s + 1)
                    act.wait_ge(input_ready, i * STEPS + max(s - RING + 1, 0))
                    nc.scalar.activation(bs[:, s % RING, :], b_ps[s % B_RING][:, :], ACT.Copy).then_inc(b_kept, 1)
                    if s == 0:
                        nc.scalar.activation(du_b[:, :, :], du[:, :, cols(i)], ACT.Copy).then_inc(du_kept, 1)
                    nc.scalar.activation(dA[:, s % RING, :], delta[:, r, cols(i)], ACT.Exp,
                                         scale=decay[:, n:n + 1]).then_inc(decay_ready, 1)

        @block.gpsimd
        def _(pool):
            with pool.Fori(0, B) as i:
                for s in range(STEPS):
                    r = s // STATES
                    if s == 0:
                        pool.wait_ge(du_kept, i + 1)
                    pool.wait_ge(b_kept, i * STEPS + s + 1)
                    pool.wait_ge(scanned, i * STEPS + max(s - RING + 1, 0))
                    nc.gpsimd.tensor_tensor(dbu[:, s % RING, :], du_b[:, r, :], bs[:, s % RING, :],
                                            ALU.mult).then_inc(input_ready, 1)

        @block.vector
        def _(dve):
            with dve.Fori(0, B) as i:
                for s in range(STEPS + 1):
                    if s < STEPS:
                        dve.wait_ge(decay_ready, i * STEPS + s + 1)
                        dve.wait_ge(input_ready, i * STEPS + s + 1)
                        dve.wait_ge(read_out, i * STEPS + max(s - RING + 1, 0))
                        nc.vector.tensor_tensor_scan(h[:, s % RING, :], dA[:, s % RING, :], dbu[:, s % RING, :], 0.0,
                                                     ALU.mult, ALU.add).then_inc(scanned, 1)
                    d = s - 1
                    if d >= 0:
                        dve.wait_ge(scanned, i * STEPS + d + 1)
                        dve.wait_ge(c_ready, i * STEPS + d + 1)
                        dve.wait_ge(summed, i * STEPS + max(d - RING + 1, 0))
                        nc.vector.tensor_tensor(hc[:, d % RING, :], c_ps[d % C_RING][:, :], h[:, d % RING, :],
                                                ALU.mult).then_inc(read_out, 1)
                dve.wait_ge(summed, (i + 1) * STEPS)
                dve.wait_ge(finished, i)
                nc.vector.tensor_tensor(y[:, :], y_ps[:, :], ud[:, cols(i)], ALU.add).then_inc(gate_ready, 1)
                dve.wait_ge(gate_ready, i + 1)
                nc.vector.tensor_tensor(y[:, :], y[:, :], z[:, cols(i)], ALU.mult).then_inc(y_ready, 1)
                dve.wait_ge(y_ready, i + 1)
                nc.vector.scalar_tensor_tensor(out=xT[:, cols(i)], in0=xT[:, cols(i)], scalar=2.0, in1=y[:, :],
                                               op0=ALU.mult, op1=ALU.add).then_inc(finished, 1)


EXPERTS = 8
MOE_HID = 256
MOE_HT = MOE_HID // P
CAPACITY = -(-T * 5 // (EXPERTS * 4))


def spread(ap, size):
    return ap.unsqueeze(2).to_broadcast([ap.shape[0], ap.shape[1], size])


def moe_stage(core, A, xT):
    with ExitStack() as mem:
        combine = core.sb(mem, "m_combine", [P, TT, EXPERTS])
        moe_route(core, A, xT, combine)
        moe_experts(core, A, xT, combine)


def moe_route(core, A, xT, combine):
    nc = core.nc
    E = EXPERTS
    loaded = core.sem("m_loaded")
    logits_ready = core.sem("m_logits")
    shifted_ready = core.sem("m_shifted")
    exp_ready = core.sem("m_exp")
    mask_ready = core.sem("m_mask")
    counts_ready = core.sem("m_counts")
    step = core.sem("m_step")
    with ExitStack() as mem:
        wr = core.sb(mem, "m_wr", [C, E])
        tri = core.sb(mem, "m_tri", [P, P])
        ones = core.sb(mem, "m_ones", [P, P])
        iota = core.sb(mem, "m_iota", [P, TT, E])
        most = core.sb(mem, "m_most", [P, TT])
        shifted = core.sb(mem, "m_shifted_sb", [P, TT, E])
        top = core.sb(mem, "m_top", [P, TT, 8])
        index = core.sb(mem, "m_index", [P, TT, 8], U32)
        indexf = core.sb(mem, "m_indexf", [P, TT, 8])
        gates = core.sb(mem, "m_gates", [P, TT, E])
        mask = core.sb(mem, "m_mask_sb", [P, TT, E])
        second = core.sb(mem, "m_second", [P, TT, E])
        totals = core.sb(mem, "m_totals", [P, TT, E])
        place = core.sb(mem, "m_place", [P, TT, E])
        total = core.sb(mem, "m_total", [P, TT])
        logits_ps = core.ps(mem, "m_logits_ps", [P, TT, E])
        prefix_ps = core.ps(mem, "m_prefix_ps", [P, TT, E])
        totals_ps = core.ps(mem, "m_totals_ps", [P, TT, E])
        block = mem.enter_context(nc.Block())

        @block.sync
        def _(sp):
            for dst, name in ((wr[:, :], "m_wr"), (tri[:, :], "tri"), (ones[:, :], "ones"), (iota[:, :, :], "m_iota")):
                sp.dma_start(dst, A[name]).then_inc(loaded, 16)

        @block.tensor
        def _(pe):
            pe.wait_ge(loaded, 64)
            for t in range(TT):
                last = nc.tensor.matmul(logits_ps[:, t, :], xT[:, t * P:(t + 1) * P], wr[:, :], start=True, stop=True)
            last.then_inc(logits_ready, 1)
            pe.wait_ge(mask_ready, 1)
            nc.tensor.matmul(prefix_ps[:, :, :], tri[:, :], mask[:, :, :], start=True, stop=True)
            nc.tensor.matmul(totals_ps[:, :, :], ones[:, :], mask[:, :, :], start=True,
                             stop=True).then_inc(counts_ready, 1)

        @block.scalar
        def _(act):
            act.wait_ge(shifted_ready, 1)
            nc.scalar.activation(gates[:, :, :], shifted[:, :, :], ACT.Exp).then_inc(exp_ready, 1)

        @block.vector
        def _(dve):
            done = [0]

            def then(instruction):
                instruction.then_inc(step, 1)
                done[0] += 1
                dve.wait_ge(step, done[0])

            dve.wait_ge(loaded, 64)
            dve.wait_ge(logits_ready, 1)
            then(nc.vector.tensor_reduce(most[:, :], logits_ps[:, :, :], axis=AX.X, op=ALU.max))
            nc.vector.tensor_tensor(shifted[:, :, :], logits_ps[:, :, :], spread(most[:, :], E),
                                    ALU.subtract).then_inc(shifted_ready, 1)
            dve.wait_ge(exp_ready, 1)
            then(nc.vector.tensor_reduce(total[:, :], gates[:, :, :], axis=AX.X, op=ALU.add))
            then(nc.vector.reciprocal(total[:, :], total[:, :]))
            then(nc.vector.tensor_tensor(gates[:, :, :], gates[:, :, :], spread(total[:, :], E), ALU.mult))
            for t in range(TT):
                last = nc.vector.max(top[:, t, :], gates[:, t, :])
            then(last)
            for t in range(TT):
                last = nc.vector.max_index(index[:, t, :], top[:, t, :], gates[:, t, :])
            then(last)
            then(nc.vector.tensor_copy(indexf[:, :, :], index[:, :, :]))
            nc.vector.tensor_tensor(mask[:, :, :], iota[:, :, :], spread(indexf[:, :, 0], E), ALU.is_equal)
            then(nc.vector.tensor_tensor(second[:, :, :], iota[:, :, :], spread(indexf[:, :, 1], E), ALU.is_equal))
            nc.vector.tensor_tensor(mask[:, :, :], mask[:, :, :], second[:, :, :], ALU.add).then_inc(mask_ready, 1)
            dve.wait_ge(counts_ready, 1)
            then(nc.vector.tensor_copy(totals[:, :, :], totals_ps[:, :, :]))
            for e in range(E):
                last = nc.vector.tensor_tensor_scan(place[:, :, e], core.ones_row[:, 0:TT], totals[:, :, e], 0.0,
                                                    ALU.mult, ALU.add)
            then(last)
            then(nc.vector.tensor_tensor(place[:, :, :], place[:, :, :], totals[:, :, :], ALU.subtract))
            then(nc.vector.tensor_tensor(place[:, :, :], place[:, :, :], prefix_ps[:, :, :], ALU.add))
            then(nc.vector.scalar_tensor_tensor(out=place[:, :, :], in0=place[:, :, :], scalar=float(CAPACITY),
                                                in1=mask[:, :, :], op0=ALU.is_le, op1=ALU.mult))
            then(nc.vector.tensor_tensor(gates[:, :, :], gates[:, :, :], place[:, :, :], ALU.mult))
            then(nc.vector.tensor_reduce(total[:, :], gates[:, :, :], axis=AX.X, op=ALU.add))
            then(nc.vector.tensor_scalar(total[:, :], total[:, :], 1e-6, None, ALU.add))
            then(nc.vector.reciprocal(total[:, :], total[:, :]))
            nc.vector.tensor_tensor(combine[:, :, :], gates[:, :, :], spread(total[:, :], E), ALU.mult)


def moe_experts(core, A, xT, combine):
    nc = core.nc
    E = EXPERTS
    NT = N // P
    PER_BANK = 512 // C
    loaded = core.sem("m_w_loaded")
    hid_ps_ready = core.sem("m_hid_ps")
    hid_ready = core.sem("m_hid")
    y_ready = core.sem("m_y")
    combined = core.sem("m_combine_kept")
    step = core.sem("m_mix_step")
    turned = core.sem("m_turned")
    added = core.sem("m_added")
    with ExitStack() as mem:
        wg = core.sb(mem, "m_wg", [C, MOE_HID])
        wd = core.sb(mem, "m_wd", [P, MOE_HT, E * C])
        hid = core.sb(mem, "m_hid_sb", [P, MOE_HT, N])
        weight = core.sb(mem, "m_weight", [P, NT, E])
        mixed = core.sb(mem, "m_mixed", [P, 2, C])
        hid_ps = [core.ps(mem, f"m_hid_ps{n}", [P, N]) for n in range(MOE_HT)]
        y_ps = [core.ps(mem, f"m_y_ps{n}", [P, E, C]) for n in range(2)]
        t_ps = core.ps(mem, "m_t_ps", [P, N])
        block = mem.enter_context(nc.Block())

        @block.sync
        def _(sp):
            sp.dma_start(wg[:, :], A["m_wg"]).then_inc(loaded, 16)
            sp.dma_start(wd[:, :, :], A["m_wd"]).then_inc(loaded, 16)

        @block.tensor
        def _(pe):
            pe.wait_ge(loaded, 32)
            with pe.Fori(0, B) as i:
                pe.wait_ge(hid_ready, MOE_HT * i)
                for m in range(MOE_HT):
                    nc.tensor.matmul(hid_ps[m][:, :], wg[:, m * P:(m + 1) * P], xT[:, cols(i)],
                                     start=True, stop=True).then_inc(hid_ps_ready, 1)
                pe.wait_ge(hid_ready, MOE_HT * (i + 1))
                for t in range(NT + 1):
                    if t < NT:
                        pe.wait_ge(step, (i * NT + max(t - 1, 0)) * E)
                        for half in range(E // PER_BANK):
                            out = y_ps[t % 2][:, half * PER_BANK:(half + 1) * PER_BANK, :]
                            for k in range(MOE_HT):
                                last = nc.tensor.matmul(out, hid[:, k, t * P:(t + 1) * P],
                                                        wd[:, k, half * 512:(half + 1) * 512],
                                                        start=(k == 0), stop=(k == MOE_HT - 1))
                        last.then_inc(y_ready, 1)
                    if t == 1:
                        pe.wait_ge(added, i)
                    if t > 0:
                        pe.wait_ge(step, (i * NT + t) * E)
                        nc.tensor.transpose(t_ps[:, (t - 1) * P:t * P], mixed[:, (t - 1) % 2, :],
                                            core.ident[:, :]).then_inc(turned, 1)

        @block.scalar
        def _(act):
            with act.Fori(0, B) as i:
                act.wait_ge(y_ready, NT * i)
                for m in range(MOE_HT):
                    act.wait_ge(hid_ps_ready, MOE_HT * i + m + 1)
                    nc.scalar.activation(hid[:, m, :], hid_ps[m][:, :], ACT.Silu).then_inc(hid_ready, 1)

        @block.vector
        def _(dve):
            with dve.Fori(0, B) as i:
                nc.vector.tensor_copy(weight[:, :, :], combine[:, bass.ds(i * NT, NT), :]).then_inc(combined, 1)
                dve.wait_ge(combined, i + 1)
                for t in range(NT):
                    dve.wait_ge(y_ready, NT * i + t + 1)
                    dve.wait_ge(turned, NT * i + max(t - 1, 0))
                    for e in range(E):
                        if e:
                            dve.wait_ge(step, (i * NT + t) * E + e)
                            last = nc.vector.scalar_tensor_tensor(
                                out=mixed[:, t % 2, :], in0=y_ps[t % 2][:, e, :], scalar=weight[:, t, e:e + 1],
                                in1=mixed[:, t % 2, :], op0=ALU.mult, op1=ALU.add)
                        else:
                            last = nc.vector.tensor_scalar(mixed[:, t % 2, :], y_ps[t % 2][:, e, :],
                                                           weight[:, t, e:e + 1], None, ALU.mult)
                        last.then_inc(step, 1)
                dve.wait_ge(turned, NT * (i + 1))
                nc.vector.tensor_tensor(xT[:, cols(i)], t_ps[:, :], xT[:, cols(i)], ALU.add).then_inc(added, 1)


QH = 8
QK = 64
VD = C // QH
HTOK = N // QH
KEY_TILES = QH * HTOK // P
VPAD = 32
QUNITS = QH * KEY_TILES


def query_softmax_stage(core, A, xT):
    nc = core.nc
    loaded = core.sem("q_loaded")
    cleared = core.sem("q_cleared")
    x_copied = core.sem("q_x_copied")
    proj_ready = core.sem("q_proj")
    kept_act = core.sem("q_kept_act")
    kept_dve = core.sem("q_kept_dve")
    v_ps_ready = core.sem("q_v_ps")
    v_kept = core.sem("q_v_kept")
    scores_ready = core.sem("q_scores")
    most_ready = core.sem("q_most")
    probs_ready = core.sem("q_probs")
    inverse_ready = core.sem("q_inverse")
    scaled_ready = core.sem("q_scaled")
    out_ready = core.sem("q_out")
    out_kept = core.sem("q_out_kept")
    y_ready = core.sem("q_y")
    added = core.sem("q_added")
    RING = 3
    with ExitStack() as mem:
        wqk = core.sb(mem, "q_wqk", [C, 2, QH * QK])
        wv = core.sb(mem, "q_wv", [C, C])
        place = core.sb(mem, "q_place", [P, 2, C])
        xb = core.sb(mem, "q_xb", [C, N])
        xd = core.sb(mem, "q_xd", [C, QH, 2, HTOK])
        qk = core.sb(mem, "q_qk", [QK, 2, QH, QH, HTOK])
        v = core.sb(mem, "q_v", [P, KEY_TILES, QH, VD])
        vs = core.sb(mem, "q_vs", [P, 2, KEY_TILES * QH, VPAD])
        most = core.sb(mem, "q_most_sb", [P, QUNITS])
        sums = core.sb(mem, "q_sums", [P, QUNITS])
        inverse = core.sb(mem, "q_inv", [P, QUNITS])
        probs = core.sb(mem, "q_probs_sb", [P, 2, KEY_TILES, N])
        outs = core.sb(mem, "q_outs", [P, 2, N])
        p_ps = core.ps(mem, "q_p_ps", [P, 2, N])
        s_ps = [core.ps(mem, f"q_s_ps{n}", [P, N]) for n in range(RING)]
        o_ps = core.ps(mem, "q_o_ps", [P, 2, N])
        y_ps = core.ps(mem, "q_y_ps", [P, N])
        block = mem.enter_context(nc.Block())
        PAIRS = QH // 2

        def by_head(ap):
            return ap.rearrange("p (h k) -> p h k", h=QH)

        @block.sync
        def _(sp):
            for dst, name in ((wqk[:, :, :], "q_wqk"), (wv[:, :], "q_wv"), (place[:, :, :], "q_place")):
                sp.dma_start(dst, A[name]).then_inc(loaded, 16)

        @block.gpsimd
        def _(pool):
            nc.gpsimd.memset(vs[:, :, :, :], 0.0).then_inc(cleared, 1)

        @block.tensor
        def _(pe):
            pe.wait_ge(loaded, 48)
            with pe.Fori(0, B) as i:
                pe.wait_ge(x_copied, 2 * i + 2)
                pe.wait_ge(v_kept, 2 * i)
                for n in range(2 * PAIRS):
                    if n >= 2:
                        pe.wait_ge(kept_act, 2 * PAIRS * i + n - 1)
                        pe.wait_ge(kept_dve, 2 * PAIRS * i + n - 1)
                    a, b = divmod(n, PAIRS)
                    nc.tensor.matmul(p_ps[:, n % 2, :], wqk[:, a, b * P:(b + 1) * P], xb[:, :],
                                     start=True, stop=True).then_inc(proj_ready, 1)
                pe.wait_ge(kept_act, 2 * PAIRS * (i + 1))
                pe.wait_ge(kept_dve, 2 * PAIRS * (i + 1))
                for h in range(QH):
                    last = nc.tensor.matmul(p_ps[:, h // 4, (h % 4) * P:(h % 4 + 1) * P],
                                            xd[:, h, :, :], wv[:, :], start=True, stop=True)
                last.then_inc(v_ps_ready, 1)

                def scores(u):
                    h, t = divmod(u, KEY_TILES)
                    pe.wait_ge(probs_ready, i * QUNITS + max(u - RING + 1, 0))
                    nc.tensor.matmul(s_ps[u % RING][:, :], qk[:, 1, h, 2 * t:2 * t + 2, :], qk[:, 0, h, :, :],
                                     start=True, stop=True).then_inc(scores_ready, 1)

                def outputs(h):
                    if h == 0:
                        pe.wait_ge(out_kept, 2 * i)
                    pe.wait_ge(scaled_ready, i * QH + h + 1)
                    tok = slice(h * HTOK, (h + 1) * HTOK)
                    for j in range(QH):
                        rows = slice(j % 4 * VPAD, j % 4 * VPAD + VPAD)
                        for t in range(KEY_TILES):
                            last = nc.tensor.matmul(o_ps[rows, j // 4, tok], vs[:, h % 2, t * QH + j, :],
                                                    probs[:, h % 2, t, j * HTOK:(j + 1) * HTOK],
                                                    start=(t == 0), stop=(t == KEY_TILES - 1))
                    last.then_inc(out_ready, 1)

                for h in range(QH + 1):
                    if h < QH:
                        for t in range(KEY_TILES):
                            scores(h * KEY_TILES + t)
                    if h > 0:
                        outputs(h - 1)
                pe.wait_ge(out_kept, 2 * i + 2)
                pe.wait_ge(added, i)
                for g in range(2):
                    last = nc.tensor.matmul(y_ps[:, :], place[:, g, :], outs[:, g, :], start=(g == 0), stop=(g == 1))
                last.then_inc(y_ready, 1)

        @block.scalar
        def _(act):
            with act.Fori(0, B) as i:
                act.wait_ge(v_ps_ready, i)
                nc.scalar.activation(xb[:, :], xT[:, cols(i)], ACT.Copy).then_inc(x_copied, 1)
                act.wait_ge(out_ready, QH * i)
                for n in range(2 * PAIRS):
                    act.wait_ge(proj_ready, 2 * PAIRS * i + n + 1)
                    a, b = divmod(n, PAIRS)
                    nc.scalar.activation(qk[:, a, :, 2 * b, :], by_head(p_ps[0:QK, n % 2, :]), ACT.Copy,
                                         scale=QK ** -0.5 if a == 0 else 1.0).then_inc(kept_act, 1)
                act.wait_ge(v_ps_ready, i + 1)
                nc.scalar.activation(v[0:QK, :, :, :].rearrange("p t h d -> p t h d"),
                                     p_ps[0:QK, :, :].rearrange("p a (b t s d) -> p t s (a b) d", b=4, s=2,
                                                                d=VD)[:, :, 0, :, :],
                                     ACT.Copy).then_inc(v_kept, 1)
                for u in range(QUNITS):
                    act.wait_ge(most_ready, i * QUNITS + u + 1)
                    h, t = divmod(u, KEY_TILES)
                    if t == 0:
                        act.wait_ge(out_ready, QH * i + max(h - 1, 0))
                    nc.scalar.activation(probs[:, h % 2, t, :], s_ps[u % RING][:, :], ACT.Exp,
                                         bias=most[:, u:u + 1], accum_out=sums[:, u:u + 1]).then_inc(probs_ready, 1)
                for g in range(2):
                    if g == 0:
                        act.wait_ge(out_ready, QH * (i + 1))
                        act.wait_ge(y_ready, i)
                    nc.scalar.activation(outs[:, g, :], o_ps[:, g, :], ACT.Copy).then_inc(out_kept, 1)

        @block.vector
        def _(dve):
            dve.wait_ge(cleared, 1)
            with dve.Fori(0, B) as i:
                dve.wait_ge(x_copied, 2 * i + 1)
                for a in range(2):
                    last = nc.vector.tensor_copy(xd[:, :, a, :], xb[:, :].rearrange("p (h k) -> p h k", h=QH))
                last.then_inc(x_copied, 1)
                for n in range(2 * PAIRS):
                    dve.wait_ge(proj_ready, 2 * PAIRS * i + n + 1)
                    a, b = divmod(n, PAIRS)
                    nc.vector.tensor_scalar(qk[:, a, :, 2 * b + 1, :], by_head(p_ps[QK:P, n % 2, :]),
                                            QK ** -0.5 if a == 0 else 1.0, None, ALU.mult).then_inc(kept_dve, 1)
                dve.wait_ge(v_ps_ready, i + 1)
                nc.vector.tensor_copy(v[QK:P, :, :, :],
                                      p_ps[QK:P, :, :].rearrange("p a (b t s d) -> p t s (a b) d", b=4, s=2,
                                                                 d=VD)[:, :, 1, :, :]).then_inc(v_kept, 1)
                dve.wait_ge(v_kept, 2 * i + 2)
                for h in range(QH):
                    for t in range(KEY_TILES):
                        u = h * KEY_TILES + t
                        dve.wait_ge(scores_ready, i * QUNITS + u + 1)
                        nc.vector.tensor_reduce(most[:, u:u + 1], s_ps[u % RING][:, :], axis=AX.X, op=ALU.max,
                                                negate=True).then_inc(most_ready, 1)
                    dve.wait_ge(probs_ready, i * QUNITS + (h + 1) * KEY_TILES)
                    us = slice(h * KEY_TILES, (h + 1) * KEY_TILES)
                    nc.vector.reciprocal(inverse[:, us], sums[:, us]).then_inc(inverse_ready, 1)
                    dve.wait_ge(inverse_ready, i * QH + h + 1)
                    dve.wait_ge(out_ready, i * QH + max(h - 1, 0))
                    nc.vector.tensor_tensor(
                        vs[:, h % 2, :, 0:VD].rearrange("p (t h) d -> p t h d", h=QH), v[:, :, :, :],
                        inverse[:, us].unsqueeze(2).unsqueeze(3).to_broadcast([P, KEY_TILES, QH, VD]),
                        ALU.mult).then_inc(scaled_ready, 1)
                dve.wait_ge(y_ready, i + 1)
                nc.vector.tensor_tensor(xT[:, cols(i)], y_ps[:, :], xT[:, cols(i)], ALU.add).then_inc(added, 1)


X_EXPERTS = 32
X_CAP = T * 5 // (4 * X_EXPERTS)
X_GROUPS = 16
X_INTER = 256
X_ROUTER = C // 2
X_STATS = 6
X_SLOTS = X_EXPERTS * X_CAP
X_ST = X_SLOTS // P
ADAPTER_SCALE = 0.05
TAKEN = -2.0


def sparse_stage(core, A, xT):
    nc = core.nc
    slots_dram = nc.dram_tensor("x_slots", (X_SLOTS, C), F32).ap()
    results_dram = nc.dram_tensor("x_results", (X_SLOTS + 1, C), F32).ap()
    w_loaded = core.sem("x_w_loaded")
    dispatched = core.sem("x_dispatched")
    with ExitStack() as mem:
        weight = core.sb(mem, "x_weight", [P, 2, TT])
        slot = core.sb(mem, "x_slot", [P, 2, TT], I32)
        wu = core.sb(mem, "x_wu", [C, X_EXPERTS, 2 * X_INTER])
        wd = core.sb(mem, "x_wd", [P, X_EXPERTS, X_INTER // P, C])
        wau = core.sb(mem, "x_wau", [C, X_GROUPS, 2 * P])
        wad = core.sb(mem, "x_wad", [P, X_GROUPS, C])

        with nc.Block() as block:
            @block.sync
            def _(sp):
                for dst, name in ((wu[:, :, :], "x_wu"), (wau[:, :, :], "x_wau"), (wd[:, :, :, :], "x_wd"),
                                  (wad[:, :, :], "x_wad")):
                    half = dst.shape[1] // 2
                    for n in range(2):
                        sp.dma_start(dst[:, n * half:(n + 1) * half], A[name][:, n * half:(n + 1) * half]) \
                            .then_inc(w_loaded, 16)
        with ExitStack() as routing:
            xt = core.sb(routing, "x_xt", [P, TT, C])
            hT = core.sb(routing, "x_hT", [X_ROUTER, T])
            sparse_stats(core, A, xT, xt, hT)
            sparse_route(core, A, xt, hT, weight, slot, slots_dram, results_dram, dispatched)
        sparse_experts(core, slots_dram, results_dram, wu, wd, wau, wad, w_loaded)
        sparse_combine(core, xT, results_dram, weight, slot)


def sparse_stats(core, A, xT, xt, hT):
    nc = core.nc
    loaded = core.sem("x_r_loaded")
    turned = core.sem("x_turned")
    kept = core.sem("x_kept")
    squares_ready = core.sem("x_squares")
    sizes_ready = core.sem("x_sizes_ready")
    variance_ready = core.sem("x_variance")
    roots_ready = core.sem("x_roots")
    stats_ready = core.sem("x_stats_ready")
    stats_turned = core.sem("x_stats_turned")
    stats_kept = core.sem("x_stats_kept")
    hidden_ready = core.sem("x_hidden")
    step = core.sem("x_stats_step")
    with ExitStack() as mem:
        r1x = core.sb(mem, "x_r1x", [C, X_ROUTER])
        r1s = core.sb(mem, "x_r1s", [X_STATS, X_ROUTER])
        r1b = core.sb(mem, "x_r1b", [X_ROUTER, 1])
        stats = core.sb(mem, "x_stats", [P, TT, X_STATS])
        statsT = core.sb(mem, "x_statsT", [X_STATS, T])
        sums = core.sb(mem, "x_sums", [P, TT])
        spreads = core.sb(mem, "x_spreads", [P, 2, TT])
        roots = core.sb(mem, "x_roots_sb", [P, 2, TT])
        squares = core.sb(mem, "x_sq", [P, TT, C])
        centred = core.sb(mem, "x_xc", [P, TT, C])
        sizes = core.sb(mem, "x_sizes", [P, TT, C])
        a_ps = core.ps(mem, "x_a_ps", [P, T])
        b_ps = core.ps(mem, "x_b_ps", [X_STATS, T])
        block = mem.enter_context(nc.Block())

        @block.sync
        def _(sp):
            for dst, name in ((r1x[:, :], "x_r1x"), (r1s[:, :], "x_r1s"), (r1b[:, :], "x_r1b")):
                sp.dma_start(dst, A[name]).then_inc(loaded, 16)

        @block.tensor
        def _(pe):
            for t in range(TT):
                nc.tensor.transpose(a_ps[:, t * P:(t + 1) * P], xT[:, t * P:(t + 1) * P],
                                    core.ident[:, :]).then_inc(turned, 1)
            pe.wait_ge(loaded, 48)
            pe.wait_ge(kept, B)
            pe.wait_ge(stats_ready, 1)
            for t in range(TT):
                last = nc.tensor.transpose(b_ps[:, t * P:(t + 1) * P], stats[:, t, :], core.ident[:, :])
            last.then_inc(stats_turned, 1)
            pe.wait_ge(stats_kept, 1)
            for i in range(B):
                nc.tensor.matmul(a_ps[0:X_ROUTER, cols(i)], r1x[:, :], xT[:, cols(i)], start=True, stop=False)
                nc.tensor.matmul(a_ps[0:X_ROUTER, cols(i)], r1s[:, :], statsT[:, cols(i)], start=False,
                                 stop=True).then_inc(hidden_ready, 1)

        @block.scalar
        def _(act):
            for i in range(B):
                act.wait_ge(turned, (TT // B) * (i + 1))
                nc.scalar.activation(xt[:, 4 * i:4 * i + 4, :].rearrange("p t c -> p (t c)"), a_ps[:, cols(i)],
                                     ACT.Copy).then_inc(kept, 1)
            act.wait_ge(kept, B)
            nc.scalar.activation(sizes[:, :, :], xt[:, :, :], ACT.Abs).then_inc(sizes_ready, 1)
            act.wait_ge(variance_ready, 1)
            nc.scalar.activation(roots[:, :, :], spreads[:, :, :], ACT.Sqrt).then_inc(roots_ready, 1)
            act.wait_ge(stats_turned, 1)
            nc.scalar.activation(statsT[:, :], b_ps[:, :], ACT.Copy).then_inc(stats_kept, 1)
            act.wait_ge(loaded, 48)
            act.wait_ge(hidden_ready, B)
            nc.scalar.activation(hT[:, :], a_ps[0:X_ROUTER, :], ACT.Gelu, bias=r1b[:, 0:1])

        @block.gpsimd
        def _(pool):
            pool.wait_ge(kept, B)
            nc.gpsimd.tensor_tensor(squares[:, :, :], xt[:, :, :], xt[:, :, :], ALU.mult).then_inc(squares_ready, 1)

        @block.vector
        def _(dve):
            done = [0]

            def then(instruction):
                instruction.then_inc(step, 1)
                done[0] += 1
                dve.wait_ge(step, done[0])

            def reduce(out, src, op):
                return nc.vector.tensor_reduce(out, src, axis=AX.X, op=op)

            dve.wait_ge(kept, B)
            then(reduce(sums[:, :], xt[:, :, :], ALU.add))
            then(nc.vector.tensor_scalar(stats[:, :, 0], sums[:, :], 1.0 / C, None, ALU.mult))
            then(nc.vector.tensor_tensor(centred[:, :, :], xt[:, :, :], spread(stats[:, :, 0], C), ALU.subtract))
            then(nc.vector.tensor_tensor(centred[:, :, :], centred[:, :, :], centred[:, :, :], ALU.mult))
            then(reduce(sums[:, :], centred[:, :, :], ALU.add))
            nc.vector.tensor_scalar(spreads[:, 0, :], sums[:, :], 1.0 / (C - 1), None, ALU.mult)
            dve.wait_ge(squares_ready, 1)
            reduce(spreads[:, 1, :], squares[:, :, :], ALU.add).then_inc(variance_ready, 1)
            reduce(stats[:, :, 2], xt[:, :, :], ALU.min)
            then(reduce(stats[:, :, 3], xt[:, :, :], ALU.max))
            dve.wait_ge(sizes_ready, 1)
            then(nc.vector.tensor_scalar(centred[:, :, :], sizes[:, :, :], 1e-6, None, ALU.is_lt))
            then(reduce(sums[:, :], centred[:, :, :], ALU.add))
            nc.vector.tensor_scalar(stats[:, :, 5], sums[:, :], 1.0 / C, None, ALU.mult)
            dve.wait_ge(roots_ready, 1)
            nc.vector.tensor_copy(stats[:, :, 1], roots[:, 0, :])
            nc.vector.tensor_copy(stats[:, :, 4], roots[:, 1, :]).then_inc(stats_ready, 1)


def sparse_route(core, A, xt, hT, weight, slot, slots_dram, results_dram, dispatched):
    nc = core.nc
    E = X_EXPERTS
    loaded = core.sem("x_r2_loaded")
    zeroed = core.sem("x_zeroed")
    slots_zeroed = core.sem("x_slots_zeroed")
    logits_ready = core.sem("x_logits")
    shifted_ready = core.sem("x_shifted")
    exp_ready = core.sem("x_exp")
    score_ready = core.sem("x_score")
    score_turned = core.sem("x_score_turned")
    place_ready = core.sem("x_place")
    place_turned = core.sem("x_place_turned")
    slot_ready = core.sem("x_slot_ready")
    step = core.sem("x_step")
    with ExitStack() as mem:
        r2 = core.sb(mem, "x_r2", [X_ROUTER, E])
        iota = core.sb(mem, "x_iota", [P, TT, E])
        base = core.sb(mem, "x_base", [E, 1])
        zero = core.sb(mem, "x_zero", [P, C])
        most = core.sb(mem, "x_most", [P, TT])
        probs = core.sb(mem, "x_probs", [P, TT, E])
        top = core.sb(mem, "x_top", [P, TT, 8])
        index = core.sb(mem, "x_index", [P, TT, 8], U32)
        indexf = core.sb(mem, "x_indexf", [P, TT, 8])
        hits = core.sb(mem, "x_hits", [P, 2, TT, E])
        score = core.sb(mem, "x_score_sb", [P, TT, E])
        mask = core.sb(mem, "x_mask", [P, TT, E])
        total = core.sb(mem, "x_total", [P, TT])
        slotf = core.sb(mem, "x_slotf", [P, 2, TT])
        isnt = core.sb(mem, "x_isnt", [P, 2, TT])
        scoreT = core.sb(mem, "x_scoreT", [E, T])
        work = core.sb(mem, "x_work", [E, T])
        best = core.sb(mem, "x_best", [E, 8])
        placeT = core.sb(mem, "x_placeT", [E, T])
        logits_ps = core.ps(mem, "x_logits_ps", [P, TT, E])
        turn_ps = core.ps(mem, "x_turn_ps", [E, T])
        place_ps = core.ps(mem, "x_place_ps", [P, TT, E])
        block = mem.enter_context(nc.Block())

        @block.sync
        def _(sp):
            for dst, name in ((r2[:, :], "x_r2"), (iota[:, :, :], "x_iota"), (base[:, :], "x_base")):
                sp.dma_start(dst, A[name]).then_inc(loaded, 16)
            sp.wait_ge(zeroed, 1)
            for n in range(X_ST):
                sp.dma_start(slots_dram[n * P:(n + 1) * P, :], zero[:, :]).then_inc(slots_zeroed, 16)
            sp.dma_start(results_dram[X_SLOTS:X_SLOTS + 1, :], zero[0:1, :]).then_inc(slots_zeroed, 16)
            sp.wait_ge(slots_zeroed, 16 * (X_ST + 1))

        @block.tensor
        def _(pe):
            pe.wait_ge(loaded, 48)
            for t in range(TT):
                last = nc.tensor.matmul(logits_ps[:, t, :], hT[:, t * P:(t + 1) * P], r2[:, :], start=True, stop=True)
            last.then_inc(logits_ready, 1)
            pe.wait_ge(score_ready, 1)
            for t in range(TT):
                last = nc.tensor.transpose(turn_ps[:, t * P:(t + 1) * P], score[:, t, :], core.ident[:, :])
            last.then_inc(score_turned, 1)
            pe.wait_ge(place_ready, 1)
            for t in range(TT):
                last = nc.tensor.transpose(place_ps[:, t, :], placeT[:, t * P:(t + 1) * P], core.ident[0:E, 0:E])
            last.then_inc(place_turned, 1)

        @block.scalar
        def _(act):
            act.wait_ge(shifted_ready, 1)
            nc.scalar.activation(probs[:, :, :], score[:, :, :], ACT.Exp).then_inc(exp_ready, 1)

        @block.gpsimd
        def _(pool):
            nc.gpsimd.memset(zero[:, :], 0.0).then_inc(zeroed, 1)
            pool.wait_ge(slots_zeroed, 16 * (X_ST + 1))
            pool.wait_ge(slot_ready, 1)
            for k in range(2):
                for t in range(TT):
                    nc.gpsimd.indirect_dma_start(
                        out=slots_dram, out_offset=bass.IndirectOffsetOnAxis(ap=slot[:, k, t:t + 1], axis=0),
                        in_=xt[:, t, :], in_offset=None, bounds_check=X_SLOTS - 1,
                        oob_is_err=False).then_inc(dispatched, 16)
            pool.wait_ge(dispatched, 16 * 2 * TT)

        @block.vector
        def _(dve):
            done = [0]

            def then(instruction):
                instruction.then_inc(step, 1)
                done[0] += 1
                dve.wait_ge(step, done[0])

            dve.wait_ge(loaded, 48)
            dve.wait_ge(logits_ready, 1)
            then(nc.vector.tensor_reduce(most[:, :], logits_ps[:, :, :], axis=AX.X, op=ALU.max))
            nc.vector.tensor_tensor(score[:, :, :], logits_ps[:, :, :], spread(most[:, :], E),
                                    ALU.subtract).then_inc(shifted_ready, 1)
            dve.wait_ge(exp_ready, 1)
            then(nc.vector.tensor_reduce(total[:, :], probs[:, :, :], axis=AX.X, op=ALU.add))
            then(nc.vector.reciprocal(total[:, :], total[:, :]))
            then(nc.vector.tensor_tensor(probs[:, :, :], probs[:, :, :], spread(total[:, :], E), ALU.mult))
            for t in range(TT):
                last = nc.vector.max(top[:, t, :], probs[:, t, :])
            then(last)
            for t in range(TT):
                last = nc.vector.max_index(index[:, t, :], top[:, t, :], probs[:, t, :])
            then(last)
            then(nc.vector.tensor_copy(indexf[:, :, :], index[:, :, :]))
            for k in range(2):
                last = nc.vector.tensor_tensor(hits[:, k, :, :], iota[:, :, :], spread(indexf[:, :, k], E),
                                               ALU.is_equal)
            then(last)
            then(nc.vector.tensor_tensor(mask[:, :, :], hits[:, 0, :, :], hits[:, 1, :, :], ALU.add))
            then(nc.vector.tensor_tensor(score[:, :, :], probs[:, :, :], mask[:, :, :], ALU.mult))
            then(nc.vector.tensor_scalar(mask[:, :, :], mask[:, :, :], -1.0, None, ALU.add))
            nc.vector.tensor_tensor(score[:, :, :], score[:, :, :], mask[:, :, :], ALU.add).then_inc(score_ready, 1)
            then(nc.vector.tensor_tensor(total[:, :], top[:, :, 0], top[:, :, 1], ALU.add))
            then(nc.vector.reciprocal(total[:, :], total[:, :]))
            for k in range(2):
                last = nc.vector.tensor_tensor(weight[:, k, :], top[:, :, k], total[:, :], ALU.mult)
            then(last)
            dve.wait_ge(score_turned, 1)
            nc.vector.tensor_copy(scoreT[:, :], turn_ps[:, :])
            then(nc.vector.tensor_copy(work[:, :], turn_ps[:, :]))
            for n in range(X_CAP // 8):
                then(nc.vector.max(best[:, :], work[:, :]))
                then(nc.vector.match_replace(work[:, :], best[:, :], work[:, :], TAKEN))
            then(nc.vector.tensor_scalar(work[:, :], work[:, :], TAKEN, None, ALU.is_equal))
            then(nc.vector.scalar_tensor_tensor(out=work[:, :], in0=scoreT[:, :], scalar=0.0, in1=work[:, :],
                                                op0=ALU.is_ge, op1=ALU.mult))
            then(nc.vector.tensor_tensor_scan(placeT[:, :], core.ones_row[0:E, 0:1].to_broadcast([E, T]), work[:, :], 0.0,
                                              ALU.mult, ALU.add))
            nc.vector.scalar_tensor_tensor(out=placeT[:, :], in0=placeT[:, :], scalar=base[:, 0:1], in1=work[:, :],
                                           op0=ALU.add, op1=ALU.mult).then_inc(place_ready, 1)
            dve.wait_ge(place_turned, 1)
            for k in range(2):
                then(nc.vector.tensor_tensor(score[:, :, :], hits[:, k, :, :], place_ps[:, :, :], ALU.mult))
                then(nc.vector.tensor_reduce(slotf[:, k, :], score[:, :, :], axis=AX.X, op=ALU.add))
            then(nc.vector.tensor_scalar(isnt[:, :, :], slotf[:, :, :], 0.0, float(X_SLOTS + 1), ALU.is_equal,
                                         ALU.mult))
            then(nc.vector.scalar_tensor_tensor(out=slotf[:, :, :], in0=slotf[:, :, :], scalar=-1.0,
                                                in1=isnt[:, :, :], op0=ALU.add, op1=ALU.add))
            nc.vector.tensor_copy(slot[:, :, :], slotf[:, :, :]).then_inc(slot_ready, 1)


def sparse_experts(core, slots_dram, results_dram, wu, wd, wau, wad, w_loaded):
    nc = core.nc
    E, G, CAP = X_EXPERTS, X_GROUPS, X_CAP
    JT = X_INTER // P
    PAIR = E // G
    slots_loaded = core.sem("x_slots_loaded")
    turned = core.sem("x_slots_turned")
    kept = core.sem("x_slots_kept")
    up_ready = core.sem("x_up")
    silu_ready = core.sem("x_silu")
    act_ready = core.sem("x_act")
    down_ready = core.sem("x_down")
    result_ready = core.sem("x_result")
    stored = core.sem("x_stored")
    UNITS_G = PAIR + 1
    with ExitStack() as mem:
        slots = core.sb(mem, "x_slots_sb", [P, X_ST, C])
        slotsT = core.sb(mem, "x_slotsT", [C, X_SLOTS])
        silu = core.sb(mem, "x_silu_sb", [P, 2, PAIR * CAP])
        hid = core.sb(mem, "x_hid_sb", [P, 2 * UNITS_G, PAIR * CAP])
        results = core.sb(mem, "x_results_sb", [CAP, E, C])
        t_ps = [core.ps(mem, f"x_t_ps{n}", [P, N]) for n in range(2)]
        up_ps = [core.ps(mem, f"x_up_ps{n}", [P, N]) for n in range(3)]
        d_ps = [core.ps(mem, f"x_d_ps{n}", [P, C]) for n in range(2)]
        block = mem.enter_context(nc.Block())
        TURNS = X_ST // 4

        def units():
            for g in range(G):
                yield g, None
                for e in range(PAIR * g, PAIR * (g + 1)):
                    yield g, e

        UNITS_ALL = list(units())

        @block.sync
        def _(sp):
            for n in range(TURNS):
                sp.dma_start(slots[:, 4 * n:4 * n + 4, :],
                             slots_dram[4 * n * P:4 * (n + 1) * P, :].rearrange("(t p) c -> p t c", p=P)) \
                    .then_inc(slots_loaded, 16)
                sp.wait_ge(slots_loaded, 16 * (n + 1))
            for n in range(4):
                some = slice(n * E // 4, (n + 1) * E // 4)
                sp.wait_ge(result_ready, (n + 1) * E // 4)
                sp.dma_start(results_dram[n * X_SLOTS // 4:(n + 1) * X_SLOTS // 4, :]
                             .rearrange("(e s) c -> s e c", s=CAP), results[:, some, :]).then_inc(stored, 16)
            sp.wait_ge(stored, 64)

        @block.tensor
        def _(pe):
            for n in range(TURNS):
                pe.wait_ge(slots_loaded, 16 * (n + 1))
                if n >= 2:
                    pe.wait_ge(kept, n - 1)
                for t in range(4):
                    last = nc.tensor.transpose(t_ps[n % 2][:, t * P:(t + 1) * P], slots[:, 4 * n + t, :],
                                               core.ident[:, :])
                last.then_inc(turned, 1)
            pe.wait_ge(kept, TURNS)
            pe.wait_ge(w_loaded, 16 * 8)

            def up(n):
                g, e = UNITS_ALL[n]
                if n >= 3:
                    pe.wait_ge(act_ready, n - 2)
                first, count = (PAIR * g, PAIR) if e is None else (e, 1)
                src = slotsT[:, first * CAP:(first + count) * CAP]
                tiles = 2 if e is None else 2 * JT
                for m in range(tiles):
                    w = wau[:, g, m * P:(m + 1) * P] if e is None else wu[:, e, m * P:(m + 1) * P]
                    last = nc.tensor.matmul(up_ps[n % 3][:, m * count * CAP:(m + 1) * count * CAP], w, src,
                                            start=True, stop=True)
                last.then_inc(up_ready, 1)

            def down(n):
                g, e = UNITS_ALL[n]
                if e is None:
                    return
                pe.wait_ge(act_ready, n + 1)
                if e >= 2:
                    pe.wait_ge(result_ready, e - 1)
                here = n % (2 * UNITS_G)
                adapter = (n - 1 - e % PAIR) % (2 * UNITS_G)
                for j in range(JT):
                    nc.tensor.matmul(d_ps[e % 2][0:CAP, :], hid[:, here, j * CAP:(j + 1) * CAP], wd[:, e, j, :],
                                     start=(j == 0), stop=False)
                nc.tensor.matmul(d_ps[e % 2][0:CAP, :], hid[:, adapter, e % PAIR * CAP:(e % PAIR + 1) * CAP],
                                 wad[:, g, :], start=False, stop=True).then_inc(down_ready, 1)

            for n in range(len(UNITS_ALL) + 1):
                if n < len(UNITS_ALL):
                    up(n)
                if n:
                    down(n - 1)

        @block.scalar
        def _(act):
            for n, (g, e) in enumerate(UNITS_ALL):
                act.wait_ge(up_ready, n + 1)
                if n >= 2:
                    act.wait_ge(act_ready, n - 1)
                nc.scalar.activation(silu[:, n % 2, :], up_ps[n % 3][:, 0:PAIR * CAP], ACT.Silu).then_inc(silu_ready, 1)

        @block.vector
        def _(dve):
            for n in range(TURNS):
                dve.wait_ge(turned, n + 1)
                nc.vector.tensor_copy(slotsT[:, n * N:(n + 1) * N], t_ps[n % 2][:, :]).then_inc(kept, 1)

            def result(n):
                g, e = UNITS_ALL[n]
                if e is None:
                    return
                dve.wait_ge(down_ready, e + 1)
                nc.vector.tensor_copy(results[:, e, :], d_ps[e % 2][0:CAP, :]).then_inc(result_ready, 1)

            for n in range(len(UNITS_ALL) + 2):
                if n < len(UNITS_ALL):
                    g, e = UNITS_ALL[n]
                    dve.wait_ge(silu_ready, n + 1)
                    if n >= 2 * UNITS_G:
                        dve.wait_ge(down_ready, PAIR * (n // UNITS_G - 1))
                    nc.vector.scalar_tensor_tensor(
                        out=hid[:, n % (2 * UNITS_G), :], in0=up_ps[n % 3][:, PAIR * CAP:2 * PAIR * CAP],
                        scalar=ADAPTER_SCALE if e is None else 1.0, in1=silu[:, n % 2, :], op0=ALU.mult,
                        op1=ALU.mult).then_inc(act_ready, 1)
                if n >= 2:
                    result(n - 2)


def sparse_combine(core, xT, results_dram, weight, slot):
    nc = core.nc
    fetched = core.sem("x_fetched")
    scaled = core.sem("x_scaled")
    mixed = core.sem("x_mixed")
    turned = core.sem("x_mixed_turned")
    CT = TT // B
    with ExitStack() as mem:
        got = core.sb(mem, "x_got", [P, 2, TT, C])
        y = core.sb(mem, "x_y", [P, TT, C])
        y_ps = core.ps(mem, "x_y_ps", [C, T])
        block = mem.enter_context(nc.Block())

        @block.gpsimd
        def _(pool):
            for t in range(TT):
                for k in range(2):
                    nc.gpsimd.indirect_dma_start(
                        out=got[:, k, t, :], out_offset=None, in_=results_dram,
                        in_offset=bass.IndirectOffsetOnAxis(ap=slot[:, k, t:t + 1], axis=0)).then_inc(fetched, 16)

        @block.vector
        def _(dve):
            dve.wait_ge(fetched, 16 * 2 * TT)
            for t in range(TT):
                nc.vector.tensor_scalar(y[:, t, :], got[:, 0, t, :], weight[:, 0, t:t + 1], None,
                                        ALU.mult).then_inc(scaled, 1)
            for t in range(TT):
                dve.wait_ge(scaled, t + 1)
                nc.vector.scalar_tensor_tensor(out=y[:, t, :], in0=got[:, 1, t, :], scalar=weight[:, 1, t:t + 1],
                                               in1=y[:, t, :], op0=ALU.mult, op1=ALU.add).then_inc(mixed, 1)
            for i in range(B):
                dve.wait_ge(turned, CT * (i + 1))
                nc.vector.tensor_tensor(xT[:, cols(i)], y_ps[:, cols(i)], xT[:, cols(i)], ALU.add)

        @block.tensor
        def _(pe):
            for t in range(TT):
                pe.wait_ge(mixed, t + 1)
                nc.tensor.transpose(y_ps[:, t * P:(t + 1) * P], y[:, t, :], core.ident[:, :]).then_inc(turned, 1)


CH_EXPERTS = 8
CH_HID = 512
CH_HT = CH_HID // P
CH_ALL = CH_EXPERTS + 1
CHOSEN = 2 * T
BITS = 30


def choice_stage(core, A, xT):
    with ExitStack() as mem:
        gateT = core.sb(mem, "c_gateT", [CH_EXPERTS, T])
        w1 = core.sb(mem, "c_w1", [C, CH_ALL, CH_HID])
        w2 = core.sb(mem, "c_w2", [P, CH_ALL, CH_HT, C])
        w_loaded = core.sem("c_w_loaded")
        choice_route(core, A, xT, gateT, w1, w2, w_loaded)
        choice_experts(core, A, xT, gateT, w1, w2, w_loaded)


def choice_route(core, A, xT, gateT, w1, w2, w_loaded):
    nc = core.nc
    E = CH_EXPERTS
    loaded = core.sem("c_loaded")
    logits_ready = core.sem("c_logits")
    shifted_ready = core.sem("c_shifted")
    exp_ready = core.sem("c_exp")
    count_ready = core.sem("c_count")
    total_ready = core.sem("c_total")
    equal_ready = core.sem("c_equal")
    places_ready = core.sem("c_places")
    gate_ready = core.sem("c_gate")
    gate_turned = core.sem("c_gate_turned")
    step = core.sem("c_step")
    tried = core.sem("c_tried")
    passed = core.sem("c_passed")
    threshold_ready = core.sem("c_threshold")
    with ExitStack() as mem:
        wr = core.sb(mem, "c_wr", [C, E])
        tri = core.sb(mem, "c_tri", [P, P])
        ones = core.sb(mem, "c_ones", [P, P])
        bits = core.sb(mem, "c_bits", [P, BITS], I32)
        bitsf = core.sb(mem, "c_bitsf", [P, BITS])
        most = core.sb(mem, "c_most", [P, TT])
        shifted = core.sb(mem, "c_shifted_sb", [P, TT, E])
        scores = core.sb(mem, "c_scores", [P, TT, E])
        total = core.sb(mem, "c_total_sb", [P, TT])
        above = core.sb(mem, "c_above", [P, TT, E])
        equal = core.sb(mem, "c_equal_sb", [P, TT, E])
        threshold = core.sb(mem, "c_threshold_sb", [P, 1], I32)
        trial = core.sb(mem, "c_trial", [P, 1], I32)
        bit = core.sb(mem, "c_bit", [P, 1], I32)
        count = core.sb(mem, "c_count_sb", [P, 1])
        places = core.sb(mem, "c_places_sb", [P, TT, E])
        totals = core.sb(mem, "c_totals", [P, TT, E])
        before = core.sb(mem, "c_before", [P, E])
        needed = core.sb(mem, "c_needed", [P, 1])
        logits_ps = core.ps(mem, "c_logits_ps", [P, TT, E])
        total_ps = core.ps(mem, "c_total_ps", [P, 1])
        prefix_ps = core.ps(mem, "c_prefix_ps", [P, TT, E])
        totals_ps = core.ps(mem, "c_totals_ps", [P, TT, E])
        turn_ps = core.ps(mem, "c_turn_ps", [E, T])
        block = mem.enter_context(nc.Block())

        @block.sync
        def _(sp):
            for dst, name in ((wr[:, :], "c_wr"), (tri[:, :], "tri"), (ones[:, :], "ones"), (bits[:, :], "c_bits"),
                              (bitsf[:, :], "c_bitsf")):
                sp.dma_start(dst, A[name]).then_inc(loaded, 16)
            sp.dma_start(w1[:, :, :], A["c_w1"]).then_inc(w_loaded, 16)
            sp.dma_start(w2[:, :, :, :], A["c_w2"]).then_inc(w_loaded, 16)

        @block.tensor
        def _(pe):
            pe.wait_ge(loaded, 16 * 5)
            for t in range(TT):
                last = nc.tensor.matmul(logits_ps[:, t, :], xT[:, t * P:(t + 1) * P], wr[:, :], start=True, stop=True)
            last.then_inc(logits_ready, 1)
            with pe.Fori(0, BITS + 1) as i:
                pe.wait_ge(count_ready, i + 1)
                nc.tensor.matmul(total_ps[:, :], ones[:, :], count[:, :], start=True, stop=True).then_inc(total_ready, 1)
            pe.wait_ge(equal_ready, 1)
            nc.tensor.matmul(prefix_ps[:, :, :], tri[:, :], equal[:, :, :], start=True, stop=True)
            nc.tensor.matmul(totals_ps[:, :, :], ones[:, :], equal[:, :, :], start=True,
                             stop=True).then_inc(places_ready, 1)
            pe.wait_ge(gate_ready, 1)
            for t in range(TT):
                last = nc.tensor.transpose(turn_ps[:, t * P:(t + 1) * P], scores[:, t, :], core.ident[:, :])
            last.then_inc(gate_turned, 1)

        @block.scalar
        def _(act):
            act.wait_ge(shifted_ready, 1)
            nc.scalar.activation(scores[:, :, :], shifted[:, :, :], ACT.Exp).then_inc(exp_ready, 1)
            act.wait_ge(gate_turned, 1)
            nc.scalar.activation(gateT[:, :], turn_ps[:, :], ACT.Copy)

        @block.vector
        def _(dve):
            done = [0]

            def then(instruction):
                instruction.then_inc(step, 1)
                done[0] += 1
                dve.wait_ge(step, done[0])

            dve.wait_ge(loaded, 16 * 5)
            dve.wait_ge(logits_ready, 1)
            then(nc.vector.tensor_reduce(most[:, :], logits_ps[:, :, :], axis=AX.X, op=ALU.max))
            nc.vector.tensor_tensor(shifted[:, :, :], logits_ps[:, :, :], spread(most[:, :], E),
                                    ALU.subtract).then_inc(shifted_ready, 1)
            nc.vector.memset(threshold[:, :], 0).then_inc(threshold_ready, 1)
            dve.wait_ge(exp_ready, 1)
            then(nc.vector.tensor_reduce(total[:, :], scores[:, :, :], axis=AX.X, op=ALU.add))
            then(nc.vector.reciprocal(total[:, :], total[:, :]))
            then(nc.vector.tensor_tensor(scores[:, :, :], scores[:, :, :], spread(total[:, :], E), ALU.mult))
            flat = scores[:, :, :].rearrange("p t e -> p (t e)")
            scratch = above[:, :, :].rearrange("p t e -> p (t e)")
            with dve.Fori(0, BITS) as i:
                dve.wait_ge(threshold_ready, i + 1)
                nc.vector.tensor_tensor(trial[:, :], threshold[:, :], bits[:, bass.ds(i, 1)],
                                        ALU.bitwise_or).then_inc(tried, 1)
                dve.wait_ge(tried, i + 1)
                nc.vector.tensor_scalar(scratch, flat, trial[:, :].bitcast(F32), None, ALU.is_ge, ALU.add,
                                        accum_out=count[:, :]).then_inc(count_ready, 1)
                dve.wait_ge(total_ready, i + 1)
                nc.vector.tensor_scalar(bit[:, :], total_ps[:, :], float(CHOSEN), bitsf[:, bass.ds(i, 1)],
                                        ALU.is_ge, ALU.mult).then_inc(passed, 1)
                dve.wait_ge(passed, i + 1)
                nc.vector.tensor_tensor(threshold[:, :], threshold[:, :], bit[:, :],
                                        ALU.bitwise_or).then_inc(threshold_ready, 1)
            dve.wait_ge(threshold_ready, BITS + 1)
            least = threshold[:, :].bitcast(F32)
            nc.vector.tensor_scalar(scratch, flat, least, None, ALU.is_gt, ALU.add,
                                    accum_out=count[:, :]).then_inc(count_ready, 1)
            nc.vector.tensor_scalar(equal[:, :, :], scores[:, :, :], least, None, ALU.is_equal).then_inc(equal_ready, 1)
            dve.wait_ge(total_ready, BITS + 1)
            then(nc.vector.tensor_scalar(needed[:, :], total_ps[:, :], -1.0, float(CHOSEN), ALU.mult, ALU.add))
            dve.wait_ge(places_ready, 1)
            then(nc.vector.tensor_copy(totals[:, :, :], totals_ps[:, :, :]))
            for e in range(E):
                last = nc.vector.tensor_tensor_scan(places[:, :, e], core.ones_row[:, 0:TT], totals[:, :, e], 0.0,
                                                    ALU.mult, ALU.add)
            then(last)
            then(nc.vector.tensor_tensor_scan(before[:, :], core.ones_row[:, 0:E], places[:, TT - 1, :], 0.0,
                                              ALU.mult, ALU.add))
            then(nc.vector.tensor_tensor(before[:, :], before[:, :], places[:, TT - 1, :], ALU.subtract))
            then(nc.vector.tensor_tensor(places[:, :, :], places[:, :, :], totals[:, :, :], ALU.subtract))
            then(nc.vector.tensor_tensor(places[:, :, :], places[:, :, :], prefix_ps[:, :, :], ALU.add))
            then(nc.vector.tensor_tensor(places[:, :, :], places[:, :, :],
                                         before[:, :].unsqueeze(1).to_broadcast([P, TT, E]), ALU.add))
            then(nc.vector.scalar_tensor_tensor(out=places[:, :, :], in0=places[:, :, :], scalar=needed[:, 0:1],
                                                in1=equal[:, :, :], op0=ALU.is_le, op1=ALU.mult))
            then(nc.vector.tensor_tensor(above[:, :, :], above[:, :, :], places[:, :, :], ALU.add))
            nc.vector.tensor_tensor(scores[:, :, :], scores[:, :, :], above[:, :, :], ALU.mult).then_inc(gate_ready, 1)


def choice_experts(core, A, xT, gateT, w1, w2, w_loaded):
    nc = core.nc
    E = CH_EXPERTS
    RING = 3
    PER = CH_ALL * CH_HT
    loaded = core.sem("c_b_loaded")
    up_ready = core.sem("c_up")
    gelu_ready = core.sem("c_gelu")
    spread_ready = core.sem("c_spread")
    gated_ready = core.sem("c_gated")
    down_ready = core.sem("c_down")
    added = core.sem("c_added")
    with ExitStack() as mem:
        b1 = core.sb(mem, "c_b1", [P, CH_ALL, CH_HT])
        b2 = core.sb(mem, "c_b2", [E, C])
        bs2 = core.sb(mem, "c_bs2", [C, 1])
        select = core.sb(mem, "c_select", [E, E, P])
        hid = core.sb(mem, "c_hid", [P, 2, CH_HT, N])
        gated = core.sb(mem, "c_gated_sb", [P, 2, CH_HT, N])
        up_ps = [core.ps(mem, f"c_up_ps{n}", [P, N]) for n in range(RING)]
        g_ps = [core.ps(mem, f"c_g_ps{n}", [P, N]) for n in range(2)]
        y_ps = core.ps(mem, "c_y_ps", [C, N])
        block = mem.enter_context(nc.Block())

        @block.sync
        def _(sp):
            for dst, name in ((b1[:, :, :], "c_b1"), (b2[:, :], "c_b2"), (bs2[:, :], "c_bs2"),
                              (select[:, :, :], "c_select")):
                sp.dma_start(dst, A[name]).then_inc(loaded, 16)

        @block.tensor
        def _(pe):
            pe.wait_ge(loaded, 64)
            pe.wait_ge(w_loaded, 32)
            with pe.Fori(0, B) as i:
                def up(e):
                    for m in range(CH_HT):
                        u = e * CH_HT + m
                        if m == CH_HT - 1 and e < E:
                            pe.wait_ge(gated_ready, i * E + max(e - 1, 0))
                        pe.wait_ge(gelu_ready, i * PER + max(u - RING + 1, 0))
                        nc.tensor.matmul(up_ps[u % RING][:, :], w1[:, e, m * P:(m + 1) * P], xT[:, cols(i)],
                                         start=True, stop=True).then_inc(up_ready, 1)
                    if e < E:
                        nc.tensor.matmul(g_ps[e % 2][:, :], select[:, e, :], gateT[:, cols(i)],
                                         start=True, stop=True).then_inc(spread_ready, 1)

                def down(e):
                    if e < E:
                        pe.wait_ge(gated_ready, i * E + e + 1)
                        src = gated
                    else:
                        pe.wait_ge(gelu_ready, (i + 1) * PER)
                        src = hid
                    if e == 0:
                        pe.wait_ge(added, i)
                    for k in range(CH_HT):
                        last = nc.tensor.matmul(y_ps[:, :], w2[:, e, k, :], src[:, e % 2, k, :],
                                                start=(e == 0 and k == 0), stop=(e == E and k == CH_HT - 1))
                        if e == 0 and k == 0:
                            nc.tensor.matmul(y_ps[:, :], b2[:, :], gateT[:, cols(i)], start=False, stop=False)
                    last.then_inc(down_ready, 1)

                for e in range(CH_ALL + 1):
                    if e < CH_ALL:
                        up(e)
                    if e:
                        down(e - 1)

        @block.scalar
        def _(act):
            act.wait_ge(loaded, 64)
            with act.Fori(0, B) as i:
                for e in range(CH_ALL):
                    for m in range(CH_HT):
                        u = e * CH_HT + m
                        if m == 0:
                            act.wait_ge(gated_ready, i * E + max(e - 1, 0))
                            act.wait_ge(down_ready, i * CH_ALL)
                        act.wait_ge(up_ready, i * PER + u + 1)
                        nc.scalar.activation(hid[:, e % 2, m, :], up_ps[u % RING][:, :], ACT.Gelu_apprx_tanh,
                                             bias=b1[:, e, m:m + 1]).then_inc(gelu_ready, 1)

        @block.vector
        def _(dve):
            dve.wait_ge(loaded, 64)
            with dve.Fori(0, B) as i:
                for e in range(E):
                    dve.wait_ge(spread_ready, i * E + e + 1)
                    dve.wait_ge(down_ready, i * CH_ALL + max(e - 1, 0))
                    dve.wait_ge(gelu_ready, i * PER + (e + 1) * CH_HT)
                    nc.vector.tensor_tensor(gated[:, e % 2, :, :], hid[:, e % 2, :, :],
                                            g_ps[e % 2][:, :].unsqueeze(1).to_broadcast([P, CH_HT, N]),
                                            ALU.mult).then_inc(gated_ready, 1)
                dve.wait_ge(down_ready, (i + 1) * CH_ALL)
                nc.vector.scalar_tensor_tensor(out=xT[:, cols(i)], in0=y_ps[:, :], scalar=bs2[:, 0:1],
                                               in1=xT[:, cols(i)], op0=ALU.add, op1=ALU.add).then_inc(added, 1)


def rope_tables(angles, order):
    freq, sign = order
    theta = np.arange(N, dtype=np.float32)[None, :] * angles.astype(np.float32)[:, None]
    cos, sin = np.cos(theta)[freq], np.sin(theta)[freq] * np.array(sign, np.float32)[:, None]
    scale = np.float32(-(HD ** -0.5))
    one = np.stack([cos * scale, sin * scale, cos, sin], 1).astype(np.float32)
    return np.tile(one, (HEADS, 1, 1))


def lay_attention(tag, wq, wk, wv, wproj, turn, tables):
    order = (np.arange(HEADS)[:, None] * HD + np.array(turn)[None, :]).ravel()
    w = np.stack([wq.T, wq[order].T, wk.T, wk[order].T, wv.T], 1)
    return {f"{tag}_wqkv": w, f"{tag}_rope": tables, f"{tag}_wproj": wproj.T}




def lay_attention0(I):
    L = {}
    half = HD // 2
    qkv = I["L0_attn_qkv_w"]
    angles = 1.0 / np.power(np.float32(10000.0), np.arange(0, HD, 2, dtype=np.float32) / np.float32(HD))
    L |= lay_attention("a0", qkv[:C], qkv[C:2 * C], qkv[2 * C:], I["L0_attn_proj_w"],
                       [(d + half) % HD for d in range(HD)],
                       rope_tables(angles, ([d % half for d in range(HD)], [-1] * half + [1] * half)))
    L["a0_bproj"] = I["L0_attn_proj_b"].reshape(C, 1)
    L["a0_window"] = np.maximum(8.0 * (np.arange(P)[:, None] + (QT - 1) * P - np.arange(WINDOW)[None, :]),
                                0.0).astype(np.float32)
    L["a0_slopes"] = np.broadcast_to(I["L0_attn_slopes"][None, :], (P, HEADS))
    return L


def lay_gated_mlp(I):
    L = {}
    L["f0_w12"] = np.stack([I["L0_ffn_w1_w"].T, I["L0_ffn_w2_w"].T], 1)
    L["f0_wh"] = np.stack([I[f"L0_ffn_{n}_w"].T.reshape(HT, P, HID).transpose(1, 0, 2) for n in ("h1", "h2")], 1)
    L["f0_w3"] = I["L0_ffn_w3_w"].T.reshape(HT, P, C).transpose(1, 0, 2)
    L["f0_scales"] = np.concatenate([I[f"L0_ffn_{n}_s"].reshape(-1, P).T for n in ("w1", "w2", "h1", "h2", "w3")], 1)
    return L


def lay_ssm(I):
    L = {}
    S = {k[8:]: a for k, a in I.items() if k.startswith("L1_attn_")}
    L["s_wide"] = np.stack([S["proj_W"].T, S["fconv_W"].T, S["bconv_W"].T], 1)
    L["s_wdr"] = S["deltaBC_W"][:DT_RANK].T
    L["s_wbc"] = np.tile(S["deltaBC_W"][DT_RANK:].T, (1, 3))
    L["s_wdt"] = np.tile(S["dt_W"].T, (BRANCHES, 1))
    L["s_cst"] = np.stack([S[n] for n in ("ln_w", "ln_b", "proj_b", "fconv_b", "bconv_b", "dt_b", "D")], 1)
    L["s_alog"] = S["A_log"]
    rows = np.arange(3 * BC)[:, None, None] % BC == np.arange(BC)[None, :, None]
    L["s_select"] = np.broadcast_to(rows, (3 * BC, BC, P)).astype(mybir.dt.np(BF16))
    return L


def lay_moe(I):
    L = {}
    L["m_wr"] = I["L1_ffn_w_router"].T
    L["m_iota"] = np.broadcast_to(np.arange(EXPERTS, dtype=np.float32), (P, TT, EXPERTS))
    L["m_wg"] = I["L1_ffn_w_gate"].T
    L["m_wd"] = I["L1_ffn_w_down"].transpose(2, 0, 1).reshape(MOE_HT, P, EXPERTS * C).transpose(1, 0, 2)
    return L


def lay_query_softmax(I):
    L = {}
    L["q_wqk"] = np.stack([I["L2_attn_Mq"], I["L2_attn_Mk"]], 1)
    L["q_wv"] = I["L2_attn_Mv"]
    place = np.zeros((4, VPAD, 2, 2, 4, VD), np.float32)
    for j in range(QH):
        for d in range(VD):
            place[j % 4, d, j // 4, j // 4, j % 4, d] = 1.0
    L["q_place"] = place.reshape(P, 2, C)
    return L


def lay_sparse(I):
    L = {}
    S = {k[7:]: a for k, a in I.items() if k.startswith("L2_ffn_")}
    L["x_wu"] = S["w_up"].transpose(2, 0, 1)
    L["x_wd"] = S["w_down"].reshape(X_EXPERTS, C, X_INTER // P, P).transpose(3, 0, 2, 1)
    L["x_wau"] = S["a_up"].transpose(2, 0, 1)
    L["x_wad"] = S["a_down"].transpose(2, 0, 1)
    L["x_r1x"] = S["r1_w"][:, :C].T
    L["x_r1s"] = S["r1_w"][:, C:].T
    L["x_r1b"] = S["r1_b"].reshape(X_ROUTER, 1)
    L["x_r2"] = S["r2_w"].T
    L["x_iota"] = np.broadcast_to(np.arange(X_EXPERTS, dtype=np.float32), (P, TT, X_EXPERTS))
    L["x_base"] = (np.arange(X_EXPERTS, dtype=np.float32) * X_CAP).reshape(X_EXPERTS, 1)
    return L


def lay_attention3(I):
    L = {}
    half = HD // 2
    angles = np.power(np.float32(10000.0), np.float32(2.0) * np.arange(half, dtype=np.float32) / np.float32(HD))
    L |= lay_attention("a3", I["L3_attn_w_q"], I["L3_attn_w_k"], I["L3_attn_w_v"], I["L3_attn_w_o"],
                       [d ^ 1 for d in range(HD)],
                       rope_tables(angles, ([d // 2 for d in range(HD)], [-1, 1] * half)))
    L["a3_bproj"] = np.zeros((C, 1), np.float32)
    return L


def lay_choice(I):
    L = {}
    L["c_wr"] = I["L3_ffn_gate_weight"].T
    bits = (1 << np.arange(BITS - 1, -1, -1)).astype(np.int32)
    L["c_bits"] = np.broadcast_to(bits, (P, BITS))
    L["c_bitsf"] = L["c_bits"].astype(np.float32)
    L["c_w1"] = np.concatenate([I["L3_ffn_W1"], I["L3_ffn_Ws1"][None]], 0).transpose(1, 0, 2)
    L["c_w2"] = np.concatenate([I["L3_ffn_W2"], I["L3_ffn_Ws2"][None]], 0) \
        .reshape(CH_ALL, CH_HT, P, C).transpose(2, 0, 1, 3)
    L["c_b1"] = np.concatenate([I["L3_ffn_b1"], I["L3_ffn_bs1"][None]], 0) \
        .reshape(CH_ALL, CH_HT, P).transpose(2, 0, 1)
    L["c_b2"] = I["L3_ffn_b2"]
    L["c_bs2"] = I["L3_ffn_bs2"].reshape(C, 1)
    L["c_select"] = np.broadcast_to(np.eye(CH_EXPERTS, dtype=np.float32)[:, :, None], (CH_EXPERTS, CH_EXPERTS, P))
    return L


def attention0_stage(core, A, xT):
    attention_stage(core, A, xT, "a0", alibi=True)


def attention3_stage(core, A, xT):
    attention_stage(core, A, xT, "a3", alibi=False)


STAGES = [(attention0_stage, lay_attention0), (gated_mlp_stage, lay_gated_mlp), (ssm_stage, lay_ssm),
          (moe_stage, lay_moe), (query_softmax_stage, lay_query_softmax), (sparse_stage, lay_sparse),
          (attention3_stage, lay_attention3), (choice_stage, lay_choice)]


def lay_out(I):
    L = {"x": I["L0_attn_x"].reshape(T, C).T,
         "tri": (np.arange(P)[:, None] <= np.arange(P)[None, :]).astype(np.float32),
         "ones": np.ones((P, P), np.float32)}
    for _, lay in STAGES:
        L |= lay(I)
    return L


def network(nc, A, out):
    with ExitStack() as ctx:
        core = Core(nc, ctx)
        xT = core.sb(ctx, "xT", [C, T])
        core.ident = core.sb(ctx, "ident", [P, P])
        core.avg = core.sb(ctx, "avg", [P, P])
        core.eps = core.sb(ctx, "eps", [P, 1])
        core.one = core.sb(ctx, "one", [P, 1])
        core.ones_row = core.sb(ctx, "ones_row", [P, N])
        loaded = core.sem("x_loaded")
        zeroed = core.sem("ident_zeroed")
        with nc.Block() as block:
            @block.sync
            def _(sp):
                sp.dma_start(xT[:, :], A["x"]).then_inc(loaded, 16)
                sp.wait_ge(loaded, 16)

            @block.gpsimd
            def _(pool):
                nc.gpsimd.memset(core.avg[:, :], 1.0 / C)
                nc.gpsimd.memset(core.eps[:, :], LN_EPS)
                nc.gpsimd.memset(core.one[:, :], 1.0)
                nc.gpsimd.memset(core.ones_row[:, :], 1.0)
                nc.gpsimd.memset(core.ident[:, :], 0.0).then_inc(zeroed, 1)
                pool.wait_ge(zeroed, 1)
                nc.gpsimd.affine_select(out=core.ident[:, :], in_=core.ident[:, :], compare_op=ALU.not_equal,
                                        fill=1.0, base=0, pattern=[[-1, P]], channel_multiplier=1)
        for n, (stage, _) in enumerate(STAGES):
            core.run_stage(stage, A, xT)
            layernorm_stage(core, xT, f"ln{n}")
        stored = core.sem("out_stored")
        with nc.Block() as block:
            @block.sync
            def _(sp):
                sp.dma_start(out, xT[:, :]).then_inc(stored, 16)
                sp.wait_ge(stored, 16)


def kernel(**inputs):
    import concourse.bacc as bacc
    from concourse.bass_utils import run_bass_kernel_spmd

    nc = bacc.Bacc("TRN2", target_bir_lowering=False, num_devices=1)
    arrays, args = {}, {}
    for name, a in lay_out({k: np.asarray(v) for k, v in inputs.items()}).items():
        a = np.ascontiguousarray(a)
        arrays[f"in_{name}"] = a
        args[name] = nc.dram_tensor(f"in_{name}", a.shape, mybir.dt.from_np(a.dtype), kind="ExternalInput").ap()
    out = nc.dram_tensor("out_xT", (C, T), F32, kind="ExternalOutput").ap()
    network(nc, args, out)
    result = run_bass_kernel_spmd(nc, [arrays], core_ids=[0])
    return result.results[0]["out_xT"].T.reshape(B, N, C)
```

```python
import concourse.bass as bass
from concourse import mybir
from contextlib import ExitStack

import numpy as np

F32 = mybir.dt.float32
BF16 = mybir.dt.bfloat16
I32 = mybir.dt.int32
U32 = mybir.dt.uint32
ALU = mybir.AluOpType
ACT = mybir.ActivationFunctionType
AX = mybir.AxisListType

B = 4
N = 512
T = B * N
C = 128
P = 128
TT = T // P
LN_EPS = 1e-5
START = 1


def cols(i, size=N):
    return bass.ds(i * size, size)


def spread(ap, size):
    return ap.unsqueeze(2).to_broadcast([ap.shape[0], ap.shape[1], size])


class Core:

    def __init__(self, nc, ctx):
        self.nc, self.ctx = nc, ctx
        self.stage_ctx, self.stage_sems, self.unstarted = None, [], []
        self.norms = 0
        self.norm_sems = [self.sem(f"norm_{n}") for n in ("mean", "centred", "square", "var", "logvar", "rstd")]

    def sb(self, ctx, name, shape, dt=F32):
        return ctx.enter_context(self.nc.sbuf_tensor(name, shape, dt))

    def ps(self, ctx, name, shape, dt=F32):
        return ctx.enter_context(self.nc.psum_tensor(name, shape, dt))

    def sem(self, name, software_dma=False):
        ctx = self.ctx if self.stage_ctx is None else self.stage_ctx
        handle = ctx.enter_context(self.nc.semaphore(name))
        if not software_dma:
            self.unstarted.append(handle)
        self.stage_sems.append(handle)
        return handle

    def block(self):
        if self.unstarted:
            for handle in self.unstarted:
                self.nc.gpsimd.nop().then_inc(handle, START)
            self.unstarted = []
            self.nc.all_engine_barrier()
        return self.nc.Block()

    def run_stage(self, stage, *args):
        self.stage_sems = []
        with ExitStack() as self.stage_ctx:
            stage(self, *args)
            with self.nc.Block() as block:
                @block.gpsimd
                def _(pool):
                    for handle in self.stage_sems:
                        pool.sem_clear(handle)
        self.stage_ctx = None


def layernorm_stage(core, xT, tag, out=None):
    out = xT if out is None else out
    nc = core.nc
    mean_ready, centred_ready, square_ready, var_ready, logvar_ready, rstd_ready = core.norm_sems
    done = core.norms * B
    core.norms += 1
    with ExitStack() as mem:
        centred = core.sb(mem, f"{tag}_xc", [P, T])
        square = core.sb(mem, f"{tag}_sq", [P, T])
        logvar = core.sb(mem, f"{tag}_lv", [P, T])
        rstd = core.sb(mem, f"{tag}_rs", [P, T])
        mean = core.ps(mem, f"{tag}_ps_mean", [P, T])
        var = core.ps(mem, f"{tag}_ps_var", [P, T])
        block = mem.enter_context(core.block())

        @block.tensor
        def _(pe):
            for i in range(B):
                nc.tensor.matmul(mean[:, cols(i)], core.avg[:, :], xT[:, cols(i)],
                                 start=True, stop=True).then_inc(mean_ready, 1)
            for i in range(B):
                pe.wait_ge(square_ready, START + done + i + 1)
                nc.tensor.matmul(var[:, cols(i)], core.avg[:, :], square[:, cols(i)],
                                 start=True, stop=True).then_inc(var_ready, 1)

        @block.gpsimd
        def _(pool):
            for i in range(B):
                pool.wait_ge(centred_ready, START + done + i + 1)
                nc.gpsimd.tensor_tensor(square[:, cols(i)], centred[:, cols(i)], centred[:, cols(i)],
                                        ALU.mult).then_inc(square_ready, 1)

        @block.scalar
        def _(act):
            for i in range(B):
                act.wait_ge(var_ready, START + done + i + 1)
                nc.scalar.activation(logvar[:, cols(i)], var[:, cols(i)], ACT.Ln,
                                     bias=core.eps[:, 0:1]).then_inc(logvar_ready, 1)
                act.wait_ge(logvar_ready, START + done + i + 1)
                nc.scalar.activation(rstd[:, cols(i)], logvar[:, cols(i)], ACT.Exp,
                                     scale=-0.5).then_inc(rstd_ready, 1)

        @block.vector
        def _(dve):
            for i in range(B):
                dve.wait_ge(mean_ready, START + done + i + 1)
                nc.vector.tensor_tensor(centred[:, cols(i)], xT[:, cols(i)], mean[:, cols(i)],
                                        ALU.subtract).then_inc(centred_ready, 1)
            for i in range(B):
                dve.wait_ge(rstd_ready, START + done + i + 1)
                nc.vector.tensor_tensor(out[:, cols(i)], centred[:, cols(i)], rstd[:, cols(i)], ALU.mult)


HEADS = 16
HD = C // HEADS
QT = N // P
KT = N // P
UNITS = HEADS * QT
Q_PARTS = (0, 0, 1, 1, 0, 2)
K_PARTS = (0, 1, 0, 1, 2, 0)
STACK = HD * len(Q_PARTS)
GROUP = 4
GROUPS = HEADS // GROUP
LEAST_AT = 96
LEAST_ROWS = 3
PAIRS_OF_TILES = QT - 1
BIAS_ROWS = 9 * PAIRS_OF_TILES
WINDOW = N + (QT - 1) * P


def attention_stage(core, A, xT, tag, alibi):
    nc = core.nc
    stacks_dram = nc.dram_tensor(f"{tag}_stacks", (2, B, STACK, HEADS, N), BF16).ap()
    rows = LEAST_AT + LEAST_ROWS + (BIAS_ROWS if alibi else 0)
    with ExitStack() as mem:
        M = {"v": core.sb(mem, f"{tag}_v", [P, TT, C]),
             "wproj": core.sb(mem, f"{tag}_wproj", [C, C]),
             "bproj": core.sb(mem, f"{tag}_bproj", [C, 1]),
             "qs": core.sb(mem, f"{tag}_qs", [rows, HEADS, N], BF16),
             "ks": core.sb(mem, f"{tag}_ks", [rows, HEADS, N], BF16)}
        if alibi:
            M["bias"] = core.sb(mem, f"{tag}_bias", [P, HEADS, WINDOW])
            M["steps"] = core.sb(mem, f"{tag}_steps", [P, P], BF16)
            M["slopes_diag"] = core.sb(mem, f"{tag}_slopes_diag", [P, 3, HEADS, P], BF16)
        project_and_split(core, A, xT, tag, stacks_dram, M)
        attend(core, A, xT, tag, stacks_dram, M)


def project_and_split(core, A, xT, tag, stacks_dram, M):
    nc = core.nc
    qs, ks, v_all, wproj, bproj = M["qs"], M["ks"], M["v"], M["wproj"], M["bproj"]
    bias = M.get("bias")
    R, PART_HEADS = BIAS_ROWS, HEADS // B
    w_loaded = core.sem(f"{tag}_w_loaded")
    qk_ready = core.sem(f"{tag}_qk_ready")
    v_ready = core.sem(f"{tag}_v_ready")
    v_kept = core.sem(f"{tag}_v_kept")
    products = core.sem(f"{tag}_rope_products")
    rotated = core.sem(f"{tag}_rotated")
    high = core.sem(f"{tag}_high")
    rest = core.sem(f"{tag}_rest")
    middle = core.sem(f"{tag}_middle")
    low = core.sem(f"{tag}_low")
    stored = [core.sem(f"{tag}_parts_stored{n}") for n in range(2)]
    slopes_loaded = core.sem(f"{tag}_slopes_loaded")
    slope_step = core.sem(f"{tag}_slope_step")
    rows_ready = core.sem(f"{tag}_bias_rows")
    rows_placed = core.sem(f"{tag}_bias_rows_placed")
    STORES = 2 * len(Q_PARTS)
    SLOPES_SPLIT = 1 + 3 * 3
    with ExitStack() as mem:
        wqkv = core.sb(mem, f"{tag}_wqkv", [C, 5, C])
        rope = core.sb(mem, f"{tag}_rope", [C, 4, N])
        prod = core.sb(mem, f"{tag}_prod", [C, 2, 2, N])
        qk = core.sb(mem, f"{tag}_qk", [C, 2, 2, N])
        left = core.sb(mem, f"{tag}_left", [C, 2, 2, N])
        parts = core.sb(mem, f"{tag}_p", [C, 2, 2, 3, N], BF16)
        if alibi := bias is not None:
            window = core.sb(mem, f"{tag}_window", [P, WINDOW])
            slopes = core.sb(mem, f"{tag}_slopes", [P, HEADS])
            slope_parts = core.sb(mem, f"{tag}_slope_parts", [P, 3, HEADS])
            slope_part = core.sb(mem, f"{tag}_slope_part", [P, 3, HEADS], BF16)
            slope_rest = core.sb(mem, f"{tag}_slope_rest", [P, HEADS])
            factor = core.sb(mem, f"{tag}_factor", [R, 2, HEADS])
            which = core.sb(mem, f"{tag}_which", [R, 2, 4])
            pattern = core.sb(mem, f"{tag}_pattern", [R, 2, N])
            rows = core.sb(mem, f"{tag}_rows", [R, 2, HEADS, N], BF16)
        qk_ps = core.ps(mem, f"{tag}_qk_ps", [C, 4, N])
        v_ps = core.ps(mem, f"{tag}_v_ps", [P, KT, C])
        block = mem.enter_context(core.block())

        @block.sync
        def _(sp):
            sp.dma_start(wqkv[:, :, :], A[f"{tag}_wqkv"]).then_inc(w_loaded, 16)
            sp.dma_start(rope[:, :, :], A[f"{tag}_rope"]).then_inc(w_loaded, 16)
            sp.dma_start(wproj[:, :], A[f"{tag}_wproj"]).then_inc(w_loaded, 16)
            sp.dma_start(bproj[:, :], A[f"{tag}_bproj"]).then_inc(w_loaded, 16)
            if alibi:
                for dst, name in ((slopes[:, :], "slopes"), (which[:, :, :], "which"), (window[:, :], "window"),
                                  (pattern[:, :, :], "pattern"), (M["steps"][:, :], "steps")):
                    sp.dma_start(dst, A[f"{tag}_{name}"]).then_inc(slopes_loaded, 16)
            for i in range(B):
                for done, last_part in ((high, 0), (middle, 1), (low, 2)):
                    sp.wait_ge(done, START + i + 1)
                    for s in range(len(Q_PARTS)):
                        for a, part in enumerate((Q_PARTS[s], K_PARTS[s])):
                            if part == last_part:
                                sp.dma_start(stacks_dram[a, i, s * HD:(s + 1) * HD].rearrange("d h t -> h d t"),
                                             parts[:, i % 2, a, part, :]).then_inc(stored[i % 2], 16)
            if alibi:
                for a, dst in enumerate((qs, ks)):
                    sp.wait_ge(rows_ready, START + 2 * B)
                    sp.dma_start(dst[LEAST_AT + LEAST_ROWS:, :, :], rows[:, a, :, :]).then_inc(rows_placed, 16)
                sp.wait_ge(rows_placed, START + 32)
            for n in range(2):
                sp.wait_ge(stored[n], START + 16 * STORES * B // 2)

        @block.tensor
        def _(pe):
            pe.wait_ge(w_loaded, START + 16 * 4)
            for i in range(B):
                for n in range(4):
                    if i > 0:
                        pe.wait_ge(products, START + 4 * (i - 1) + n + 1)
                    nc.tensor.matmul(qk_ps[:, n, :], wqkv[:, n, :], xT[:, cols(i)],
                                     start=True, stop=True).then_inc(qk_ready, 1)
                if i > 0:
                    pe.wait_ge(v_kept, START + i)
                for t in range(KT):
                    at = (i * KT + t) * P
                    last = nc.tensor.matmul(v_ps[:, t, :], xT[:, at:at + P], wqkv[:, 4, :],
                                            start=True, stop=True)
                last.then_inc(v_ready, 1)

        @block.scalar
        def _(act):
            def copy_middle(i):
                act.wait_ge(rest, START + i + 1)
                nc.scalar.activation(parts[:, i % 2, :, 1, :], left[:, i % 2, :, :], ACT.Copy).then_inc(middle, 1)

            if alibi:
                act.wait_ge(slopes_loaded, START + 16 * 5)
            for i in range(B):
                act.wait_ge(rotated, START + i + 1)
                if i > 1:
                    act.wait_ge(stored[i % 2], START + 16 * STORES * (i // 2))
                nc.scalar.activation(parts[:, i % 2, :, 0, :], qk[:, i % 2, :, :], ACT.Copy).then_inc(high, 1)
                act.wait_ge(v_ready, START + i + 1)
                nc.scalar.activation(v_all[:, i * KT:(i + 1) * KT, :], v_ps[:, :, :], ACT.Copy).then_inc(v_kept, 1)
                if i > 0:
                    copy_middle(i - 1)
                if alibi:
                    for h in range(i * PART_HEADS, (i + 1) * PART_HEADS):
                        nc.scalar.activation(bias[:, h, :], window[:, :], ACT.Copy, scale=slopes[:, h:h + 1])
            copy_middle(B - 1)

        @block.vector
        def _(dve):
            steps = [0]

            def then(instruction):
                instruction.then_inc(slope_step, 1)
                steps[0] += 1
                dve.wait_ge(slope_step, START + steps[0])

            nc.vector.memset(qs[0:LEAST_AT, :, :], 0.0)
            if alibi:
                dve.wait_ge(slopes_loaded, START + 16 * 5)
                then(nc.vector.tensor_scalar(slope_rest[:, :], slopes[:, :], 8.0, None, ALU.mult))
                for n in range(3):
                    then(nc.vector.tensor_copy(slope_part[:, n, :], slope_rest[:, :]))
                    then(nc.vector.tensor_copy(slope_parts[:, n, :], slope_part[:, n, :]))
                    then(nc.vector.tensor_tensor(slope_rest[:, :], slope_rest[:, :], slope_parts[:, n, :],
                                                 ALU.subtract))
                for a in range(2):
                    then(nc.vector.tensor_scalar(factor[:, a, :], slope_parts[0:R, 0, :], which[:, a, 0:1],
                                                 which[:, a, 3:4], ALU.mult, ALU.add))
                    for n in (1, 2):
                        then(nc.vector.scalar_tensor_tensor(out=factor[:, a, :], in0=slope_parts[0:R, n, :],
                                                            scalar=which[:, a, n:n + 1], in1=factor[:, a, :],
                                                            op0=ALU.mult, op1=ALU.add))
            dve.wait_ge(w_loaded, START + 16 * 4)
            for i in range(B):
                if i > 0:
                    dve.wait_ge(rotated, START + i)
                for n in range(4):
                    dve.wait_ge(qk_ready, START + 4 * i + n + 1)
                    nc.vector.tensor_tensor(prod[:, n // 2, n % 2, :], qk_ps[:, n, :], rope[:, n, :],
                                            ALU.mult).then_inc(products, 1)
                dve.wait_ge(products, START + 4 * i + 4)
                if i > 1:
                    dve.wait_ge(rest, START + i - 1)
                nc.vector.tensor_tensor(qk[:, i % 2, :, :], prod[:, :, 0, :], prod[:, :, 1, :],
                                        ALU.add).then_inc(rotated, 1)
                if alibi:
                    mine = slice(i * PART_HEADS, (i + 1) * PART_HEADS)
                    for a in range(2):
                        nc.vector.tensor_tensor(
                            rows[:, a, mine, :], pattern[:, a, :].unsqueeze(1).to_broadcast([R, PART_HEADS, N]),
                            spread(factor[:, a, mine], N), ALU.mult).then_inc(rows_ready, 1)

        @block.gpsimd
        def _(pool):
            def subtract_middle(i):
                pool.wait_ge(middle, START + i + 1)
                nc.gpsimd.tensor_tensor(parts[:, i % 2, :, 2, :], left[:, i % 2, :, :], parts[:, i % 2, :, 1, :],
                                        ALU.subtract).then_inc(low, 1)

            nc.gpsimd.memset(ks[0:LEAST_AT, :, :], 0.0)
            for i in range(B):
                pool.wait_ge(high, START + i + 1)
                if i > 1:
                    pool.wait_ge(low, START + i - 1)
                nc.gpsimd.tensor_tensor(left[:, i % 2, :, :], qk[:, i % 2, :, :], parts[:, i % 2, :, 0, :],
                                        ALU.subtract).then_inc(rest, 1)
                if i > 0:
                    subtract_middle(i - 1)
                if alibi:
                    pool.wait_ge(slope_step, START + SLOPES_SPLIT)
                    for n in range(3):
                        for h in range(i * PART_HEADS, (i + 1) * PART_HEADS):
                            nc.gpsimd.tensor_scalar(M["slopes_diag"][:, n, h, :], core.ident[:, :],
                                                    slope_parts[:, n, h:h + 1], None, ALU.mult)
            subtract_middle(B - 1)


def attend(core, A, xT, tag, stacks_dram, M):
    nc = core.nc
    qs, ks, v_all, wproj, bproj = M["qs"], M["ks"], M["v"], M["wproj"], M["bproj"]
    bias = M.get("bias")
    ROWS = qs.shape[0]
    U = GROUP * QT
    VPAD = 32
    stacks = [core.sem(f"{tag}_stack{g}_loaded") for g in range(GROUPS)]
    scores_ready = core.sem(f"{tag}_scores")
    least_ready = core.sem(f"{tag}_least")
    least_turned = core.sem(f"{tag}_least_turned")
    turn_read = core.sem(f"{tag}_turn_read")
    split_step = core.sem(f"{tag}_split_step")
    least_split = core.sem(f"{tag}_least_split")
    least_placed = [core.sem(f"{tag}_least_placed{n}") for n in range(2)]
    minus_ready = core.sem(f"{tag}_minus_ready")
    minus_placed = core.sem(f"{tag}_minus_placed")
    turned_ready = core.sem(f"{tag}_turned_scores")
    probs_ready = core.sem(f"{tag}_probs")
    v_cleared = core.sem(f"{tag}_v_cleared")
    v_ready = core.sem(f"{tag}_v_padded")
    values_ready = core.sem(f"{tag}_values")
    values_kept = core.sem(f"{tag}_values_kept")
    tail_written = core.sem(f"{tag}_tail_written")
    tail_read = core.sem(f"{tag}_tail_read")
    inverse_ready = core.sem(f"{tag}_inverse")
    LOADS = 2
    TAIL = QT + 2

    with ExitStack() as mem:
        vpad = core.sb(mem, f"{tag}_vpad", [P, KT, HEADS, VPAD])
        minus = core.sb(mem, f"{tag}_minus", [LEAST_ROWS, HEADS, N], BF16)
        least = core.sb(mem, f"{tag}_least_sb", [P, 2, U])
        least_parts = core.sb(mem, f"{tag}_least_parts", [U, 2, LEAST_ROWS, P], BF16)
        least_rest = core.sb(mem, f"{tag}_least_rest", [U, P])
        probs = core.sb(mem, f"{tag}_probs_sb", [P, 4, 2, N])
        values = core.sb(mem, f"{tag}_values_sb", [P, GROUPS, N])
        inverse = core.sb(mem, f"{tag}_inv", [P, 2, HEADS])
        heads = core.sb(mem, f"{tag}_o", [P, QT, C])
        headsT = core.sb(mem, f"{tag}_oT", [C, N])
        biased = core.sb(mem, f"{tag}_biased", [P, 2, N]) if bias is not None else None
        spacer = core.sb(mem, f"{tag}_spacer", [1, U])
        s_ps = [core.ps(mem, f"{tag}_s_ps{n}", [P, N]) for n in range(2)]
        t_ps = [core.ps(mem, f"{tag}_t_ps{n}", [P, 2, N]) for n in range(2)]
        o_ps = core.ps(mem, f"{tag}_o_ps", [P, N])
        tail_ps = core.ps(mem, f"{tag}_tail_ps", [P, N])
        block = mem.enter_context(core.block())

        def wait(engine, semaphore, value):
            if not isinstance(value, int) or value > 0:
                engine.wait_ge(semaphore, START + value)

        def has_scores(i):
            return not (isinstance(i, int) and i == B)

        def has_turned(i, g, lag=2):
            if isinstance(i, int):
                return 0 <= GROUPS * i + g - lag < GROUPS * B
            return True

        def before(i, g, lag):
            return (i, g - lag) if g >= lag else (i - 1, g - lag + GROUPS)

        def run(engine, body):
            body(0)
            with engine.Fori(1, B) as i:
                body(i)
            body(B)

        @block.sync
        def _(sp):
            def load(g, batch):
                mine = slice(g * GROUP, (g + 1) * GROUP)
                for a, dst in enumerate((qs, ks)):
                    sp.dma_start(dst[0:STACK, mine, :], stacks_dram[a, batch, :, mine, :]).then_inc(stacks[g], 16)

            def steps(i, first=False, last=False):
                for g in range(GROUPS):
                    k = GROUPS * i + g
                    sp.wait_ge(least_split, START + k + 1)
                    for r in range(LEAST_ROWS):
                        sp.dma_start(qs[LEAST_AT + r:LEAST_AT + r + 1, g * GROUP:(g + 1) * GROUP, :]
                                     .rearrange("r h (t p) -> r (h t) p", p=P),
                                     least_parts[:, g % 2, r, :]).then_inc(least_placed[g % 2], 16)
                    if not (first if g < 2 else last):
                        sp.wait_ge(turned_ready, START + U * (k - 1))
                        load((g + 2) % GROUPS, i if g < 2 else i + 1)

            for g in range(GROUPS):
                load(g, 0)
            sp.wait_ge(minus_ready, START + 1)
            sp.dma_start(ks[LEAST_AT:LEAST_AT + LEAST_ROWS, :, :], minus[:, :, :]).then_inc(minus_placed, 16)
            steps(0, first=True)
            with sp.Fori(1, B - 1) as i:
                steps(i)
            steps(B - 1, last=True)

        @block.gpsimd
        def _(pool):
            nc.gpsimd.memset(minus[:, :, :], -1.0).then_inc(minus_ready, 1)
            nc.gpsimd.memset(vpad[:, :, :, :], 0.0).then_inc(v_cleared, 1)
            pool.wait_ge(v_cleared, START + 1)
            nc.gpsimd.memset(vpad[:, :, :, HD:HD + 1], 1.0).then_inc(v_cleared, 1)
            pool.wait_ge(v_cleared, START + 2)
            with pool.Fori(0, B) as i:
                pool.wait_ge(values_ready, START + KT * GROUPS * i)
                nc.gpsimd.tensor_copy(vpad[:, :, :, 0:HD].rearrange("p k h d -> p (k h) d"),
                                      v_all[:, bass.ds(i * KT, KT), :].rearrange("p k (h d) -> p (k h) d", d=HD)) \
                    .then_inc(v_ready, 1)

        @block.tensor
        def _(pe):
            def scores(i, g, n):
                k = GROUPS * i + g
                h, t = g * GROUP + n // QT, n % QT
                if n == 0:
                    pe.wait_ge(stacks[g], START + (i + 1) * 16 * LOADS)
                if n == 1:
                    wait(pe, turn_read, k)
                else:
                    wait(pe, least_ready, U * k + max(n - 1, 0))
                nc.tensor.matmul(s_ps[(g + n) % 2][:, :], qs[0:LEAST_AT, h, t * P:(t + 1) * P], ks[0:LEAST_AT, h, :],
                                 start=True, stop=True).then_inc(scores_ready, 1)

            def turn_least(i, g):
                pe.wait_ge(least_ready, START + U * (GROUPS * i + g + 1))
                nc.tensor.transpose(s_ps[g % 2][0:U, 0:P], least[:, g % 2, :], core.ident[:, :]) \
                    .then_inc(least_turned, 1)

            def turned(i, g, n):
                k = GROUPS * i + g
                h, t = g * GROUP + n % GROUP, n // GROUP
                if n == 0:
                    pe.wait_ge(least_placed[g % 2], START + 16 * LEAST_ROWS * (2 * i + g // 2 + 1))
                    if isinstance(i, int) and i == 0 and g == 0:
                        pe.wait_ge(minus_placed, START + 16)
                if n % 2 == 0:
                    wait(pe, probs_ready, U // 2 * k + n // 2 - 1)
                out = t_ps[n // 2 % 2]
                last = nc.tensor.matmul(out[:, n % 2, :], ks[0:ROWS, h, t * P:(t + 1) * P], qs[0:ROWS, h, :],
                                        start=True, stop=bias is None)
                if bias is not None:
                    for r in range(3):
                        last = nc.tensor.matmul(out[:, n % 2, t * P:(t + 1) * P], M["slopes_diag"][:, r, h, :],
                                                M["steps"][:, :], start=False, stop=(r == 2))
                last.then_inc(turned_ready, 1)

            def sum_values(i, g, t):
                k = GROUPS * i + g
                pe.wait_ge(probs_ready, START + U // 2 * k + 2 * t + 2)
                if t == 0:
                    pe.wait_ge(v_ready, START + i + 1)
                    wait(pe, values_kept, k)
                for h in range(GROUP):
                    pair = 2 * t + h // 2
                    last = nc.tensor.matmul(o_ps[h * VPAD:(h + 1) * VPAD, :], vpad[:, t, g * GROUP + h, :],
                                            probs[:, pair % 4, h % 2, :], start=(t == 0), stop=(t == KT - 1))
                last.then_inc(values_ready, 1)

            def tail(i, use):
                wait(pe, tail_read, TAIL * i + use)
                if use < QT:
                    if use == 0:
                        pe.wait_ge(values_kept, START + GROUPS * (i + 1))
                    for g in range(GROUPS):
                        last = nc.tensor.transpose(tail_ps[:, g * P:(g + 1) * P], values[:, g, use * P:(use + 1) * P],
                                                   core.ident[:, :])
                elif use == QT:
                    for t in range(QT):
                        last = nc.tensor.transpose(tail_ps[:, t * P:(t + 1) * P], heads[:, t, :], core.ident[:, :])
                else:
                    last = nc.tensor.matmul(tail_ps[:, :], wproj[:, :], headsT[:, :], start=True, stop=True)
                last.then_inc(tail_written, 1)

            def steps(i):
                for g in range(GROUPS):
                    for n in range(U):
                        if has_scores(i):
                            scores(i, g, n)
                        if has_turned(i, g):
                            turned(*before(i, g, 2), n)
                        if n == 2 and has_turned(i, g, 3):
                            sum_values(*before(i, g, 3), KT - 1)
                        if n % 4 == 2 and n > 2 and has_turned(i, g):
                            sum_values(*before(i, g, 2), n // 4 - 1)
                        if g == 2 and n in (5, 8, 11, 14) and has_turned(i, 0, 1):
                            tail(i - 1, (n - 5) // 3)
                        if g == 3 and n in (2, 8) and has_turned(i, 0, 1):
                            tail(i - 1, QT + n // 8)
                    if has_scores(i):
                        turn_least(i, g)

            run(pe, steps)

        @block.scalar
        def _(act):
            def exps(i, g, j):
                k = GROUPS * i + g
                wait(act, values_ready, KT * k + j // 2 - 1)
                act.wait_ge(turned_ready, START + U * k + 2 * j + 2)
                nc.scalar.activation(probs[:, j % 4, :, :], t_ps[j % 2][:, :, :], ACT.Exp,
                                     scale=-1.0).then_inc(probs_ready, 1)

            def keep_values(i, g):
                k = GROUPS * i + g
                if g == 0:
                    wait(act, tail_written, TAIL * (i - 1) + QT)
                act.wait_ge(values_ready, START + KT * (k + 1))
                nc.scalar.activation(values[:, g, :], o_ps[:, :], ACT.Copy).then_inc(values_kept, 1)

            def steps(i):
                for g in range(GROUPS):
                    for j in range(U // 2):
                        if has_turned(i, g):
                            exps(*before(i, g, 2), j)
                        if j == 1 and has_turned(i, g, 3):
                            keep_values(*before(i, g, 3))
                        if g == 3 and j == 2 and has_turned(i, 0, 1):
                            act.wait_ge(tail_written, START + TAIL * (i - 1) + QT + 1)
                            nc.scalar.activation(headsT[:, :], tail_ps[:, :], ACT.Copy).then_inc(tail_read, 1)

            run(act, steps)

        @block.vector
        def _(dve):
            def least_of(i, g, n):
                k = GROUPS * i + g
                h, t = g * GROUP + n // QT, n % QT
                dve.wait_ge(scores_ready, START + U * k + n + 1)
                src = s_ps[(g + n) % 2][:, :]
                if bias is not None:
                    nc.vector.memset(spacer[:, n:n + 1], 0.0)
                    at = (QT - 1 - t) * P
                    nc.vector.tensor_tensor_reduce(
                        out=biased[:, n % 2, :], in0=src, in1=bias[:, h, at:at + N], scale=1.0, scalar=3.0e38,
                        op0=ALU.add, op1=ALU.min, accum_out=least[:, g % 2, n:n + 1]).then_inc(least_ready, 1)
                else:
                    nc.vector.tensor_reduce(least[:, g % 2, n:n + 1], src, axis=AX.X,
                                            op=ALU.min).then_inc(least_ready, 1)

            def split_least(i, g):
                k = GROUPS * i + g
                src = s_ps[g % 2][0:U, 0:P]
                part = [least_parts[:, g % 2, r, :] for r in range(LEAST_ROWS)]
                dve.wait_ge(least_turned, START + k + 1)
                nc.vector.tensor_copy(part[0], src).then_inc(split_step, 1)
                dve.wait_ge(split_step, START + 2 * k + 1)
                nc.vector.tensor_tensor(least_rest[:, :], src, part[0], ALU.subtract).then_inc(turn_read, 1)
                dve.wait_ge(turn_read, START + k + 1)
                nc.vector.tensor_copy(part[1], least_rest[:, :]).then_inc(split_step, 1)
                dve.wait_ge(split_step, START + 2 * k + 2)
                nc.vector.tensor_tensor(part[2], least_rest[:, :], part[1], ALU.subtract).then_inc(least_split, 1)

            def normalise(i, t):
                src = tail_ps[:, :].rearrange("p (h d) -> p h d", d=VPAD)
                dve.wait_ge(tail_written, START + TAIL * i + t + 1)
                nc.vector.reciprocal(inverse[:, t % 2, :], src[:, :, HD]).then_inc(inverse_ready, 1)
                dve.wait_ge(inverse_ready, START + QT * i + t + 1)
                nc.vector.tensor_tensor(heads[:, t, :].rearrange("p (h d) -> p h d", d=HD), src[:, :, 0:HD],
                                        spread(inverse[:, t % 2, :], HD), ALU.mult).then_inc(tail_read, 1)

            def add(i):
                dve.wait_ge(tail_written, START + TAIL * (i + 1))
                nc.vector.scalar_tensor_tensor(out=xT[:, cols(i)], in0=tail_ps[:, :], scalar=bproj[:, 0:1],
                                               in1=xT[:, cols(i)], op0=ALU.add, op1=ALU.add).then_inc(tail_read, 1)

            def steps(i):
                for g in range(GROUPS):
                    for n in range(U):
                        if has_scores(i):
                            least_of(i, g, n)
                        if n == 0 and has_turned(i, g, 1):
                            split_least(*before(i, g, 1))
                        if has_turned(i, 0, 1):
                            if g == 2 and n in (7, 10, 13):
                                normalise(i - 1, (n - 7) // 3)
                            if g == 3 and n == 1:
                                normalise(i - 1, QT - 1)
                            if g == 3 and n == 11:
                                add(i - 1)

            run(dve, steps)


HID = 512
HT = HID // P


def gated_mlp_stage(core, A, xT):
    nc = core.nc
    w_loaded = core.sem("f0_w_loaded")
    hidden_loaded = core.sem("f0_hidden_loaded")
    up_ready = core.sem("f0_up")
    silu_ready = core.sem("f0_silu")
    gated_ready = core.sem("f0_gated")
    hid1_ready = core.sem("f0_hid1")
    gelu1_ready = core.sem("f0_gelu1")
    hid2_ready = core.sem("f0_hid2")
    gelu2_ready = core.sem("f0_gelu2")
    out_ready = core.sem("f0_out")
    added = core.sem("f0_added")
    with ExitStack() as mem:
        w12 = core.sb(mem, "f0_w12", [C, 2, HID])
        wh = core.sb(mem, "f0_wh", [P, 2, HT, HID])
        w3 = core.sb(mem, "f0_w3", [P, HT, C])
        scales = core.sb(mem, "f0_scales", [P, 4 * HT + 1])
        silu = core.sb(mem, "f0_silu_sb", [P, 2, N])
        gated = core.sb(mem, "f0_gated_sb", [P, HT, N])
        hid1 = core.sb(mem, "f0_hid1_sb", [P, HT, N])
        hid2 = core.sb(mem, "f0_hid2_sb", [P, HT, N])
        up_ps = [core.ps(mem, f"f0_up_ps{n}", [P, N]) for n in range(4)]
        hid_ps = [core.ps(mem, f"f0_hid_ps{n}", [P, N]) for n in range(HT)]
        block = mem.enter_context(core.block())

        def scale(n, m=0):
            return scales[:, n * HT + m:n * HT + m + 1]

        @block.sync
        def _(sp):
            sp.dma_start(w12[:, :, :], A["f0_w12"]).then_inc(w_loaded, 16)
            sp.dma_start(scales[:, :], A["f0_scales"]).then_inc(w_loaded, 16)
            sp.dma_start(wh[:, :, :, :], A["f0_wh"]).then_inc(hidden_loaded, 16)
            sp.dma_start(w3[:, :, :], A["f0_w3"]).then_inc(hidden_loaded, 16)

        @block.tensor
        def _(pe):
            def up(i):
                for m in range(HT):
                    pe.wait_ge(gated_ready, START + HT * i + max(m - 1, 0))
                    for n in range(2):
                        last = nc.tensor.matmul(up_ps[2 * (m % 2) + n][:, :], w12[:, n, m * P:(m + 1) * P],
                                                xT[:, cols(i)], start=True, stop=True)
                    last.then_inc(up_ready, 1)

            def hidden(layer, src, ready):
                for m in range(HT):
                    for k in range(HT):
                        last = nc.tensor.matmul(hid_ps[m][:, :], wh[:, layer, k, m * P:(m + 1) * P], src[:, k, :],
                                                start=(k == 0), stop=(k == HT - 1))
                    last.then_inc(ready, 1)

            def first(i):
                pe.wait_ge(gated_ready, START + HT * (i + 1))
                pe.wait_ge(added, START + i)
                hidden(0, gated, hid1_ready)

            def second_and_out(i):
                pe.wait_ge(gelu1_ready, START + HT * (i + 1))
                hidden(1, hid1, hid2_ready)
                pe.wait_ge(gelu2_ready, START + HT * (i + 1))
                for k in range(HT):
                    last = nc.tensor.matmul(hid_ps[0][:, :], w3[:, k, :], hid2[:, k, :],
                                            start=(k == 0), stop=(k == HT - 1))
                last.then_inc(out_ready, 1)

            pe.wait_ge(w_loaded, START + 32)
            up(0)
            pe.wait_ge(hidden_loaded, START + 32)
            with pe.Fori(0, B - 1) as i:
                first(i)
                up(i + 1)
                second_and_out(i)
            first(B - 1)
            second_and_out(B - 1)

        @block.scalar
        def _(act):
            def silus(i):
                for m in range(HT):
                    act.wait_ge(up_ready, START + HT * i + m + 1)
                    act.wait_ge(gated_ready, START + HT * i + max(m - 1, 0))
                    nc.scalar.activation(silu[:, m % 2, :], up_ps[2 * (m % 2)][:, :], ACT.Silu,
                                         scale=scale(0, m)).then_inc(silu_ready, 1)

            def gelu1(i):
                act.wait_ge(hid2_ready, START + HT * i)
                for m in range(HT):
                    act.wait_ge(hid1_ready, START + HT * i + m + 1)
                    nc.scalar.activation(hid1[:, m, :], hid_ps[m][:, :], ACT.Gelu,
                                         scale=scale(2, m)).then_inc(gelu1_ready, 1)

            def gelu2(i):
                act.wait_ge(out_ready, START + i)
                for m in range(HT):
                    act.wait_ge(hid2_ready, START + HT * i + m + 1)
                    nc.scalar.activation(hid2[:, m, :], hid_ps[m][:, :], ACT.Gelu,
                                         scale=scale(3, m)).then_inc(gelu2_ready, 1)

            act.wait_ge(w_loaded, START + 32)
            silus(0)
            with act.Fori(0, B - 1) as i:
                gelu1(i)
                silus(i + 1)
                gelu2(i)
            gelu1(B - 1)
            gelu2(B - 1)

        @block.vector
        def _(dve):
            def gate(i):
                for m in range(HT):
                    dve.wait_ge(silu_ready, START + HT * i + m + 1)
                    if m == 0:
                        dve.wait_ge(hid1_ready, START + HT * i)
                    nc.vector.scalar_tensor_tensor(out=gated[:, m, :], in0=up_ps[2 * (m % 2) + 1][:, :],
                                                   scalar=scale(1, m), in1=silu[:, m % 2, :], op0=ALU.mult,
                                                   op1=ALU.mult).then_inc(gated_ready, 1)

            def add(i):
                dve.wait_ge(out_ready, START + i + 1)
                nc.vector.scalar_tensor_tensor(out=xT[:, cols(i)], in0=hid_ps[0][:, :], scalar=scale(4),
                                               in1=xT[:, cols(i)], op0=ALU.mult, op1=ALU.add).then_inc(added, 1)

            gate(0)
            with dve.Fori(0, B - 1) as i:
                gate(i + 1)
                add(i)
            add(B - 1)


BRANCHES = 2
STATES = 16
DT_RANK = 64
BC = 2 * STATES
STEPS = BRANCHES * STATES


def ssm_stage(core, A, xT):
    nc = core.nc
    with ExitStack() as mem:
        xn = core.sb(mem, "s_xn", [C, T])
        delta = core.sb(mem, "s_delta", [C, BRANCHES, T])
        du = core.sb(mem, "s_du", [C, BRANCHES, T])
        ud = core.sb(mem, "s_ud", [C, T])
        z = core.sb(mem, "s_z", [C, T])
        bc_parts = core.sb(mem, "s_bc_parts", [3 * BC, BRANCHES, T], BF16)
        decay = core.sb(mem, "s_decay", [C, STATES])
        select = core.sb(mem, "s_select", [3 * BC, BC, P], BF16)
        layernorm_stage(core, xT, "s_ln", out=xn)
        ssm_prepare(core, A, xn, delta, du, ud, z, bc_parts, decay, select)
        ssm_scan(core, xT, delta, du, ud, z, bc_parts, decay, select)


def ssm_prepare(core, A, xn, delta, du, ud, z, bc_parts, decay, select):
    nc = core.nc
    loaded = core.sem("s_loaded")
    affine_ready = core.sem("s_affine")
    xp_ps_ready = core.sem("s_xp_ps")
    xp_ready = core.sem("s_xp")
    z_ready = core.sem("s_z_ready")
    v_ps_ready = core.sem("s_v_ps")
    v_kept = core.sem("s_v_kept")
    abs_ready = core.sem("s_abs")
    exp_ready = core.sem("s_exp")
    log_ready = core.sem("s_log")
    u_ready = core.sem("s_u")
    rank_ps_ready = core.sem("s_rank_ps")
    rank_ready = core.sem("s_rank")
    bc_ps_ready = core.sem("s_bc_ps")
    high_ready = core.sem("s_high")
    left_ready = core.sem("s_left")
    middle_ready = core.sem("s_middle")
    exp_a_ready = core.sem("s_exp_a")
    sum_ready = core.sem("s_usum")
    delta_ready = core.sem("s_delta_ready")
    with ExitStack() as mem:
        wide = core.sb(mem, "s_wide", [C, 3, C])
        wdr = core.sb(mem, "s_wdr", [C, DT_RANK])
        wbc = core.sb(mem, "s_wbc", [C, 3 * BC])
        wdt = core.sb(mem, "s_wdt", [BRANCHES * DT_RANK, C])
        cst = core.sb(mem, "s_cst", [C, 7])
        alog = core.sb(mem, "s_alog", [C, STATES])
        xp = core.sb(mem, "s_xp_sb", [C, T])
        v = core.sb(mem, "s_v", [C, BRANCHES, T])
        e = core.sb(mem, "s_e", [C, BRANCHES, T])
        u = core.sb(mem, "s_u_sb", [C, BRANCHES, T])
        rank = core.sb(mem, "s_rank_sb", [BRANCHES * DT_RANK, T])
        left = core.sb(mem, "s_left_sb", [3 * BC, T])
        middle = core.sb(mem, "s_middle_sb", [3 * BC, T], BF16)
        ps = [core.ps(mem, f"s_ps{n}", [P, T]) for n in range(2)]
        block = mem.enter_context(core.block())
        LOADS = 7

        @block.sync
        def _(sp):
            for dst, name in ((wide[:, :, :], "wide"), (wdr[:, :], "wdr"), (wbc[:, :], "wbc"), (wdt[:, :], "wdt"),
                              (cst[:, :], "cst"), (alog[:, :], "alog"), (select[:, :, :], "select")):
                sp.dma_start(dst, A[f"s_{name}"]).then_inc(loaded, 16)

        @block.tensor
        def _(pe):
            def product(out, lhsT, rhs, ready):
                for i in range(B):
                    last = nc.tensor.matmul(out[:, cols(i)], lhsT, rhs[:, cols(i)], start=True, stop=True)
                last.then_inc(ready, 1)

            pe.wait_ge(loaded, START + 16 * LOADS)
            pe.wait_ge(affine_ready, START + 1)
            product(ps[0], wide[:, 0, :], xn, xp_ps_ready)
            pe.wait_ge(xp_ready, START + 1)
            product(ps[1], wide[:, 1, :], xp, v_ps_ready)
            pe.wait_ge(z_ready, START + 1)
            product(ps[0], wide[:, 2, :], xp, v_ps_ready)
            pe.wait_ge(u_ready, START + 1)
            for r in range(BRANCHES):
                product(ps[1][r * DT_RANK:(r + 1) * DT_RANK, :], wdr[:, :], u[:, r, :], rank_ps_ready)
            product(ps[0][0:3 * BC, :], wbc[:, :], u[:, 0, :], bc_ps_ready)
            pe.wait_ge(rank_ready, START + 1)
            product(ps[1][0:3 * BC, :], wbc[:, :], u[:, 1, :], bc_ps_ready)
            for r in range(BRANCHES):
                pe.wait_ge(left_ready, START + r + 1)
                rows = slice(r * DT_RANK, (r + 1) * DT_RANK)
                product(ps[r], wdt[rows, :], rank[rows, :], v_ps_ready)

        @block.scalar
        def _(act):
            act.wait_ge(loaded, START + 16 * LOADS)
            nc.scalar.activation(decay[:, :], alog[:, :], ACT.Exp).then_inc(exp_a_ready, 1)
            act.wait_ge(xp_ps_ready, START + 1)
            nc.scalar.activation(xp[:, :], ps[0][:, :], ACT.Identity, bias=cst[:, 2:3]).then_inc(xp_ready, 1)
            nc.scalar.activation(z[:, :], ps[0][:, :], ACT.Silu, bias=cst[:, 2:3]).then_inc(z_ready, 1)

            def softplus_terms(n):
                for r in range(BRANCHES):
                    src = ps[1 - r] if n == 0 else ps[r]
                    bias = cst[:, 3 + r:4 + r] if n == 0 else cst[:, 5:6]
                    act.wait_ge(v_ps_ready, START + 2 * n + r + 1)
                    if n == 1:
                        act.wait_ge(u_ready, START + 1)
                    nc.scalar.activation(v[:, r, :], src[:, :], ACT.Identity, bias=bias).then_inc(v_kept, 1)
                    nc.scalar.activation(e[:, r, :], src[:, :], ACT.Abs, bias=bias).then_inc(abs_ready, 1)
                act.wait_ge(abs_ready, START + 2 * n + 2)
                nc.scalar.activation(e[:, :, :], e[:, :, :], ACT.Exp, scale=-1.0).then_inc(exp_ready, 1)
                act.wait_ge(exp_ready, START + n + 1)
                nc.scalar.activation(e[:, :, :], e[:, :, :], ACT.Ln, bias=core.one[:, 0:1]).then_inc(log_ready, 1)

            softplus_terms(0)
            act.wait_ge(rank_ps_ready, START + 2)
            nc.scalar.activation(rank[:, :], ps[1][:, :], ACT.Copy).then_inc(rank_ready, 1)
            softplus_terms(1)

        @block.vector
        def _(dve):
            dve.wait_ge(loaded, START + 16 * LOADS)
            nc.vector.tensor_scalar(xn[:, :], xn[:, :], cst[:, 0:1], cst[:, 1:2], ALU.mult,
                                    ALU.add).then_inc(affine_ready, 1)
            dve.wait_ge(exp_a_ready, START + 1)
            nc.vector.tensor_scalar(decay[:, :], decay[:, :], -1.0, None, ALU.mult)
            dve.wait_ge(log_ready, START + 1)
            nc.vector.scalar_tensor_tensor(out=u[:, :, :], in0=v[:, :, :], scalar=0.0, in1=e[:, :, :],
                                           op0=ALU.max, op1=ALU.add).then_inc(u_ready, 1)
            for r in range(BRANCHES):
                dve.wait_ge(bc_ps_ready, START + r + 1)
                nc.vector.tensor_copy(bc_parts[:, r, :], ps[r][0:3 * BC, :]).then_inc(high_ready, 1)
                dve.wait_ge(high_ready, START + r + 1)
                if r == 1:
                    dve.wait_ge(middle_ready, START + 3)
                nc.vector.tensor_tensor(left[:, :], ps[r][0:3 * BC, :], bc_parts[:, r, :],
                                        ALU.subtract).then_inc(left_ready, 1)
            dve.wait_ge(log_ready, START + 2)
            nc.vector.scalar_tensor_tensor(out=delta[:, :, :], in0=v[:, :, :], scalar=0.0, in1=e[:, :, :],
                                           op0=ALU.max, op1=ALU.add).then_inc(delta_ready, 1)
            dve.wait_ge(delta_ready, START + 1)
            nc.vector.tensor_tensor(du[:, :, :], delta[:, :, :], u[:, :, :], ALU.mult)

        @block.gpsimd
        def _(pool):
            pool.wait_ge(u_ready, START + 1)
            nc.gpsimd.tensor_tensor(ud[:, :], u[:, 0, :], u[:, 1, :], ALU.add).then_inc(sum_ready, 1)
            pool.wait_ge(sum_ready, START + 1)
            nc.gpsimd.tensor_scalar(ud[:, :], ud[:, :], cst[:, 6:7], None, ALU.mult)
            for r in range(BRANCHES):
                pool.wait_ge(left_ready, START + r + 1)
                nc.gpsimd.tensor_copy(middle[:, :], left[:, :]).then_inc(middle_ready, 1)
                pool.wait_ge(middle_ready, START + 3 * r + 1)
                nc.gpsimd.tensor_copy(bc_parts[BC:2 * BC, r, :], middle[BC:2 * BC, :]).then_inc(middle_ready, 1)
                nc.gpsimd.tensor_tensor(bc_parts[2 * BC:3 * BC, r, :], left[2 * BC:3 * BC, :],
                                        middle[2 * BC:3 * BC, :], ALU.subtract).then_inc(middle_ready, 1)
                pool.wait_ge(middle_ready, START + 3 * r + 3)


def ssm_scan(core, xT, delta, du, ud, z, bc_parts, decay, select):
    nc = core.nc
    RING, C_RING, B_RING = 4, 4, 3
    decay_ready = core.sem("s_decay_ready")
    b_ready = core.sem("s_b_ps")
    c_ready = core.sem("s_c_ps")
    b_kept = core.sem("s_b_kept")
    du_kept = core.sem("s_du_kept")
    input_ready = core.sem("s_input")
    scanned = core.sem("s_scanned")
    read_out = core.sem("s_read_out")
    summed = core.sem("s_summed")
    y_ready = core.sem("s_y")
    gate_ready = core.sem("s_gate")
    finished = core.sem("s_finished")
    with ExitStack() as mem:
        dA = core.sb(mem, "s_dA", [C, RING, N])
        du_b = core.sb(mem, "s_du_b", [C, BRANCHES, N])
        bs = core.sb(mem, "s_bs", [C, RING, N])
        dbu = core.sb(mem, "s_dbu", [C, RING, N])
        h = core.sb(mem, "s_h", [C, RING, N])
        hc = core.sb(mem, "s_hc", [C, RING, N])
        y = core.sb(mem, "s_ysb", [C, N])
        b_ps = [core.ps(mem, f"s_b_ps{n}", [C, N]) for n in range(B_RING)]
        c_ps = [core.ps(mem, f"s_c_ps{n}", [C, N]) for n in range(C_RING)]
        y_ps = core.ps(mem, "s_y_ps", [C, N])
        block = mem.enter_context(core.block())

        @block.tensor
        def _(pe):
            with pe.Fori(0, B) as i:
                for s in range(STEPS + RING):
                    if s < STEPS:
                        r, n = divmod(s, STATES)
                        pe.wait_ge(b_kept, START + i * STEPS + max(s - B_RING + 1, 0))
                        nc.tensor.matmul(b_ps[s % B_RING][:, :], select[:, n, :], bc_parts[:, r, cols(i)],
                                         start=True, stop=True).then_inc(b_ready, 1)
                        pe.wait_ge(read_out, START + i * STEPS + max(s - C_RING + 1, 0))
                        nc.tensor.matmul(c_ps[s % C_RING][:, :], select[:, STATES + n, :], bc_parts[:, r, cols(i)],
                                         start=True, stop=True).then_inc(c_ready, 1)
                    d = s - RING
                    if d >= 0:
                        if d == 0:
                            pe.wait_ge(gate_ready, START + i)
                        pe.wait_ge(read_out, START + i * STEPS + d + 1)
                        nc.tensor.matmul(y_ps[:, :], core.ident[:, :], hc[:, d % RING, :], start=(d == 0),
                                         stop=(d == STEPS - 1)).then_inc(summed, 1)

        @block.scalar
        def _(act):
            with act.Fori(0, B) as i:
                for s in range(STEPS):
                    r, n = divmod(s, STATES)
                    act.wait_ge(scanned, START + i * STEPS + max(s - RING + 1, 0))
                    act.wait_ge(b_ready, START + i * STEPS + s + 1)
                    act.wait_ge(input_ready, START + i * STEPS + max(s - RING + 1, 0))
                    nc.scalar.activation(bs[:, s % RING, :], b_ps[s % B_RING][:, :], ACT.Copy).then_inc(b_kept, 1)
                    if s == 0:
                        nc.scalar.activation(du_b[:, :, :], du[:, :, cols(i)], ACT.Copy).then_inc(du_kept, 1)
                    nc.scalar.activation(dA[:, s % RING, :], delta[:, r, cols(i)], ACT.Exp,
                                         scale=decay[:, n:n + 1]).then_inc(decay_ready, 1)

        @block.gpsimd
        def _(pool):
            with pool.Fori(0, B) as i:
                for s in range(STEPS):
                    r = s // STATES
                    if s == 0:
                        pool.wait_ge(du_kept, START + i + 1)
                    pool.wait_ge(b_kept, START + i * STEPS + s + 1)
                    pool.wait_ge(scanned, START + i * STEPS + max(s - RING + 1, 0))
                    nc.gpsimd.tensor_tensor(dbu[:, s % RING, :], du_b[:, r, :], bs[:, s % RING, :],
                                            ALU.mult).then_inc(input_ready, 1)

        @block.vector
        def _(dve):
            with dve.Fori(0, B) as i:
                for s in range(STEPS + 1):
                    if s < STEPS:
                        dve.wait_ge(decay_ready, START + i * STEPS + s + 1)
                        dve.wait_ge(input_ready, START + i * STEPS + s + 1)
                        dve.wait_ge(read_out, START + i * STEPS + max(s - RING + 1, 0))
                        nc.vector.tensor_tensor_scan(h[:, s % RING, :], dA[:, s % RING, :], dbu[:, s % RING, :], 0.0,
                                                     ALU.mult, ALU.add).then_inc(scanned, 1)
                    d = s - 1
                    if d >= 0:
                        dve.wait_ge(scanned, START + i * STEPS + d + 1)
                        dve.wait_ge(c_ready, START + i * STEPS + d + 1)
                        dve.wait_ge(summed, START + i * STEPS + max(d - RING + 1, 0))
                        nc.vector.tensor_tensor(hc[:, d % RING, :], c_ps[d % C_RING][:, :], h[:, d % RING, :],
                                                ALU.mult).then_inc(read_out, 1)
                dve.wait_ge(summed, START + (i + 1) * STEPS)
                dve.wait_ge(finished, START + i)
                nc.vector.tensor_tensor(y[:, :], y_ps[:, :], ud[:, cols(i)], ALU.add).then_inc(gate_ready, 1)
                dve.wait_ge(gate_ready, START + i + 1)
                nc.vector.tensor_tensor(y[:, :], y[:, :], z[:, cols(i)], ALU.mult).then_inc(y_ready, 1)
                dve.wait_ge(y_ready, START + i + 1)
                nc.vector.scalar_tensor_tensor(out=xT[:, cols(i)], in0=xT[:, cols(i)], scalar=2.0, in1=y[:, :],
                                               op0=ALU.mult, op1=ALU.add).then_inc(finished, 1)


EXPERTS = 8
MOE_HID = 256
MOE_HT = MOE_HID // P
CAPACITY = -(-T * 5 // (EXPERTS * 4))


def moe_stage(core, A, xT):
    with ExitStack() as mem:
        combine = core.sb(mem, "m_combine", [P, TT, EXPERTS])
        moe_route(core, A, xT, combine)
        moe_experts(core, A, xT, combine)


def moe_route(core, A, xT, combine):
    nc = core.nc
    E = EXPERTS
    loaded = core.sem("m_loaded")
    logits_ready = core.sem("m_logits")
    shifted_ready = core.sem("m_shifted")
    exp_ready = core.sem("m_exp")
    mask_ready = core.sem("m_mask")
    counts_ready = core.sem("m_counts")
    step = core.sem("m_step")
    with ExitStack() as mem:
        wr = core.sb(mem, "m_wr", [C, E])
        tri = core.sb(mem, "m_tri", [P, P])
        ones = core.sb(mem, "m_ones", [P, P])
        iota = core.sb(mem, "m_iota", [P, TT, E])
        most = core.sb(mem, "m_most", [P, TT])
        shifted = core.sb(mem, "m_shifted_sb", [P, TT, E])
        top = core.sb(mem, "m_top", [P, TT, 8])
        index = core.sb(mem, "m_index", [P, TT, 8], U32)
        indexf = core.sb(mem, "m_indexf", [P, TT, 8])
        gates = core.sb(mem, "m_gates", [P, TT, E])
        mask = core.sb(mem, "m_mask_sb", [P, TT, E])
        second = core.sb(mem, "m_second", [P, TT, E])
        totals = core.sb(mem, "m_totals", [P, TT, E])
        place = core.sb(mem, "m_place", [P, TT, E])
        total = core.sb(mem, "m_total", [P, TT])
        logits_ps = core.ps(mem, "m_logits_ps", [P, TT, E])
        prefix_ps = core.ps(mem, "m_prefix_ps", [P, TT, E])
        totals_ps = core.ps(mem, "m_totals_ps", [P, TT, E])
        block = mem.enter_context(core.block())

        @block.sync
        def _(sp):
            for dst, name in ((wr[:, :], "m_wr"), (tri[:, :], "tri"), (ones[:, :], "ones"), (iota[:, :, :], "m_iota")):
                sp.dma_start(dst, A[name]).then_inc(loaded, 16)

        @block.tensor
        def _(pe):
            pe.wait_ge(loaded, START + 64)
            for t in range(TT):
                last = nc.tensor.matmul(logits_ps[:, t, :], xT[:, t * P:(t + 1) * P], wr[:, :], start=True, stop=True)
            last.then_inc(logits_ready, 1)
            pe.wait_ge(mask_ready, START + 1)
            nc.tensor.matmul(prefix_ps[:, :, :], tri[:, :], mask[:, :, :], start=True, stop=True)
            nc.tensor.matmul(totals_ps[:, :, :], ones[:, :], mask[:, :, :], start=True,
                             stop=True).then_inc(counts_ready, 1)

        @block.scalar
        def _(act):
            act.wait_ge(shifted_ready, START + 1)
            nc.scalar.activation(gates[:, :, :], shifted[:, :, :], ACT.Exp).then_inc(exp_ready, 1)

        @block.vector
        def _(dve):
            done = [0]

            def then(instruction):
                instruction.then_inc(step, 1)
                done[0] += 1
                dve.wait_ge(step, START + done[0])

            dve.wait_ge(loaded, START + 64)
            dve.wait_ge(logits_ready, START + 1)
            then(nc.vector.tensor_reduce(most[:, :], logits_ps[:, :, :], axis=AX.X, op=ALU.max))
            nc.vector.tensor_tensor(shifted[:, :, :], logits_ps[:, :, :], spread(most[:, :], E),
                                    ALU.subtract).then_inc(shifted_ready, 1)
            dve.wait_ge(exp_ready, START + 1)
            then(nc.vector.tensor_reduce(total[:, :], gates[:, :, :], axis=AX.X, op=ALU.add))
            then(nc.vector.reciprocal(total[:, :], total[:, :]))
            then(nc.vector.tensor_tensor(gates[:, :, :], gates[:, :, :], spread(total[:, :], E), ALU.mult))
            for t in range(TT):
                last = nc.vector.max(top[:, t, :], gates[:, t, :])
            then(last)
            for t in range(TT):
                last = nc.vector.max_index(index[:, t, :], top[:, t, :], gates[:, t, :])
            then(last)
            then(nc.vector.tensor_copy(indexf[:, :, :], index[:, :, :]))
            nc.vector.tensor_tensor(mask[:, :, :], iota[:, :, :], spread(indexf[:, :, 0], E), ALU.is_equal)
            then(nc.vector.tensor_tensor(second[:, :, :], iota[:, :, :], spread(indexf[:, :, 1], E), ALU.is_equal))
            nc.vector.tensor_tensor(mask[:, :, :], mask[:, :, :], second[:, :, :], ALU.add).then_inc(mask_ready, 1)
            dve.wait_ge(counts_ready, START + 1)
            then(nc.vector.tensor_copy(totals[:, :, :], totals_ps[:, :, :]))
            for e in range(E):
                last = nc.vector.tensor_tensor_scan(place[:, :, e], core.ones_row[:, 0:TT], totals[:, :, e], 0.0,
                                                    ALU.mult, ALU.add)
            then(last)
            then(nc.vector.tensor_tensor(place[:, :, :], place[:, :, :], totals[:, :, :], ALU.subtract))
            then(nc.vector.tensor_tensor(place[:, :, :], place[:, :, :], prefix_ps[:, :, :], ALU.add))
            then(nc.vector.scalar_tensor_tensor(out=place[:, :, :], in0=place[:, :, :], scalar=float(CAPACITY),
                                                in1=mask[:, :, :], op0=ALU.is_le, op1=ALU.mult))
            then(nc.vector.tensor_tensor(gates[:, :, :], gates[:, :, :], place[:, :, :], ALU.mult))
            then(nc.vector.tensor_reduce(total[:, :], gates[:, :, :], axis=AX.X, op=ALU.add))
            then(nc.vector.tensor_scalar(total[:, :], total[:, :], 1e-6, None, ALU.add))
            then(nc.vector.reciprocal(total[:, :], total[:, :]))
            nc.vector.tensor_tensor(combine[:, :, :], gates[:, :, :], spread(total[:, :], E), ALU.mult)


def moe_experts(core, A, xT, combine):
    nc = core.nc
    E = EXPERTS
    NT = N // P
    PER_BANK = 512 // C
    loaded = core.sem("m_w_loaded")
    hid_ps_ready = core.sem("m_hid_ps")
    hid_ready = core.sem("m_hid")
    y_ready = core.sem("m_y")
    combined = core.sem("m_combine_kept")
    step = core.sem("m_mix_step")
    turned = core.sem("m_turned")
    added = core.sem("m_added")
    with ExitStack() as mem:
        wg = core.sb(mem, "m_wg", [C, MOE_HID])
        wd = core.sb(mem, "m_wd", [P, MOE_HT, E * C])
        hid = core.sb(mem, "m_hid_sb", [P, MOE_HT, N])
        weight = core.sb(mem, "m_weight", [P, NT, E])
        mixed = core.sb(mem, "m_mixed", [P, 2, C])
        hid_ps = [core.ps(mem, f"m_hid_ps{n}", [P, N]) for n in range(MOE_HT)]
        y_ps = [core.ps(mem, f"m_y_ps{n}", [P, E, C]) for n in range(2)]
        t_ps = core.ps(mem, "m_t_ps", [P, N])
        block = mem.enter_context(core.block())

        @block.sync
        def _(sp):
            sp.dma_start(wg[:, :], A["m_wg"]).then_inc(loaded, 16)
            sp.dma_start(wd[:, :, :], A["m_wd"]).then_inc(loaded, 16)

        @block.tensor
        def _(pe):
            pe.wait_ge(loaded, START + 32)
            with pe.Fori(0, B) as i:
                pe.wait_ge(hid_ready, START + MOE_HT * i)
                for m in range(MOE_HT):
                    nc.tensor.matmul(hid_ps[m][:, :], wg[:, m * P:(m + 1) * P], xT[:, cols(i)],
                                     start=True, stop=True).then_inc(hid_ps_ready, 1)
                pe.wait_ge(hid_ready, START + MOE_HT * (i + 1))
                for t in range(NT + 1):
                    if t < NT:
                        pe.wait_ge(step, START + (i * NT + max(t - 1, 0)) * E)
                        for half in range(E // PER_BANK):
                            out = y_ps[t % 2][:, half * PER_BANK:(half + 1) * PER_BANK, :]
                            for k in range(MOE_HT):
                                last = nc.tensor.matmul(out, hid[:, k, t * P:(t + 1) * P],
                                                        wd[:, k, half * 512:(half + 1) * 512],
                                                        start=(k == 0), stop=(k == MOE_HT - 1))
                        last.then_inc(y_ready, 1)
                    if t == 1:
                        pe.wait_ge(added, START + i)
                    if t > 0:
                        pe.wait_ge(step, START + (i * NT + t) * E)
                        nc.tensor.transpose(t_ps[:, (t - 1) * P:t * P], mixed[:, (t - 1) % 2, :],
                                            core.ident[:, :]).then_inc(turned, 1)

        @block.scalar
        def _(act):
            with act.Fori(0, B) as i:
                act.wait_ge(y_ready, START + NT * i)
                for m in range(MOE_HT):
                    act.wait_ge(hid_ps_ready, START + MOE_HT * i + m + 1)
                    nc.scalar.activation(hid[:, m, :], hid_ps[m][:, :], ACT.Silu).then_inc(hid_ready, 1)

        @block.vector
        def _(dve):
            with dve.Fori(0, B) as i:
                nc.vector.tensor_copy(weight[:, :, :], combine[:, bass.ds(i * NT, NT), :]).then_inc(combined, 1)
                dve.wait_ge(combined, START + i + 1)
                for t in range(NT):
                    dve.wait_ge(y_ready, START + NT * i + t + 1)
                    dve.wait_ge(turned, START + NT * i + max(t - 1, 0))
                    for e in range(E):
                        if e:
                            dve.wait_ge(step, START + (i * NT + t) * E + e)
                            last = nc.vector.scalar_tensor_tensor(
                                out=mixed[:, t % 2, :], in0=y_ps[t % 2][:, e, :], scalar=weight[:, t, e:e + 1],
                                in1=mixed[:, t % 2, :], op0=ALU.mult, op1=ALU.add)
                        else:
                            last = nc.vector.tensor_scalar(mixed[:, t % 2, :], y_ps[t % 2][:, e, :],
                                                           weight[:, t, e:e + 1], None, ALU.mult)
                        last.then_inc(step, 1)
                dve.wait_ge(turned, START + NT * (i + 1))
                nc.vector.tensor_tensor(xT[:, cols(i)], t_ps[:, :], xT[:, cols(i)], ALU.add).then_inc(added, 1)


QH = 8
QK = 64
VD = C // QH
HTOK = N // QH
KEY_TILES = QH * HTOK // P
VPAD = 32
QUNITS = QH * KEY_TILES


def query_softmax_stage(core, A, xT):
    nc = core.nc
    loaded = core.sem("q_loaded")
    cleared = core.sem("q_cleared")
    x_copied = core.sem("q_x_copied")
    proj_ready = core.sem("q_proj")
    kept_act = core.sem("q_kept_act")
    kept_dve = core.sem("q_kept_dve")
    v_ps_ready = core.sem("q_v_ps")
    v_kept = core.sem("q_v_kept")
    scores_ready = core.sem("q_scores")
    most_ready = core.sem("q_most")
    probs_ready = core.sem("q_probs")
    inverse_ready = core.sem("q_inverse")
    scaled_ready = core.sem("q_scaled")
    out_ready = core.sem("q_out")
    out_kept = core.sem("q_out_kept")
    y_ready = core.sem("q_y")
    added = core.sem("q_added")
    RING = 3
    with ExitStack() as mem:
        wqk = core.sb(mem, "q_wqk", [C, 2, QH * QK])
        wv = core.sb(mem, "q_wv", [C, C])
        place = core.sb(mem, "q_place", [P, 2, C])
        xb = core.sb(mem, "q_xb", [C, N])
        xd = core.sb(mem, "q_xd", [C, QH, 2, HTOK])
        qk = core.sb(mem, "q_qk", [QK, 2, QH, QH, HTOK])
        v = core.sb(mem, "q_v", [P, KEY_TILES, QH, VD])
        vs = core.sb(mem, "q_vs", [P, 2, KEY_TILES * QH, VPAD])
        most = core.sb(mem, "q_most_sb", [P, QUNITS])
        sums = core.sb(mem, "q_sums", [P, QUNITS])
        inverse = core.sb(mem, "q_inv", [P, QUNITS])
        probs = core.sb(mem, "q_probs_sb", [P, 2, KEY_TILES, N])
        outs = core.sb(mem, "q_outs", [P, 2, N])
        p_ps = core.ps(mem, "q_p_ps", [P, 2, N])
        s_ps = [core.ps(mem, f"q_s_ps{n}", [P, N]) for n in range(RING)]
        o_ps = core.ps(mem, "q_o_ps", [P, 2, N])
        y_ps = core.ps(mem, "q_y_ps", [P, N])
        block = mem.enter_context(core.block())
        PAIRS = QH // 2

        def by_head(ap):
            return ap.rearrange("p (h k) -> p h k", h=QH)

        @block.sync
        def _(sp):
            for dst, name in ((wqk[:, :, :], "q_wqk"), (wv[:, :], "q_wv"), (place[:, :, :], "q_place")):
                sp.dma_start(dst, A[name]).then_inc(loaded, 16)

        @block.gpsimd
        def _(pool):
            nc.gpsimd.memset(vs[:, :, :, :], 0.0).then_inc(cleared, 1)

        @block.tensor
        def _(pe):
            pe.wait_ge(loaded, START + 48)
            with pe.Fori(0, B) as i:
                pe.wait_ge(x_copied, START + 2 * i + 2)
                pe.wait_ge(v_kept, START + 2 * i)
                for n in range(2 * PAIRS):
                    if n >= 2:
                        pe.wait_ge(kept_act, START + 2 * PAIRS * i + n - 1)
                        pe.wait_ge(kept_dve, START + 2 * PAIRS * i + n - 1)
                    a, b = divmod(n, PAIRS)
                    nc.tensor.matmul(p_ps[:, n % 2, :], wqk[:, a, b * P:(b + 1) * P], xb[:, :],
                                     start=True, stop=True).then_inc(proj_ready, 1)
                pe.wait_ge(kept_act, START + 2 * PAIRS * (i + 1))
                pe.wait_ge(kept_dve, START + 2 * PAIRS * (i + 1))
                for h in range(QH):
                    last = nc.tensor.matmul(p_ps[:, h // 4, (h % 4) * P:(h % 4 + 1) * P],
                                            xd[:, h, :, :], wv[:, :], start=True, stop=True)
                last.then_inc(v_ps_ready, 1)

                def scores(u):
                    h, t = divmod(u, KEY_TILES)
                    pe.wait_ge(probs_ready, START + i * QUNITS + max(u - RING + 1, 0))
                    nc.tensor.matmul(s_ps[u % RING][:, :], qk[:, 1, h, 2 * t:2 * t + 2, :], qk[:, 0, h, :, :],
                                     start=True, stop=True).then_inc(scores_ready, 1)

                def outputs(h):
                    if h == 0:
                        pe.wait_ge(out_kept, START + 2 * i)
                    pe.wait_ge(scaled_ready, START + i * QH + h + 1)
                    tok = slice(h * HTOK, (h + 1) * HTOK)
                    for j in range(QH):
                        rows = slice(j % 4 * VPAD, j % 4 * VPAD + VPAD)
                        for t in range(KEY_TILES):
                            last = nc.tensor.matmul(o_ps[rows, j // 4, tok], vs[:, h % 2, t * QH + j, :],
                                                    probs[:, h % 2, t, j * HTOK:(j + 1) * HTOK],
                                                    start=(t == 0), stop=(t == KEY_TILES - 1))
                    last.then_inc(out_ready, 1)

                for h in range(QH + 1):
                    if h < QH:
                        for t in range(KEY_TILES):
                            scores(h * KEY_TILES + t)
                    if h > 0:
                        outputs(h - 1)
                pe.wait_ge(out_kept, START + 2 * i + 2)
                pe.wait_ge(added, START + i)
                for g in range(2):
                    last = nc.tensor.matmul(y_ps[:, :], place[:, g, :], outs[:, g, :], start=(g == 0), stop=(g == 1))
                last.then_inc(y_ready, 1)

        @block.scalar
        def _(act):
            with act.Fori(0, B) as i:
                act.wait_ge(v_ps_ready, START + i)
                nc.scalar.activation(xb[:, :], xT[:, cols(i)], ACT.Copy).then_inc(x_copied, 1)
                act.wait_ge(out_ready, START + QH * i)
                for n in range(2 * PAIRS):
                    act.wait_ge(proj_ready, START + 2 * PAIRS * i + n + 1)
                    a, b = divmod(n, PAIRS)
                    nc.scalar.activation(qk[:, a, :, 2 * b, :], by_head(p_ps[0:QK, n % 2, :]), ACT.Copy,
                                         scale=QK ** -0.5 if a == 0 else 1.0).then_inc(kept_act, 1)
                act.wait_ge(v_ps_ready, START + i + 1)
                nc.scalar.activation(v[0:QK, :, :, :].rearrange("p t h d -> p t h d"),
                                     p_ps[0:QK, :, :].rearrange("p a (b t s d) -> p t s (a b) d", b=4, s=2,
                                                                d=VD)[:, :, 0, :, :],
                                     ACT.Copy).then_inc(v_kept, 1)
                for u in range(QUNITS):
                    act.wait_ge(most_ready, START + i * QUNITS + u + 1)
                    h, t = divmod(u, KEY_TILES)
                    if t == 0:
                        act.wait_ge(out_ready, START + QH * i + max(h - 1, 0))
                    nc.scalar.activation(probs[:, h % 2, t, :], s_ps[u % RING][:, :], ACT.Exp,
                                         bias=most[:, u:u + 1], accum_out=sums[:, u:u + 1]).then_inc(probs_ready, 1)
                for g in range(2):
                    if g == 0:
                        act.wait_ge(out_ready, START + QH * (i + 1))
                        act.wait_ge(y_ready, START + i)
                    nc.scalar.activation(outs[:, g, :], o_ps[:, g, :], ACT.Copy).then_inc(out_kept, 1)

        @block.vector
        def _(dve):
            dve.wait_ge(cleared, START + 1)
            with dve.Fori(0, B) as i:
                dve.wait_ge(x_copied, START + 2 * i + 1)
                for a in range(2):
                    last = nc.vector.tensor_copy(xd[:, :, a, :], xb[:, :].rearrange("p (h k) -> p h k", h=QH))
                last.then_inc(x_copied, 1)
                for n in range(2 * PAIRS):
                    dve.wait_ge(proj_ready, START + 2 * PAIRS * i + n + 1)
                    a, b = divmod(n, PAIRS)
                    nc.vector.tensor_scalar(qk[:, a, :, 2 * b + 1, :], by_head(p_ps[QK:P, n % 2, :]),
                                            QK ** -0.5 if a == 0 else 1.0, None, ALU.mult).then_inc(kept_dve, 1)
                dve.wait_ge(v_ps_ready, START + i + 1)
                nc.vector.tensor_copy(v[QK:P, :, :, :],
                                      p_ps[QK:P, :, :].rearrange("p a (b t s d) -> p t s (a b) d", b=4, s=2,
                                                                 d=VD)[:, :, 1, :, :]).then_inc(v_kept, 1)
                dve.wait_ge(v_kept, START + 2 * i + 2)
                for h in range(QH):
                    for t in range(KEY_TILES):
                        u = h * KEY_TILES + t
                        dve.wait_ge(scores_ready, START + i * QUNITS + u + 1)
                        nc.vector.tensor_reduce(most[:, u:u + 1], s_ps[u % RING][:, :], axis=AX.X, op=ALU.max,
                                                negate=True).then_inc(most_ready, 1)
                    dve.wait_ge(probs_ready, START + i * QUNITS + (h + 1) * KEY_TILES)
                    us = slice(h * KEY_TILES, (h + 1) * KEY_TILES)
                    nc.vector.reciprocal(inverse[:, us], sums[:, us]).then_inc(inverse_ready, 1)
                    dve.wait_ge(inverse_ready, START + i * QH + h + 1)
                    dve.wait_ge(out_ready, START + i * QH + max(h - 1, 0))
                    nc.vector.tensor_tensor(
                        vs[:, h % 2, :, 0:VD].rearrange("p (t h) d -> p t h d", h=QH), v[:, :, :, :],
                        inverse[:, us].unsqueeze(2).unsqueeze(3).to_broadcast([P, KEY_TILES, QH, VD]),
                        ALU.mult).then_inc(scaled_ready, 1)
                dve.wait_ge(y_ready, START + i + 1)
                nc.vector.tensor_tensor(xT[:, cols(i)], y_ps[:, :], xT[:, cols(i)], ALU.add).then_inc(added, 1)


X_EXPERTS = 32
X_CAP = T * 5 // (4 * X_EXPERTS)
X_GROUPS = 16
X_INTER = 256
X_ROUTER = C // 2
X_STATS = 6
X_SLOTS = X_EXPERTS * X_CAP
X_ST = X_SLOTS // P
ADAPTER_SCALE = 0.05
TAKEN = -2.0


def sparse_stage(core, A, xT):
    nc = core.nc
    slots_dram = nc.dram_tensor("x_slots", (X_SLOTS, C), F32).ap()
    results_dram = nc.dram_tensor("x_results", (X_SLOTS + 1, C), F32).ap()
    w_loaded = core.sem("x_w_loaded")
    dispatched = core.sem("x_dispatched", software_dma=True)
    with ExitStack() as mem:
        weight = core.sb(mem, "x_weight", [P, 2, TT])
        slot = core.sb(mem, "x_slot", [P, 2, TT], I32)
        wu = core.sb(mem, "x_wu", [C, X_EXPERTS, 2 * X_INTER])
        wd = core.sb(mem, "x_wd", [P, X_EXPERTS, X_INTER // P, C])
        wau = core.sb(mem, "x_wau", [C, X_GROUPS, 2 * P])
        wad = core.sb(mem, "x_wad", [P, X_GROUPS, C])

        with core.block() as block:
            @block.sync
            def _(sp):
                for dst, name in ((wu[:, :, :], "x_wu"), (wau[:, :, :], "x_wau"), (wd[:, :, :, :], "x_wd"),
                                  (wad[:, :, :], "x_wad")):
                    half = dst.shape[1] // 2
                    for n in range(2):
                        sp.dma_start(dst[:, n * half:(n + 1) * half], A[name][:, n * half:(n + 1) * half]) \
                            .then_inc(w_loaded, 16)
        with ExitStack() as routing:
            xt = core.sb(routing, "x_xt", [P, TT, C])
            hT = core.sb(routing, "x_hT", [X_ROUTER, T])
            sparse_stats(core, A, xT, xt, hT)
            sparse_route(core, A, xt, hT, weight, slot, slots_dram, results_dram, dispatched)
        sparse_experts(core, slots_dram, results_dram, wu, wd, wau, wad, w_loaded)
        sparse_combine(core, xT, results_dram, weight, slot)


def sparse_stats(core, A, xT, xt, hT):
    nc = core.nc
    loaded = core.sem("x_r_loaded")
    turned = core.sem("x_turned")
    kept = core.sem("x_kept")
    squares_ready = core.sem("x_squares")
    sizes_ready = core.sem("x_sizes_ready")
    variance_ready = core.sem("x_variance")
    roots_ready = core.sem("x_roots")
    stats_ready = core.sem("x_stats_ready")
    stats_turned = core.sem("x_stats_turned")
    stats_kept = core.sem("x_stats_kept")
    hidden_ready = core.sem("x_hidden")
    step = core.sem("x_stats_step")
    with ExitStack() as mem:
        r1x = core.sb(mem, "x_r1x", [C, X_ROUTER])
        r1s = core.sb(mem, "x_r1s", [X_STATS, X_ROUTER])
        r1b = core.sb(mem, "x_r1b", [X_ROUTER, 1])
        stats = core.sb(mem, "x_stats", [P, TT, X_STATS])
        statsT = core.sb(mem, "x_statsT", [X_STATS, T])
        sums = core.sb(mem, "x_sums", [P, TT])
        spreads = core.sb(mem, "x_spreads", [P, 2, TT])
        roots = core.sb(mem, "x_roots_sb", [P, 2, TT])
        squares = core.sb(mem, "x_sq", [P, TT, C])
        centred = core.sb(mem, "x_xc", [P, TT, C])
        sizes = core.sb(mem, "x_sizes", [P, TT, C])
        a_ps = core.ps(mem, "x_a_ps", [P, T])
        b_ps = core.ps(mem, "x_b_ps", [X_STATS, T])
        block = mem.enter_context(core.block())

        @block.sync
        def _(sp):
            for dst, name in ((r1x[:, :], "x_r1x"), (r1s[:, :], "x_r1s"), (r1b[:, :], "x_r1b")):
                sp.dma_start(dst, A[name]).then_inc(loaded, 16)

        @block.tensor
        def _(pe):
            for t in range(TT):
                nc.tensor.transpose(a_ps[:, t * P:(t + 1) * P], xT[:, t * P:(t + 1) * P],
                                    core.ident[:, :]).then_inc(turned, 1)
            pe.wait_ge(loaded, START + 48)
            pe.wait_ge(kept, START + B)
            pe.wait_ge(stats_ready, START + 1)
            for t in range(TT):
                last = nc.tensor.transpose(b_ps[:, t * P:(t + 1) * P], stats[:, t, :], core.ident[:, :])
            last.then_inc(stats_turned, 1)
            pe.wait_ge(stats_kept, START + 1)
            for i in range(B):
                nc.tensor.matmul(a_ps[0:X_ROUTER, cols(i)], r1x[:, :], xT[:, cols(i)], start=True, stop=False)
                nc.tensor.matmul(a_ps[0:X_ROUTER, cols(i)], r1s[:, :], statsT[:, cols(i)], start=False,
                                 stop=True).then_inc(hidden_ready, 1)

        @block.scalar
        def _(act):
            for i in range(B):
                act.wait_ge(turned, START + (TT // B) * (i + 1))
                nc.scalar.activation(xt[:, 4 * i:4 * i + 4, :].rearrange("p t c -> p (t c)"), a_ps[:, cols(i)],
                                     ACT.Copy).then_inc(kept, 1)
            act.wait_ge(kept, START + B)
            nc.scalar.activation(sizes[:, :, :], xt[:, :, :], ACT.Abs).then_inc(sizes_ready, 1)
            act.wait_ge(variance_ready, START + 1)
            nc.scalar.activation(roots[:, :, :], spreads[:, :, :], ACT.Sqrt).then_inc(roots_ready, 1)
            act.wait_ge(stats_turned, START + 1)
            nc.scalar.activation(statsT[:, :], b_ps[:, :], ACT.Copy).then_inc(stats_kept, 1)
            act.wait_ge(loaded, START + 48)
            act.wait_ge(hidden_ready, START + B)
            nc.scalar.activation(hT[:, :], a_ps[0:X_ROUTER, :], ACT.Gelu, bias=r1b[:, 0:1])

        @block.gpsimd
        def _(pool):
            pool.wait_ge(kept, START + B)
            nc.gpsimd.tensor_tensor(squares[:, :, :], xt[:, :, :], xt[:, :, :], ALU.mult).then_inc(squares_ready, 1)

        @block.vector
        def _(dve):
            done = [0]

            def then(instruction):
                instruction.then_inc(step, 1)
                done[0] += 1
                dve.wait_ge(step, START + done[0])

            def reduce(out, src, op):
                return nc.vector.tensor_reduce(out, src, axis=AX.X, op=op)

            dve.wait_ge(kept, START + B)
            then(reduce(sums[:, :], xt[:, :, :], ALU.add))
            then(nc.vector.tensor_scalar(stats[:, :, 0], sums[:, :], 1.0 / C, None, ALU.mult))
            then(nc.vector.tensor_tensor(centred[:, :, :], xt[:, :, :], spread(stats[:, :, 0], C), ALU.subtract))
            then(nc.vector.tensor_tensor(centred[:, :, :], centred[:, :, :], centred[:, :, :], ALU.mult))
            then(reduce(sums[:, :], centred[:, :, :], ALU.add))
            nc.vector.tensor_scalar(spreads[:, 0, :], sums[:, :], 1.0 / (C - 1), None, ALU.mult)
            dve.wait_ge(squares_ready, START + 1)
            reduce(spreads[:, 1, :], squares[:, :, :], ALU.add).then_inc(variance_ready, 1)
            reduce(stats[:, :, 2], xt[:, :, :], ALU.min)
            then(reduce(stats[:, :, 3], xt[:, :, :], ALU.max))
            dve.wait_ge(sizes_ready, START + 1)
            then(nc.vector.tensor_scalar(centred[:, :, :], sizes[:, :, :], 1e-6, None, ALU.is_lt))
            then(reduce(sums[:, :], centred[:, :, :], ALU.add))
            nc.vector.tensor_scalar(stats[:, :, 5], sums[:, :], 1.0 / C, None, ALU.mult)
            dve.wait_ge(roots_ready, START + 1)
            nc.vector.tensor_copy(stats[:, :, 1], roots[:, 0, :])
            nc.vector.tensor_copy(stats[:, :, 4], roots[:, 1, :]).then_inc(stats_ready, 1)


def sparse_route(core, A, xt, hT, weight, slot, slots_dram, results_dram, dispatched):
    nc = core.nc
    E = X_EXPERTS
    loaded = core.sem("x_r2_loaded")
    zeroed = core.sem("x_zeroed")
    slots_zeroed = core.sem("x_slots_zeroed")
    logits_ready = core.sem("x_logits")
    shifted_ready = core.sem("x_shifted")
    exp_ready = core.sem("x_exp")
    score_ready = core.sem("x_score")
    score_turned = core.sem("x_score_turned")
    place_ready = core.sem("x_place")
    place_turned = core.sem("x_place_turned")
    slot_ready = core.sem("x_slot_ready")
    step = core.sem("x_step")
    with ExitStack() as mem:
        r2 = core.sb(mem, "x_r2", [X_ROUTER, E])
        iota = core.sb(mem, "x_iota", [P, TT, E])
        base = core.sb(mem, "x_base", [E, 1])
        zero = core.sb(mem, "x_zero", [P, C])
        most = core.sb(mem, "x_most", [P, TT])
        probs = core.sb(mem, "x_probs", [P, TT, E])
        top = core.sb(mem, "x_top", [P, TT, 8])
        index = core.sb(mem, "x_index", [P, TT, 8], U32)
        indexf = core.sb(mem, "x_indexf", [P, TT, 8])
        hits = core.sb(mem, "x_hits", [P, 2, TT, E])
        score = core.sb(mem, "x_score_sb", [P, TT, E])
        mask = core.sb(mem, "x_mask", [P, TT, E])
        total = core.sb(mem, "x_total", [P, TT])
        slotf = core.sb(mem, "x_slotf", [P, 2, TT])
        isnt = core.sb(mem, "x_isnt", [P, 2, TT])
        scoreT = core.sb(mem, "x_scoreT", [E, T])
        work = core.sb(mem, "x_work", [E, T])
        best = core.sb(mem, "x_best", [E, 8])
        placeT = core.sb(mem, "x_placeT", [E, T])
        logits_ps = core.ps(mem, "x_logits_ps", [P, TT, E])
        turn_ps = core.ps(mem, "x_turn_ps", [E, T])
        place_ps = core.ps(mem, "x_place_ps", [P, TT, E])
        block = mem.enter_context(core.block())

        @block.sync
        def _(sp):
            for dst, name in ((r2[:, :], "x_r2"), (iota[:, :, :], "x_iota"), (base[:, :], "x_base")):
                sp.dma_start(dst, A[name]).then_inc(loaded, 16)
            sp.wait_ge(zeroed, START + 1)
            for n in range(X_ST):
                sp.dma_start(slots_dram[n * P:(n + 1) * P, :], zero[:, :]).then_inc(slots_zeroed, 16)
            sp.dma_start(results_dram[X_SLOTS:X_SLOTS + 1, :], zero[0:1, :]).then_inc(slots_zeroed, 16)
            sp.wait_ge(slots_zeroed, START + 16 * (X_ST + 1))

        @block.tensor
        def _(pe):
            pe.wait_ge(loaded, START + 48)
            for t in range(TT):
                last = nc.tensor.matmul(logits_ps[:, t, :], hT[:, t * P:(t + 1) * P], r2[:, :], start=True, stop=True)
            last.then_inc(logits_ready, 1)
            pe.wait_ge(score_ready, START + 1)
            for t in range(TT):
                last = nc.tensor.transpose(turn_ps[:, t * P:(t + 1) * P], score[:, t, :], core.ident[:, :])
            last.then_inc(score_turned, 1)
            pe.wait_ge(place_ready, START + 1)
            for t in range(TT):
                last = nc.tensor.transpose(place_ps[:, t, :], placeT[:, t * P:(t + 1) * P], core.ident[0:E, 0:E])
            last.then_inc(place_turned, 1)

        @block.scalar
        def _(act):
            act.wait_ge(shifted_ready, START + 1)
            nc.scalar.activation(probs[:, :, :], score[:, :, :], ACT.Exp).then_inc(exp_ready, 1)

        @block.gpsimd
        def _(pool):
            nc.gpsimd.memset(zero[:, :], 0.0).then_inc(zeroed, 1)
            pool.wait_ge(slots_zeroed, START + 16 * (X_ST + 1))
            pool.wait_ge(slot_ready, START + 1)
            for k in range(2):
                for t in range(TT):
                    nc.gpsimd.indirect_dma_start(
                        out=slots_dram, out_offset=bass.IndirectOffsetOnAxis(ap=slot[:, k, t:t + 1], axis=0),
                        in_=xt[:, t, :], in_offset=None, bounds_check=X_SLOTS - 1,
                        oob_is_err=False).then_inc(dispatched, 16)
            pool.wait_ge(dispatched, 16 * 2 * TT)

        @block.vector
        def _(dve):
            done = [0]

            def then(instruction):
                instruction.then_inc(step, 1)
                done[0] += 1
                dve.wait_ge(step, START + done[0])

            dve.wait_ge(loaded, START + 48)
            dve.wait_ge(logits_ready, START + 1)
            then(nc.vector.tensor_reduce(most[:, :], logits_ps[:, :, :], axis=AX.X, op=ALU.max))
            nc.vector.tensor_tensor(score[:, :, :], logits_ps[:, :, :], spread(most[:, :], E),
                                    ALU.subtract).then_inc(shifted_ready, 1)
            dve.wait_ge(exp_ready, START + 1)
            then(nc.vector.tensor_reduce(total[:, :], probs[:, :, :], axis=AX.X, op=ALU.add))
            then(nc.vector.reciprocal(total[:, :], total[:, :]))
            then(nc.vector.tensor_tensor(probs[:, :, :], probs[:, :, :], spread(total[:, :], E), ALU.mult))
            for t in range(TT):
                last = nc.vector.max(top[:, t, :], probs[:, t, :])
            then(last)
            for t in range(TT):
                last = nc.vector.max_index(index[:, t, :], top[:, t, :], probs[:, t, :])
            then(last)
            then(nc.vector.tensor_copy(indexf[:, :, :], index[:, :, :]))
            for k in range(2):
                last = nc.vector.tensor_tensor(hits[:, k, :, :], iota[:, :, :], spread(indexf[:, :, k], E),
                                               ALU.is_equal)
            then(last)
            then(nc.vector.tensor_tensor(mask[:, :, :], hits[:, 0, :, :], hits[:, 1, :, :], ALU.add))
            then(nc.vector.tensor_tensor(score[:, :, :], probs[:, :, :], mask[:, :, :], ALU.mult))
            then(nc.vector.tensor_scalar(mask[:, :, :], mask[:, :, :], -1.0, None, ALU.add))
            nc.vector.tensor_tensor(score[:, :, :], score[:, :, :], mask[:, :, :], ALU.add).then_inc(score_ready, 1)
            then(nc.vector.tensor_tensor(total[:, :], top[:, :, 0], top[:, :, 1], ALU.add))
            then(nc.vector.reciprocal(total[:, :], total[:, :]))
            for k in range(2):
                last = nc.vector.tensor_tensor(weight[:, k, :], top[:, :, k], total[:, :], ALU.mult)
            then(last)
            dve.wait_ge(score_turned, START + 1)
            nc.vector.tensor_copy(scoreT[:, :], turn_ps[:, :])
            then(nc.vector.tensor_copy(work[:, :], turn_ps[:, :]))
            for n in range(X_CAP // 8):
                then(nc.vector.max(best[:, :], work[:, :]))
                then(nc.vector.match_replace(work[:, :], best[:, :], work[:, :], TAKEN))
            then(nc.vector.tensor_scalar(work[:, :], work[:, :], TAKEN, None, ALU.is_equal))
            then(nc.vector.scalar_tensor_tensor(out=work[:, :], in0=scoreT[:, :], scalar=0.0, in1=work[:, :],
                                                op0=ALU.is_ge, op1=ALU.mult))
            then(nc.vector.tensor_tensor_scan(placeT[:, :], core.ones_row[0:E, 0:1].to_broadcast([E, T]), work[:, :], 0.0,
                                              ALU.mult, ALU.add))
            nc.vector.scalar_tensor_tensor(out=placeT[:, :], in0=placeT[:, :], scalar=base[:, 0:1], in1=work[:, :],
                                           op0=ALU.add, op1=ALU.mult).then_inc(place_ready, 1)
            dve.wait_ge(place_turned, START + 1)
            for k in range(2):
                then(nc.vector.tensor_tensor(score[:, :, :], hits[:, k, :, :], place_ps[:, :, :], ALU.mult))
                then(nc.vector.tensor_reduce(slotf[:, k, :], score[:, :, :], axis=AX.X, op=ALU.add))
            then(nc.vector.tensor_scalar(isnt[:, :, :], slotf[:, :, :], 0.0, float(X_SLOTS + 1), ALU.is_equal,
                                         ALU.mult))
            then(nc.vector.scalar_tensor_tensor(out=slotf[:, :, :], in0=slotf[:, :, :], scalar=-1.0,
                                                in1=isnt[:, :, :], op0=ALU.add, op1=ALU.add))
            nc.vector.tensor_copy(slot[:, :, :], slotf[:, :, :]).then_inc(slot_ready, 1)


def sparse_experts(core, slots_dram, results_dram, wu, wd, wau, wad, w_loaded):
    nc = core.nc
    E, G, CAP = X_EXPERTS, X_GROUPS, X_CAP
    JT = X_INTER // P
    PAIR = E // G
    slots_loaded = core.sem("x_slots_loaded")
    turned = core.sem("x_slots_turned")
    kept = core.sem("x_slots_kept")
    up_ready = core.sem("x_up")
    silu_ready = core.sem("x_silu")
    act_ready = core.sem("x_act")
    down_ready = core.sem("x_down")
    result_ready = core.sem("x_result")
    stored = core.sem("x_stored")
    UNITS_G = PAIR + 1
    with ExitStack() as mem:
        slots = core.sb(mem, "x_slots_sb", [P, X_ST, C])
        slotsT = core.sb(mem, "x_slotsT", [C, X_SLOTS])
        silu = core.sb(mem, "x_silu_sb", [P, 2, PAIR * CAP])
        hid = core.sb(mem, "x_hid_sb", [P, 2 * UNITS_G, PAIR * CAP])
        results = core.sb(mem, "x_results_sb", [CAP, E, C])
        t_ps = [core.ps(mem, f"x_t_ps{n}", [P, N]) for n in range(2)]
        up_ps = [core.ps(mem, f"x_up_ps{n}", [P, N]) for n in range(3)]
        d_ps = [core.ps(mem, f"x_d_ps{n}", [P, C]) for n in range(2)]
        block = mem.enter_context(core.block())
        TURNS = X_ST // 4

        def units():
            for g in range(G):
                yield g, None
                for e in range(PAIR * g, PAIR * (g + 1)):
                    yield g, e

        UNITS_ALL = list(units())

        @block.sync
        def _(sp):
            for n in range(TURNS):
                sp.dma_start(slots[:, 4 * n:4 * n + 4, :],
                             slots_dram[4 * n * P:4 * (n + 1) * P, :].rearrange("(t p) c -> p t c", p=P)) \
                    .then_inc(slots_loaded, 16)
                sp.wait_ge(slots_loaded, START + 16 * (n + 1))
            for n in range(4):
                some = slice(n * E // 4, (n + 1) * E // 4)
                sp.wait_ge(result_ready, START + (n + 1) * E // 4)
                sp.dma_start(results_dram[n * X_SLOTS // 4:(n + 1) * X_SLOTS // 4, :]
                             .rearrange("(e s) c -> s e c", s=CAP), results[:, some, :]).then_inc(stored, 16)
            sp.wait_ge(stored, START + 64)

        @block.tensor
        def _(pe):
            for n in range(TURNS):
                pe.wait_ge(slots_loaded, START + 16 * (n + 1))
                if n >= 2:
                    pe.wait_ge(kept, START + n - 1)
                for t in range(4):
                    last = nc.tensor.transpose(t_ps[n % 2][:, t * P:(t + 1) * P], slots[:, 4 * n + t, :],
                                               core.ident[:, :])
                last.then_inc(turned, 1)
            pe.wait_ge(kept, START + TURNS)
            pe.wait_ge(w_loaded, START + 16 * 8)

            def up(n):
                g, e = UNITS_ALL[n]
                if n >= 3:
                    pe.wait_ge(act_ready, START + n - 2)
                first, count = (PAIR * g, PAIR) if e is None else (e, 1)
                src = slotsT[:, first * CAP:(first + count) * CAP]
                tiles = 2 if e is None else 2 * JT
                for m in range(tiles):
                    w = wau[:, g, m * P:(m + 1) * P] if e is None else wu[:, e, m * P:(m + 1) * P]
                    last = nc.tensor.matmul(up_ps[n % 3][:, m * count * CAP:(m + 1) * count * CAP], w, src,
                                            start=True, stop=True)
                last.then_inc(up_ready, 1)

            def down(n):
                g, e = UNITS_ALL[n]
                if e is None:
                    return
                pe.wait_ge(act_ready, START + n + 1)
                if e >= 2:
                    pe.wait_ge(result_ready, START + e - 1)
                here = n % (2 * UNITS_G)
                adapter = (n - 1 - e % PAIR) % (2 * UNITS_G)
                for j in range(JT):
                    nc.tensor.matmul(d_ps[e % 2][0:CAP, :], hid[:, here, j * CAP:(j + 1) * CAP], wd[:, e, j, :],
                                     start=(j == 0), stop=False)
                nc.tensor.matmul(d_ps[e % 2][0:CAP, :], hid[:, adapter, e % PAIR * CAP:(e % PAIR + 1) * CAP],
                                 wad[:, g, :], start=False, stop=True).then_inc(down_ready, 1)

            for n in range(len(UNITS_ALL) + 1):
                if n < len(UNITS_ALL):
                    up(n)
                if n:
                    down(n - 1)

        @block.scalar
        def _(act):
            for n, (g, e) in enumerate(UNITS_ALL):
                act.wait_ge(up_ready, START + n + 1)
                if n >= 2:
                    act.wait_ge(act_ready, START + n - 1)
                nc.scalar.activation(silu[:, n % 2, :], up_ps[n % 3][:, 0:PAIR * CAP], ACT.Silu).then_inc(silu_ready, 1)

        @block.vector
        def _(dve):
            for n in range(TURNS):
                dve.wait_ge(turned, START + n + 1)
                nc.vector.tensor_copy(slotsT[:, n * N:(n + 1) * N], t_ps[n % 2][:, :]).then_inc(kept, 1)

            def result(n):
                g, e = UNITS_ALL[n]
                if e is None:
                    return
                dve.wait_ge(down_ready, START + e + 1)
                nc.vector.tensor_copy(results[:, e, :], d_ps[e % 2][0:CAP, :]).then_inc(result_ready, 1)

            for n in range(len(UNITS_ALL) + 2):
                if n < len(UNITS_ALL):
                    g, e = UNITS_ALL[n]
                    dve.wait_ge(silu_ready, START + n + 1)
                    if n >= 2 * UNITS_G:
                        dve.wait_ge(down_ready, START + PAIR * (n // UNITS_G - 1))
                    nc.vector.scalar_tensor_tensor(
                        out=hid[:, n % (2 * UNITS_G), :], in0=up_ps[n % 3][:, PAIR * CAP:2 * PAIR * CAP],
                        scalar=ADAPTER_SCALE if e is None else 1.0, in1=silu[:, n % 2, :], op0=ALU.mult,
                        op1=ALU.mult).then_inc(act_ready, 1)
                if n >= 2:
                    result(n - 2)


def sparse_combine(core, xT, results_dram, weight, slot):
    nc = core.nc
    fetched = [core.sem(f"x_fetched{i}", software_dma=True) for i in range(B)]
    scaled = core.sem("x_scaled")
    mixed = core.sem("x_mixed")
    turned = core.sem("x_mixed_turned")
    CT = TT // B
    with ExitStack() as mem:
        got = core.sb(mem, "x_got", [P, 2, TT, C])
        y = core.sb(mem, "x_y", [P, TT, C])
        y_ps = core.ps(mem, "x_y_ps", [C, T])
        block = mem.enter_context(core.block())

        @block.gpsimd
        def _(pool):
            for t in range(TT):
                for k in range(2):
                    nc.gpsimd.indirect_dma_start(
                        out=got[:, k, t, :], out_offset=None, in_=results_dram,
                        in_offset=bass.IndirectOffsetOnAxis(ap=slot[:, k, t:t + 1], axis=0)).then_inc(fetched[t // CT], 16)

        @block.vector
        def _(dve):
            for t in range(TT):
                dve.wait_ge(fetched[t // CT], 16 * 2 * CT)
                nc.vector.tensor_scalar(y[:, t, :], got[:, 0, t, :], weight[:, 0, t:t + 1], None,
                                        ALU.mult).then_inc(scaled, 1)
            for t in range(TT):
                dve.wait_ge(scaled, START + t + 1)
                nc.vector.scalar_tensor_tensor(out=y[:, t, :], in0=got[:, 1, t, :], scalar=weight[:, 1, t:t + 1],
                                               in1=y[:, t, :], op0=ALU.mult, op1=ALU.add).then_inc(mixed, 1)
            for i in range(B):
                dve.wait_ge(turned, START + CT * (i + 1))
                nc.vector.tensor_tensor(xT[:, cols(i)], y_ps[:, cols(i)], xT[:, cols(i)], ALU.add)

        @block.tensor
        def _(pe):
            for t in range(TT):
                pe.wait_ge(mixed, START + t + 1)
                nc.tensor.transpose(y_ps[:, t * P:(t + 1) * P], y[:, t, :], core.ident[:, :]).then_inc(turned, 1)


CH_EXPERTS = 8
CH_HID = 512
CH_HT = CH_HID // P
CH_ALL = CH_EXPERTS + 1
CHOSEN = 2 * T
BITS = 30


def choice_stage(core, A, xT):
    with ExitStack() as mem:
        gateT = core.sb(mem, "c_gateT", [CH_EXPERTS, T])
        w1 = core.sb(mem, "c_w1", [C, CH_ALL, CH_HID])
        w2 = core.sb(mem, "c_w2", [P, CH_ALL, CH_HT, C])
        w_loaded = core.sem("c_w_loaded")
        choice_route(core, A, xT, gateT, w1, w2, w_loaded)
        choice_experts(core, A, xT, gateT, w1, w2, w_loaded)


def choice_route(core, A, xT, gateT, w1, w2, w_loaded):
    nc = core.nc
    E = CH_EXPERTS
    loaded = core.sem("c_loaded")
    logits_ready = core.sem("c_logits")
    shifted_ready = core.sem("c_shifted")
    exp_ready = core.sem("c_exp")
    count_ready = core.sem("c_count")
    total_ready = core.sem("c_total")
    equal_ready = core.sem("c_equal")
    places_ready = core.sem("c_places")
    gate_ready = core.sem("c_gate")
    gate_turned = core.sem("c_gate_turned")
    step = core.sem("c_step")
    tried = core.sem("c_tried")
    passed = core.sem("c_passed")
    threshold_ready = core.sem("c_threshold")
    with ExitStack() as mem:
        wr = core.sb(mem, "c_wr", [C, E])
        tri = core.sb(mem, "c_tri", [P, P])
        ones = core.sb(mem, "c_ones", [P, P])
        bits = core.sb(mem, "c_bits", [P, BITS], I32)
        bitsf = core.sb(mem, "c_bitsf", [P, BITS])
        most = core.sb(mem, "c_most", [P, TT])
        shifted = core.sb(mem, "c_shifted_sb", [P, TT, E])
        scores = core.sb(mem, "c_scores", [P, TT, E])
        total = core.sb(mem, "c_total_sb", [P, TT])
        above = core.sb(mem, "c_above", [P, TT, E])
        equal = core.sb(mem, "c_equal_sb", [P, TT, E])
        threshold = core.sb(mem, "c_threshold_sb", [P, 1], I32)
        trial = core.sb(mem, "c_trial", [P, 1], I32)
        bit = core.sb(mem, "c_bit", [P, 1], I32)
        count = core.sb(mem, "c_count_sb", [P, 1])
        places = core.sb(mem, "c_places_sb", [P, TT, E])
        totals = core.sb(mem, "c_totals", [P, TT, E])
        before = core.sb(mem, "c_before", [P, E])
        needed = core.sb(mem, "c_needed", [P, 1])
        logits_ps = core.ps(mem, "c_logits_ps", [P, TT, E])
        total_ps = core.ps(mem, "c_total_ps", [P, 1])
        prefix_ps = core.ps(mem, "c_prefix_ps", [P, TT, E])
        totals_ps = core.ps(mem, "c_totals_ps", [P, TT, E])
        turn_ps = core.ps(mem, "c_turn_ps", [E, T])
        block = mem.enter_context(core.block())

        @block.sync
        def _(sp):
            for dst, name in ((wr[:, :], "c_wr"), (tri[:, :], "tri"), (ones[:, :], "ones"), (bits[:, :], "c_bits"),
                              (bitsf[:, :], "c_bitsf")):
                sp.dma_start(dst, A[name]).then_inc(loaded, 16)
            sp.dma_start(w1[:, :, :], A["c_w1"]).then_inc(w_loaded, 16)
            sp.dma_start(w2[:, :, :, :], A["c_w2"]).then_inc(w_loaded, 16)

        @block.tensor
        def _(pe):
            pe.wait_ge(loaded, START + 16 * 5)
            for t in range(TT):
                last = nc.tensor.matmul(logits_ps[:, t, :], xT[:, t * P:(t + 1) * P], wr[:, :], start=True, stop=True)
            last.then_inc(logits_ready, 1)
            with pe.Fori(0, BITS + 1) as i:
                pe.wait_ge(count_ready, START + i + 1)
                nc.tensor.matmul(total_ps[:, :], ones[:, :], count[:, :], start=True, stop=True).then_inc(total_ready, 1)
            pe.wait_ge(equal_ready, START + 1)
            nc.tensor.matmul(prefix_ps[:, :, :], tri[:, :], equal[:, :, :], start=True, stop=True)
            nc.tensor.matmul(totals_ps[:, :, :], ones[:, :], equal[:, :, :], start=True,
                             stop=True).then_inc(places_ready, 1)
            pe.wait_ge(gate_ready, START + 1)
            for t in range(TT):
                last = nc.tensor.transpose(turn_ps[:, t * P:(t + 1) * P], scores[:, t, :], core.ident[:, :])
            last.then_inc(gate_turned, 1)

        @block.scalar
        def _(act):
            act.wait_ge(shifted_ready, START + 1)
            nc.scalar.activation(scores[:, :, :], shifted[:, :, :], ACT.Exp).then_inc(exp_ready, 1)
            act.wait_ge(gate_turned, START + 1)
            nc.scalar.activation(gateT[:, :], turn_ps[:, :], ACT.Copy)

        @block.vector
        def _(dve):
            done = [0]

            def then(instruction):
                instruction.then_inc(step, 1)
                done[0] += 1
                dve.wait_ge(step, START + done[0])

            dve.wait_ge(loaded, START + 16 * 5)
            dve.wait_ge(logits_ready, START + 1)
            then(nc.vector.tensor_reduce(most[:, :], logits_ps[:, :, :], axis=AX.X, op=ALU.max))
            nc.vector.tensor_tensor(shifted[:, :, :], logits_ps[:, :, :], spread(most[:, :], E),
                                    ALU.subtract).then_inc(shifted_ready, 1)
            nc.vector.memset(threshold[:, :], 0).then_inc(threshold_ready, 1)
            dve.wait_ge(exp_ready, START + 1)
            then(nc.vector.tensor_reduce(total[:, :], scores[:, :, :], axis=AX.X, op=ALU.add))
            then(nc.vector.reciprocal(total[:, :], total[:, :]))
            then(nc.vector.tensor_tensor(scores[:, :, :], scores[:, :, :], spread(total[:, :], E), ALU.mult))
            flat = scores[:, :, :].rearrange("p t e -> p (t e)")
            scratch = above[:, :, :].rearrange("p t e -> p (t e)")
            with dve.Fori(0, BITS) as i:
                dve.wait_ge(threshold_ready, START + i + 1)
                nc.vector.tensor_tensor(trial[:, :], threshold[:, :], bits[:, bass.ds(i, 1)],
                                        ALU.bitwise_or).then_inc(tried, 1)
                dve.wait_ge(tried, START + i + 1)
                nc.vector.tensor_scalar(scratch, flat, trial[:, :].bitcast(F32), None, ALU.is_ge, ALU.add,
                                        accum_out=count[:, :]).then_inc(count_ready, 1)
                dve.wait_ge(total_ready, START + i + 1)
                nc.vector.tensor_scalar(bit[:, :], total_ps[:, :], float(CHOSEN), bitsf[:, bass.ds(i, 1)],
                                        ALU.is_ge, ALU.mult).then_inc(passed, 1)
                dve.wait_ge(passed, START + i + 1)
                nc.vector.tensor_tensor(threshold[:, :], threshold[:, :], bit[:, :],
                                        ALU.bitwise_or).then_inc(threshold_ready, 1)
            dve.wait_ge(threshold_ready, START + BITS + 1)
            least = threshold[:, :].bitcast(F32)
            nc.vector.tensor_scalar(scratch, flat, least, None, ALU.is_gt, ALU.add,
                                    accum_out=count[:, :]).then_inc(count_ready, 1)
            nc.vector.tensor_scalar(equal[:, :, :], scores[:, :, :], least, None, ALU.is_equal).then_inc(equal_ready, 1)
            dve.wait_ge(total_ready, START + BITS + 1)
            then(nc.vector.tensor_scalar(needed[:, :], total_ps[:, :], -1.0, float(CHOSEN), ALU.mult, ALU.add))
            dve.wait_ge(places_ready, START + 1)
            then(nc.vector.tensor_copy(totals[:, :, :], totals_ps[:, :, :]))
            for e in range(E):
                last = nc.vector.tensor_tensor_scan(places[:, :, e], core.ones_row[:, 0:TT], totals[:, :, e], 0.0,
                                                    ALU.mult, ALU.add)
            then(last)
            then(nc.vector.tensor_tensor_scan(before[:, :], core.ones_row[:, 0:E], places[:, TT - 1, :], 0.0,
                                              ALU.mult, ALU.add))
            then(nc.vector.tensor_tensor(before[:, :], before[:, :], places[:, TT - 1, :], ALU.subtract))
            then(nc.vector.tensor_tensor(places[:, :, :], places[:, :, :], totals[:, :, :], ALU.subtract))
            then(nc.vector.tensor_tensor(places[:, :, :], places[:, :, :], prefix_ps[:, :, :], ALU.add))
            then(nc.vector.tensor_tensor(places[:, :, :], places[:, :, :],
                                         before[:, :].unsqueeze(1).to_broadcast([P, TT, E]), ALU.add))
            then(nc.vector.scalar_tensor_tensor(out=places[:, :, :], in0=places[:, :, :], scalar=needed[:, 0:1],
                                                in1=equal[:, :, :], op0=ALU.is_le, op1=ALU.mult))
            then(nc.vector.tensor_tensor(above[:, :, :], above[:, :, :], places[:, :, :], ALU.add))
            nc.vector.tensor_tensor(scores[:, :, :], scores[:, :, :], above[:, :, :], ALU.mult).then_inc(gate_ready, 1)


def choice_experts(core, A, xT, gateT, w1, w2, w_loaded):
    nc = core.nc
    E = CH_EXPERTS
    RING = 3
    PER = CH_ALL * CH_HT
    loaded = core.sem("c_b_loaded")
    up_ready = core.sem("c_up")
    gelu_ready = core.sem("c_gelu")
    spread_ready = core.sem("c_spread")
    gated_ready = core.sem("c_gated")
    down_ready = core.sem("c_down")
    added = core.sem("c_added")
    with ExitStack() as mem:
        b1 = core.sb(mem, "c_b1", [P, CH_ALL, CH_HT])
        b2 = core.sb(mem, "c_b2", [E, C])
        bs2 = core.sb(mem, "c_bs2", [C, 1])
        select = core.sb(mem, "c_select", [E, E, P])
        hid = core.sb(mem, "c_hid", [P, 2, CH_HT, N])
        gated = core.sb(mem, "c_gated_sb", [P, 2, CH_HT, N])
        up_ps = [core.ps(mem, f"c_up_ps{n}", [P, N]) for n in range(RING)]
        g_ps = [core.ps(mem, f"c_g_ps{n}", [P, N]) for n in range(2)]
        y_ps = core.ps(mem, "c_y_ps", [C, N])
        block = mem.enter_context(core.block())

        @block.sync
        def _(sp):
            for dst, name in ((b1[:, :, :], "c_b1"), (b2[:, :], "c_b2"), (bs2[:, :], "c_bs2"),
                              (select[:, :, :], "c_select")):
                sp.dma_start(dst, A[name]).then_inc(loaded, 16)

        @block.tensor
        def _(pe):
            pe.wait_ge(loaded, START + 64)
            pe.wait_ge(w_loaded, START + 32)
            with pe.Fori(0, B) as i:
                def up(e):
                    for m in range(CH_HT):
                        u = e * CH_HT + m
                        if m == CH_HT - 1 and e < E:
                            pe.wait_ge(gated_ready, START + i * E + max(e - 1, 0))
                        pe.wait_ge(gelu_ready, START + i * PER + max(u - RING + 1, 0))
                        nc.tensor.matmul(up_ps[u % RING][:, :], w1[:, e, m * P:(m + 1) * P], xT[:, cols(i)],
                                         start=True, stop=True).then_inc(up_ready, 1)
                    if e < E:
                        nc.tensor.matmul(g_ps[e % 2][:, :], select[:, e, :], gateT[:, cols(i)],
                                         start=True, stop=True).then_inc(spread_ready, 1)

                def down(e):
                    if e < E:
                        pe.wait_ge(gated_ready, START + i * E + e + 1)
                        src = gated
                    else:
                        pe.wait_ge(gelu_ready, START + (i + 1) * PER)
                        src = hid
                    if e == 0:
                        pe.wait_ge(added, START + i)
                    for k in range(CH_HT):
                        last = nc.tensor.matmul(y_ps[:, :], w2[:, e, k, :], src[:, e % 2, k, :],
                                                start=(e == 0 and k == 0), stop=(e == E and k == CH_HT - 1))
                        if e == 0 and k == 0:
                            nc.tensor.matmul(y_ps[:, :], b2[:, :], gateT[:, cols(i)], start=False, stop=False)
                    last.then_inc(down_ready, 1)

                for e in range(CH_ALL + 1):
                    if e < CH_ALL:
                        up(e)
                    if e:
                        down(e - 1)

        @block.scalar
        def _(act):
            act.wait_ge(loaded, START + 64)
            with act.Fori(0, B) as i:
                for e in range(CH_ALL):
                    for m in range(CH_HT):
                        u = e * CH_HT + m
                        if m == 0:
                            act.wait_ge(gated_ready, START + i * E + max(e - 1, 0))
                            act.wait_ge(down_ready, START + i * CH_ALL)
                        act.wait_ge(up_ready, START + i * PER + u + 1)
                        nc.scalar.activation(hid[:, e % 2, m, :], up_ps[u % RING][:, :], ACT.Gelu_apprx_tanh,
                                             bias=b1[:, e, m:m + 1]).then_inc(gelu_ready, 1)

        @block.vector
        def _(dve):
            dve.wait_ge(loaded, START + 64)
            with dve.Fori(0, B) as i:
                for e in range(E):
                    dve.wait_ge(spread_ready, START + i * E + e + 1)
                    dve.wait_ge(down_ready, START + i * CH_ALL + max(e - 1, 0))
                    dve.wait_ge(gelu_ready, START + i * PER + (e + 1) * CH_HT)
                    nc.vector.tensor_tensor(gated[:, e % 2, :, :], hid[:, e % 2, :, :],
                                            g_ps[e % 2][:, :].unsqueeze(1).to_broadcast([P, CH_HT, N]),
                                            ALU.mult).then_inc(gated_ready, 1)
                dve.wait_ge(down_ready, START + (i + 1) * CH_ALL)
                nc.vector.scalar_tensor_tensor(out=xT[:, cols(i)], in0=y_ps[:, :], scalar=bs2[:, 0:1],
                                               in1=xT[:, cols(i)], op0=ALU.add, op1=ALU.add).then_inc(added, 1)


def rope_tables(angles, order):
    freq, sign = order
    theta = np.arange(N, dtype=np.float32)[None, :] * angles.astype(np.float32)[:, None]
    cos, sin = np.cos(theta)[freq], np.sin(theta)[freq] * np.array(sign, np.float32)[:, None]
    scale = np.float32(-(HD ** -0.5))
    one = np.stack([cos * scale, sin * scale, cos, sin], 1).astype(np.float32)
    return np.tile(one, (HEADS, 1, 1))


def lay_attention(tag, wq, wk, wv, wproj, turn, tables):
    order = (np.arange(HEADS)[:, None] * HD + np.array(turn)[None, :]).ravel()
    w = np.stack([wq.T, wq[order].T, wk.T, wk[order].T, wv.T], 1)
    return {f"{tag}_wqkv": w, f"{tag}_rope": tables, f"{tag}_wproj": wproj.T}




def lay_attention0(I):
    L = {}
    half = HD // 2
    qkv = I["L0_attn_qkv_w"]
    angles = 1.0 / np.power(np.float32(10000.0), np.arange(0, HD, 2, dtype=np.float32) / np.float32(HD))
    L |= lay_attention("a0", qkv[:C], qkv[C:2 * C], qkv[2 * C:], I["L0_attn_proj_w"],
                       [(d + half) % HD for d in range(HD)],
                       rope_tables(angles, ([d % half for d in range(HD)], [-1] * half + [1] * half)))
    L["a0_bproj"] = I["L0_attn_proj_b"].reshape(C, 1)
    L["a0_window"] = np.maximum(8.0 * (np.arange(P)[:, None] + (QT - 1) * P - np.arange(WINDOW)[None, :]),
                                0.0).astype(np.float32)
    which, pattern = np.zeros((BIAS_ROWS, 2, 4), np.float32), np.zeros((BIAS_ROWS, 2, N), np.float32)
    token = np.arange(N)
    for j in range(PAIRS_OF_TILES):
        end = (j + 1) * P - 1
        past = np.where(token > end, token - end, 0)
        here = (token > end - P) & (token <= end)
        for part in range(3):
            r = 9 * j + 3 * part
            for n, distance in enumerate((past - past % 2, past % 2)):
                which[r + n, 0, 3] = which[r + n, 1, part] = 1.0
                pattern[r + n, 0], pattern[r + n, 1] = distance, here
            which[r + 2, 0, part] = which[r + 2, 1, 3] = 1.0
            pattern[r + 2, 0], pattern[r + 2, 1] = past > 0, np.where(here, end - token, 0)
    L["a0_which"], L["a0_pattern"] = which, pattern
    L["a0_steps"] = np.maximum(np.arange(P)[None, :] - np.arange(P)[:, None], 0).astype(mybir.dt.np(BF16))
    L["a0_slopes"] = np.broadcast_to(I["L0_attn_slopes"][None, :], (P, HEADS))
    return L


def lay_gated_mlp(I):
    L = {}
    L["f0_w12"] = np.stack([I["L0_ffn_w1_w"].T, I["L0_ffn_w2_w"].T], 1)
    L["f0_wh"] = np.stack([I[f"L0_ffn_{n}_w"].T.reshape(HT, P, HID).transpose(1, 0, 2) for n in ("h1", "h2")], 1)
    L["f0_w3"] = I["L0_ffn_w3_w"].T.reshape(HT, P, C).transpose(1, 0, 2)
    L["f0_scales"] = np.concatenate([I[f"L0_ffn_{n}_s"].reshape(-1, P).T for n in ("w1", "w2", "h1", "h2", "w3")], 1)
    return L


def lay_ssm(I):
    L = {}
    S = {k[8:]: a for k, a in I.items() if k.startswith("L1_attn_")}
    L["s_wide"] = np.stack([S["proj_W"].T, S["fconv_W"].T, S["bconv_W"].T], 1)
    L["s_wdr"] = S["deltaBC_W"][:DT_RANK].T
    L["s_wbc"] = np.tile(S["deltaBC_W"][DT_RANK:].T, (1, 3))
    L["s_wdt"] = np.tile(S["dt_W"].T, (BRANCHES, 1))
    L["s_cst"] = np.stack([S[n] for n in ("ln_w", "ln_b", "proj_b", "fconv_b", "bconv_b", "dt_b", "D")], 1)
    L["s_alog"] = S["A_log"]
    rows = np.arange(3 * BC)[:, None, None] % BC == np.arange(BC)[None, :, None]
    L["s_select"] = np.broadcast_to(rows, (3 * BC, BC, P)).astype(mybir.dt.np(BF16))
    return L


def lay_moe(I):
    L = {}
    L["m_wr"] = I["L1_ffn_w_router"].T
    L["m_iota"] = np.broadcast_to(np.arange(EXPERTS, dtype=np.float32), (P, TT, EXPERTS))
    L["m_wg"] = I["L1_ffn_w_gate"].T
    L["m_wd"] = I["L1_ffn_w_down"].transpose(2, 0, 1).reshape(MOE_HT, P, EXPERTS * C).transpose(1, 0, 2)
    return L


def lay_query_softmax(I):
    L = {}
    L["q_wqk"] = np.stack([I["L2_attn_Mq"], I["L2_attn_Mk"]], 1)
    L["q_wv"] = I["L2_attn_Mv"]
    place = np.zeros((4, VPAD, 2, 2, 4, VD), np.float32)
    for j in range(QH):
        for d in range(VD):
            place[j % 4, d, j // 4, j // 4, j % 4, d] = 1.0
    L["q_place"] = place.reshape(P, 2, C)
    return L


def lay_sparse(I):
    L = {}
    S = {k[7:]: a for k, a in I.items() if k.startswith("L2_ffn_")}
    L["x_wu"] = S["w_up"].transpose(2, 0, 1)
    L["x_wd"] = S["w_down"].reshape(X_EXPERTS, C, X_INTER // P, P).transpose(3, 0, 2, 1)
    L["x_wau"] = S["a_up"].transpose(2, 0, 1)
    L["x_wad"] = S["a_down"].transpose(2, 0, 1)
    L["x_r1x"] = S["r1_w"][:, :C].T
    L["x_r1s"] = S["r1_w"][:, C:].T
    L["x_r1b"] = S["r1_b"].reshape(X_ROUTER, 1)
    L["x_r2"] = S["r2_w"].T
    L["x_iota"] = np.broadcast_to(np.arange(X_EXPERTS, dtype=np.float32), (P, TT, X_EXPERTS))
    L["x_base"] = (np.arange(X_EXPERTS, dtype=np.float32) * X_CAP).reshape(X_EXPERTS, 1)
    return L


def lay_attention3(I):
    L = {}
    half = HD // 2
    angles = np.power(np.float32(10000.0), np.float32(2.0) * np.arange(half, dtype=np.float32) / np.float32(HD))
    L |= lay_attention("a3", I["L3_attn_w_q"], I["L3_attn_w_k"], I["L3_attn_w_v"], I["L3_attn_w_o"],
                       [d ^ 1 for d in range(HD)],
                       rope_tables(angles, ([d // 2 for d in range(HD)], [-1, 1] * half)))
    L["a3_bproj"] = np.zeros((C, 1), np.float32)
    return L


def lay_choice(I):
    L = {}
    L["c_wr"] = I["L3_ffn_gate_weight"].T
    bits = (1 << np.arange(BITS - 1, -1, -1)).astype(np.int32)
    L["c_bits"] = np.broadcast_to(bits, (P, BITS))
    L["c_bitsf"] = L["c_bits"].astype(np.float32)
    L["c_w1"] = np.concatenate([I["L3_ffn_W1"], I["L3_ffn_Ws1"][None]], 0).transpose(1, 0, 2)
    L["c_w2"] = np.concatenate([I["L3_ffn_W2"], I["L3_ffn_Ws2"][None]], 0) \
        .reshape(CH_ALL, CH_HT, P, C).transpose(2, 0, 1, 3)
    L["c_b1"] = np.concatenate([I["L3_ffn_b1"], I["L3_ffn_bs1"][None]], 0) \
        .reshape(CH_ALL, CH_HT, P).transpose(2, 0, 1)
    L["c_b2"] = I["L3_ffn_b2"]
    L["c_bs2"] = I["L3_ffn_bs2"].reshape(C, 1)
    L["c_select"] = np.broadcast_to(np.eye(CH_EXPERTS, dtype=np.float32)[:, :, None], (CH_EXPERTS, CH_EXPERTS, P))
    return L


def attention0_stage(core, A, xT):
    attention_stage(core, A, xT, "a0", alibi=True)


def attention3_stage(core, A, xT):
    attention_stage(core, A, xT, "a3", alibi=False)


STAGES = [(attention0_stage, lay_attention0), (gated_mlp_stage, lay_gated_mlp), (ssm_stage, lay_ssm),
          (moe_stage, lay_moe), (query_softmax_stage, lay_query_softmax), (sparse_stage, lay_sparse),
          (attention3_stage, lay_attention3), (choice_stage, lay_choice)]


def lay_out(I):
    L = {"x": I["L0_attn_x"].reshape(T, C).T,
         "tri": (np.arange(P)[:, None] <= np.arange(P)[None, :]).astype(np.float32),
         "ones": np.ones((P, P), np.float32)}
    for _, lay in STAGES:
        L |= lay(I)
    return L


def network(nc, A, out):
    with ExitStack() as ctx:
        core = Core(nc, ctx)
        xT = core.sb(ctx, "xT", [C, T])
        core.ident = core.sb(ctx, "ident", [P, P])
        core.avg = core.sb(ctx, "avg", [P, P])
        core.eps = core.sb(ctx, "eps", [P, 1])
        core.one = core.sb(ctx, "one", [P, 1])
        core.ones_row = core.sb(ctx, "ones_row", [P, N])
        loaded = core.sem("x_loaded")
        zeroed = core.sem("ident_zeroed")
        with core.block() as block:
            @block.sync
            def _(sp):
                sp.dma_start(xT[:, :], A["x"]).then_inc(loaded, 16)
                sp.wait_ge(loaded, START + 16)

            @block.gpsimd
            def _(pool):
                nc.gpsimd.memset(core.avg[:, :], 1.0 / C)
                nc.gpsimd.memset(core.eps[:, :], LN_EPS)
                nc.gpsimd.memset(core.one[:, :], 1.0)
                nc.gpsimd.memset(core.ones_row[:, :], 1.0)
                nc.gpsimd.memset(core.ident[:, :], 0.0).then_inc(zeroed, 1)
                pool.wait_ge(zeroed, START + 1)
                nc.gpsimd.affine_select(out=core.ident[:, :], in_=core.ident[:, :], compare_op=ALU.not_equal,
                                        fill=1.0, base=0, pattern=[[-1, P]], channel_multiplier=1)
        for n, (stage, _) in enumerate(STAGES):
            core.run_stage(stage, A, xT)
            layernorm_stage(core, xT, f"ln{n}")
        stored = core.sem("out_stored")
        with core.block() as block:
            @block.sync
            def _(sp):
                sp.dma_start(out, xT[:, :]).then_inc(stored, 16)
                sp.wait_ge(stored, START + 16)


def kernel(**inputs):
    import concourse.bacc as bacc
    from concourse.bass_utils import run_bass_kernel_spmd

    nc = bacc.Bacc("TRN2", target_bir_lowering=False, num_devices=1)
    arrays, args = {}, {}
    for name, a in lay_out({k: np.asarray(v) for k, v in inputs.items()}).items():
        a = np.ascontiguousarray(a)
        arrays[f"in_{name}"] = a
        args[name] = nc.dram_tensor(f"in_{name}", a.shape, mybir.dt.from_np(a.dtype), kind="ExternalInput").ap()
    out = nc.dram_tensor("out_xT", (C, T), F32, kind="ExternalOutput").ap()
    network(nc, args, out)
    result = run_bass_kernel_spmd(nc, [arrays], core_ids=[0])
    return result.results[0]["out_xT"].T.reshape(B, N, C)
```

```python
import concourse.bass as bass
from concourse import mybir
from contextlib import ExitStack

import numpy as np

F32 = mybir.dt.float32
BF16 = mybir.dt.bfloat16
I32 = mybir.dt.int32
U32 = mybir.dt.uint32
ALU = mybir.AluOpType
ACT = mybir.ActivationFunctionType
AX = mybir.AxisListType

B = 4
N = 512
T = B * N
C = 128
P = 128
TT = T // P
LN_EPS = 1e-5
START = 1


def cols(i, size=N):
    return bass.ds(i * size, size)


def spread(ap, size):
    return ap.unsqueeze(2).to_broadcast([ap.shape[0], ap.shape[1], size])


class Core:

    def __init__(self, nc, ctx):
        self.nc, self.ctx = nc, ctx
        self.stage_ctx, self.stage_sems, self.unstarted = None, [], []
        self.norms = 0
        self.norm_sems = [self.sem(f"norm_{n}") for n in ("mean", "centred", "square", "var", "logvar", "rstd")]

    def sb(self, ctx, name, shape, dt=F32):
        return ctx.enter_context(self.nc.sbuf_tensor(name, shape, dt))

    def ps(self, ctx, name, shape, dt=F32):
        return ctx.enter_context(self.nc.psum_tensor(name, shape, dt))

    def sem(self, name, software_dma=False):
        ctx = self.ctx if self.stage_ctx is None else self.stage_ctx
        handle = ctx.enter_context(self.nc.semaphore(name))
        if not software_dma:
            self.unstarted.append(handle)
        self.stage_sems.append(handle)
        return handle

    def block(self):
        if self.unstarted:
            for handle in self.unstarted:
                self.nc.gpsimd.nop().then_inc(handle, START)
            self.unstarted = []
            self.nc.all_engine_barrier()
        return self.nc.Block()

    def run_stage(self, stage, *args):
        self.stage_sems = []
        with ExitStack() as self.stage_ctx:
            stage(self, *args)
            with self.nc.Block() as block:
                @block.gpsimd
                def _(pool):
                    for handle in self.stage_sems:
                        pool.sem_clear(handle)
        self.stage_ctx = None


def layernorm_stage(core, xT, tag, out=None, prefetch=None):
    out = xT if out is None else out
    nc = core.nc
    mean_ready, centred_ready, square_ready, var_ready, logvar_ready, rstd_ready = core.norm_sems
    done = core.norms * B
    core.norms += 1
    with ExitStack() as mem:
        centred = core.sb(mem, f"{tag}_xc", [P, T])
        square = core.sb(mem, f"{tag}_sq", [P, T])
        logvar = core.sb(mem, f"{tag}_lv", [P, T])
        rstd = core.sb(mem, f"{tag}_rs", [P, T])
        mean = core.ps(mem, f"{tag}_ps_mean", [P, T])
        var = core.ps(mem, f"{tag}_ps_var", [P, T])
        block = mem.enter_context(core.block())

        @block.sync
        def _(sp):
            if prefetch:
                prefetch(sp)

        @block.tensor
        def _(pe):
            for i in range(B):
                nc.tensor.matmul(mean[:, cols(i)], core.avg[:, :], xT[:, cols(i)],
                                 start=True, stop=True).then_inc(mean_ready, 1)
            for i in range(B):
                pe.wait_ge(square_ready, START + done + i + 1)
                nc.tensor.matmul(var[:, cols(i)], core.avg[:, :], square[:, cols(i)],
                                 start=True, stop=True).then_inc(var_ready, 1)

        @block.scalar
        def _(act):
            for i in range(B):
                act.wait_ge(centred_ready, START + done + i + 1)
                nc.scalar.activation(square[:, cols(i)], centred[:, cols(i)], ACT.Square).then_inc(square_ready, 1)
            for i in range(B):
                act.wait_ge(var_ready, START + done + i + 1)
                nc.scalar.activation(logvar[:, cols(i)], var[:, cols(i)], ACT.Ln,
                                     bias=core.eps[:, 0:1]).then_inc(logvar_ready, 1)
            for i in range(B):
                act.wait_ge(logvar_ready, START + done + i + 1)
                nc.scalar.activation(rstd[:, cols(i)], logvar[:, cols(i)], ACT.Exp,
                                     scale=-0.5).then_inc(rstd_ready, 1)

        @block.vector
        def _(dve):
            for i in range(B):
                dve.wait_ge(mean_ready, START + done + i + 1)
                nc.vector.tensor_tensor(centred[:, cols(i)], xT[:, cols(i)], mean[:, cols(i)],
                                        ALU.subtract).then_inc(centred_ready, 1)
            for i in range(B):
                dve.wait_ge(rstd_ready, START + done + i + 1)
                nc.vector.tensor_tensor(out[:, cols(i)], centred[:, cols(i)], rstd[:, cols(i)], ALU.mult)


HEADS = 16
HD = C // HEADS
QT = N // P
KT = N // P
Q_PARTS = (0, 0, 0, 1, 2, 1)
K_PARTS = (1, 2, 0, 0, 0, 1)
STACK = HD * len(Q_PARTS)
GROUP = 4
GROUPS = HEADS // GROUP
VPAD = 32
LEAST_AT = 96
LEAST_ROWS = 3
PAIRS_OF_TILES = QT - 1
LOWER_ROWS = LEAST_ROWS + 9 * PAIRS_OF_TILES
WINDOW = N + (QT - 1) * P


def attention_stage(core, A, xT, tag, alibi, first):
    nc = core.nc
    stacks_dram = nc.dram_tensor(f"{tag}_stacks", (2, B, C, len(Q_PARTS), N), BF16).ap()
    rows = LEAST_AT + (LOWER_ROWS if alibi else LEAST_ROWS)
    with ExitStack() as mem:
        M = {"v": core.sb(mem, f"{tag}_v", [P, TT, C]),
             "wproj": core.sb(mem, f"{tag}_wproj", [C, C]),
             "bproj": core.sb(mem, f"{tag}_bproj", [C, 1]),
             "qs": core.sb(mem, f"{tag}_qs", [rows, HEADS, N], BF16),
             "ks": core.sb(mem, f"{tag}_ks", [rows, HEADS, N], BF16),
             "vpad": core.sb(mem, f"{tag}_vpad", [P, KT, HEADS, VPAD]),
             "stacks": [core.sem(f"{tag}_stack{g}_loaded") for g in range(GROUPS)]}
        if alibi:
            M["bias"] = core.sb(mem, f"{tag}_bias", [P, HEADS, WINDOW])
            M["steps"] = core.sb(mem, f"{tag}_steps", [P, P], BF16)
            M["slopes_diag"] = core.sb(mem, f"{tag}_slopes_diag", [P, 3, HEADS, P], BF16)
        M |= {"wqkv": core.sb(mem, f"{tag}_wqkv", [C, 5, C]),
              "rope": core.sb(mem, f"{tag}_rope", [C, 4, N]),
              "w_loaded": core.sem(f"{tag}_w_loaded")}

        def load_weights(sp):
            for name in ("wqkv", "rope", "wproj", "bproj"):
                whole = tuple(slice(None) for _ in M[name].shape)
                sp.dma_start(M[name][whole], A[f"{tag}_{name}"]).then_inc(M["w_loaded"], 16)

        if first:
            project_and_split(core, A, xT, tag, stacks_dram, M, load_weights)
        else:
            layernorm_stage(core, xT, f"{tag}_ln", prefetch=load_weights)
            project_and_split(core, A, xT, tag, stacks_dram, M, None)
        attend(core, A, xT, tag, stacks_dram, M)


def load_stacks(sp, stacks_dram, M, g, batch):
    mine = slice(g * GROUP, (g + 1) * GROUP)
    for a, dst in enumerate((M["qs"], M["ks"])):
        sp.dma_start(dst[0:STACK, mine, :],
                     stacks_dram[a, batch].rearrange("(h d) s t -> (d s) h t", d=HD)[:, mine, :]) \
            .then_inc(M["stacks"][g], 16)


def project_and_split(core, A, xT, tag, stacks_dram, M, load_weights):
    nc = core.nc
    qs, ks, v_all, vpad = M["qs"], M["ks"], M["v"], M["vpad"]
    wproj, bproj, bias = M["wproj"], M["bproj"], M.get("bias")
    R, PART_HEADS = LOWER_ROWS, HEADS // B
    wqkv, rope, w_loaded = M["wqkv"], M["rope"], M["w_loaded"]
    qk_ready = core.sem(f"{tag}_qk_ready")
    v_ready = core.sem(f"{tag}_v_ready")
    v_kept = core.sem(f"{tag}_v_kept")
    products = core.sem(f"{tag}_rope_products")
    rotated = core.sem(f"{tag}_rotated")
    high = core.sem(f"{tag}_high")
    rest = core.sem(f"{tag}_rest")
    middle = core.sem(f"{tag}_middle")
    low = core.sem(f"{tag}_low")
    stored = [core.sem(f"{tag}_parts_stored{n}") for n in range(2)]
    slopes_loaded = core.sem(f"{tag}_slopes_loaded")
    slope_step = core.sem(f"{tag}_slope_step")
    q_cleared = core.sem(f"{tag}_q_cleared")
    k_cleared = core.sem(f"{tag}_k_cleared")
    v_cleared = core.sem(f"{tag}_v_cleared")
    STORES = 2 * 3
    with ExitStack() as mem:
        prod = core.sb(mem, f"{tag}_prod", [C, 2, 2, N])
        qk = core.sb(mem, f"{tag}_qk", [C, 2, 2, N])
        left = core.sb(mem, f"{tag}_left", [C, 2, 2, N])
        parts = core.sb(mem, f"{tag}_p", [C, 2, 2, 3, N], BF16)
        if alibi := bias is not None:
            window = core.sb(mem, f"{tag}_window", [P, WINDOW])
            slopes = core.sb(mem, f"{tag}_slopes", [P, HEADS])
            slope_parts = core.sb(mem, f"{tag}_slope_parts", [P, 3, HEADS])
            slope_part = core.sb(mem, f"{tag}_slope_part", [P, 3, HEADS], BF16)
            slope_rest = core.sb(mem, f"{tag}_slope_rest", [P, HEADS])
            factor = core.sb(mem, f"{tag}_factor", [R, 2, HEADS])
            which = core.sb(mem, f"{tag}_which", [R, 2, 4])
            pattern = core.sb(mem, f"{tag}_pattern", [R, 2, N])
        qk_ps = core.ps(mem, f"{tag}_qk_ps", [C, 4, N])
        v_ps = core.ps(mem, f"{tag}_v_ps", [P, KT, C])
        block = mem.enter_context(core.block())

        @block.sync
        def _(sp):
            if load_weights:
                load_weights(sp)
            if alibi:
                for dst, name in ((slopes[:, :], "slopes"), (which[:, :, :], "which"), (window[:, :], "window"),
                                  (pattern[:, :, :], "pattern"), (M["steps"][:, :], "steps")):
                    sp.dma_start(dst, A[f"{tag}_{name}"]).then_inc(slopes_loaded, 16)
            for i in range(B):
                for done, part_done in ((high, 0), (middle, 1), (low, 2)):
                    sp.wait_ge(done, START + i + 1)
                    for a, which_part in enumerate((Q_PARTS, K_PARTS)):
                        at = [s for s, part in enumerate(which_part) if part == part_done]
                        slots = slice(at[0], at[-1] + 1, at[1] - at[0] if at[1:] else 1)
                        sp.dma_start(stacks_dram[a, i, :, slots],
                                     parts[:, i % 2, a, part_done, :].unsqueeze(1).to_broadcast([C, len(at), N])) \
                            .then_inc(stored[i % 2], 16)
                if i == 1:
                    sp.wait_ge(stored[0], START + 16 * STORES)
                    sp.wait_ge(q_cleared, START + 1)
                    sp.wait_ge(k_cleared, START + 1)
                    for g in range(GROUPS):
                        load_stacks(sp, stacks_dram, M, g, 0)
            for n in range(2):
                sp.wait_ge(stored[n], START + 16 * STORES * B // 2)

        @block.tensor
        def _(pe):
            pe.wait_ge(w_loaded, START + 16 * 4)
            for i in range(B):
                for n in range(4):
                    if i > 0:
                        pe.wait_ge(products, START + 4 * (i - 1) + n + 1)
                    nc.tensor.matmul(qk_ps[:, n, :], wqkv[:, n, :], xT[:, cols(i)],
                                     start=True, stop=True).then_inc(qk_ready, 1)
                if i > 0:
                    pe.wait_ge(v_kept, START + i)
                for t in range(KT):
                    at = (i * KT + t) * P
                    last = nc.tensor.matmul(v_ps[:, t, :], xT[:, at:at + P], wqkv[:, 4, :],
                                            start=True, stop=True)
                last.then_inc(v_ready, 1)

        @block.scalar
        def _(act):
            def copy_middle(i):
                act.wait_ge(rest, START + i + 1)
                nc.scalar.activation(parts[:, i % 2, :, 1, :], left[:, i % 2, :, :], ACT.Copy).then_inc(middle, 1)

            if alibi:
                act.wait_ge(slopes_loaded, START + 16 * 5)
            for i in range(B):
                act.wait_ge(rotated, START + i + 1)
                if i > 1:
                    act.wait_ge(stored[i % 2], START + 16 * STORES * (i // 2))
                nc.scalar.activation(parts[:, i % 2, :, 0, :], qk[:, i % 2, :, :], ACT.Copy).then_inc(high, 1)
                act.wait_ge(v_ready, START + i + 1)
                nc.scalar.activation(v_all[:, i * KT:(i + 1) * KT, :], v_ps[:, :, :], ACT.Copy).then_inc(v_kept, 1)
                if i > 0:
                    copy_middle(i - 1)
                if alibi:
                    for h in range(i * PART_HEADS, (i + 1) * PART_HEADS):
                        nc.scalar.activation(bias[:, h, :], window[:, :], ACT.Copy, scale=slopes[:, h:h + 1])
            copy_middle(B - 1)

        @block.vector
        def _(dve):
            steps = [0]

            def then(instruction):
                instruction.then_inc(slope_step, 1)
                steps[0] += 1
                dve.wait_ge(slope_step, START + steps[0])

            nc.vector.memset(qs[0:LEAST_AT, :, :], 0.0).then_inc(q_cleared, 1)
            if alibi:
                dve.wait_ge(slopes_loaded, START + 16 * 5)
                then(nc.vector.tensor_scalar(slope_rest[:, :], slopes[:, :], 8.0, None, ALU.mult))
                for n in range(3):
                    then(nc.vector.tensor_copy(slope_part[:, n, :], slope_rest[:, :]))
                    then(nc.vector.tensor_copy(slope_parts[:, n, :], slope_part[:, n, :]))
                    then(nc.vector.tensor_tensor(slope_rest[:, :], slope_rest[:, :], slope_parts[:, n, :],
                                                 ALU.subtract))
                for a in range(2):
                    then(nc.vector.tensor_scalar(factor[:, a, :], slope_parts[0:R, 0, :], which[:, a, 0:1],
                                                 which[:, a, 3:4], ALU.mult, ALU.add))
                    for n in (1, 2):
                        then(nc.vector.scalar_tensor_tensor(out=factor[:, a, :], in0=slope_parts[0:R, n, :],
                                                            scalar=which[:, a, n:n + 1], in1=factor[:, a, :],
                                                            op0=ALU.mult, op1=ALU.add))
            dve.wait_ge(w_loaded, START + 16 * 4)
            for i in range(B):
                if i > 0:
                    dve.wait_ge(rotated, START + i)
                for n in range(4):
                    dve.wait_ge(qk_ready, START + 4 * i + n + 1)
                    nc.vector.tensor_tensor(prod[:, n // 2, n % 2, :], qk_ps[:, n, :], rope[:, n, :],
                                            ALU.mult).then_inc(products, 1)
                dve.wait_ge(products, START + 4 * i + 4)
                if i > 1:
                    dve.wait_ge(rest, START + i - 1)
                nc.vector.tensor_tensor(qk[:, i % 2, :, :], prod[:, :, 0, :], prod[:, :, 1, :],
                                        ALU.add).then_inc(rotated, 1)
                if alibi:
                    mine = slice(i * PART_HEADS, (i + 1) * PART_HEADS)
                    for a, dst in enumerate((qs, ks)):
                        nc.vector.tensor_tensor(
                            dst[LEAST_AT:LEAST_AT + R, mine, :],
                            pattern[:, a, :].unsqueeze(1).to_broadcast([R, PART_HEADS, N]),
                            spread(factor[:, a, mine], N), ALU.mult)
                    shape = [P, 3, PART_HEADS, P]
                    nc.vector.tensor_tensor(M["slopes_diag"][:, :, mine, :],
                                            core.ident[:, :].unsqueeze(1).unsqueeze(1).to_broadcast(shape),
                                            slope_parts[:, :, mine].unsqueeze(3).to_broadcast(shape), ALU.mult)
            if not alibi:
                nc.vector.memset(ks[LEAST_AT:LEAST_AT + LEAST_ROWS, :, :], -1.0)

        @block.gpsimd
        def _(pool):
            def subtract_middle(i):
                pool.wait_ge(middle, START + i + 1)
                nc.gpsimd.tensor_tensor(parts[:, i % 2, :, 2, :], left[:, i % 2, :, :], parts[:, i % 2, :, 1, :],
                                        ALU.subtract).then_inc(low, 1)

            nc.gpsimd.memset(ks[0:LEAST_AT, :, :], 0.0).then_inc(k_cleared, 1)
            nc.gpsimd.memset(vpad[:, :, :, :], 0.0).then_inc(v_cleared, 1)
            pool.wait_ge(v_cleared, START + 1)
            nc.gpsimd.memset(vpad[:, :, :, HD:HD + 1], 1.0)
            for i in range(B):
                pool.wait_ge(high, START + i + 1)
                if i > 1:
                    pool.wait_ge(low, START + i - 1)
                nc.gpsimd.tensor_tensor(left[:, i % 2, :, :], qk[:, i % 2, :, :], parts[:, i % 2, :, 0, :],
                                        ALU.subtract).then_inc(rest, 1)
                if i > 0:
                    subtract_middle(i - 1)
            subtract_middle(B - 1)


def attend(core, A, xT, tag, stacks_dram, M):
    nc = core.nc
    qs, ks, v_all, vpad, wproj, bproj = M["qs"], M["ks"], M["v"], M["vpad"], M["wproj"], M["bproj"]
    bias = M.get("bias")
    ROWS = qs.shape[0]
    U = GROUP * QT
    stacks = M["stacks"]
    scores_ready = core.sem(f"{tag}_scores")
    least_ready = core.sem(f"{tag}_least")
    least_turned = core.sem(f"{tag}_least_turned")
    turn_read = core.sem(f"{tag}_turn_read")
    split_step = core.sem(f"{tag}_split_step")
    least_split = core.sem(f"{tag}_least_split")
    least_placed = [core.sem(f"{tag}_least_placed{n}") for n in range(2)]
    turned_ready = core.sem(f"{tag}_turned_scores")
    probs_ready = core.sem(f"{tag}_probs")
    v_ready = core.sem(f"{tag}_v_padded")
    values_ready = core.sem(f"{tag}_values")
    values_kept = core.sem(f"{tag}_values_kept")
    tail_written = core.sem(f"{tag}_tail_written")
    tail_read = core.sem(f"{tag}_tail_read")
    inverse_ready = core.sem(f"{tag}_inverse")
    LOADS = 2
    TAIL = QT + 2

    with ExitStack() as mem:
        least = core.sb(mem, f"{tag}_least_sb", [P, 2, U])
        least_parts = core.sb(mem, f"{tag}_least_parts", [U, 2, LEAST_ROWS, P], BF16)
        least_rest = core.sb(mem, f"{tag}_least_rest", [U, P])
        probs = core.sb(mem, f"{tag}_probs_sb", [P, 4, 2, N])
        values = core.sb(mem, f"{tag}_values_sb", [P, GROUPS, N])
        inverse = core.sb(mem, f"{tag}_inv", [P, 2, HEADS])
        heads = core.sb(mem, f"{tag}_o", [P, QT, C])
        headsT = core.sb(mem, f"{tag}_oT", [C, N])
        biased = core.sb(mem, f"{tag}_biased", [P, 2, N]) if bias is not None else None
        spacer = core.sb(mem, f"{tag}_spacer", [1, U])
        s_ps = [core.ps(mem, f"{tag}_s_ps{n}", [P, N]) for n in range(2)]
        t_ps = [core.ps(mem, f"{tag}_t_ps{n}", [P, 2, N]) for n in range(2)]
        o_ps = core.ps(mem, f"{tag}_o_ps", [P, N])
        tail_ps = core.ps(mem, f"{tag}_tail_ps", [P, N])
        block = mem.enter_context(core.block())

        def wait(engine, semaphore, value):
            if not isinstance(value, int) or value > 0:
                engine.wait_ge(semaphore, START + value)

        def has_scores(i):
            return not (isinstance(i, int) and i == B)

        def has_turned(i, g, lag=2):
            if isinstance(i, int):
                return 0 <= GROUPS * i + g - lag < GROUPS * B
            return True

        def before(i, g, lag):
            return (i, g - lag) if g >= lag else (i - 1, g - lag + GROUPS)

        def run(engine, body):
            body(0)
            with engine.Fori(1, B) as i:
                body(i)
            body(B)

        @block.sync
        def _(sp):
            def steps(i, first=False, last=False):
                for g in range(GROUPS):
                    k = GROUPS * i + g
                    sp.wait_ge(least_split, START + k + 1)
                    for r in range(LEAST_ROWS):
                        sp.dma_start(qs[LEAST_AT + r:LEAST_AT + r + 1, g * GROUP:(g + 1) * GROUP, :]
                                     .rearrange("r h (t p) -> r (h t) p", p=P),
                                     least_parts[:, g % 2, r, :]).then_inc(least_placed[g % 2], 16)
                    if not (first if g < 2 else last):
                        sp.wait_ge(turned_ready, START + U * (k - 1))
                        load_stacks(sp, stacks_dram, M, (g + 2) % GROUPS, i if g < 2 else i + 1)

            steps(0, first=True)
            with sp.Fori(1, B - 1) as i:
                steps(i)
            steps(B - 1, last=True)

        @block.gpsimd
        def _(pool):
            with pool.Fori(0, B) as i:
                pool.wait_ge(values_ready, START + 2 * KT * GROUPS * i)
                nc.gpsimd.tensor_copy(vpad[:, :, :, 0:HD].rearrange("p k h d -> p (k h) d"),
                                      v_all[:, bass.ds(i * KT, KT), :].rearrange("p k (h d) -> p (k h) d", d=HD)) \
                    .then_inc(v_ready, 1)

        @block.tensor
        def _(pe):
            def scores(i, g, n):
                k = GROUPS * i + g
                h, t = g * GROUP + n // QT, n % QT
                if n == 0:
                    pe.wait_ge(stacks[g], START + (i + 1) * 16 * LOADS)
                if n == 1:
                    wait(pe, turn_read, k)
                else:
                    wait(pe, least_ready, U * k + n - 1)
                nc.tensor.matmul(s_ps[n % 2][:, :], qs[0:LEAST_AT, h, t * P:(t + 1) * P], ks[0:LEAST_AT, h, :],
                                 start=True, stop=True).then_inc(scores_ready, 1)

            def turn_least(i, g):
                pe.wait_ge(least_ready, START + U * (GROUPS * i + g + 1))
                nc.tensor.transpose(s_ps[1][0:U, 0:P], least[:, g % 2, :], core.ident[:, :]) \
                    .then_inc(least_turned, 1)

            def turned(i, g, n):
                k = GROUPS * i + g
                h, t = g * GROUP + n % GROUP, n // GROUP
                if n == 0:
                    pe.wait_ge(least_placed[g % 2], START + 16 * LEAST_ROWS * (2 * i + g // 2 + 1))
                if n % 2 == 0:
                    wait(pe, probs_ready, U // 2 * k + n // 2 - 1)
                out = t_ps[n // 2 % 2]
                last = nc.tensor.matmul(out[:, n % 2, :], ks[0:ROWS, h, t * P:(t + 1) * P], qs[0:ROWS, h, :],
                                        start=True, stop=bias is None)
                if bias is not None:
                    for r in range(3):
                        last = nc.tensor.matmul(out[:, n % 2, t * P:(t + 1) * P], M["slopes_diag"][:, r, h, :],
                                                M["steps"][:, :], start=False, stop=(r == 2))
                last.then_inc(turned_ready, 1)

            def sum_values(i, g, t, half):
                k = GROUPS * i + g
                queries = slice(half * N // 2, (half + 1) * N // 2)
                pe.wait_ge(probs_ready, START + U // 2 * k + 2 * t + 2)
                if t == 0 and half == 0:
                    pe.wait_ge(v_ready, START + i + 1)
                    wait(pe, values_kept, k)
                for h in range(GROUP):
                    pair = 2 * t + h // 2
                    last = nc.tensor.matmul(o_ps[h * VPAD:(h + 1) * VPAD, queries], vpad[:, t, g * GROUP + h, :],
                                            probs[:, pair % 4, h % 2, queries],
                                            start=(t == 0 and half == 0), stop=(t == KT - 1 and half == 1))
                last.then_inc(values_ready, 1)

            def tail(i, use):
                wait(pe, tail_read, TAIL * i + use)
                if use < QT:
                    if use == 0:
                        pe.wait_ge(values_kept, START + GROUPS * (i + 1))
                    for g in range(GROUPS):
                        last = nc.tensor.transpose(tail_ps[:, g * P:(g + 1) * P], values[:, g, use * P:(use + 1) * P],
                                                   core.ident[:, :])
                elif use == QT:
                    for t in range(QT):
                        last = nc.tensor.transpose(tail_ps[:, t * P:(t + 1) * P], heads[:, t, :], core.ident[:, :])
                else:
                    last = nc.tensor.matmul(tail_ps[:, :], wproj[:, :], headsT[:, :], start=True, stop=True)
                last.then_inc(tail_written, 1)

            def steps(i):
                for g in range(GROUPS):
                    for n in range(U):
                        if has_scores(i):
                            scores(i, g, n)
                        if has_turned(i, g):
                            turned(*before(i, g, 2), n)
                        if n == 0 and has_turned(i, g, 1):
                            turn_least(*before(i, g, 1))
                        if n in (1, 3) and has_turned(i, g, 3):
                            sum_values(*before(i, g, 3), KT - 1, n // 2)
                        if n % 2 == 1 and n >= 5 and has_turned(i, g):
                            sum_values(*before(i, g, 2), *divmod((n - 5) // 2, 2))
                        if g == 2 and n in (6, 9, 12, 15) and has_turned(i, 0, 1):
                            tail(i - 1, (n - 6) // 3)
                        if g == 3 and n in (3, 8) and has_turned(i, 0, 1):
                            tail(i - 1, QT + n // 8)

            run(pe, steps)

        @block.scalar
        def _(act):
            def exps(i, g, j):
                k = GROUPS * i + g
                wait(act, values_ready, 2 * (KT * k + j // 2 - 1))
                act.wait_ge(turned_ready, START + U * k + 2 * j + 2)
                nc.scalar.activation(probs[:, j % 4, :, :], t_ps[j % 2][:, :, :], ACT.Exp,
                                     scale=-1.0).then_inc(probs_ready, 1)

            def keep_values(i, g):
                k = GROUPS * i + g
                if g == 0:
                    wait(act, tail_written, TAIL * (i - 1) + QT)
                act.wait_ge(values_ready, START + 2 * KT * (k + 1))
                nc.scalar.activation(values[:, g, :], o_ps[:, :], ACT.Copy).then_inc(values_kept, 1)

            def steps(i):
                for g in range(GROUPS):
                    for j in range(U // 2):
                        if has_turned(i, g):
                            exps(*before(i, g, 2), j)
                        if j == 1 and has_turned(i, g, 3):
                            keep_values(*before(i, g, 3))
                        if g == 3 and j == 2 and has_turned(i, 0, 1):
                            act.wait_ge(tail_written, START + TAIL * (i - 1) + QT + 1)
                            nc.scalar.activation(headsT[:, :], tail_ps[:, :], ACT.Copy).then_inc(tail_read, 1)

            run(act, steps)

        @block.vector
        def _(dve):
            def least_of(i, g, n):
                k = GROUPS * i + g
                h, t = g * GROUP + n // QT, n % QT
                dve.wait_ge(scores_ready, START + U * k + n + 1)
                src = s_ps[n % 2][:, :]
                if bias is not None:
                    nc.vector.memset(spacer[:, n:n + 1], 0.0)
                    at = (QT - 1 - t) * P
                    nc.vector.tensor_tensor_reduce(
                        out=biased[:, n % 2, :], in0=src, in1=bias[:, h, at:at + N], scale=1.0, scalar=3.0e38,
                        op0=ALU.add, op1=ALU.min, accum_out=least[:, g % 2, n:n + 1]).then_inc(least_ready, 1)
                else:
                    nc.vector.tensor_reduce(least[:, g % 2, n:n + 1], src, axis=AX.X,
                                            op=ALU.min).then_inc(least_ready, 1)

            def split_least(i, g, n):
                k = GROUPS * i + g
                src = s_ps[1][0:U, 0:P]
                part = [least_parts[:, g % 2, r, :] for r in range(LEAST_ROWS)]
                if n == 0:
                    dve.wait_ge(least_turned, START + k + 1)
                    nc.vector.tensor_copy(part[0], src).then_inc(split_step, 1)
                if n == 1:
                    dve.wait_ge(split_step, START + 2 * k + 1)
                    nc.vector.tensor_tensor(least_rest[:, :], src, part[0], ALU.subtract).then_inc(turn_read, 1)
                if n == 2:
                    dve.wait_ge(turn_read, START + k + 1)
                    nc.vector.tensor_copy(part[1], least_rest[:, :]).then_inc(split_step, 1)
                if n == 3:
                    dve.wait_ge(split_step, START + 2 * k + 2)
                    nc.vector.tensor_tensor(part[2], least_rest[:, :], part[1], ALU.subtract).then_inc(least_split, 1)

            def normalise(i, t):
                src = tail_ps[:, :].rearrange("p (h d) -> p h d", d=VPAD)
                dve.wait_ge(tail_written, START + TAIL * i + t + 1)
                nc.vector.reciprocal(inverse[:, t % 2, :], src[:, :, HD]).then_inc(inverse_ready, 1)
                dve.wait_ge(inverse_ready, START + QT * i + t + 1)
                nc.vector.tensor_tensor(heads[:, t, :].rearrange("p (h d) -> p h d", d=HD), src[:, :, 0:HD],
                                        spread(inverse[:, t % 2, :], HD), ALU.mult).then_inc(tail_read, 1)

            def add(i):
                dve.wait_ge(tail_written, START + TAIL * (i + 1))
                nc.vector.scalar_tensor_tensor(out=xT[:, cols(i)], in0=tail_ps[:, :], scalar=bproj[:, 0:1],
                                               in1=xT[:, cols(i)], op0=ALU.add, op1=ALU.add).then_inc(tail_read, 1)

            def steps(i):
                for g in range(GROUPS):
                    for n in range(U):
                        if has_scores(i):
                            least_of(i, g, n)
                        if n < 2 and has_turned(i, g, 1):
                            for step in ((0, 1, 2), (3,))[n]:
                                split_least(*before(i, g, 1), step)
                        if has_turned(i, 0, 1):
                            if g == 2 and n in (8, 11, 14):
                                normalise(i - 1, (n - 8) // 3)
                            if g == 3 and n == 1:
                                normalise(i - 1, QT - 1)
                            if g == 3 and n == 11:
                                add(i - 1)

            run(dve, steps)


HID = 512
HT = HID // P


def gated_mlp_stage(core, A, xT):
    nc = core.nc
    w_loaded = core.sem("f0_w_loaded")
    hidden_loaded = core.sem("f0_hidden_loaded")
    up_ready = core.sem("f0_up")
    silu_ready = core.sem("f0_silu")
    gated_ready = core.sem("f0_gated")
    hid1_ready = core.sem("f0_hid1")
    gelu1_ready = core.sem("f0_gelu1")
    hid2_ready = core.sem("f0_hid2")
    gelu2_ready = core.sem("f0_gelu2")
    out_ready = core.sem("f0_out")
    added = core.sem("f0_added")
    with ExitStack() as mem:
        w12 = core.sb(mem, "f0_w12", [C, 2, HID])
        wh = core.sb(mem, "f0_wh", [P, 2, HT, HID])
        w3 = core.sb(mem, "f0_w3", [P, HT, C])
        scales = core.sb(mem, "f0_scales", [P, 4 * HT + 1])

        def load_weights(sp):
            sp.dma_start(w12[:, :, :], A["f0_w12"]).then_inc(w_loaded, 16)
            sp.dma_start(scales[:, :], A["f0_scales"]).then_inc(w_loaded, 16)
            sp.dma_start(wh[:, :, :, :], A["f0_wh"]).then_inc(hidden_loaded, 16)
            sp.dma_start(w3[:, :, :], A["f0_w3"]).then_inc(hidden_loaded, 16)

        layernorm_stage(core, xT, "f0_ln", prefetch=load_weights)
        silu = core.sb(mem, "f0_silu_sb", [P, 2, N])
        gated = core.sb(mem, "f0_gated_sb", [P, HT, N])
        hid1 = core.sb(mem, "f0_hid1_sb", [P, HT, N])
        hid2 = core.sb(mem, "f0_hid2_sb", [P, HT, N])
        up_ps = [core.ps(mem, f"f0_up_ps{n}", [P, N]) for n in range(4)]
        hid_ps = [core.ps(mem, f"f0_hid_ps{n}", [P, N]) for n in range(HT)]
        block = mem.enter_context(core.block())

        def scale(n, m=0):
            return scales[:, n * HT + m:n * HT + m + 1]

        @block.tensor
        def _(pe):
            def up(i):
                for m in range(HT):
                    pe.wait_ge(gated_ready, START + HT * i + max(m - 1, 0))
                    for n in range(2):
                        last = nc.tensor.matmul(up_ps[2 * (m % 2) + n][:, :], w12[:, n, m * P:(m + 1) * P],
                                                xT[:, cols(i)], start=True, stop=True)
                    last.then_inc(up_ready, 1)

            def hidden(layer, src, ready):
                for m in range(HT):
                    for k in range(HT):
                        last = nc.tensor.matmul(hid_ps[m][:, :], wh[:, layer, k, m * P:(m + 1) * P], src[:, k, :],
                                                start=(k == 0), stop=(k == HT - 1))
                    last.then_inc(ready, 1)

            def first(i):
                pe.wait_ge(gated_ready, START + HT * (i + 1))
                pe.wait_ge(added, START + i)
                hidden(0, gated, hid1_ready)

            def second_and_out(i):
                pe.wait_ge(gelu1_ready, START + HT * (i + 1))
                hidden(1, hid1, hid2_ready)
                pe.wait_ge(gelu2_ready, START + HT * (i + 1))
                for k in range(HT):
                    last = nc.tensor.matmul(hid_ps[0][:, :], w3[:, k, :], hid2[:, k, :],
                                            start=(k == 0), stop=(k == HT - 1))
                last.then_inc(out_ready, 1)

            pe.wait_ge(w_loaded, START + 32)
            up(0)
            pe.wait_ge(hidden_loaded, START + 32)
            with pe.Fori(0, B - 1) as i:
                first(i)
                up(i + 1)
                second_and_out(i)
            first(B - 1)
            second_and_out(B - 1)

        @block.scalar
        def _(act):
            def silus(i):
                for m in range(HT):
                    act.wait_ge(up_ready, START + HT * i + m + 1)
                    act.wait_ge(gated_ready, START + HT * i + max(m - 1, 0))
                    nc.scalar.activation(silu[:, m % 2, :], up_ps[2 * (m % 2)][:, :], ACT.Silu,
                                         scale=scale(0, m)).then_inc(silu_ready, 1)

            def gelu1(i):
                act.wait_ge(hid2_ready, START + HT * i)
                for m in range(HT):
                    act.wait_ge(hid1_ready, START + HT * i + m + 1)
                    nc.scalar.activation(hid1[:, m, :], hid_ps[m][:, :], ACT.Gelu,
                                         scale=scale(2, m)).then_inc(gelu1_ready, 1)

            def gelu2(i):
                act.wait_ge(out_ready, START + i)
                for m in range(HT):
                    act.wait_ge(hid2_ready, START + HT * i + m + 1)
                    nc.scalar.activation(hid2[:, m, :], hid_ps[m][:, :], ACT.Gelu,
                                         scale=scale(3, m)).then_inc(gelu2_ready, 1)

            act.wait_ge(w_loaded, START + 32)
            silus(0)
            with act.Fori(0, B - 1) as i:
                gelu1(i)
                silus(i + 1)
                gelu2(i)
            gelu1(B - 1)
            gelu2(B - 1)

        @block.vector
        def _(dve):
            def gate(i):
                for m in range(HT):
                    dve.wait_ge(silu_ready, START + HT * i + m + 1)
                    if m == 0:
                        dve.wait_ge(hid1_ready, START + HT * i)
                    nc.vector.scalar_tensor_tensor(out=gated[:, m, :], in0=up_ps[2 * (m % 2) + 1][:, :],
                                                   scalar=scale(1, m), in1=silu[:, m % 2, :], op0=ALU.mult,
                                                   op1=ALU.mult).then_inc(gated_ready, 1)

            def add(i):
                dve.wait_ge(out_ready, START + i + 1)
                nc.vector.scalar_tensor_tensor(out=xT[:, cols(i)], in0=hid_ps[0][:, :], scalar=scale(4),
                                               in1=xT[:, cols(i)], op0=ALU.mult, op1=ALU.add).then_inc(added, 1)

            gate(0)
            with dve.Fori(0, B - 1) as i:
                gate(i + 1)
                add(i)
            add(B - 1)


BRANCHES = 2
STATES = 16
DT_RANK = 64
BC = 2 * STATES
STEPS = BRANCHES * STATES


def ssm_stage(core, A, xT):
    nc = core.nc
    with ExitStack() as mem:
        xn = core.sb(mem, "s_xn", [C, T])
        delta = core.sb(mem, "s_delta", [C, BRANCHES, T])
        du = core.sb(mem, "s_du", [C, BRANCHES, T])
        ud = core.sb(mem, "s_ud", [C, T])
        z = core.sb(mem, "s_z", [C, T])
        bc_parts = core.sb(mem, "s_bc_parts", [3 * BC, BRANCHES, T], BF16)
        decay = core.sb(mem, "s_decay", [C, STATES])
        select = core.sb(mem, "s_select", [3 * BC, BC, P], BF16)
        wide = core.sb(mem, "s_wide", [C, 3, C])
        wdr = core.sb(mem, "s_wdr", [C, DT_RANK])
        wbc = core.sb(mem, "s_wbc", [C, 3 * BC])
        wdt = core.sb(mem, "s_wdt", [BRANCHES * DT_RANK, C])
        cst = core.sb(mem, "s_cst", [C, 7])
        alog = core.sb(mem, "s_alog", [C, STATES])
        loaded = core.sem("s_loaded")

        def load_weights(sp):
            for dst, name in ((wide[:, :, :], "wide"), (wdr[:, :], "wdr"), (wbc[:, :], "wbc"), (wdt[:, :], "wdt"),
                              (cst[:, :], "cst"), (alog[:, :], "alog"), (select[:, :, :], "select")):
                sp.dma_start(dst, A[f"s_{name}"]).then_inc(loaded, 16)

        layernorm_stage(core, xT, "s_first_ln", prefetch=load_weights)
        layernorm_stage(core, xT, "s_ln", out=xn)
        ssm_prepare(core, wide, wdr, wbc, wdt, cst, alog, loaded, xn, delta, du, ud, z, bc_parts, decay)
        ssm_scan(core, xT, delta, du, ud, z, bc_parts, decay, select)


def ssm_prepare(core, wide, wdr, wbc, wdt, cst, alog, loaded, xn, delta, du, ud, z, bc_parts, decay):
    nc = core.nc
    affine_ready = core.sem("s_affine")
    xp_ps_ready = core.sem("s_xp_ps")
    xp_ready = core.sem("s_xp")
    z_ready = core.sem("s_z_ready")
    v_ps_ready = core.sem("s_v_ps")
    v_kept = core.sem("s_v_kept")
    abs_ready = core.sem("s_abs")
    exp_ready = core.sem("s_exp")
    log_ready = core.sem("s_log")
    u_ready = core.sem("s_u")
    rank_ps_ready = core.sem("s_rank_ps")
    rank_ready = core.sem("s_rank")
    bc_ps_ready = core.sem("s_bc_ps")
    high_ready = core.sem("s_high")
    left_ready = core.sem("s_left")
    middle_ready = core.sem("s_middle")
    exp_a_ready = core.sem("s_exp_a")
    sum_ready = core.sem("s_usum")
    delta_ready = core.sem("s_delta_ready")
    with ExitStack() as mem:
        xp = core.sb(mem, "s_xp_sb", [C, T])
        v = core.sb(mem, "s_v", [C, BRANCHES, T])
        e = core.sb(mem, "s_e", [C, BRANCHES, T])
        u = core.sb(mem, "s_u_sb", [C, BRANCHES, T])
        rank = core.sb(mem, "s_rank_sb", [BRANCHES * DT_RANK, T])
        left = core.sb(mem, "s_left_sb", [3 * BC, BRANCHES, T])
        middle = core.sb(mem, "s_middle_sb", [3 * BC, BRANCHES, T], BF16)
        ps = [core.ps(mem, f"s_ps{n}", [P, T]) for n in range(2)]
        block = mem.enter_context(core.block())
        LOADS = 7

        @block.tensor
        def _(pe):
            def product(out, lhsT, rhs, ready):
                for i in range(B):
                    last = nc.tensor.matmul(out[:, cols(i)], lhsT, rhs[:, cols(i)], start=True, stop=True)
                last.then_inc(ready, 1)

            pe.wait_ge(loaded, START + 16 * LOADS)
            pe.wait_ge(affine_ready, START + 1)
            product(ps[0], wide[:, 0, :], xn, xp_ps_ready)
            pe.wait_ge(xp_ready, START + 1)
            product(ps[1], wide[:, 1, :], xp, v_ps_ready)
            pe.wait_ge(z_ready, START + 1)
            product(ps[0], wide[:, 2, :], xp, v_ps_ready)
            for r in range(BRANCHES):
                pe.wait_ge(u_ready, START + r + 1)
                product(ps[1][r * DT_RANK:(r + 1) * DT_RANK, :], wdr[:, :], u[:, r, :], rank_ps_ready)
            product(ps[0][0:3 * BC, :], wbc[:, :], u[:, 0, :], bc_ps_ready)
            pe.wait_ge(rank_ready, START + 1)
            product(ps[1][0:3 * BC, :], wbc[:, :], u[:, 1, :], bc_ps_ready)
            for r in range(BRANCHES):
                pe.wait_ge(left_ready, START + r + 1)
                rows = slice(r * DT_RANK, (r + 1) * DT_RANK)
                product(ps[r], wdt[rows, :], rank[rows, :], v_ps_ready)

        @block.scalar
        def _(act):
            act.wait_ge(loaded, START + 16 * LOADS)
            nc.scalar.activation(decay[:, :], alog[:, :], ACT.Exp).then_inc(exp_a_ready, 1)
            act.wait_ge(xp_ps_ready, START + 1)
            nc.scalar.activation(xp[:, :], ps[0][:, :], ACT.Identity, bias=cst[:, 2:3]).then_inc(xp_ready, 1)
            nc.scalar.activation(z[:, :], ps[0][:, :], ACT.Silu, bias=cst[:, 2:3]).then_inc(z_ready, 1)

            def softplus_terms(n):
                for r in range(BRANCHES):
                    src = ps[1 - r] if n == 0 else ps[r]
                    bias = cst[:, 3 + r:4 + r] if n == 0 else cst[:, 5:6]
                    act.wait_ge(v_ps_ready, START + 2 * n + r + 1)
                    if n == 1:
                        act.wait_ge(u_ready, START + BRANCHES)
                    nc.scalar.activation(v[:, r, :], src[:, :], ACT.Identity, bias=bias).then_inc(v_kept, 1)
                    nc.scalar.activation(e[:, r, :], src[:, :], ACT.Abs, bias=bias).then_inc(abs_ready, 1)
                act.wait_ge(abs_ready, START + 2 * n + 2)
                nc.scalar.activation(e[:, :, :], e[:, :, :], ACT.Exp, scale=-1.0).then_inc(exp_ready, 1)
                act.wait_ge(exp_ready, START + n + 1)
                for r in range(BRANCHES):
                    nc.scalar.activation(e[:, r, :], e[:, r, :], ACT.Ln, bias=core.one[:, 0:1]).then_inc(log_ready, 1)

            softplus_terms(0)
            act.wait_ge(rank_ps_ready, START + 2)
            nc.scalar.activation(rank[:, :], ps[1][:, :], ACT.Copy).then_inc(rank_ready, 1)
            softplus_terms(1)

        @block.vector
        def _(dve):
            dve.wait_ge(loaded, START + 16 * LOADS)
            nc.vector.tensor_scalar(xn[:, :], xn[:, :], cst[:, 0:1], cst[:, 1:2], ALU.mult,
                                    ALU.add).then_inc(affine_ready, 1)
            dve.wait_ge(exp_a_ready, START + 1)
            nc.vector.tensor_scalar(decay[:, :], decay[:, :], -1.0, None, ALU.mult)
            for r in range(BRANCHES):
                dve.wait_ge(log_ready, START + r + 1)
                nc.vector.scalar_tensor_tensor(out=u[:, r, :], in0=v[:, r, :], scalar=0.0, in1=e[:, r, :],
                                               op0=ALU.max, op1=ALU.add).then_inc(u_ready, 1)
            for r in range(BRANCHES):
                dve.wait_ge(bc_ps_ready, START + r + 1)
                nc.vector.tensor_copy(bc_parts[:, r, :], ps[r][0:3 * BC, :]).then_inc(high_ready, 1)
                dve.wait_ge(high_ready, START + r + 1)
                nc.vector.tensor_tensor(left[:, r, :], ps[r][0:3 * BC, :], bc_parts[:, r, :],
                                        ALU.subtract).then_inc(left_ready, 1)
            for r in range(BRANCHES):
                dve.wait_ge(left_ready, START + r + 1)
                nc.vector.tensor_copy(middle[:, r, :], left[:, r, :]).then_inc(middle_ready, 1)
                dve.wait_ge(middle_ready, START + r + 1)
                nc.vector.tensor_copy(bc_parts[BC:2 * BC, r, :], middle[BC:2 * BC, r, :])
                nc.vector.tensor_tensor(bc_parts[2 * BC:3 * BC, r, :], left[2 * BC:3 * BC, r, :],
                                        middle[2 * BC:3 * BC, r, :], ALU.subtract)
            for r in range(BRANCHES):
                dve.wait_ge(log_ready, START + BRANCHES + r + 1)
                nc.vector.scalar_tensor_tensor(out=delta[:, r, :], in0=v[:, r, :], scalar=0.0, in1=e[:, r, :],
                                               op0=ALU.max, op1=ALU.add).then_inc(delta_ready, 1)
                dve.wait_ge(delta_ready, START + r + 1)
                nc.vector.tensor_tensor(du[:, r, :], delta[:, r, :], u[:, r, :], ALU.mult)

        @block.gpsimd
        def _(pool):
            pool.wait_ge(u_ready, START + BRANCHES)
            nc.gpsimd.tensor_tensor(ud[:, :], u[:, 0, :], u[:, 1, :], ALU.add).then_inc(sum_ready, 1)
            pool.wait_ge(sum_ready, START + 1)
            nc.gpsimd.tensor_scalar(ud[:, :], ud[:, :], cst[:, 6:7], None, ALU.mult)


def ssm_scan(core, xT, delta, du, ud, z, bc_parts, decay, select):
    nc = core.nc
    RING, C_RING, B_RING = 4, 4, 3
    decay_ready = core.sem("s_decay_ready")
    b_ready = core.sem("s_b_ps")
    c_ready = core.sem("s_c_ps")
    b_kept = core.sem("s_b_kept")
    du_kept = core.sem("s_du_kept")
    input_ready = core.sem("s_input")
    scanned = core.sem("s_scanned")
    read_out = core.sem("s_read_out")
    summed = core.sem("s_summed")
    y_ready = core.sem("s_y")
    gate_ready = core.sem("s_gate")
    finished = core.sem("s_finished")
    with ExitStack() as mem:
        dA = core.sb(mem, "s_dA", [C, RING, N])
        du_b = core.sb(mem, "s_du_b", [C, BRANCHES, N])
        bs = core.sb(mem, "s_bs", [C, RING, N])
        dbu = core.sb(mem, "s_dbu", [C, RING, N])
        h = core.sb(mem, "s_h", [C, RING, N])
        hc = core.sb(mem, "s_hc", [C, RING, N])
        y = core.sb(mem, "s_ysb", [C, N])
        b_ps = [core.ps(mem, f"s_b_ps{n}", [C, N]) for n in range(B_RING)]
        c_ps = [core.ps(mem, f"s_c_ps{n}", [C, N]) for n in range(C_RING)]
        y_ps = core.ps(mem, "s_y_ps", [C, N])
        block = mem.enter_context(core.block())

        @block.tensor
        def _(pe):
            with pe.Fori(0, B) as i:
                for s in range(STEPS + RING):
                    if s < STEPS:
                        r, n = divmod(s, STATES)
                        pe.wait_ge(b_kept, START + i * STEPS + max(s - B_RING + 1, 0))
                        nc.tensor.matmul(b_ps[s % B_RING][:, :], select[:, n, :], bc_parts[:, r, cols(i)],
                                         start=True, stop=True).then_inc(b_ready, 1)
                        pe.wait_ge(read_out, START + i * STEPS + max(s - C_RING + 1, 0))
                        nc.tensor.matmul(c_ps[s % C_RING][:, :], select[:, STATES + n, :], bc_parts[:, r, cols(i)],
                                         start=True, stop=True).then_inc(c_ready, 1)
                    d = s - RING
                    if d >= 0:
                        if d == 0:
                            pe.wait_ge(gate_ready, START + i)
                        pe.wait_ge(read_out, START + i * STEPS + d + 1)
                        nc.tensor.matmul(y_ps[:, :], core.ident[:, :], hc[:, d % RING, :], start=(d == 0),
                                         stop=(d == STEPS - 1)).then_inc(summed, 1)

        @block.scalar
        def _(act):
            with act.Fori(0, B) as i:
                for s in range(STEPS):
                    r, n = divmod(s, STATES)
                    act.wait_ge(scanned, START + i * STEPS + max(s - RING + 1, 0))
                    act.wait_ge(b_ready, START + i * STEPS + s + 1)
                    act.wait_ge(input_ready, START + i * STEPS + max(s - RING + 1, 0))
                    nc.scalar.activation(bs[:, s % RING, :], b_ps[s % B_RING][:, :], ACT.Copy).then_inc(b_kept, 1)
                    if s == 0:
                        nc.scalar.activation(du_b[:, :, :], du[:, :, cols(i)], ACT.Copy).then_inc(du_kept, 1)
                    nc.scalar.activation(dA[:, s % RING, :], delta[:, r, cols(i)], ACT.Exp,
                                         scale=decay[:, n:n + 1]).then_inc(decay_ready, 1)

        @block.gpsimd
        def _(pool):
            with pool.Fori(0, B) as i:
                for s in range(STEPS):
                    r = s // STATES
                    if s == 0:
                        pool.wait_ge(du_kept, START + i + 1)
                    pool.wait_ge(b_kept, START + i * STEPS + s + 1)
                    pool.wait_ge(scanned, START + i * STEPS + max(s - RING + 1, 0))
                    nc.gpsimd.tensor_tensor(dbu[:, s % RING, :], du_b[:, r, :], bs[:, s % RING, :],
                                            ALU.mult).then_inc(input_ready, 1)

        @block.vector
        def _(dve):
            with dve.Fori(0, B) as i:
                for s in range(STEPS + 1):
                    if s < STEPS:
                        dve.wait_ge(decay_ready, START + i * STEPS + s + 1)
                        dve.wait_ge(input_ready, START + i * STEPS + s + 1)
                        dve.wait_ge(read_out, START + i * STEPS + max(s - RING + 1, 0))
                        nc.vector.tensor_tensor_scan(h[:, s % RING, :], dA[:, s % RING, :], dbu[:, s % RING, :], 0.0,
                                                     ALU.mult, ALU.add).then_inc(scanned, 1)
                    d = s - 1
                    if d >= 0:
                        dve.wait_ge(scanned, START + i * STEPS + d + 1)
                        dve.wait_ge(c_ready, START + i * STEPS + d + 1)
                        dve.wait_ge(summed, START + i * STEPS + max(d - RING + 1, 0))
                        nc.vector.tensor_tensor(hc[:, d % RING, :], c_ps[d % C_RING][:, :], h[:, d % RING, :],
                                                ALU.mult).then_inc(read_out, 1)
                dve.wait_ge(summed, START + (i + 1) * STEPS)
                dve.wait_ge(finished, START + i)
                nc.vector.tensor_tensor(y[:, :], y_ps[:, :], ud[:, cols(i)], ALU.add).then_inc(gate_ready, 1)
                dve.wait_ge(gate_ready, START + i + 1)
                nc.vector.tensor_tensor(y[:, :], y[:, :], z[:, cols(i)], ALU.mult).then_inc(y_ready, 1)
                dve.wait_ge(y_ready, START + i + 1)
                nc.vector.scalar_tensor_tensor(out=xT[:, cols(i)], in0=xT[:, cols(i)], scalar=2.0, in1=y[:, :],
                                               op0=ALU.mult, op1=ALU.add).then_inc(finished, 1)


EXPERTS = 8
MOE_HID = 256
MOE_HT = MOE_HID // P
CAPACITY = -(-T * 5 // (EXPERTS * 4))


def moe_stage(core, A, xT):
    with ExitStack() as mem:
        combine = core.sb(mem, "m_combine", [P, TT, EXPERTS])
        wr = core.sb(mem, "m_wr", [C, EXPERTS])
        tri = core.sb(mem, "m_tri", [P, P])
        ones = core.sb(mem, "m_ones", [P, P])
        iota = core.sb(mem, "m_iota", [P, TT, EXPERTS])
        wg = core.sb(mem, "m_wg", [C, MOE_HID])
        wd = core.sb(mem, "m_wd", [P, MOE_HT, EXPERTS * C])
        route_loaded = core.sem("m_loaded")
        w_loaded = core.sem("m_w_loaded")

        def load_weights(sp):
            for dst, name in ((wr[:, :], "m_wr"), (tri[:, :], "tri"), (ones[:, :], "ones"), (iota[:, :, :], "m_iota")):
                sp.dma_start(dst, A[name]).then_inc(route_loaded, 16)
            sp.dma_start(wg[:, :], A["m_wg"]).then_inc(w_loaded, 16)
            sp.dma_start(wd[:, :, :], A["m_wd"]).then_inc(w_loaded, 16)

        layernorm_stage(core, xT, "m_ln", prefetch=load_weights)
        moe_route(core, xT, wr, tri, ones, iota, route_loaded, combine)
        moe_experts(core, xT, wg, wd, w_loaded, combine)


def moe_route(core, xT, wr, tri, ones, iota, loaded, combine):
    nc = core.nc
    E = EXPERTS
    logits_ready = core.sem("m_logits")
    shifted_ready = core.sem("m_shifted")
    exp_ready = core.sem("m_exp")
    mask_ready = core.sem("m_mask")
    counts_ready = core.sem("m_counts")
    step = core.sem("m_step")
    with ExitStack() as mem:
        most = core.sb(mem, "m_most", [P, TT])
        shifted = core.sb(mem, "m_shifted_sb", [P, TT, E])
        top = core.sb(mem, "m_top", [P, TT, 8])
        index = core.sb(mem, "m_index", [P, TT, 8], U32)
        indexf = core.sb(mem, "m_indexf", [P, TT, 8])
        gates = core.sb(mem, "m_gates", [P, TT, E])
        mask = core.sb(mem, "m_mask_sb", [P, TT, E])
        second = core.sb(mem, "m_second", [P, TT, E])
        totals = core.sb(mem, "m_totals", [P, TT, E])
        place = core.sb(mem, "m_place", [P, TT, E])
        total = core.sb(mem, "m_total", [P, TT])
        logits_ps = core.ps(mem, "m_logits_ps", [P, TT, E])
        prefix_ps = core.ps(mem, "m_prefix_ps", [P, TT, E])
        totals_ps = core.ps(mem, "m_totals_ps", [P, TT, E])
        block = mem.enter_context(core.block())

        @block.tensor
        def _(pe):
            pe.wait_ge(loaded, START + 64)
            for t in range(TT):
                last = nc.tensor.matmul(logits_ps[:, t, :], xT[:, t * P:(t + 1) * P], wr[:, :], start=True, stop=True)
            last.then_inc(logits_ready, 1)
            pe.wait_ge(mask_ready, START + 1)
            nc.tensor.matmul(prefix_ps[:, :, :], tri[:, :], mask[:, :, :], start=True, stop=True)
            nc.tensor.matmul(totals_ps[:, :, :], ones[:, :], mask[:, :, :], start=True,
                             stop=True).then_inc(counts_ready, 1)

        @block.scalar
        def _(act):
            act.wait_ge(shifted_ready, START + 1)
            nc.scalar.activation(gates[:, :, :], shifted[:, :, :], ACT.Exp).then_inc(exp_ready, 1)

        @block.vector
        def _(dve):
            done = [0]

            def then(instruction):
                instruction.then_inc(step, 1)
                done[0] += 1
                dve.wait_ge(step, START + done[0])

            dve.wait_ge(loaded, START + 64)
            dve.wait_ge(logits_ready, START + 1)
            then(nc.vector.tensor_reduce(most[:, :], logits_ps[:, :, :], axis=AX.X, op=ALU.max))
            nc.vector.tensor_tensor(shifted[:, :, :], logits_ps[:, :, :], spread(most[:, :], E),
                                    ALU.subtract).then_inc(shifted_ready, 1)
            dve.wait_ge(exp_ready, START + 1)
            then(nc.vector.tensor_reduce(total[:, :], gates[:, :, :], axis=AX.X, op=ALU.add))
            then(nc.vector.reciprocal(total[:, :], total[:, :]))
            then(nc.vector.tensor_tensor(gates[:, :, :], gates[:, :, :], spread(total[:, :], E), ALU.mult))
            for t in range(TT):
                last = nc.vector.max(top[:, t, :], gates[:, t, :])
            then(last)
            for t in range(TT):
                last = nc.vector.max_index(index[:, t, :], top[:, t, :], gates[:, t, :])
            then(last)
            then(nc.vector.tensor_copy(indexf[:, :, :], index[:, :, :]))
            nc.vector.tensor_tensor(mask[:, :, :], iota[:, :, :], spread(indexf[:, :, 0], E), ALU.is_equal)
            then(nc.vector.tensor_tensor(second[:, :, :], iota[:, :, :], spread(indexf[:, :, 1], E), ALU.is_equal))
            nc.vector.tensor_tensor(mask[:, :, :], mask[:, :, :], second[:, :, :], ALU.add).then_inc(mask_ready, 1)
            dve.wait_ge(counts_ready, START + 1)
            then(nc.vector.tensor_copy(totals[:, :, :], totals_ps[:, :, :]))
            for e in range(E):
                last = nc.vector.tensor_tensor_scan(place[:, :, e], core.ones_row[:, 0:TT], totals[:, :, e], 0.0,
                                                    ALU.mult, ALU.add)
            then(last)
            then(nc.vector.tensor_tensor(place[:, :, :], place[:, :, :], totals[:, :, :], ALU.subtract))
            then(nc.vector.tensor_tensor(place[:, :, :], place[:, :, :], prefix_ps[:, :, :], ALU.add))
            then(nc.vector.scalar_tensor_tensor(out=place[:, :, :], in0=place[:, :, :], scalar=float(CAPACITY),
                                                in1=mask[:, :, :], op0=ALU.is_le, op1=ALU.mult))
            then(nc.vector.tensor_tensor(gates[:, :, :], gates[:, :, :], place[:, :, :], ALU.mult))
            then(nc.vector.tensor_reduce(total[:, :], gates[:, :, :], axis=AX.X, op=ALU.add))
            then(nc.vector.tensor_scalar(total[:, :], total[:, :], 1e-6, None, ALU.add))
            then(nc.vector.reciprocal(total[:, :], total[:, :]))
            nc.vector.tensor_tensor(combine[:, :, :], gates[:, :, :], spread(total[:, :], E), ALU.mult)


def moe_experts(core, xT, wg, wd, loaded, combine):
    nc = core.nc
    E = EXPERTS
    NT = N // P
    PER_BANK = 512 // C
    hid_ps_ready = core.sem("m_hid_ps")
    hid_ready = core.sem("m_hid")
    y_ready = core.sem("m_y")
    combined = core.sem("m_combine_kept")
    step = core.sem("m_mix_step")
    turned = core.sem("m_turned")
    added = core.sem("m_added")
    with ExitStack() as mem:
        hid = core.sb(mem, "m_hid_sb", [P, MOE_HT, N])
        weight = core.sb(mem, "m_weight", [P, NT, E])
        mixed = core.sb(mem, "m_mixed", [P, 2, C])
        hid_ps = [core.ps(mem, f"m_hid_ps{n}", [P, N]) for n in range(MOE_HT)]
        y_ps = [core.ps(mem, f"m_y_ps{n}", [P, E, C]) for n in range(2)]
        t_ps = core.ps(mem, "m_t_ps", [P, N])
        block = mem.enter_context(core.block())

        @block.tensor
        def _(pe):
            pe.wait_ge(loaded, START + 32)
            with pe.Fori(0, B) as i:
                pe.wait_ge(hid_ready, START + MOE_HT * i)
                for m in range(MOE_HT):
                    nc.tensor.matmul(hid_ps[m][:, :], wg[:, m * P:(m + 1) * P], xT[:, cols(i)],
                                     start=True, stop=True).then_inc(hid_ps_ready, 1)
                pe.wait_ge(hid_ready, START + MOE_HT * (i + 1))
                for t in range(NT + 1):
                    if t < NT:
                        pe.wait_ge(step, START + (i * NT + max(t - 1, 0)) * E)
                        for half in range(E // PER_BANK):
                            out = y_ps[t % 2][:, half * PER_BANK:(half + 1) * PER_BANK, :]
                            for k in range(MOE_HT):
                                last = nc.tensor.matmul(out, hid[:, k, t * P:(t + 1) * P],
                                                        wd[:, k, half * 512:(half + 1) * 512],
                                                        start=(k == 0), stop=(k == MOE_HT - 1))
                        last.then_inc(y_ready, 1)
                    if t == 1:
                        pe.wait_ge(added, START + i)
                    if t > 0:
                        pe.wait_ge(step, START + (i * NT + t) * E)
                        nc.tensor.transpose(t_ps[:, (t - 1) * P:t * P], mixed[:, (t - 1) % 2, :],
                                            core.ident[:, :]).then_inc(turned, 1)

        @block.scalar
        def _(act):
            with act.Fori(0, B) as i:
                act.wait_ge(y_ready, START + NT * i)
                for m in range(MOE_HT):
                    act.wait_ge(hid_ps_ready, START + MOE_HT * i + m + 1)
                    nc.scalar.activation(hid[:, m, :], hid_ps[m][:, :], ACT.Silu).then_inc(hid_ready, 1)

        @block.vector
        def _(dve):
            with dve.Fori(0, B) as i:
                nc.vector.tensor_copy(weight[:, :, :], combine[:, bass.ds(i * NT, NT), :]).then_inc(combined, 1)
                dve.wait_ge(combined, START + i + 1)
                for t in range(NT):
                    dve.wait_ge(y_ready, START + NT * i + t + 1)
                    dve.wait_ge(turned, START + NT * i + max(t - 1, 0))
                    for e in range(E):
                        if e:
                            dve.wait_ge(step, START + (i * NT + t) * E + e)
                            last = nc.vector.scalar_tensor_tensor(
                                out=mixed[:, t % 2, :], in0=y_ps[t % 2][:, e, :], scalar=weight[:, t, e:e + 1],
                                in1=mixed[:, t % 2, :], op0=ALU.mult, op1=ALU.add)
                        else:
                            last = nc.vector.tensor_scalar(mixed[:, t % 2, :], y_ps[t % 2][:, e, :],
                                                           weight[:, t, e:e + 1], None, ALU.mult)
                        last.then_inc(step, 1)
                dve.wait_ge(turned, START + NT * (i + 1))
                nc.vector.tensor_tensor(xT[:, cols(i)], t_ps[:, :], xT[:, cols(i)], ALU.add).then_inc(added, 1)


QH = 8
QK = 64
VD = C // QH
HTOK = N // QH
KEY_TILES = QH * HTOK // P
VPAD = 32
QUNITS = QH * KEY_TILES


def query_softmax_stage(core, A, xT):
    nc = core.nc
    loaded = core.sem("q_loaded")
    cleared = core.sem("q_cleared")
    x_copied = core.sem("q_x_copied")
    proj_ready = core.sem("q_proj")
    kept_act = core.sem("q_kept_act")
    kept_dve = core.sem("q_kept_dve")
    v_ps_ready = core.sem("q_v_ps")
    v_kept = core.sem("q_v_kept")
    scores_ready = core.sem("q_scores")
    most_ready = core.sem("q_most")
    probs_ready = core.sem("q_probs")
    inverse_ready = core.sem("q_inverse")
    scaled_ready = core.sem("q_scaled")
    out_ready = core.sem("q_out")
    out_kept = core.sem("q_out_kept")
    y_ready = core.sem("q_y")
    added = core.sem("q_added")
    RING = 3
    with ExitStack() as mem:
        wqk = core.sb(mem, "q_wqk", [C, 2, QH * QK])
        wv = core.sb(mem, "q_wv", [C, C])
        place = core.sb(mem, "q_place", [P, 2, C])

        def load_weights(sp):
            for dst, name in ((wqk[:, :, :], "q_wqk"), (wv[:, :], "q_wv"), (place[:, :, :], "q_place")):
                sp.dma_start(dst, A[name]).then_inc(loaded, 16)

        layernorm_stage(core, xT, "q_ln", prefetch=load_weights)
        xb = core.sb(mem, "q_xb", [C, N])
        xd = core.sb(mem, "q_xd", [C, QH, 2, HTOK])
        qk = core.sb(mem, "q_qk", [P, 2, QH, QH, HTOK])
        v = core.sb(mem, "q_v", [P, KEY_TILES, QH, VD])
        vs = core.sb(mem, "q_vs", [P, 2, KEY_TILES * QH, VPAD])
        most = core.sb(mem, "q_most_sb", [P, QUNITS])
        sums = core.sb(mem, "q_sums", [P, QUNITS])
        inverse = core.sb(mem, "q_inv", [P, QUNITS])
        probs = core.sb(mem, "q_probs_sb", [P, 2, KEY_TILES, N])
        outs = core.sb(mem, "q_outs", [P, 2, N])
        p_ps = core.ps(mem, "q_p_ps", [P, 2, N])
        s_ps = [core.ps(mem, f"q_s_ps{n}", [P, N]) for n in range(RING)]
        o_ps = core.ps(mem, "q_o_ps", [P, 2, N])
        y_ps = core.ps(mem, "q_y_ps", [P, N])
        block = mem.enter_context(core.block())
        PAIRS = QH // 2

        def by_head(ap):
            return ap.rearrange("p (h k) -> p h k", h=QH)

        @block.gpsimd
        def _(pool):
            nc.gpsimd.memset(vs[:, :, :, :], 0.0).then_inc(cleared, 1)
            pool.wait_ge(cleared, START + 1)
            nc.gpsimd.memset(qk[QK:P, :, :, :, :], 0.0).then_inc(cleared, 1)

        @block.tensor
        def _(pe):
            pe.wait_ge(loaded, START + 48)
            with pe.Fori(0, B) as i:
                pe.wait_ge(x_copied, START + 2 * i + 2)
                pe.wait_ge(v_kept, START + 2 * i)
                for n in range(2 * PAIRS):
                    if n >= 2:
                        pe.wait_ge(kept_act, START + 2 * PAIRS * i + n - 1)
                        pe.wait_ge(kept_dve, START + 2 * PAIRS * i + n - 1)
                    a, b = divmod(n, PAIRS)
                    nc.tensor.matmul(p_ps[:, n % 2, :], wqk[:, a, b * P:(b + 1) * P], xb[:, :],
                                     start=True, stop=True).then_inc(proj_ready, 1)
                pe.wait_ge(cleared, START + 2)
                pe.wait_ge(kept_act, START + 2 * PAIRS * (i + 1))
                pe.wait_ge(kept_dve, START + 2 * PAIRS * (i + 1))
                for h in range(QH):
                    last = nc.tensor.matmul(p_ps[:, h // 4, (h % 4) * P:(h % 4 + 1) * P],
                                            xd[:, h, :, :], wv[:, :], start=True, stop=True)
                last.then_inc(v_ps_ready, 1)

                def scores(u):
                    h, t = divmod(u, KEY_TILES)
                    pe.wait_ge(probs_ready, START + i * QUNITS + max(u - RING + 1, 0))
                    nc.tensor.matmul(s_ps[u % RING][:, :], qk[:, 1, h, 2 * t:2 * t + 2, :], qk[:, 0, h, :, :],
                                     start=True, stop=True).then_inc(scores_ready, 1)

                def outputs(h):
                    if h == 0:
                        pe.wait_ge(out_kept, START + 2 * i)
                    pe.wait_ge(scaled_ready, START + i * QH + h + 1)
                    tok = slice(h * HTOK, (h + 1) * HTOK)
                    for half in range(2):
                        for t in range(KEY_TILES):
                            for b in range(4):
                                j = half * 4 + b
                                last = nc.tensor.matmul(o_ps[b * VPAD:(b + 1) * VPAD, half, tok],
                                                        vs[:, h % 2, t * QH + j, :],
                                                        probs[:, h % 2, t, j * HTOK:(j + 1) * HTOK],
                                                        start=(t == 0), stop=(t == KEY_TILES - 1))
                    last.then_inc(out_ready, 1)

                for h in range(QH + 1):
                    if h < QH:
                        for t in range(KEY_TILES):
                            scores(h * KEY_TILES + t)
                    if h > 0:
                        outputs(h - 1)
                pe.wait_ge(out_kept, START + 2 * i + 2)
                pe.wait_ge(added, START + i)
                for g in range(2):
                    last = nc.tensor.matmul(y_ps[:, :], place[:, g, :], outs[:, g, :], start=(g == 0), stop=(g == 1))
                last.then_inc(y_ready, 1)

        @block.scalar
        def _(act):
            with act.Fori(0, B) as i:
                act.wait_ge(v_ps_ready, START + i)
                nc.scalar.activation(xb[:, :], xT[:, cols(i)], ACT.Copy).then_inc(x_copied, 1)
                act.wait_ge(out_ready, START + QH * i)
                for n in range(2 * PAIRS):
                    act.wait_ge(proj_ready, START + 2 * PAIRS * i + n + 1)
                    a, b = divmod(n, PAIRS)
                    nc.scalar.activation(qk[0:QK, a, :, 2 * b, :], by_head(p_ps[0:QK, n % 2, :]), ACT.Copy,
                                         scale=QK ** -0.5 if a == 0 else 1.0).then_inc(kept_act, 1)
                act.wait_ge(v_ps_ready, START + i + 1)
                nc.scalar.activation(v[0:QK, :, :, :].rearrange("p t h d -> p t h d"),
                                     p_ps[0:QK, :, :].rearrange("p a (b t s d) -> p t s (a b) d", b=4, s=2,
                                                                d=VD)[:, :, 0, :, :],
                                     ACT.Copy).then_inc(v_kept, 1)
                for u in range(QUNITS):
                    act.wait_ge(most_ready, START + i * QUNITS + u + 1)
                    h, t = divmod(u, KEY_TILES)
                    if t == 0:
                        act.wait_ge(out_ready, START + QH * i + max(h - 1, 0))
                    nc.scalar.activation(probs[:, h % 2, t, :], s_ps[u % RING][:, :], ACT.Exp,
                                         bias=most[:, u:u + 1], accum_out=sums[:, u:u + 1]).then_inc(probs_ready, 1)
                for g in range(2):
                    if g == 0:
                        act.wait_ge(out_ready, START + QH * (i + 1))
                        act.wait_ge(y_ready, START + i)
                    nc.scalar.activation(outs[:, g, :], o_ps[:, g, :], ACT.Copy).then_inc(out_kept, 1)

        @block.vector
        def _(dve):
            dve.wait_ge(cleared, START + 1)
            with dve.Fori(0, B) as i:
                dve.wait_ge(x_copied, START + 2 * i + 1)
                for a in range(2):
                    last = nc.vector.tensor_copy(xd[:, :, a, :], xb[:, :].rearrange("p (h k) -> p h k", h=QH))
                last.then_inc(x_copied, 1)
                for n in range(2 * PAIRS):
                    dve.wait_ge(proj_ready, START + 2 * PAIRS * i + n + 1)
                    a, b = divmod(n, PAIRS)
                    nc.vector.tensor_scalar(qk[0:QK, a, :, 2 * b + 1, :], by_head(p_ps[QK:P, n % 2, :]),
                                            QK ** -0.5 if a == 0 else 1.0, None, ALU.mult).then_inc(kept_dve, 1)
                dve.wait_ge(v_ps_ready, START + i + 1)
                nc.vector.tensor_copy(v[QK:P, :, :, :],
                                      p_ps[QK:P, :, :].rearrange("p a (b t s d) -> p t s (a b) d", b=4, s=2,
                                                                 d=VD)[:, :, 1, :, :]).then_inc(v_kept, 1)
                dve.wait_ge(v_kept, START + 2 * i + 2)
                for h in range(QH):
                    for t in range(KEY_TILES):
                        u = h * KEY_TILES + t
                        dve.wait_ge(scores_ready, START + i * QUNITS + u + 1)
                        nc.vector.tensor_reduce(most[:, u:u + 1], s_ps[u % RING][:, :], axis=AX.X, op=ALU.max,
                                                negate=True).then_inc(most_ready, 1)
                    dve.wait_ge(probs_ready, START + i * QUNITS + (h + 1) * KEY_TILES)
                    us = slice(h * KEY_TILES, (h + 1) * KEY_TILES)
                    nc.vector.reciprocal(inverse[:, us], sums[:, us]).then_inc(inverse_ready, 1)
                    dve.wait_ge(inverse_ready, START + i * QH + h + 1)
                    dve.wait_ge(out_ready, START + i * QH + max(h - 1, 0))
                    nc.vector.tensor_tensor(
                        vs[:, h % 2, :, 0:VD].rearrange("p (t h) d -> p t h d", h=QH), v[:, :, :, :],
                        inverse[:, us].unsqueeze(2).unsqueeze(3).to_broadcast([P, KEY_TILES, QH, VD]),
                        ALU.mult).then_inc(scaled_ready, 1)
                dve.wait_ge(y_ready, START + i + 1)
                nc.vector.tensor_tensor(xT[:, cols(i)], y_ps[:, :], xT[:, cols(i)], ALU.add).then_inc(added, 1)


X_EXPERTS = 32
X_CAP = T * 5 // (4 * X_EXPERTS)
X_GROUPS = 16
X_INTER = 256
X_ROUTER = C // 2
PART_ROWS = 32
STAT_ROWS = 3 * PART_ROWS
X_SLOTS = X_EXPERTS * X_CAP
X_ST = X_SLOTS // P
ADAPTER_SCALE = 0.05
TAKEN = -2.0


def sparse_stage(core, A, xT):
    nc = core.nc
    slots_dram = nc.dram_tensor("x_slots", (X_SLOTS, C), F32).ap()
    results_dram = nc.dram_tensor("x_results", (X_SLOTS + 1, C), F32).ap()
    w_loaded = core.sem("x_w_loaded")
    dispatched = core.sem("x_dispatched", software_dma=True)
    with ExitStack() as mem:
        weight = core.sb(mem, "x_weight", [P, 2, TT])
        slot = core.sb(mem, "x_slot", [P, 2, TT], I32)
        wu = core.sb(mem, "x_wu", [C, X_EXPERTS, 2 * X_INTER])
        wd = core.sb(mem, "x_wd", [P, X_EXPERTS, X_INTER // P, C])
        wau = core.sb(mem, "x_wau", [C, X_GROUPS, 2 * P])
        wad = core.sb(mem, "x_wad", [P, X_GROUPS, C])

        r1x = core.sb(mem, "x_r1x", [C, X_ROUTER])
        r1s = core.sb(mem, "x_r1s", [STAT_ROWS, X_ROUTER])
        pick = core.sb(mem, "x_pick", [C, 4, 2])
        r1b = core.sb(mem, "x_r1b", [X_ROUTER, 1])
        r_loaded = core.sem("x_r_loaded")

        def load_weights(sp):
            for dst, name in ((r1x[:, :], "x_r1x"), (r1s[:, :], "x_r1s"), (r1b[:, :], "x_r1b"),
                              (pick[:, :, :], "x_pick")):
                sp.dma_start(dst, A[name]).then_inc(r_loaded, 16)
            for dst, name in ((wu[:, :, :], "x_wu"), (wau[:, :, :], "x_wau"), (wd[:, :, :, :], "x_wd"),
                              (wad[:, :, :], "x_wad")):
                half = dst.shape[1] // 2
                for n in range(2):
                    sp.dma_start(dst[:, n * half:(n + 1) * half], A[name][:, n * half:(n + 1) * half]) \
                        .then_inc(w_loaded, 16)

        layernorm_stage(core, xT, "x_ln", prefetch=load_weights)
        with ExitStack() as routing:
            xt = core.sb(routing, "x_xt", [P, TT, C])
            hT = core.sb(routing, "x_hT", [X_ROUTER, T])
            sparse_stats(core, xT, r1x, r1s, r1b, pick, r_loaded, xt, hT)
            sparse_route(core, A, xt, hT, weight, slot, slots_dram, results_dram, dispatched)
        sparse_experts(core, slots_dram, results_dram, wu, wd, wau, wad, w_loaded)
        sparse_combine(core, xT, results_dram, weight, slot)


def sparse_stats(core, xT, r1x, r1s, r1b, pick, loaded, xt, hT):
    nc = core.nc
    turned = core.sem("x_turned")
    kept = core.sem("x_kept")
    mean_ready = core.sem("x_mean")
    centred_ready = core.sem("x_centred")
    squares_ready = core.sem("x_squares")
    sizes_ready = core.sem("x_sizes_ready")
    small_ready = core.sem("x_small")
    sums_ready = core.sem("x_sums_ready")
    ends_ready = core.sem("x_ends")
    ends_turned = core.sem("x_ends_turned")
    cleared = core.sem("x_stats_cleared")
    stats_kept = core.sem("x_stats_kept")
    hidden_ready = core.sem("x_hidden")
    with ExitStack() as mem:
        statsT = core.sb(mem, "x_statsT", [STAT_ROWS, T])
        centred = core.sb(mem, "x_xc", [C, T])
        squares = core.sb(mem, "x_sq", [C, 2, T])
        sizes = core.sb(mem, "x_sizes", [C, T])
        small = core.sb(mem, "x_small_sb", [C, T])
        ends = core.sb(mem, "x_ends_sb", [P, TT, 2])
        a_ps = core.ps(mem, "x_a_ps", [P, T])
        b_ps = core.ps(mem, "x_b_ps", [P, T])
        block = mem.enter_context(core.block())
        ENDS, ROOTS, MEANS = (slice(n * PART_ROWS, n * PART_ROWS + 2) for n in range(3))

        @block.tensor
        def _(pe):
            for i in range(B):
                nc.tensor.matmul(b_ps[:, cols(i)], core.avg[:, :], xT[:, cols(i)], start=True,
                                 stop=True).then_inc(mean_ready, 1)
            for t in range(TT):
                nc.tensor.transpose(a_ps[:, t * P:(t + 1) * P], xT[:, t * P:(t + 1) * P],
                                    core.ident[:, :]).then_inc(turned, 1)
            pe.wait_ge(loaded, START + 64)
            pe.wait_ge(centred_ready, START + B)
            for rows, first, second, ready, value in (
                    (MEANS, (0, xT[:, :]), (1, small[:, :]), small_ready, 1),
                    (ROOTS, (2, squares[:, 1, :]), (3, squares[:, 0, :]), squares_ready, 2)):
                pe.wait_ge(ready, START + value)
                for i in range(B):
                    for (n, src), start in ((first, True), (second, False)):
                        last = nc.tensor.matmul(b_ps[rows, cols(i)], pick[:, n, :], src[:, cols(i)],
                                                start=start, stop=not start)
                last.then_inc(sums_ready, 1)
            pe.wait_ge(ends_ready, START + 1)
            for t in range(TT):
                last = nc.tensor.transpose(b_ps[ENDS, t * P:(t + 1) * P], ends[:, t, :], core.ident[:, :])
            last.then_inc(ends_turned, 1)
            pe.wait_ge(kept, START + B)
            pe.wait_ge(stats_kept, START + 3)
            for i in range(B):
                nc.tensor.matmul(a_ps[0:X_ROUTER, cols(i)], r1x[:, :], xT[:, cols(i)], start=True, stop=False)
                nc.tensor.matmul(a_ps[0:X_ROUTER, cols(i)], r1s[:, :], statsT[:, cols(i)], start=False,
                                 stop=True).then_inc(hidden_ready, 1)

        @block.scalar
        def _(act):
            nc.scalar.activation(sizes[:, :], xT[:, :], ACT.Abs).then_inc(sizes_ready, 1)
            nc.scalar.activation(squares[:, 1, :], xT[:, :], ACT.Square).then_inc(squares_ready, 1)
            for i in range(B):
                act.wait_ge(turned, START + (TT // B) * (i + 1))
                nc.scalar.activation(xt[:, 4 * i:4 * i + 4, :].rearrange("p t c -> p (t c)"), a_ps[:, cols(i)],
                                     ACT.Copy).then_inc(kept, 1)
            act.wait_ge(centred_ready, START + B)
            nc.scalar.activation(squares[:, 0, :], centred[:, :], ACT.Square).then_inc(squares_ready, 1)
            act.wait_ge(cleared, START + 1)
            act.wait_ge(sums_ready, START + 1)
            nc.scalar.activation(statsT[MEANS, :], b_ps[MEANS, :], ACT.Copy).then_inc(stats_kept, 1)
            act.wait_ge(sums_ready, START + 2)
            nc.scalar.activation(statsT[ROOTS, :], b_ps[ROOTS, :], ACT.Sqrt).then_inc(stats_kept, 1)
            act.wait_ge(loaded, START + 64)
            act.wait_ge(hidden_ready, START + B)
            nc.scalar.activation(hT[:, :], a_ps[0:X_ROUTER, :], ACT.Gelu, bias=r1b[:, 0:1])

        @block.gpsimd
        def _(pool):
            nc.gpsimd.memset(statsT[:, :], 0.0).then_inc(cleared, 1)

        @block.vector
        def _(dve):
            for i in range(B):
                dve.wait_ge(mean_ready, START + i + 1)
                nc.vector.tensor_tensor(centred[:, cols(i)], xT[:, cols(i)], b_ps[:, cols(i)],
                                        ALU.subtract).then_inc(centred_ready, 1)
            dve.wait_ge(sizes_ready, START + 1)
            nc.vector.tensor_scalar(small[:, :], sizes[:, :], 1e-6, None, ALU.is_lt).then_inc(small_ready, 1)
            dve.wait_ge(kept, START + B)
            nc.vector.tensor_reduce(ends[:, :, 0], xt[:, :, :], axis=AX.X, op=ALU.min)
            nc.vector.tensor_reduce(ends[:, :, 1], xt[:, :, :], axis=AX.X, op=ALU.max).then_inc(ends_ready, 1)
            dve.wait_ge(cleared, START + 1)
            dve.wait_ge(ends_turned, START + 1)
            nc.vector.tensor_copy(statsT[ENDS, :], b_ps[ENDS, :]).then_inc(stats_kept, 1)


def sparse_route(core, A, xt, hT, weight, slot, slots_dram, results_dram, dispatched):
    nc = core.nc
    E = X_EXPERTS
    loaded = core.sem("x_r2_loaded")
    zeroed = core.sem("x_zeroed")
    slots_zeroed = core.sem("x_slots_zeroed")
    logits_ready = core.sem("x_logits")
    shifted_ready = core.sem("x_shifted")
    exp_ready = core.sem("x_exp")
    score_ready = core.sem("x_score")
    score_turned = core.sem("x_score_turned")
    place_ready = core.sem("x_place")
    place_turned = core.sem("x_place_turned")
    slot_ready = core.sem("x_slot_ready")
    step = core.sem("x_step")
    with ExitStack() as mem:
        r2 = core.sb(mem, "x_r2", [X_ROUTER, E])
        iota = core.sb(mem, "x_iota", [P, TT, E])
        base = core.sb(mem, "x_base", [E, 1])
        zero = core.sb(mem, "x_zero", [P, C])
        most = core.sb(mem, "x_most", [P, TT])
        probs = core.sb(mem, "x_probs", [P, TT, E])
        top = core.sb(mem, "x_top", [P, TT, 8])
        index = core.sb(mem, "x_index", [P, TT, 8], U32)
        indexf = core.sb(mem, "x_indexf", [P, TT, 8])
        hits = core.sb(mem, "x_hits", [P, 2, TT, E])
        score = core.sb(mem, "x_score_sb", [P, TT, E])
        mask = core.sb(mem, "x_mask", [P, TT, E])
        total = core.sb(mem, "x_total", [P, TT])
        slotf = core.sb(mem, "x_slotf", [P, 2, TT])
        isnt = core.sb(mem, "x_isnt", [P, 2, TT])
        scoreT = core.sb(mem, "x_scoreT", [E, T])
        work = core.sb(mem, "x_work", [E, T])
        best = core.sb(mem, "x_best", [E, 8])
        placeT = core.sb(mem, "x_placeT", [E, T])
        logits_ps = core.ps(mem, "x_logits_ps", [P, TT, E])
        turn_ps = core.ps(mem, "x_turn_ps", [E, T])
        place_ps = core.ps(mem, "x_place_ps", [P, TT, E])
        block = mem.enter_context(core.block())

        @block.sync
        def _(sp):
            for dst, name in ((r2[:, :], "x_r2"), (iota[:, :, :], "x_iota"), (base[:, :], "x_base")):
                sp.dma_start(dst, A[name]).then_inc(loaded, 16)
            sp.wait_ge(zeroed, START + 1)
            for n in range(X_ST):
                sp.dma_start(slots_dram[n * P:(n + 1) * P, :], zero[:, :]).then_inc(slots_zeroed, 16)
            sp.dma_start(results_dram[X_SLOTS:X_SLOTS + 1, :], zero[0:1, :]).then_inc(slots_zeroed, 16)
            sp.wait_ge(slots_zeroed, START + 16 * (X_ST + 1))

        @block.tensor
        def _(pe):
            pe.wait_ge(loaded, START + 48)
            for t in range(TT):
                last = nc.tensor.matmul(logits_ps[:, t, :], hT[:, t * P:(t + 1) * P], r2[:, :], start=True, stop=True)
            last.then_inc(logits_ready, 1)
            pe.wait_ge(score_ready, START + 1)
            for t in range(TT):
                last = nc.tensor.transpose(turn_ps[:, t * P:(t + 1) * P], score[:, t, :], core.ident[:, :])
            last.then_inc(score_turned, 1)
            pe.wait_ge(place_ready, START + 1)
            for t in range(TT):
                last = nc.tensor.transpose(place_ps[:, t, :], placeT[:, t * P:(t + 1) * P], core.ident[0:E, 0:E])
            last.then_inc(place_turned, 1)

        @block.scalar
        def _(act):
            act.wait_ge(shifted_ready, START + 1)
            nc.scalar.activation(probs[:, :, :], score[:, :, :], ACT.Exp).then_inc(exp_ready, 1)

        @block.gpsimd
        def _(pool):
            nc.gpsimd.memset(zero[:, :], 0.0).then_inc(zeroed, 1)
            pool.wait_ge(slots_zeroed, START + 16 * (X_ST + 1))
            pool.wait_ge(slot_ready, START + 1)
            for k in range(2):
                for t in range(TT):
                    nc.gpsimd.indirect_dma_start(
                        out=slots_dram, out_offset=bass.IndirectOffsetOnAxis(ap=slot[:, k, t:t + 1], axis=0),
                        in_=xt[:, t, :], in_offset=None, bounds_check=X_SLOTS - 1,
                        oob_is_err=False).then_inc(dispatched, 16)
            pool.wait_ge(dispatched, 16 * 2 * TT)

        @block.vector
        def _(dve):
            done = [0]

            def then(instruction):
                instruction.then_inc(step, 1)
                done[0] += 1
                dve.wait_ge(step, START + done[0])

            dve.wait_ge(loaded, START + 48)
            dve.wait_ge(logits_ready, START + 1)
            then(nc.vector.tensor_reduce(most[:, :], logits_ps[:, :, :], axis=AX.X, op=ALU.max))
            nc.vector.tensor_tensor(score[:, :, :], logits_ps[:, :, :], spread(most[:, :], E),
                                    ALU.subtract).then_inc(shifted_ready, 1)
            dve.wait_ge(exp_ready, START + 1)
            then(nc.vector.tensor_reduce(total[:, :], probs[:, :, :], axis=AX.X, op=ALU.add))
            then(nc.vector.reciprocal(total[:, :], total[:, :]))
            then(nc.vector.tensor_tensor(probs[:, :, :], probs[:, :, :], spread(total[:, :], E), ALU.mult))
            for t in range(TT):
                last = nc.vector.max(top[:, t, :], probs[:, t, :])
            then(last)
            for t in range(TT):
                last = nc.vector.max_index(index[:, t, :], top[:, t, :], probs[:, t, :])
            then(last)
            then(nc.vector.tensor_copy(indexf[:, :, :], index[:, :, :]))
            for k in range(2):
                last = nc.vector.tensor_tensor(hits[:, k, :, :], iota[:, :, :], spread(indexf[:, :, k], E),
                                               ALU.is_equal)
            then(last)
            then(nc.vector.tensor_tensor(mask[:, :, :], hits[:, 0, :, :], hits[:, 1, :, :], ALU.add))
            then(nc.vector.tensor_tensor(score[:, :, :], probs[:, :, :], mask[:, :, :], ALU.mult))
            then(nc.vector.tensor_scalar(mask[:, :, :], mask[:, :, :], -1.0, None, ALU.add))
            nc.vector.tensor_tensor(score[:, :, :], score[:, :, :], mask[:, :, :], ALU.add).then_inc(score_ready, 1)
            then(nc.vector.tensor_tensor(total[:, :], top[:, :, 0], top[:, :, 1], ALU.add))
            then(nc.vector.reciprocal(total[:, :], total[:, :]))
            for k in range(2):
                last = nc.vector.tensor_tensor(weight[:, k, :], top[:, :, k], total[:, :], ALU.mult)
            then(last)
            dve.wait_ge(score_turned, START + 1)
            nc.vector.tensor_copy(scoreT[:, :], turn_ps[:, :])
            then(nc.vector.tensor_copy(work[:, :], turn_ps[:, :]))
            for n in range(X_CAP // 8):
                then(nc.vector.max(best[:, :], work[:, :]))
                then(nc.vector.match_replace(work[:, :], best[:, :], work[:, :], TAKEN))
            then(nc.vector.tensor_scalar(work[:, :], work[:, :], TAKEN, None, ALU.is_equal))
            then(nc.vector.scalar_tensor_tensor(out=work[:, :], in0=scoreT[:, :], scalar=0.0, in1=work[:, :],
                                                op0=ALU.is_ge, op1=ALU.mult))
            then(nc.vector.tensor_tensor_scan(placeT[:, :], core.ones_row[0:E, 0:1].to_broadcast([E, T]), work[:, :], 0.0,
                                              ALU.mult, ALU.add))
            nc.vector.scalar_tensor_tensor(out=placeT[:, :], in0=placeT[:, :], scalar=base[:, 0:1], in1=work[:, :],
                                           op0=ALU.add, op1=ALU.mult).then_inc(place_ready, 1)
            dve.wait_ge(place_turned, START + 1)
            for k in range(2):
                then(nc.vector.tensor_tensor(score[:, :, :], hits[:, k, :, :], place_ps[:, :, :], ALU.mult))
                then(nc.vector.tensor_reduce(slotf[:, k, :], score[:, :, :], axis=AX.X, op=ALU.add))
            then(nc.vector.tensor_scalar(isnt[:, :, :], slotf[:, :, :], 0.0, float(X_SLOTS + 1), ALU.is_equal,
                                         ALU.mult))
            then(nc.vector.scalar_tensor_tensor(out=slotf[:, :, :], in0=slotf[:, :, :], scalar=-1.0,
                                                in1=isnt[:, :, :], op0=ALU.add, op1=ALU.add))
            nc.vector.tensor_copy(slot[:, :, :], slotf[:, :, :]).then_inc(slot_ready, 1)


def sparse_experts(core, slots_dram, results_dram, wu, wd, wau, wad, w_loaded):
    nc = core.nc
    E, G, CAP = X_EXPERTS, X_GROUPS, X_CAP
    JT = X_INTER // P
    PAIR = E // G
    slots_loaded = core.sem("x_slots_loaded")
    turned = core.sem("x_slots_turned")
    kept = core.sem("x_slots_kept")
    up_ready = core.sem("x_up")
    silu_ready = core.sem("x_silu")
    act_ready = core.sem("x_act")
    down_ready = core.sem("x_down")
    result_ready = core.sem("x_result")
    stored = core.sem("x_stored")
    UNITS_G = PAIR + 1
    with ExitStack() as mem:
        slots = core.sb(mem, "x_slots_sb", [P, X_ST, C])
        slotsT = core.sb(mem, "x_slotsT", [C, X_SLOTS])
        silu = core.sb(mem, "x_silu_sb", [P, 2, PAIR * CAP])
        hid = core.sb(mem, "x_hid_sb", [P, 2 * UNITS_G, PAIR * CAP])
        results = core.sb(mem, "x_results_sb", [CAP, E, C])
        t_ps = [core.ps(mem, f"x_t_ps{n}", [P, N]) for n in range(2)]
        up_ps = [core.ps(mem, f"x_up_ps{n}", [P, N]) for n in range(3)]
        d_ps = [core.ps(mem, f"x_d_ps{n}", [P, C]) for n in range(2)]
        block = mem.enter_context(core.block())
        TURNS = X_ST // 4

        def units():
            for g in range(G):
                yield g, None
                for e in range(PAIR * g, PAIR * (g + 1)):
                    yield g, e

        UNITS_ALL = list(units())

        @block.sync
        def _(sp):
            for n in range(TURNS):
                sp.dma_start(slots[:, 4 * n:4 * n + 4, :],
                             slots_dram[4 * n * P:4 * (n + 1) * P, :].rearrange("(t p) c -> p t c", p=P)) \
                    .then_inc(slots_loaded, 16)
                sp.wait_ge(slots_loaded, START + 16 * (n + 1))
            for n in range(4):
                some = slice(n * E // 4, (n + 1) * E // 4)
                sp.wait_ge(result_ready, START + (n + 1) * E // 4)
                sp.dma_start(results_dram[n * X_SLOTS // 4:(n + 1) * X_SLOTS // 4, :]
                             .rearrange("(e s) c -> s e c", s=CAP), results[:, some, :]).then_inc(stored, 16)
            sp.wait_ge(stored, START + 64)

        @block.tensor
        def _(pe):
            for n in range(TURNS):
                pe.wait_ge(slots_loaded, START + 16 * (n + 1))
                if n >= 2:
                    pe.wait_ge(kept, START + n - 1)
                for t in range(4):
                    last = nc.tensor.transpose(t_ps[n % 2][:, t * P:(t + 1) * P], slots[:, 4 * n + t, :],
                                               core.ident[:, :])
                last.then_inc(turned, 1)
            pe.wait_ge(kept, START + TURNS)
            pe.wait_ge(w_loaded, START + 16 * 8)

            def up(n):
                g, e = UNITS_ALL[n]
                if n >= 3:
                    pe.wait_ge(act_ready, START + n - 2)
                first, count = (PAIR * g, PAIR) if e is None else (e, 1)
                src = slotsT[:, first * CAP:(first + count) * CAP]
                tiles = 2 if e is None else 2 * JT
                for m in range(tiles):
                    w = wau[:, g, m * P:(m + 1) * P] if e is None else wu[:, e, m * P:(m + 1) * P]
                    last = nc.tensor.matmul(up_ps[n % 3][:, m * count * CAP:(m + 1) * count * CAP], w, src,
                                            start=True, stop=True)
                last.then_inc(up_ready, 1)

            def down(n):
                g, e = UNITS_ALL[n]
                if e is None:
                    return
                pe.wait_ge(act_ready, START + n + 1)
                if e >= 2:
                    pe.wait_ge(result_ready, START + e - 1)
                here = n % (2 * UNITS_G)
                adapter = (n - 1 - e % PAIR) % (2 * UNITS_G)
                for j in range(JT):
                    nc.tensor.matmul(d_ps[e % 2][0:CAP, :], hid[:, here, j * CAP:(j + 1) * CAP], wd[:, e, j, :],
                                     start=(j == 0), stop=False)
                nc.tensor.matmul(d_ps[e % 2][0:CAP, :], hid[:, adapter, e % PAIR * CAP:(e % PAIR + 1) * CAP],
                                 wad[:, g, :], start=False, stop=True).then_inc(down_ready, 1)

            for n in range(len(UNITS_ALL) + 1):
                if n < len(UNITS_ALL):
                    up(n)
                if n:
                    down(n - 1)

        @block.scalar
        def _(act):
            for n, (g, e) in enumerate(UNITS_ALL):
                act.wait_ge(up_ready, START + n + 1)
                if n >= 2:
                    act.wait_ge(act_ready, START + n - 1)
                nc.scalar.activation(silu[:, n % 2, :], up_ps[n % 3][:, 0:PAIR * CAP], ACT.Silu).then_inc(silu_ready, 1)

        @block.vector
        def _(dve):
            for n in range(TURNS):
                dve.wait_ge(turned, START + n + 1)
                nc.vector.tensor_copy(slotsT[:, n * N:(n + 1) * N], t_ps[n % 2][:, :]).then_inc(kept, 1)

            def result(n):
                g, e = UNITS_ALL[n]
                if e is None:
                    return
                dve.wait_ge(down_ready, START + e + 1)
                nc.vector.tensor_copy(results[:, e, :], d_ps[e % 2][0:CAP, :]).then_inc(result_ready, 1)

            for n in range(len(UNITS_ALL) + 2):
                if n < len(UNITS_ALL):
                    g, e = UNITS_ALL[n]
                    dve.wait_ge(silu_ready, START + n + 1)
                    if n >= 2 * UNITS_G:
                        dve.wait_ge(down_ready, START + PAIR * (n // UNITS_G - 1))
                    nc.vector.scalar_tensor_tensor(
                        out=hid[:, n % (2 * UNITS_G), :], in0=up_ps[n % 3][:, PAIR * CAP:2 * PAIR * CAP],
                        scalar=ADAPTER_SCALE if e is None else 1.0, in1=silu[:, n % 2, :], op0=ALU.mult,
                        op1=ALU.mult).then_inc(act_ready, 1)
                if n >= 2:
                    result(n - 2)


def sparse_combine(core, xT, results_dram, weight, slot):
    nc = core.nc
    fetched = [core.sem(f"x_fetched{i}", software_dma=True) for i in range(B)]
    scaled = core.sem("x_scaled")
    mixed = core.sem("x_mixed")
    turned = core.sem("x_mixed_turned")
    CT = TT // B
    with ExitStack() as mem:
        got = core.sb(mem, "x_got", [P, 2, TT, C])
        y = core.sb(mem, "x_y", [P, TT, C])
        y_ps = core.ps(mem, "x_y_ps", [C, T])
        block = mem.enter_context(core.block())

        @block.gpsimd
        def _(pool):
            for t in range(TT):
                for k in range(2):
                    nc.gpsimd.indirect_dma_start(
                        out=got[:, k, t, :], out_offset=None, in_=results_dram,
                        in_offset=bass.IndirectOffsetOnAxis(ap=slot[:, k, t:t + 1], axis=0)).then_inc(fetched[t // CT], 16)

        @block.vector
        def _(dve):
            for t in range(TT):
                dve.wait_ge(fetched[t // CT], 16 * 2 * CT)
                nc.vector.tensor_scalar(y[:, t, :], got[:, 0, t, :], weight[:, 0, t:t + 1], None,
                                        ALU.mult).then_inc(scaled, 1)
            for t in range(TT):
                dve.wait_ge(scaled, START + t + 1)
                nc.vector.scalar_tensor_tensor(out=y[:, t, :], in0=got[:, 1, t, :], scalar=weight[:, 1, t:t + 1],
                                               in1=y[:, t, :], op0=ALU.mult, op1=ALU.add).then_inc(mixed, 1)
            for i in range(B):
                dve.wait_ge(turned, START + CT * (i + 1))
                nc.vector.tensor_tensor(xT[:, cols(i)], y_ps[:, cols(i)], xT[:, cols(i)], ALU.add)

        @block.tensor
        def _(pe):
            for t in range(TT):
                pe.wait_ge(mixed, START + t + 1)
                nc.tensor.transpose(y_ps[:, t * P:(t + 1) * P], y[:, t, :], core.ident[:, :]).then_inc(turned, 1)


CH_EXPERTS = 8
CH_HID = 512
CH_HT = CH_HID // P
CH_ALL = CH_EXPERTS + 1
CHOSEN = 2 * T
SEARCH_STEPS = 16
TRIES = 3
PART_AT = 32
GATE_ROWS = 3 * PART_AT


def choice_stage(core, A, xT):
    with ExitStack() as mem:
        M = {"gates": core.sb(mem, "c_gates", [GATE_ROWS, T]),
             "gates_b": core.sb(mem, "c_gates_b", [GATE_ROWS, T], BF16),
             "w1": core.sb(mem, "c_w1", [C, CH_ALL, CH_HID]),
             "w2": core.sb(mem, "c_w2", [P, CH_ALL, CH_HT, C]),
             "b1": core.sb(mem, "c_b1", [P, CH_ALL, CH_HT]),
             "bs2": core.sb(mem, "c_bs2", [C, 1]),
             "kept": core.sb(mem, "c_kept", [C, T])}
        wr = core.sb(mem, "c_wr", [C, CH_EXPERTS])
        tri = core.sb(mem, "c_tri", [P, P])
        ones = core.sb(mem, "c_ones", [P, P])
        ones_b = core.sb(mem, "c_ones_b", [P, P], BF16)
        bits = core.sb(mem, "c_bits", [P, SEARCH_STEPS, TRIES], I32)
        unit = core.sb(mem, "c_unit", [P, SEARCH_STEPS])
        w_loaded = core.sem("c_w_loaded")
        loaded = core.sem("c_loaded")
        shared_loaded = core.sem("c_shared_loaded")
        w1, w2, b1, bs2, E = M["w1"], M["w2"], M["b1"], M["bs2"], CH_EXPERTS

        def load_weights(sp):
            for dst, name in ((wr[:, :], "c_wr"), (tri[:, :], "tri"), (ones[:, :], "ones"),
                              (ones_b[:, :], "c_ones_b"), (bits[:, :, :], "c_bits"), (unit[:, :], "c_unit")):
                sp.dma_start(dst, A[name]).then_inc(loaded, 16)
            for dst, src in ((w1[:, E, :], A["c_w1"][:, E]), (w2[:, E, :, :], A["c_w2"][:, E]),
                             (b1[:, :, :], A["c_b1"]), (bs2[:, :], A["c_bs2"])):
                sp.dma_start(dst, src).then_inc(shared_loaded, 16)
            sp.dma_start(w1[:, 0:E, :], A["c_w1"][:, 0:E]).then_inc(w_loaded, 16)
            sp.dma_start(w2[:, 0:E, :, :], A["c_w2"][:, 0:E]).then_inc(w_loaded, 16)

        layernorm_stage(core, xT, "c_ln", prefetch=load_weights)
        choice_route(core, xT, M, wr, tri, ones, ones_b, bits, unit, loaded, shared_loaded)
        choice_experts(core, A, xT, M, w_loaded)


def choice_route(core, xT, M, wr, tri, ones, ones_b, bits, unit, loaded, shared_loaded):
    nc = core.nc
    E = CH_EXPERTS
    gates, gates_b, w1, w2, b1, bs2, kept = (M[n] for n in ("gates", "gates_b", "w1", "w2", "b1", "bs2", "kept"))
    logits_ready = core.sem("c_logits")
    shifted_ready = core.sem("c_shifted")
    exp_ready = core.sem("c_exp")
    count_ready = core.sem("c_count")
    total_ready = core.sem("c_total")
    equal_ready = core.sem("c_equal")
    places_ready = core.sem("c_places")
    padded = core.sem("c_padded")
    gate_ready = core.sem("c_gate")
    gate_turned = core.sem("c_gate_turned")
    gates_copied = core.sem("c_gates_copied")
    step = core.sem("c_step")
    tried = core.sem("c_tried")
    passed = core.sem("c_passed")
    grown = core.sem("c_grown")
    threshold_ready = core.sem("c_threshold")
    up_ready = core.sem("c_shared_up")
    gelu_ready = core.sem("c_shared_gelu")
    down_ready = core.sem("c_shared_down")
    y_copied = core.sem("c_shared_copied")
    with ExitStack() as mem:
        most = core.sb(mem, "c_most", [P, TT])
        shifted = core.sb(mem, "c_shifted_sb", [P, TT, E])
        scores = core.sb(mem, "c_scores", [P, TT, E])
        total = core.sb(mem, "c_total_sb", [P, TT])
        above = core.sb(mem, "c_above", [P, TT, E])
        equal = core.sb(mem, "c_equal_sb", [P, TT, E])
        scratch = core.sb(mem, "c_scratch", [P, TRIES, TT * E])
        threshold = core.sb(mem, "c_threshold_sb", [P, 1], I32)
        trial = core.sb(mem, "c_trial", [P, TRIES], I32)
        growth = core.sb(mem, "c_growth", [P, 1], I32)
        count = core.sb(mem, "c_count_sb", [P, TRIES], BF16)
        is_enough = core.sb(mem, "c_is_enough", [P, TRIES])
        enough = core.sb(mem, "c_enough", [P, 1])
        places = core.sb(mem, "c_places_sb", [P, TT, E])
        totals = core.sb(mem, "c_totals", [P, TT, E])
        before = core.sb(mem, "c_before", [P, E])
        needed = core.sb(mem, "c_needed", [P, 1])
        high = core.sb(mem, "c_high", [P, TT, E], BF16)
        middle = core.sb(mem, "c_middle", [P, TT, E], BF16)
        gate_parts = core.sb(mem, "c_gate_parts", [P, TT, 3, PART_AT])
        hid = core.sb(mem, "c_shared_hid", [P, CH_HT, N])
        logits_ps = core.ps(mem, "c_logits_ps", [P, TT, E])
        total_ps = core.ps(mem, "c_total_ps", [P, TRIES])
        places_ps = core.ps(mem, "c_places_ps", [P, 2, TT, E])
        up_ps = [core.ps(mem, f"c_shared_up_ps{n}", [P, N]) for n in range(2)]
        y_ps = core.ps(mem, "c_shared_y_ps", [C, N])
        last_ps = core.ps(mem, "c_last_ps", [P, N])
        turn_ps = [*up_ps, y_ps, last_ps]
        block = mem.enter_context(core.block())

        def run(engine, body):
            body(0)
            with engine.Fori(1, B) as i:
                body(i)

        @block.tensor
        def _(pe):
            def count_all(s):
                pe.wait_ge(count_ready, START + s + 1)
                nc.tensor.matmul(total_ps[:, :], ones_b[:, :], count[:, :], start=True,
                                 stop=True).then_inc(total_ready, 1)

            def up(i, m):
                if not (isinstance(i, int) and CH_HT * i + m < 2):
                    pe.wait_ge(gelu_ready, START + CH_HT * i + m - 1)
                nc.tensor.matmul(up_ps[m % 2][:, :], w1[:, E, m * P:(m + 1) * P], xT[:, cols(i)],
                                 start=True, stop=True).then_inc(up_ready, 1)

            def down(i, m):
                pe.wait_ge(gelu_ready, START + CH_HT * i + m + 1)
                if m == 0 and not (isinstance(i, int) and i == 0):
                    pe.wait_ge(y_copied, START + i)
                nc.tensor.matmul(y_ps[:, :], w2[:, E, m, :], hid[:, m, :], start=(m == 0),
                                 stop=(m == CH_HT - 1)).then_inc(down_ready, 1)

            def chunk(i):
                for m in range(CH_HT):
                    count_all(CH_HT * i + m)
                    up(i, m)
                    if not isinstance(i, int):
                        down(i - 1, m)

            pe.wait_ge(loaded, START + 16 * 6)
            for t in range(TT):
                last = nc.tensor.matmul(logits_ps[:, t, :], xT[:, t * P:(t + 1) * P], wr[:, :], start=True, stop=True)
            last.then_inc(logits_ready, 1)
            pe.wait_ge(shared_loaded, START + 16 * 4)
            run(pe, chunk)
            count_all(SEARCH_STEPS)
            for m in range(CH_HT):
                down(B - 1, m)
            pe.wait_ge(equal_ready, START + 1)
            for n, summed in enumerate((tri, ones)):
                last = nc.tensor.matmul(places_ps[:, n, :, :], summed[:, :], equal[:, :, :], start=True, stop=True)
            last.then_inc(places_ready, 1)
            pe.wait_ge(gate_ready, START + 1)
            pe.wait_ge(y_copied, START + B)
            for t in range(TT):
                last = nc.tensor.transpose(turn_ps[t // 4][0:GATE_ROWS, t % 4 * P:(t % 4 + 1) * P],
                                           gate_parts[:, t, :, :], core.ident[:, :]).then_inc(gate_turned, 1)

        @block.scalar
        def _(act):
            def copy_y(i):
                act.wait_ge(down_ready, START + CH_HT * (i + 1))
                nc.scalar.activation(kept[:, cols(i)], y_ps[:, :], ACT.Copy).then_inc(y_copied, 1)

            def chunk(i):
                for m in range(CH_HT):
                    u = CH_HT * i + m
                    if not isinstance(i, int):
                        act.wait_ge(down_ready, START + u - CH_HT + 1)
                    act.wait_ge(up_ready, START + u + 1)
                    nc.scalar.activation(hid[:, m, :], up_ps[m % 2][:, :], ACT.Gelu_apprx_tanh,
                                         bias=b1[:, E, m:m + 1]).then_inc(gelu_ready, 1)
                if not isinstance(i, int):
                    copy_y(i - 1)

            act.wait_ge(shifted_ready, START + 1)
            nc.scalar.activation(scores[:, :, :], shifted[:, :, :], ACT.Exp).then_inc(exp_ready, 1)
            act.wait_ge(shared_loaded, START + 16 * 4)
            run(act, chunk)
            copy_y(B - 1)
            for i in range(B):
                act.wait_ge(gates_copied, START + i + 1)
                nc.scalar.activation(gates_b[:, cols(i)], gates[:, cols(i)], ACT.Copy)

        @block.gpsimd
        def _(pool):
            nc.gpsimd.memset(gate_parts[:, :, :, :], 0.0).then_inc(padded, 1)
            for i in range(B):
                pool.wait_ge(y_copied, START + i + 1)
                nc.gpsimd.tensor_tensor(kept[:, cols(i)], kept[:, cols(i)], xT[:, cols(i)], ALU.add)

        @block.vector
        def _(dve):
            done = [0]

            def then(instruction):
                instruction.then_inc(step, 1)
                done[0] += 1
                dve.wait_ge(step, START + done[0])

            dve.wait_ge(loaded, START + 16 * 6)
            dve.wait_ge(logits_ready, START + 1)
            then(nc.vector.tensor_reduce(most[:, :], logits_ps[:, :, :], axis=AX.X, op=ALU.max))
            nc.vector.tensor_tensor(shifted[:, :, :], logits_ps[:, :, :], spread(most[:, :], E),
                                    ALU.subtract).then_inc(shifted_ready, 1)
            nc.vector.memset(threshold[:, :], 0).then_inc(threshold_ready, 1)
            dve.wait_ge(exp_ready, START + 1)
            then(nc.vector.tensor_reduce(total[:, :], scores[:, :, :], axis=AX.X, op=ALU.add))
            then(nc.vector.reciprocal(total[:, :], total[:, :]))
            then(nc.vector.tensor_tensor(scores[:, :, :], scores[:, :, :], spread(total[:, :], E), ALU.mult))
            flat = scores[:, :, :].rearrange("p t e -> p (t e)")
            with dve.Fori(0, SEARCH_STEPS) as i:
                dve.wait_ge(threshold_ready, START + i + 1)
                nc.vector.tensor_tensor(trial[:, :], threshold[:, 0:1].to_broadcast([P, TRIES]),
                                        bits[:, bass.ds(i, 1), :].rearrange("p i n -> p (i n)"),
                                        ALU.bitwise_or).then_inc(tried, 1)
                dve.wait_ge(tried, START + i + 1)
                for n in range(TRIES):
                    last = nc.vector.tensor_scalar(scratch[:, n, :], flat, trial[:, n:n + 1].bitcast(F32), None,
                                                   ALU.is_ge, ALU.add, accum_out=count[:, n:n + 1])
                last.then_inc(count_ready, 1)
                dve.wait_ge(total_ready, START + i + 1)
                nc.vector.tensor_scalar(is_enough[:, :], total_ps[:, :], float(CHOSEN), None, ALU.is_ge, ALU.add,
                                        accum_out=enough[:, :]).then_inc(passed, 1)
                dve.wait_ge(passed, START + i + 1)
                nc.vector.tensor_scalar(growth[:, :], enough[:, :], unit[:, bass.ds(i, 1)], None,
                                        ALU.mult).then_inc(grown, 1)
                dve.wait_ge(grown, START + i + 1)
                nc.vector.tensor_tensor(threshold[:, :], threshold[:, :], growth[:, :],
                                        ALU.bitwise_or).then_inc(threshold_ready, 1)
            dve.wait_ge(threshold_ready, START + SEARCH_STEPS + 1)
            least = threshold[:, :].bitcast(F32)
            nc.vector.tensor_scalar(above[:, :, :].rearrange("p t e -> p (t e)"), flat, least, None, ALU.is_gt, ALU.add,
                                    accum_out=count[:, 0:1]).then_inc(count_ready, 1)
            nc.vector.tensor_scalar(equal[:, :, :], scores[:, :, :], least, None, ALU.is_equal).then_inc(equal_ready, 1)
            dve.wait_ge(total_ready, START + SEARCH_STEPS + 1)
            then(nc.vector.tensor_scalar(needed[:, :], total_ps[:, 0:1], -1.0, float(CHOSEN), ALU.mult, ALU.add))
            dve.wait_ge(places_ready, START + 1)
            then(nc.vector.tensor_copy(totals[:, :, :], places_ps[:, 1, :, :]))
            for e in range(E):
                last = nc.vector.tensor_tensor_scan(places[:, :, e], core.ones_row[:, 0:TT], totals[:, :, e], 0.0,
                                                    ALU.mult, ALU.add)
            then(last)
            then(nc.vector.tensor_tensor_scan(before[:, :], core.ones_row[:, 0:E], places[:, TT - 1, :], 0.0,
                                              ALU.mult, ALU.add))
            then(nc.vector.tensor_tensor(before[:, :], before[:, :], places[:, TT - 1, :], ALU.subtract))
            then(nc.vector.tensor_tensor(places[:, :, :], places[:, :, :], totals[:, :, :], ALU.subtract))
            then(nc.vector.tensor_tensor(places[:, :, :], places[:, :, :], places_ps[:, 0, :, :], ALU.add))
            then(nc.vector.tensor_tensor(places[:, :, :], places[:, :, :],
                                         before[:, :].unsqueeze(1).to_broadcast([P, TT, E]), ALU.add))
            then(nc.vector.scalar_tensor_tensor(out=places[:, :, :], in0=places[:, :, :], scalar=needed[:, 0:1],
                                                in1=equal[:, :, :], op0=ALU.is_le, op1=ALU.mult))
            then(nc.vector.tensor_tensor(above[:, :, :], above[:, :, :], places[:, :, :], ALU.add))
            then(nc.vector.tensor_tensor(scores[:, :, :], scores[:, :, :], above[:, :, :], ALU.mult))
            dve.wait_ge(padded, START + 1)
            then(nc.vector.tensor_copy(high[:, :, :], scores[:, :, :]))
            nc.vector.tensor_copy(gate_parts[:, :, 0, 0:E], high[:, :, :])
            then(nc.vector.tensor_tensor(scores[:, :, :], scores[:, :, :], high[:, :, :], ALU.subtract))
            then(nc.vector.tensor_copy(middle[:, :, :], scores[:, :, :]))
            nc.vector.tensor_copy(gate_parts[:, :, 1, 0:E], middle[:, :, :])
            nc.vector.tensor_tensor(gate_parts[:, :, 2, 0:E], scores[:, :, :], middle[:, :, :],
                                    ALU.subtract).then_inc(gate_ready, 1)
            for i in range(B):
                dve.wait_ge(gate_turned, START + TT // B * (i + 1))
                nc.vector.tensor_copy(gates[:, cols(i)], turn_ps[i][0:GATE_ROWS, :]).then_inc(gates_copied, 1)


def choice_experts(core, A, xT, M, w_loaded):
    nc = core.nc
    E = CH_EXPERTS
    gates, gates_b, w1, w2, b1, bs2, kept = (M[n] for n in ("gates", "gates_b", "w1", "w2", "b1", "bs2", "kept"))
    RING = 3
    PER = E * CH_HT
    loaded = core.sem("c_b_loaded")
    up_ready = core.sem("c_up")
    gelu_ready = core.sem("c_gelu")
    spread_ready = core.sem("c_spread")
    gated_ready = core.sem("c_gated")
    down_ready = core.sem("c_down")
    added = core.sem("c_added")
    with ExitStack() as mem:
        b2 = core.sb(mem, "c_b2", [GATE_ROWS, C])
        select = core.sb(mem, "c_select", [GATE_ROWS, E, P], BF16)
        hid = core.sb(mem, "c_hid", [P, 2, CH_HT, N])
        gated = core.sb(mem, "c_gated_sb", [P, 2, CH_HT, N])
        up_ps = [core.ps(mem, f"c_up_ps{n}", [P, N]) for n in range(RING)]
        g_ps = [core.ps(mem, f"c_g_ps{n}", [P, N]) for n in range(2)]
        y_ps = core.ps(mem, "c_y_ps", [C, N])
        block = mem.enter_context(core.block())

        @block.sync
        def _(sp):
            for dst, name in ((b2[:, :], "c_b2"), (select[:, :, :], "c_select")):
                sp.dma_start(dst, A[name]).then_inc(loaded, 16)

        @block.tensor
        def _(pe):
            pe.wait_ge(loaded, START + 32)
            pe.wait_ge(w_loaded, START + 32)
            with pe.Fori(0, B) as i:
                def up(e):
                    for m in range(CH_HT):
                        u = e * CH_HT + m
                        if m == CH_HT - 1:
                            pe.wait_ge(gated_ready, START + i * E + max(e - 1, 0))
                        pe.wait_ge(gelu_ready, START + i * PER + max(u - RING + 1, 0))
                        nc.tensor.matmul(up_ps[u % RING][:, :], w1[:, e, m * P:(m + 1) * P], xT[:, cols(i)],
                                         start=True, stop=True).then_inc(up_ready, 1)
                    nc.tensor.matmul(g_ps[e % 2][:, :], select[:, e, :], gates_b[:, cols(i)],
                                     start=True, stop=True).then_inc(spread_ready, 1)

                def down(e):
                    pe.wait_ge(gated_ready, START + i * E + e + 1)
                    if e == 0:
                        pe.wait_ge(added, START + i)
                    for k in range(CH_HT):
                        last = nc.tensor.matmul(y_ps[:, :], w2[:, e, k, :], gated[:, e % 2, k, :],
                                                start=(e == 0 and k == 0), stop=(e == E - 1 and k == CH_HT - 1))
                        if e == 0 and k == 0:
                            nc.tensor.matmul(y_ps[:, :], b2[:, :], gates[:, cols(i)], start=False, stop=False)
                    last.then_inc(down_ready, 1)

                for e in range(E + 1):
                    if e < E:
                        up(e)
                    if e:
                        down(e - 1)

        @block.scalar
        def _(act):
            with act.Fori(0, B) as i:
                for e in range(E):
                    for m in range(CH_HT):
                        u = e * CH_HT + m
                        if m == 0:
                            act.wait_ge(gated_ready, START + i * E + max(e - 1, 0))
                        act.wait_ge(up_ready, START + i * PER + u + 1)
                        nc.scalar.activation(hid[:, e % 2, m, :], up_ps[u % RING][:, :], ACT.Gelu_apprx_tanh,
                                             bias=b1[:, e, m:m + 1]).then_inc(gelu_ready, 1)

        @block.vector
        def _(dve):
            with dve.Fori(0, B) as i:
                for e in range(E):
                    dve.wait_ge(spread_ready, START + i * E + e + 1)
                    dve.wait_ge(down_ready, START + i * E + max(e - 1, 0))
                    dve.wait_ge(gelu_ready, START + i * PER + (e + 1) * CH_HT)
                    nc.vector.tensor_tensor(gated[:, e % 2, :, :], hid[:, e % 2, :, :],
                                            g_ps[e % 2][:, :].unsqueeze(1).to_broadcast([P, CH_HT, N]),
                                            ALU.mult).then_inc(gated_ready, 1)
                dve.wait_ge(down_ready, START + (i + 1) * E)
                nc.vector.scalar_tensor_tensor(out=xT[:, cols(i)], in0=y_ps[:, :], scalar=bs2[:, 0:1],
                                               in1=kept[:, cols(i)], op0=ALU.add, op1=ALU.add).then_inc(added, 1)


def rope_tables(angles, order):
    freq, sign = order
    theta = np.arange(N, dtype=np.float32)[None, :] * angles.astype(np.float32)[:, None]
    cos, sin = np.cos(theta)[freq], np.sin(theta)[freq] * np.array(sign, np.float32)[:, None]
    scale = np.float32(-(HD ** -0.5))
    one = np.stack([cos * scale, sin * scale, cos, sin], 1).astype(np.float32)
    return np.tile(one, (HEADS, 1, 1))


def lay_attention(tag, wq, wk, wv, wproj, turn, tables):
    order = (np.arange(HEADS)[:, None] * HD + np.array(turn)[None, :]).ravel()
    w = np.stack([wq.T, wq[order].T, wk.T, wk[order].T, wv.T], 1)
    return {f"{tag}_wqkv": w, f"{tag}_rope": tables, f"{tag}_wproj": wproj.T}




def lay_attention0(I):
    L = {}
    half = HD // 2
    qkv = I["L0_attn_qkv_w"]
    angles = 1.0 / np.power(np.float32(10000.0), np.arange(0, HD, 2, dtype=np.float32) / np.float32(HD))
    L |= lay_attention("a0", qkv[:C], qkv[C:2 * C], qkv[2 * C:], I["L0_attn_proj_w"],
                       [(d + half) % HD for d in range(HD)],
                       rope_tables(angles, ([d % half for d in range(HD)], [-1] * half + [1] * half)))
    L["a0_bproj"] = I["L0_attn_proj_b"].reshape(C, 1)
    L["a0_window"] = np.maximum(8.0 * (np.arange(P)[:, None] + (QT - 1) * P - np.arange(WINDOW)[None, :]),
                                0.0).astype(np.float32)
    which, pattern = np.zeros((LOWER_ROWS, 2, 4), np.float32), np.zeros((LOWER_ROWS, 2, N), np.float32)
    which[:LEAST_ROWS, :, 3], pattern[:LEAST_ROWS, 1] = 1.0, -1.0
    token = np.arange(N)
    for j in range(PAIRS_OF_TILES):
        end = (j + 1) * P - 1
        past = np.where(token > end, token - end, 0)
        here = (token > end - P) & (token <= end)
        for part in range(3):
            r = LEAST_ROWS + 9 * j + 3 * part
            for n, distance in enumerate((past - past % 2, past % 2)):
                which[r + n, 0, 3] = which[r + n, 1, part] = 1.0
                pattern[r + n, 0], pattern[r + n, 1] = distance, here
            which[r + 2, 0, part] = which[r + 2, 1, 3] = 1.0
            pattern[r + 2, 0], pattern[r + 2, 1] = past > 0, np.where(here, end - token, 0)
    L["a0_which"], L["a0_pattern"] = which, pattern
    L["a0_steps"] = np.maximum(np.arange(P)[None, :] - np.arange(P)[:, None], 0).astype(mybir.dt.np(BF16))
    L["a0_slopes"] = np.broadcast_to(I["L0_attn_slopes"][None, :], (P, HEADS))
    return L


def lay_gated_mlp(I):
    L = {}
    L["f0_w12"] = np.stack([I["L0_ffn_w1_w"].T, I["L0_ffn_w2_w"].T], 1)
    L["f0_wh"] = np.stack([I[f"L0_ffn_{n}_w"].T.reshape(HT, P, HID).transpose(1, 0, 2) for n in ("h1", "h2")], 1)
    L["f0_w3"] = I["L0_ffn_w3_w"].T.reshape(HT, P, C).transpose(1, 0, 2)
    L["f0_scales"] = np.concatenate([I[f"L0_ffn_{n}_s"].reshape(-1, P).T for n in ("w1", "w2", "h1", "h2", "w3")], 1)
    return L


def lay_ssm(I):
    L = {}
    S = {k[8:]: a for k, a in I.items() if k.startswith("L1_attn_")}
    L["s_wide"] = np.stack([S["proj_W"].T, S["fconv_W"].T, S["bconv_W"].T], 1)
    L["s_wdr"] = S["deltaBC_W"][:DT_RANK].T
    L["s_wbc"] = np.tile(S["deltaBC_W"][DT_RANK:].T, (1, 3))
    L["s_wdt"] = np.tile(S["dt_W"].T, (BRANCHES, 1))
    L["s_cst"] = np.stack([S[n] for n in ("ln_w", "ln_b", "proj_b", "fconv_b", "bconv_b", "dt_b", "D")], 1)
    L["s_alog"] = S["A_log"]
    rows = np.arange(3 * BC)[:, None, None] % BC == np.arange(BC)[None, :, None]
    L["s_select"] = np.broadcast_to(rows, (3 * BC, BC, P)).astype(mybir.dt.np(BF16))
    return L


def lay_moe(I):
    L = {}
    L["m_wr"] = I["L1_ffn_w_router"].T
    L["m_iota"] = np.broadcast_to(np.arange(EXPERTS, dtype=np.float32), (P, TT, EXPERTS))
    L["m_wg"] = I["L1_ffn_w_gate"].T
    L["m_wd"] = I["L1_ffn_w_down"].transpose(2, 0, 1).reshape(MOE_HT, P, EXPERTS * C).transpose(1, 0, 2)
    return L


def lay_query_softmax(I):
    L = {}
    L["q_wqk"] = np.stack([I["L2_attn_Mq"], I["L2_attn_Mk"]], 1)
    L["q_wv"] = I["L2_attn_Mv"]
    place = np.zeros((4, VPAD, 2, 2, 4, VD), np.float32)
    for j in range(QH):
        for d in range(VD):
            place[j % 4, d, j // 4, j // 4, j % 4, d] = 1.0
    L["q_place"] = place.reshape(P, 2, C)
    return L


def lay_sparse(I):
    L = {}
    S = {k[7:]: a for k, a in I.items() if k.startswith("L2_ffn_")}
    L["x_wu"] = S["w_up"].transpose(2, 0, 1)
    L["x_wd"] = S["w_down"].reshape(X_EXPERTS, C, X_INTER // P, P).transpose(3, 0, 2, 1)
    L["x_wau"] = S["a_up"].transpose(2, 0, 1)
    L["x_wad"] = S["a_down"].transpose(2, 0, 1)
    L["x_r1x"] = S["r1_w"][:, :C].T
    L["x_r1s"] = np.zeros((STAT_ROWS, X_ROUTER), np.float32)
    for n, stat in enumerate((2, 3, 1, 4, 0, 5)):
        L["x_r1s"][n // 2 * PART_ROWS + n % 2] = S["r1_w"][:, C + stat]
    pick = np.zeros((4, 2), np.float32)
    pick[0, 0] = pick[1, 1] = 1.0 / C
    pick[2, 1], pick[3, 0] = 1.0, 1.0 / (C - 1)
    L["x_pick"] = np.broadcast_to(pick, (C, 4, 2))
    L["x_r1b"] = S["r1_b"].reshape(X_ROUTER, 1)
    L["x_r2"] = S["r2_w"].T
    L["x_iota"] = np.broadcast_to(np.arange(X_EXPERTS, dtype=np.float32), (P, TT, X_EXPERTS))
    L["x_base"] = (np.arange(X_EXPERTS, dtype=np.float32) * X_CAP).reshape(X_EXPERTS, 1)
    return L


def lay_attention3(I):
    L = {}
    half = HD // 2
    angles = np.power(np.float32(10000.0), np.float32(2.0) * np.arange(half, dtype=np.float32) / np.float32(HD))
    L |= lay_attention("a3", I["L3_attn_w_q"], I["L3_attn_w_k"], I["L3_attn_w_v"], I["L3_attn_w_o"],
                       [d ^ 1 for d in range(HD)],
                       rope_tables(angles, ([d // 2 for d in range(HD)], [-1, 1] * half)))
    L["a3_bproj"] = np.zeros((C, 1), np.float32)
    return L


def lay_choice(I):
    L = {}
    L["c_wr"] = I["L3_ffn_gate_weight"].T
    shift = 30 - 2 * np.arange(SEARCH_STEPS)
    bits = np.arange(1, TRIES + 1)[None, :] << shift[:, None]
    bits[0] = 1 << 30
    unit = (1 << shift).astype(np.float32)
    unit[0] = 0.0
    L["c_bits"] = np.broadcast_to(bits.astype(np.int32), (P, SEARCH_STEPS, TRIES))
    L["c_unit"] = np.broadcast_to(unit, (P, SEARCH_STEPS))
    L["c_ones_b"] = np.ones((P, P), mybir.dt.np(BF16))
    L["c_w1"] = np.concatenate([I["L3_ffn_W1"], I["L3_ffn_Ws1"][None]], 0).transpose(1, 0, 2)
    L["c_w2"] = np.concatenate([I["L3_ffn_W2"], I["L3_ffn_Ws2"][None]], 0) \
        .reshape(CH_ALL, CH_HT, P, C).transpose(2, 0, 1, 3)
    L["c_b1"] = np.concatenate([I["L3_ffn_b1"], I["L3_ffn_bs1"][None]], 0) \
        .reshape(CH_ALL, CH_HT, P).transpose(2, 0, 1)
    part_rows = np.arange(3)[:, None] * PART_AT + np.arange(CH_EXPERTS)[None, :]
    L["c_b2"] = np.zeros((GATE_ROWS, C), np.float32)
    L["c_b2"][part_rows] = I["L3_ffn_b2"]
    L["c_bs2"] = I["L3_ffn_bs2"].reshape(C, 1)
    L["c_select"] = np.zeros((GATE_ROWS, CH_EXPERTS, P), mybir.dt.np(BF16))
    L["c_select"][part_rows, np.arange(CH_EXPERTS)] = 1.0
    return L


def attention0_stage(core, A, xT):
    attention_stage(core, A, xT, "a0", alibi=True, first=True)


def attention3_stage(core, A, xT):
    attention_stage(core, A, xT, "a3", alibi=False, first=False)


STAGES = [(attention0_stage, lay_attention0), (gated_mlp_stage, lay_gated_mlp), (ssm_stage, lay_ssm),
          (moe_stage, lay_moe), (query_softmax_stage, lay_query_softmax), (sparse_stage, lay_sparse),
          (attention3_stage, lay_attention3), (choice_stage, lay_choice)]


def lay_out(I):
    L = {"x": I["L0_attn_x"].reshape(T, C).T,
         "tri": (np.arange(P)[:, None] <= np.arange(P)[None, :]).astype(np.float32),
         "ones": np.ones((P, P), np.float32)}
    for _, lay in STAGES:
        L |= lay(I)
    return L


def network(nc, A, out):
    with ExitStack() as ctx:
        core = Core(nc, ctx)
        xT = core.sb(ctx, "xT", [C, T])
        core.ident = core.sb(ctx, "ident", [P, P])
        core.avg = core.sb(ctx, "avg", [P, P])
        core.eps = core.sb(ctx, "eps", [P, 1])
        core.one = core.sb(ctx, "one", [P, 1])
        core.ones_row = core.sb(ctx, "ones_row", [P, N])
        loaded = core.sem("x_loaded")
        zeroed = core.sem("ident_zeroed")
        with core.block() as block:
            @block.sync
            def _(sp):
                sp.dma_start(xT[:, :], A["x"]).then_inc(loaded, 16)
                sp.wait_ge(loaded, START + 16)

            @block.gpsimd
            def _(pool):
                nc.gpsimd.memset(core.avg[:, :], 1.0 / C)
                nc.gpsimd.memset(core.eps[:, :], LN_EPS)
                nc.gpsimd.memset(core.one[:, :], 1.0)
                nc.gpsimd.memset(core.ones_row[:, :], 1.0)
                nc.gpsimd.memset(core.ident[:, :], 0.0).then_inc(zeroed, 1)
                pool.wait_ge(zeroed, START + 1)
                nc.gpsimd.affine_select(out=core.ident[:, :], in_=core.ident[:, :], compare_op=ALU.not_equal,
                                        fill=1.0, base=0, pattern=[[-1, P]], channel_multiplier=1)
        for stage, _ in STAGES:
            core.run_stage(stage, A, xT)
        layernorm_stage(core, xT, "last_ln")
        stored = core.sem("out_stored")
        with core.block() as block:
            @block.sync
            def _(sp):
                sp.dma_start(out, xT[:, :]).then_inc(stored, 16)
                sp.wait_ge(stored, START + 16)


def kernel(**inputs):
    import concourse.bacc as bacc
    from concourse.bass_utils import run_bass_kernel_spmd

    nc = bacc.Bacc("TRN2", target_bir_lowering=False, num_devices=1)
    arrays, args = {}, {}
    for name, a in lay_out({k: np.asarray(v) for k, v in inputs.items()}).items():
        a = np.ascontiguousarray(a)
        arrays[f"in_{name}"] = a
        args[name] = nc.dram_tensor(f"in_{name}", a.shape, mybir.dt.from_np(a.dtype), kind="ExternalInput").ap()
    out = nc.dram_tensor("out_xT", (C, T), F32, kind="ExternalOutput").ap()
    network(nc, args, out)
    result = run_bass_kernel_spmd(nc, [arrays], core_ids=[0])
    return result.results[0]["out_xT"].T.reshape(B, N, C)
```
